# Optimizing a Trainium2 kernel written in Bass

```python
import numpy as np
import jax
import jax.numpy as jnp

def _softmax(x, axis=-1):
    return jax.nn.softmax(x, axis=axis)

def _gelu(x):
    return jax.nn.gelu(x, approximate=True)

def _silu(x):
    return jax.nn.silu(x)

def _sigmoid(x):
    return jax.nn.sigmoid(x)

def _layernorm(x, axis=-1, eps=1e-05):
    m = jnp.mean(x, axis=axis, keepdims=True)
    v = jnp.var(x, axis=axis, keepdims=True)
    return (x - m) / jnp.sqrt(v + eps)

def _scatter_add(tgt, idx, src, axis=0):
    return tgt.at[idx].add(src)

def _segment_sum(src, seg, n):
    return jax.ops.segment_sum(src, seg, n)
kernel_name = 'mk_xattn_ffn_d4_seqx_r8_e4fb69'

def setup_inputs(seed: int=0):
    np.random.seed(seed)
    _w = jnp.asarray

    def _rec_inputs():
        import jax
        import jax.numpy as jnp
        _rk = jax.random.key(seed)
        x = -7.109e-05 + 0.9999 * jax.random.normal(jax.random.fold_in(_rk, 1), (64, 64, 128), jnp.float32)
        _lenS = 64 - jax.random.randint(jax.random.fold_in(_rk, 7), (64,), 0, max(1, 64 // 4) + 1, jnp.int32)
        _lenS2 = 64 - jax.random.randint(jax.random.fold_in(_rk, 8), (64,), 0, max(1, 64 // 4) + 1, jnp.int32)
        _ctx_768P = jax.random.normal(jax.random.fold_in(_rk, 11), (64, 16, 96), jnp.float32)
        _ctx_768c = jax.random.dirichlet(jax.random.fold_in(_rk, 511), 0.3 * jnp.ones((16,), jnp.float32), (64, 64))
        _ctx_768t = jnp.einsum('bsk,bkd->bsd', _ctx_768c, _ctx_768P)
        _ctx_768t = _ctx_768t * jax.lax.rsqrt(jnp.mean(jnp.square(_ctx_768t)) + 1e-12) * 0.953939
        ctx_768 = 0.000486113 + 1.00014 * (_ctx_768t + 0.3 * jax.random.normal(jax.random.fold_in(_rk, 611), (64, 64, 96), jnp.float32))
        return (x, ctx_768)
    x, ctx_768 = _rec_inputs()

    def _L0_xattn_setup():
        import jax, jax.numpy as jnp
        import numpy as np
        HEADS = 16
        DIM_HEAD = 64
        key = jax.random.key(seed)
        ks = jax.random.split(key, 8)
        B, S, D = (16, 512, 128)
        K, DE = (77, 96)
        inner = HEADS * DIM_HEAD
        hidden_states = jax.random.normal(ks[0], (B, S, D), dtype=jnp.float32)
        encoder_hidden_states = jax.random.normal(ks[1], (B, K, DE), dtype=jnp.float32)
        sc_q = 1.0 / np.sqrt(D)
        sc_kv = 1.0 / np.sqrt(DE)
        sc_o = 1.0 / np.sqrt(inner)
        Wq = jax.random.normal(ks[2], (D, inner), dtype=jnp.float32) * sc_q
        Wk = jax.random.normal(ks[3], (DE, inner), dtype=jnp.float32) * sc_kv
        Wv = jax.random.normal(ks[4], (DE, inner), dtype=jnp.float32) * sc_kv
        Wo = jax.random.normal(ks[5], (inner, D), dtype=jnp.float32) * sc_o
        bo = jax.random.normal(ks[6], (D,), dtype=jnp.float32) * 0.01
        return {'hidden_states': hidden_states, 'encoder_hidden_states': encoder_hidden_states, 'Wq': Wq, 'Wk': Wk, 'Wv': Wv, 'Wo': Wo, 'bo': bo}
    _L0_xattn_all = _L0_xattn_setup()
    _L0_xattn_in = {k: v for k, v in _L0_xattn_all.items() if k in ('Wq', 'Wk', 'Wv', 'Wo', 'bo')}
    del _L0_xattn_all

    def _L0_ffn_setup():
        import jax, jax.numpy as jnp
        import numpy as np
        D_MODEL = 128
        D_FF = 352
        N_EXPERTS = 8
        key = jax.random.key(seed)
        k_in, k1, k2, k3 = jax.random.split(key, 4)
        scale = 0.02
        inputs = jax.random.normal(k_in, (4, N_EXPERTS * 256, D_MODEL), dtype=jnp.float32)
        w1 = jax.random.normal(k1, (N_EXPERTS, D_MODEL, D_FF), dtype=jnp.float32) * scale
        w3 = jax.random.normal(k3, (N_EXPERTS, D_MODEL, D_FF), dtype=jnp.float32) * scale
        w2 = jax.random.normal(k2, (N_EXPERTS, D_FF, D_MODEL), dtype=jnp.float32) * scale
        return {'inputs': inputs, 'w1': w1, 'w3': w3, 'w2': w2}
    _L0_ffn_all = _L0_ffn_setup()
    _L0_ffn_in = {k: v for k, v in _L0_ffn_all.items() if k in ('w1', 'w3', 'w2')}
    del _L0_ffn_all

    def _L1_xattn_setup():
        import jax, jax.numpy as jnp
        import numpy as np
        import math
        E = 128
        EV = 128
        FFN = 512
        DINO = 96
        B, S, P = (64, 64, 32)

        def bitnet_linear(x, W, b):
            w_scale = jnp.maximum(jnp.mean(jnp.abs(W)), 1e-05)
            qW = jnp.sign(W) * (jnp.abs(W) > 0.5 * w_scale).astype(W.dtype)
            i_scale = jnp.maximum(jnp.max(jnp.abs(x)), 1e-08) / 127.0
            qx = jnp.clip(jnp.round(x / i_scale), -128.0, 127.0)
            out = jnp.einsum('...i,oi->...o', qx, qW) * (w_scale * i_scale)
            return out + b
        key = jax.random.key(seed)
        ks = iter(jax.random.split(key, 32))

        def lin_w(fin, fout):
            return jax.random.normal(next(ks), (fout, fin), jnp.float32) * math.sqrt(2.0 / fin)
        return {'text_embeddings': jax.random.normal(next(ks), (B, S, E), jnp.float32), 'dinov2_features': jax.random.normal(next(ks), (B, P, DINO), jnp.float32), 'W_d2v': lin_w(DINO, EV), 'b_d2v': jnp.zeros((EV,), jnp.float32), 'W_img': lin_w(EV, E), 'b_img': jnp.zeros((E,), jnp.float32), 'W_txt': lin_w(E, E), 'b_txt': jnp.zeros((E,), jnp.float32), 'W_att0': lin_w(E, E // 2), 'b_att0': jnp.zeros((E // 2,), jnp.float32), 'W_att1': lin_w(E, E // 2), 'b_att1': jnp.zeros((E // 2,), jnp.float32), 'W_f1': lin_w(2 * E, FFN), 'b_f1': jnp.zeros((FFN,), jnp.float32), 'W_f2': lin_w(FFN, E), 'b_f2': jnp.zeros((E,), jnp.float32)}
    _L1_xattn_all = _L1_xattn_setup()
    _L1_xattn_in = {k: v for k, v in _L1_xattn_all.items() if k in ('W_d2v', 'b_d2v', 'W_img', 'b_img', 'W_txt', 'b_txt', 'W_att0', 'b_att0', 'W_att1', 'b_att1', 'W_f1', 'b_f1', 'W_f2', 'b_f2')}
    del _L1_xattn_all

    def _L1_ffn_setup():
        import jax, jax.numpy as jnp
        import numpy as np
        EMB = 128
        FF = 4 * EMB

        def _ternary(w):
            scale = jnp.maximum(jnp.mean(jnp.abs(w)), 1e-08)
            w_t = jnp.clip(jnp.round(w / scale), -1.0, 1.0)
            return w + jax.lax.stop_gradient(w_t - w)
        key = jax.random.key(seed)
        kx, k1, k2, kb1, kb2 = jax.random.split(key, 5)
        x = jax.random.normal(kx, (4, 256, EMB), dtype=jnp.float32)
        lim1 = 1.0 / np.sqrt(EMB)
        lim2 = 1.0 / np.sqrt(FF)
        W1 = jax.random.uniform(k1, (FF, EMB), jnp.float32, -lim1, lim1)
        b1 = jax.random.uniform(kb1, (FF,), jnp.float32, -lim1, lim1)
        W2 = jax.random.uniform(k2, (EMB, FF), jnp.float32, -lim2, lim2)
        b2 = jax.random.uniform(kb2, (EMB,), jnp.float32, -lim2, lim2)
        return {'x': x, 'W1': W1, 'b1': b1, 'W2': W2, 'b2': b2}
    _L1_ffn_all = _L1_ffn_setup()
    _L1_ffn_in = {k: v for k, v in _L1_ffn_all.items() if k in ('W1', 'b1', 'W2', 'b2')}
    del _L1_ffn_all

    def _L2_xattn_setup():
        import jax, jax.numpy as jnp
        import numpy as np
        N_HEADS = 16
        D_EMBED = 128
        D_CROSS = 96
        D_HEAD = D_EMBED // N_HEADS
        key = jax.random.key(seed)
        ks = jax.random.split(key, 10)
        B, SQ, SKV = (8, 512, 77)
        s_e = 1.0 / np.sqrt(D_EMBED)
        s_c = 1.0 / np.sqrt(D_CROSS)
        return {'x': jax.random.normal(ks[0], (B, SQ, D_EMBED), jnp.float32), 'y': jax.random.normal(ks[1], (B, SKV, D_CROSS), jnp.float32), 'wq': jax.random.normal(ks[2], (D_EMBED, D_EMBED), jnp.float32) * s_e, 'bq': jnp.zeros((D_EMBED,), jnp.float32), 'wk': jax.random.normal(ks[3], (D_CROSS, D_EMBED), jnp.float32) * s_c, 'bk': jnp.zeros((D_EMBED,), jnp.float32), 'wv': jax.random.normal(ks[4], (D_CROSS, D_EMBED), jnp.float32) * s_c, 'bv': jnp.zeros((D_EMBED,), jnp.float32), 'wo': jax.random.normal(ks[5], (D_EMBED, D_EMBED), jnp.float32) * s_e, 'bo': jnp.zeros((D_EMBED,), jnp.float32)}
    _L2_xattn_all = _L2_xattn_setup()
    _L2_xattn_in = {k: v for k, v in _L2_xattn_all.items() if k in ('wq', 'bq', 'wk', 'bk', 'wv', 'bv', 'wo', 'bo')}
    del _L2_xattn_all

    def _L2_ffn_setup():
        import jax, jax.numpy as jnp
        import numpy as np
        H = 128
        NH = 16
        HD = H // NH
        HH = HD // 2
        L = H // 4
        I = int(H * 1.0)
        ER = 7
        TOPK = 2
        BASE = 10000.0
        EPS = 1e-05

        def rmsnorm(x, w):
            norm = jnp.sqrt(jnp.mean(x * x, axis=-1, keepdims=True)) + EPS
            return x / norm * w

        def rope_tables(seq_len):
            inv_freq = 1.0 / BASE ** (jnp.arange(0, HH, 2, dtype=jnp.float32) / HH)
            t = jnp.arange(seq_len, dtype=jnp.float32)
            freqs = jnp.einsum('i,j->ij', t, inv_freq)
            emb = jnp.concatenate([freqs, freqs], axis=-1)
            cos = jnp.cos(emb)[None, :, None, :]
            sin = jnp.sin(emb)[None, :, None, :]
            return (cos, sin)

        def rotate_half(x):
            x1, x2 = jnp.split(x, 2, axis=-1)
            return jnp.concatenate([-x2, x1], axis=-1)

        def silu(x):
            return x * jax.nn.sigmoid(x)

        def mla(xn, W_kvd, W_qd, W_ku, W_qu, W_vu, W_ropeq, W_ropek, W_o):
            B, S, _ = xn.shape
            kv_lat = xn @ W_kvd
            q_lat = xn @ W_qd
            k = (kv_lat @ W_ku).reshape(B, S, NH, HH)
            q = (q_lat @ W_qu).reshape(B, S, NH, HH)
            v = (kv_lat @ W_vu).reshape(B, S, NH, HD)
            q_rope = (q_lat @ W_ropeq).reshape(B, S, NH, HH)
            k_rope = (xn @ W_ropek).reshape(B, S, NH, HH)
            cos, sin = rope_tables(S)
            k_rope = k_rope * cos + rotate_half(k_rope) * sin
            q_rope = q_rope * cos + rotate_half(q_rope) * sin
            kk = jnp.concatenate([k, k_rope], axis=-1)
            qq = jnp.concatenate([q, q_rope], axis=-1)
            scale = 1.0 / jnp.sqrt(jnp.float32(HD))
            scores = jnp.einsum('bqhd,bkhd->bhqk', qq, kk) * scale
            causal = jnp.tril(jnp.ones((S, S), dtype=bool))
            scores = jnp.where(causal[None, None], scores, jnp.finfo(scores.dtype).min)
            probs = jax.nn.softmax(scores, axis=-1)
            y = jnp.einsum('bhqk,bkhd->bqhd', probs, v).reshape(B, S, H)
            return y @ W_o

        def moe(xn, Wg_s, Wu_s, Wd_s, Wg_r, Wu_r, Wd_r, W_router, routing_bias):
            B, S, _ = xn.shape
            xt = xn.reshape(B * S, H)
            shared = silu(xt @ Wg_s) * (xt @ Wu_s) @ Wd_s
            logits = xt @ W_router + routing_bias
            probs = jax.nn.sigmoid(logits)
            scores, idx = jax.lax.top_k(probs, TOPK)
            scores = scores / jnp.sum(scores, axis=-1, keepdims=True)
            wts = jnp.sum(jax.nn.one_hot(idx, ER, dtype=xt.dtype) * scores[..., None], axis=1)
            g = jnp.einsum('th,ehi->tei', xt, Wg_r)
            u = jnp.einsum('th,ehi->tei', xt, Wu_r)
            hmid = silu(g) * u
            combined = jnp.einsum('tei,eih,te->th', hmid, Wd_r, wts)
            return (shared + combined).reshape(B, S, H)
        key = jax.random.key(seed)
        ks = jax.random.split(key, 20)
        s = 0.02
        r = lambda k, shp: jax.random.normal(k, shp, dtype=jnp.float32) * s
        return {'x': jax.random.normal(ks[0], (4, 128, H), dtype=jnp.float32), 'w_ln1': jnp.ones((H,), jnp.float32), 'w_ln2': jnp.ones((H,), jnp.float32), 'W_kvd': r(ks[1], (H, L)), 'W_qd': r(ks[2], (H, L)), 'W_ku': r(ks[3], (L, NH * HH)), 'W_qu': r(ks[4], (L, NH * HH)), 'W_vu': r(ks[5], (L, H)), 'W_ropeq': r(ks[6], (L, H // 2)), 'W_ropek': r(ks[7], (H, H // 2)), 'W_o': r(ks[8], (H, H)), 'Wg_s': r(ks[9], (H, I)), 'Wu_s': r(ks[10], (H, I)), 'Wd_s': r(ks[11], (I, H)), 'Wg_r': r(ks[12], (ER, H, I)), 'Wu_r': r(ks[13], (ER, H, I)), 'Wd_r': r(ks[14], (ER, I, H)), 'W_router': r(ks[15], (H, ER)), 'routing_bias': jnp.zeros((ER,), jnp.float32)}
    _L2_ffn_all = _L2_ffn_setup()
    _L2_ffn_in = {k: v for k, v in _L2_ffn_all.items() if k in ('w_ln1', 'w_ln2', 'W_kvd', 'W_qd', 'W_ku', 'W_qu', 'W_vu', 'W_ropeq', 'W_ropek', 'W_o', 'Wg_s', 'Wu_s', 'Wd_s', 'Wg_r', 'Wu_r', 'Wd_r', 'W_router', 'routing_bias')}
    del _L2_ffn_all

    def _L3_xattn_setup():
        import jax, jax.numpy as jnp
        import numpy as np
        HEADS = 16
        DIM_HEAD = 64
        SCALE = DIM_HEAD ** (-0.5)
        QUERY_DIM = 128
        CONTEXT_DIM = 96
        INNER_DIM = HEADS * DIM_HEAD
        key = jax.random.key(seed)
        ks = jax.random.split(key, 7)
        B, Nq, Nk = (8, 512, 77)
        x = jax.random.normal(ks[0], (B, Nq, QUERY_DIM), dtype=jnp.float32)
        context = jax.random.normal(ks[1], (B, Nk, CONTEXT_DIM), dtype=jnp.float32)
        Wq = jax.random.normal(ks[2], (QUERY_DIM, INNER_DIM), dtype=jnp.float32) * QUERY_DIM ** (-0.5)
        Wk = jax.random.normal(ks[3], (CONTEXT_DIM, INNER_DIM), dtype=jnp.float32) * CONTEXT_DIM ** (-0.5)
        Wv = jax.random.normal(ks[4], (CONTEXT_DIM, INNER_DIM), dtype=jnp.float32) * CONTEXT_DIM ** (-0.5)
        Wo = jax.random.normal(ks[5], (INNER_DIM, QUERY_DIM), dtype=jnp.float32) * INNER_DIM ** (-0.5)
        bo = jnp.zeros((QUERY_DIM,), dtype=jnp.float32)
        return {'x': x, 'context': context, 'Wq': Wq, 'Wk': Wk, 'Wv': Wv, 'Wo': Wo, 'bo': bo}
    _L3_xattn_all = _L3_xattn_setup()
    _L3_xattn_in = {k: v for k, v in _L3_xattn_all.items() if k in ('Wq', 'Wk', 'Wv', 'Wo', 'bo')}
    del _L3_xattn_all

    def _L3_ffn_setup():
        import jax, jax.numpy as jnp
        import numpy as np
        B, S, D, F, E = (4, 256, 128, 512, 8)
        key = jax.random.key(seed)
        ks = jax.random.split(key, 7)
        s1 = 1.0 / np.sqrt(D)
        s2 = 1.0 / np.sqrt(F)
        x = jax.random.normal(ks[0], (B, S, D), dtype=jnp.float32)
        W1 = jax.random.uniform(ks[1], (E, D, F), jnp.float32, -s1, s1)
        b1 = jax.random.uniform(ks[2], (E, F), jnp.float32, -s1, s1)
        W2 = jax.random.uniform(ks[3], (E, F, D), jnp.float32, -s2, s2)
        b2 = jax.random.uniform(ks[4], (E, D), jnp.float32, -s2, s2)
        Wr = jax.random.uniform(ks[5], (D, E), jnp.float32, -s1, s1)
        br = jax.random.uniform(ks[6], (E,), jnp.float32, -s1, s1)
        return {'x': x, 'W1': W1, 'b1': b1, 'W2': W2, 'b2': b2, 'Wr': Wr, 'br': br}
    _L3_ffn_all = _L3_ffn_setup()
    _L3_ffn_in = {k: v for k, v in _L3_ffn_all.items() if k in ('W1', 'b1', 'W2', 'b2', 'Wr', 'br')}
    del _L3_ffn_all
    return {'x': x, 'ctx_768': ctx_768, 'L0_xattn_Wq': _L0_xattn_in['Wq'], 'L0_xattn_Wk': _L0_xattn_in['Wk'], 'L0_xattn_Wv': _L0_xattn_in['Wv'], 'L0_xattn_Wo': _L0_xattn_in['Wo'], 'L0_xattn_bo': _L0_xattn_in['bo'], 'L0_ffn_w1': _L0_ffn_in['w1'], 'L0_ffn_w3': _L0_ffn_in['w3'], 'L0_ffn_w2': _L0_ffn_in['w2'], 'L1_xattn_W_d2v': _L1_xattn_in['W_d2v'], 'L1_xattn_b_d2v': _L1_xattn_in['b_d2v'], 'L1_xattn_W_img': _L1_xattn_in['W_img'], 'L1_xattn_b_img': _L1_xattn_in['b_img'], 'L1_xattn_W_txt': _L1_xattn_in['W_txt'], 'L1_xattn_b_txt': _L1_xattn_in['b_txt'], 'L1_xattn_W_att0': _L1_xattn_in['W_att0'], 'L1_xattn_b_att0': _L1_xattn_in['b_att0'], 'L1_xattn_W_att1': _L1_xattn_in['W_att1'], 'L1_xattn_b_att1': _L1_xattn_in['b_att1'], 'L1_xattn_W_f1': _L1_xattn_in['W_f1'], 'L1_xattn_b_f1': _L1_xattn_in['b_f1'], 'L1_xattn_W_f2': _L1_xattn_in['W_f2'], 'L1_xattn_b_f2': _L1_xattn_in['b_f2'], 'L1_ffn_W1': _L1_ffn_in['W1'], 'L1_ffn_b1': _L1_ffn_in['b1'], 'L1_ffn_W2': _L1_ffn_in['W2'], 'L1_ffn_b2': _L1_ffn_in['b2'], 'L2_xattn_wq': _L2_xattn_in['wq'], 'L2_xattn_bq': _L2_xattn_in['bq'], 'L2_xattn_wk': _L2_xattn_in['wk'], 'L2_xattn_bk': _L2_xattn_in['bk'], 'L2_xattn_wv': _L2_xattn_in['wv'], 'L2_xattn_bv': _L2_xattn_in['bv'], 'L2_xattn_wo': _L2_xattn_in['wo'], 'L2_xattn_bo': _L2_xattn_in['bo'], 'L2_ffn_w_ln1': _L2_ffn_in['w_ln1'], 'L2_ffn_w_ln2': _L2_ffn_in['w_ln2'], 'L2_ffn_W_kvd': _L2_ffn_in['W_kvd'], 'L2_ffn_W_qd': _L2_ffn_in['W_qd'], 'L2_ffn_W_ku': _L2_ffn_in['W_ku'], 'L2_ffn_W_qu': _L2_ffn_in['W_qu'], 'L2_ffn_W_vu': _L2_ffn_in['W_vu'], 'L2_ffn_W_ropeq': _L2_ffn_in['W_ropeq'], 'L2_ffn_W_ropek': _L2_ffn_in['W_ropek'], 'L2_ffn_W_o': _L2_ffn_in['W_o'], 'L2_ffn_Wg_s': _L2_ffn_in['Wg_s'], 'L2_ffn_Wu_s': _L2_ffn_in['Wu_s'], 'L2_ffn_Wd_s': _L2_ffn_in['Wd_s'], 'L2_ffn_Wg_r': _L2_ffn_in['Wg_r'], 'L2_ffn_Wu_r': _L2_ffn_in['Wu_r'], 'L2_ffn_Wd_r': _L2_ffn_in['Wd_r'], 'L2_ffn_W_router': _L2_ffn_in['W_router'], 'L2_ffn_routing_bias': _L2_ffn_in['routing_bias'], 'L3_xattn_Wq': _L3_xattn_in['Wq'], 'L3_xattn_Wk': _L3_xattn_in['Wk'], 'L3_xattn_Wv': _L3_xattn_in['Wv'], 'L3_xattn_Wo': _L3_xattn_in['Wo'], 'L3_xattn_bo': _L3_xattn_in['bo'], 'L3_ffn_W1': _L3_ffn_in['W1'], 'L3_ffn_b1': _L3_ffn_in['b1'], 'L3_ffn_W2': _L3_ffn_in['W2'], 'L3_ffn_b2': _L3_ffn_in['b2'], 'L3_ffn_Wr': _L3_ffn_in['Wr'], 'L3_ffn_br': _L3_ffn_in['br']}

def reference(x, ctx_768, L0_xattn_Wq, L0_xattn_Wk, L0_xattn_Wv, L0_xattn_Wo, L0_xattn_bo, L0_ffn_w1, L0_ffn_w3, L0_ffn_w2, L1_xattn_W_d2v, L1_xattn_b_d2v, L1_xattn_W_img, L1_xattn_b_img, L1_xattn_W_txt, L1_xattn_b_txt, L1_xattn_W_att0, L1_xattn_b_att0, L1_xattn_W_att1, L1_xattn_b_att1, L1_xattn_W_f1, L1_xattn_b_f1, L1_xattn_W_f2, L1_xattn_b_f2, L1_ffn_W1, L1_ffn_b1, L1_ffn_W2, L1_ffn_b2, L2_xattn_wq, L2_xattn_bq, L2_xattn_wk, L2_xattn_bk, L2_xattn_wv, L2_xattn_bv, L2_xattn_wo, L2_xattn_bo, L2_ffn_w_ln1, L2_ffn_w_ln2, L2_ffn_W_kvd, L2_ffn_W_qd, L2_ffn_W_ku, L2_ffn_W_qu, L2_ffn_W_vu, L2_ffn_W_ropeq, L2_ffn_W_ropek, L2_ffn_W_o, L2_ffn_Wg_s, L2_ffn_Wu_s, L2_ffn_Wd_s, L2_ffn_Wg_r, L2_ffn_Wu_r, L2_ffn_Wd_r, L2_ffn_W_router, L2_ffn_routing_bias, L3_xattn_Wq, L3_xattn_Wk, L3_xattn_Wv, L3_xattn_Wo, L3_xattn_bo, L3_ffn_W1, L3_ffn_b1, L3_ffn_W2, L3_ffn_b2, L3_ffn_Wr, L3_ffn_br):
    import jax
    import jax.numpy as jnp

    def _L0_xattn_ref(hidden_states, encoder_hidden_states, Wq, Wk, Wv, Wo, bo):
        import jax, jax.numpy as jnp
        import numpy as np
        HEADS = 16
        DIM_HEAD = 64
        B, S, D = hidden_states.shape
        K = encoder_hidden_states.shape[1]
        H, Dh = (HEADS, DIM_HEAD)
        scale = 1.0 / np.sqrt(Dh)
        q = hidden_states @ Wq
        k = encoder_hidden_states @ Wk
        v = encoder_hidden_states @ Wv
        q = q.reshape(B, S, H, Dh).transpose(0, 2, 1, 3)
        k = k.reshape(B, K, H, Dh).transpose(0, 2, 1, 3)
        v = v.reshape(B, K, H, Dh).transpose(0, 2, 1, 3)
        scores = jnp.einsum('bhsd,bhkd->bhsk', q, k) * scale
        probs = jax.nn.softmax(scores, axis=-1)
        out = jnp.einsum('bhsk,bhkd->bhsd', probs, v)
        out = out.transpose(0, 2, 1, 3).reshape(B, S, H * Dh)
        out = out @ Wo + bo
        return out

    def _L0_ffn_ref(inputs, w1, w3, w2):
        import jax, jax.numpy as jnp
        import numpy as np
        D_MODEL = 128
        D_FF = 352
        N_EXPERTS = 8
        B, T, D = inputs.shape
        E = w1.shape[0]
        C = T // E
        x = inputs.reshape(B, E, C, D)
        gate = jnp.einsum('becd,edf->becf', x, w1)
        up = jnp.einsum('becd,edf->becf', x, w3)
        h = jax.nn.silu(gate) * up
        out = jnp.einsum('becf,efd->becd', h, w2)
        return out.reshape(B, T, D)

    def _L1_xattn_ref(text_embeddings, dinov2_features, W_d2v, b_d2v, W_img, b_img, W_txt, b_txt, W_att0, b_att0, W_att1, b_att1, W_f1, b_f1, W_f2, b_f2):
        import jax, jax.numpy as jnp
        import numpy as np
        import math
        E = 128
        EV = 128
        FFN = 512
        DINO = 96
        B, S, P = (64, 64, 32)

        def bitnet_linear(x, W, b):
            w_scale = jnp.maximum(jnp.mean(jnp.abs(W)), 1e-05)
            qW = jnp.sign(W) * (jnp.abs(W) > 0.5 * w_scale).astype(W.dtype)
            i_scale = jnp.maximum(jnp.max(jnp.abs(x)), 1e-08) / 127.0
            qx = jnp.clip(jnp.round(x / i_scale), -128.0, 127.0)
            out = jnp.einsum('...i,oi->...o', qx, qW) * (w_scale * i_scale)
            return out + b
        b, s, e = text_embeddings.shape
        vis = bitnet_linear(dinov2_features, W_d2v, b_d2v)
        image_embeds = bitnet_linear(vis, W_img, b_img)
        fused = bitnet_linear(text_embeddings, W_txt, b_txt)
        inv_sqrt_e = 1.0 / math.sqrt(e)
        for Wa, ba in ((W_att0, b_att0), (W_att1, b_att1)):
            kv = bitnet_linear(image_embeds, Wa, ba)
            k = jnp.concatenate([kv, kv], axis=-1)
            scores = jnp.einsum('bse,bpe->bsp', fused, k) * inv_sqrt_e
            attn = jax.nn.softmax(scores, axis=-1)
            fused = fused + 0.1 * jnp.einsum('bsp,bpe->bse', attn, k)
        avg_img = jnp.mean(image_embeds, axis=1, keepdims=True)
        concatenated = jnp.concatenate([fused, jnp.broadcast_to(avg_img, (b, s, e))], axis=-1)
        h = jax.nn.relu(bitnet_linear(concatenated, W_f1, b_f1))
        return bitnet_linear(h, W_f2, b_f2)

    def _L1_ffn_ref(x, W1, b1, W2, b2):
        import jax, jax.numpy as jnp
        import numpy as np
        EMB = 128
        FF = 4 * EMB

        def _ternary(w):
            scale = jnp.maximum(jnp.mean(jnp.abs(w)), 1e-08)
            w_t = jnp.clip(jnp.round(w / scale), -1.0, 1.0)
            return w + jax.lax.stop_gradient(w_t - w)
        h = jnp.einsum('bsd,fd->bsf', x, _ternary(W1)) + b1
        h = jax.nn.gelu(h, approximate=False)
        out = jnp.einsum('bsf,df->bsd', h, _ternary(W2)) + b2
        return out

    def _L2_xattn_ref(x, y, wq, bq, wk, bk, wv, bv, wo, bo):
        import jax, jax.numpy as jnp
        import numpy as np
        N_HEADS = 16
        D_EMBED = 128
        D_CROSS = 96
        D_HEAD = D_EMBED // N_HEADS
        B, SQ, _ = x.shape
        SKV = y.shape[1]
        q = (x @ wq + bq).reshape(B, SQ, N_HEADS, D_HEAD)
        k = (y @ wk + bk).reshape(B, SKV, N_HEADS, D_HEAD)
        v = (y @ wv + bv).reshape(B, SKV, N_HEADS, D_HEAD)
        scores = jnp.einsum('bqhd,bkhd->bhqk', q, k) / jnp.sqrt(jnp.asarray(D_HEAD, x.dtype))
        attn = jax.nn.softmax(scores, axis=-1)
        out = jnp.einsum('bhqk,bkhd->bqhd', attn, v).reshape(B, SQ, D_EMBED)
        return out @ wo + bo

    def _L2_ffn_ref(x, w_ln1, w_ln2, W_kvd, W_qd, W_ku, W_qu, W_vu, W_ropeq, W_ropek, W_o, Wg_s, Wu_s, Wd_s, Wg_r, Wu_r, Wd_r, W_router, routing_bias):
        import jax, jax.numpy as jnp
        import numpy as np
        H = 128
        NH = 16
        HD = H // NH
        HH = HD // 2
        L = H // 4
        I = int(H * 1.0)
        ER = 7
        TOPK = 2
        BASE = 10000.0
        EPS = 1e-05

        def rmsnorm(x, w):
            norm = jnp.sqrt(jnp.mean(x * x, axis=-1, keepdims=True)) + EPS
            return x / norm * w

        def rope_tables(seq_len):
            inv_freq = 1.0 / BASE ** (jnp.arange(0, HH, 2, dtype=jnp.float32) / HH)
            t = jnp.arange(seq_len, dtype=jnp.float32)
            freqs = jnp.einsum('i,j->ij', t, inv_freq)
            emb = jnp.concatenate([freqs, freqs], axis=-1)
            cos = jnp.cos(emb)[None, :, None, :]
            sin = jnp.sin(emb)[None, :, None, :]
            return (cos, sin)

        def rotate_half(x):
            x1, x2 = jnp.split(x, 2, axis=-1)
            return jnp.concatenate([-x2, x1], axis=-1)

        def silu(x):
            return x * jax.nn.sigmoid(x)

        def mla(xn, W_kvd, W_qd, W_ku, W_qu, W_vu, W_ropeq, W_ropek, W_o):
            B, S, _ = xn.shape
            kv_lat = xn @ W_kvd
            q_lat = xn @ W_qd
            k = (kv_lat @ W_ku).reshape(B, S, NH, HH)
            q = (q_lat @ W_qu).reshape(B, S, NH, HH)
            v = (kv_lat @ W_vu).reshape(B, S, NH, HD)
            q_rope = (q_lat @ W_ropeq).reshape(B, S, NH, HH)
            k_rope = (xn @ W_ropek).reshape(B, S, NH, HH)
            cos, sin = rope_tables(S)
            k_rope = k_rope * cos + rotate_half(k_rope) * sin
            q_rope = q_rope * cos + rotate_half(q_rope) * sin
            kk = jnp.concatenate([k, k_rope], axis=-1)
            qq = jnp.concatenate([q, q_rope], axis=-1)
            scale = 1.0 / jnp.sqrt(jnp.float32(HD))
            scores = jnp.einsum('bqhd,bkhd->bhqk', qq, kk) * scale
            causal = jnp.tril(jnp.ones((S, S), dtype=bool))
            scores = jnp.where(causal[None, None], scores, jnp.finfo(scores.dtype).min)
            probs = jax.nn.softmax(scores, axis=-1)
            y = jnp.einsum('bhqk,bkhd->bqhd', probs, v).reshape(B, S, H)
            return y @ W_o

        def moe(xn, Wg_s, Wu_s, Wd_s, Wg_r, Wu_r, Wd_r, W_router, routing_bias):
            B, S, _ = xn.shape
            xt = xn.reshape(B * S, H)
            shared = silu(xt @ Wg_s) * (xt @ Wu_s) @ Wd_s
            logits = xt @ W_router + routing_bias
            probs = jax.nn.sigmoid(logits)
            scores, idx = jax.lax.top_k(probs, TOPK)
            scores = scores / jnp.sum(scores, axis=-1, keepdims=True)
            wts = jnp.sum(jax.nn.one_hot(idx, ER, dtype=xt.dtype) * scores[..., None], axis=1)
            g = jnp.einsum('th,ehi->tei', xt, Wg_r)
            u = jnp.einsum('th,ehi->tei', xt, Wu_r)
            hmid = silu(g) * u
            combined = jnp.einsum('tei,eih,te->th', hmid, Wd_r, wts)
            return (shared + combined).reshape(B, S, H)
        x = x + mla(rmsnorm(x, w_ln1), W_kvd, W_qd, W_ku, W_qu, W_vu, W_ropeq, W_ropek, W_o)
        x = x + moe(rmsnorm(x, w_ln2), Wg_s, Wu_s, Wd_s, Wg_r, Wu_r, Wd_r, W_router, routing_bias)
        return x

    def _L3_xattn_ref(x, context, Wq, Wk, Wv, Wo, bo):
        import jax, jax.numpy as jnp
        import numpy as np
        HEADS = 16
        DIM_HEAD = 64
        SCALE = DIM_HEAD ** (-0.5)
        QUERY_DIM = 128
        CONTEXT_DIM = 96
        INNER_DIM = HEADS * DIM_HEAD
        B, Nq, _ = x.shape
        Nk = context.shape[1]
        q = x @ Wq
        k = context @ Wk
        v = context @ Wv
        q = q.reshape(B, Nq, HEADS, DIM_HEAD).transpose(0, 2, 1, 3)
        k = k.reshape(B, Nk, HEADS, DIM_HEAD).transpose(0, 2, 1, 3)
        v = v.reshape(B, Nk, HEADS, DIM_HEAD).transpose(0, 2, 1, 3)
        sim = jnp.einsum('bhid,bhjd->bhij', q, k) * SCALE
        attn = jax.nn.softmax(sim, axis=-1)
        out = jnp.einsum('bhij,bhjd->bhid', attn, v)
        out = out.transpose(0, 2, 1, 3).reshape(B, Nq, INNER_DIM)
        return out @ Wo + bo

    def _L3_ffn_ref(x, W1, b1, W2, b2, Wr, br):
        import jax, jax.numpy as jnp
        import numpy as np
        B, S, D, F, E = (4, 256, 128, 512, 8)
        b, s, d = x.shape
        e = Wr.shape[1]
        logits = x @ Wr + br
        idx = jnp.argmax(logits, axis=-1)
        probs = jax.nn.softmax(logits, axis=-1)
        gates = jnp.take_along_axis(probs, idx[..., None], axis=-1)[..., 0]
        xf = x.reshape(-1, d)
        idxf = idx.reshape(-1)
        gf = gates.reshape(-1)
        out = jnp.zeros_like(xf)
        for ei in range(e):
            h = jax.nn.gelu(xf @ W1[ei] + b1[ei], approximate=False)
            y = h @ W2[ei] + b2[ei]
            mask = (idxf == ei).astype(xf.dtype)
            out = out + y * (gf * mask)[:, None]
        return out.reshape(b, s, d)
    x = x + _L0_xattn_ref(_layernorm(x, axis=-1), ctx_768, L0_xattn_Wq, L0_xattn_Wk, L0_xattn_Wv, L0_xattn_Wo, L0_xattn_bo)
    x = x + _L0_ffn_ref(_layernorm(x, axis=-1), L0_ffn_w1, L0_ffn_w3, L0_ffn_w2)
    x = x + _L1_xattn_ref(_layernorm(x, axis=-1), ctx_768, L1_xattn_W_d2v, L1_xattn_b_d2v, L1_xattn_W_img, L1_xattn_b_img, L1_xattn_W_txt, L1_xattn_b_txt, L1_xattn_W_att0, L1_xattn_b_att0, L1_xattn_W_att1, L1_xattn_b_att1, L1_xattn_W_f1, L1_xattn_b_f1, L1_xattn_W_f2, L1_xattn_b_f2)
    x = x + _L1_ffn_ref(_layernorm(x, axis=-1), L1_ffn_W1, L1_ffn_b1, L1_ffn_W2, L1_ffn_b2)
    x = x + _L2_xattn_ref(_layernorm(x, axis=-1), ctx_768, L2_xattn_wq, L2_xattn_bq, L2_xattn_wk, L2_xattn_bk, L2_xattn_wv, L2_xattn_bv, L2_xattn_wo, L2_xattn_bo)
    x = x + _L2_ffn_ref(_layernorm(x, axis=-1), L2_ffn_w_ln1, L2_ffn_w_ln2, L2_ffn_W_kvd, L2_ffn_W_qd, L2_ffn_W_ku, L2_ffn_W_qu, L2_ffn_W_vu, L2_ffn_W_ropeq, L2_ffn_W_ropek, L2_ffn_W_o, L2_ffn_Wg_s, L2_ffn_Wu_s, L2_ffn_Wd_s, L2_ffn_Wg_r, L2_ffn_Wu_r, L2_ffn_Wd_r, L2_ffn_W_router, L2_ffn_routing_bias)
    x = x + _L3_xattn_ref(_layernorm(x, axis=-1), ctx_768, L3_xattn_Wq, L3_xattn_Wk, L3_xattn_Wv, L3_xattn_Wo, L3_xattn_bo)
    x = x + _L3_ffn_ref(_layernorm(x, axis=-1), L3_ffn_W1, L3_ffn_b1, L3_ffn_W2, L3_ffn_b2, L3_ffn_Wr, L3_ffn_br)
    return x

_drawn_inputs = setup_inputs


def setup_inputs(seed=0):
    import zlib

    import numpy as np

    out = dict(_drawn_inputs(seed))
    spreads = {'L1_xattn_b_d2v': (0.0, 0.273),
     'L1_xattn_b_img': (0.0, 0.1),
     'L1_xattn_b_txt': (0.0, 0.1),
     'L1_xattn_b_att0': (0.0, 0.8),
     'L1_xattn_b_att1': (0.0, 0.8),
     'L1_xattn_b_f1': (0.0, 0.1),
     'L1_xattn_b_f2': (0.0, 0.1),
     'L2_xattn_bq': (0.0, 0.8),
     'L2_xattn_bk': (0.0, 2.0),
     'L2_xattn_bv': (0.0, 0.8),
     'L2_xattn_bo': (0.0, 2.0),
     'L2_ffn_w_ln1': (1.0, 0.6),
     'L2_ffn_w_ln2': (1.0, 0.6),
     'L2_ffn_routing_bias': (0.0, 0.8),
     'L3_xattn_bo': (0.0, 2.0)}
    factors = {'L0_xattn_bo': 5.126,
     'L0_ffn_w1': 5.349,
     'L0_ffn_w3': 5.378,
     'L0_ffn_w2': 5.323,
     'L1_xattn_W_att0': 3.101,
     'L1_xattn_W_att1': 3.192,
     'L1_ffn_b1': 8.0,
     'L1_ffn_b2': 38.689,
     'L2_xattn_wq': 8.0,
     'L2_xattn_wk': 8.0,
     'L2_xattn_wv': 8.0,
     'L2_xattn_wo': 8.0,
     'L2_ffn_W_kvd': 8.0,
     'L2_ffn_W_qd': 8.0,
     'L2_ffn_W_ku': 8.0,
     'L2_ffn_W_qu': 8.0,
     'L2_ffn_W_vu': 8.0,
     'L2_ffn_W_ropeq': 8.0,
     'L2_ffn_W_ropek': 8.0,
     'L2_ffn_W_o': 8.0,
     'L2_ffn_Wg_s': 8.0,
     'L2_ffn_Wu_s': 8.0,
     'L2_ffn_Wd_s': 8.0,
     'L2_ffn_Wg_r': 8.0,
     'L2_ffn_Wu_r': 8.0,
     'L2_ffn_Wd_r': 8.0,
     'L2_ffn_W_router': 8.0,
     'L3_xattn_Wq': 8.0,
     'L3_xattn_Wk': 8.0,
     'L3_xattn_Wv': 8.0,
     'L3_xattn_Wo': 8.0,
     'L3_ffn_W1': 8.0,
     'L3_ffn_b1': 64.0,
     'L3_ffn_W2': 8.0,
     'L3_ffn_b2': 200.0,
     'L3_ffn_Wr': 8.0,
     'L3_ffn_br': 22.65}
    for name, (base, spread) in spreads.items():
        noise = np.random.default_rng([zlib.crc32(name.encode()), seed]).standard_normal(out[name].shape)
        drawn = base * np.exp(spread * noise) if base else spread * noise
        out[name] = jnp.asarray(drawn.astype(out[name].dtype))
    for name, factor in factors.items():
        out[name] = (out[name] * factor).astype(out[name].dtype)
    return out
```

```python
from contextlib import ExitStack

import concourse.bass as bass
from concourse import mybir

F32 = mybir.dt.float32
BF16 = mybir.dt.bfloat16
ALU = mybir.AluOpType
ACT = mybir.ActivationFunctionType
AX = mybir.AxisListType
RMAX = bass.bass_isa.ReduceOp.max
RADD = bass.bass_isa.ReduceOp.add

P = 128
D = 128
C = 96
BATCH, SEQ = 64, 64
TOK = BATCH * SEQ
TILES = TOK // P
H = 16
GT = 2 * P
GROUPS = TOK // GT
UNROLL = 4
TRIPS = TILES // UNROLL
LN_EPS = 1e-5


class Signals:

    live = []

    @classmethod
    def new(cls, nc, name):
        sem = nc.alloc_semaphore(name)
        cls.live.append(sem)
        return sem

    @classmethod
    def retire(cls, nc):
        nc.all_engine_barrier()
        nc.clear_and_free_semaphores(cls.live)
        nc.all_engine_barrier()
        cls.live = []


def after(eng, sem, count):
    if not isinstance(count, int) or count > 0:
        eng.wait_ge(sem, count)


def over_tiles(eng, slot):
    for s in range(UNROLL):
        slot(s, s)
    with eng.Fori(1, TRIPS - 1) as i:
        for s in range(UNROLL):
            slot(i * UNROLL + s, s)
    for s in range(UNROLL):
        slot(TILES - UNROLL + s, s)


def is_last(t, n=1):
    return isinstance(t, int) and t >= TILES - n


class Core:

    def __init__(self, nc, ctx, dram):
        self.nc, self.dram = nc, dram

        def sb(name, shape, dt=F32):
            return ctx.enter_context(nc.sbuf_tensor(name, shape, dt))

        self.x = sb("x", [P, TILES, D])
        self.ctxT = sb("ctxT", [C, TOK])
        self.ctx2 = sb("ctx2", [P, BATCH, C])
        self.stats = sb("stats", [P, TILES, 6])
        self.mean = sb("mean", [P, TILES])
        self.var = sb("var", [P, TILES])
        self.rstd = sb("rstd", [P, TILES])
        self.tmp = sb("tmp", [P, TILES])
        self.tmp2 = sb("tmp2", [P, TILES])
        self.eps = sb("eps", [P, 1])
        self.ident = sb("ident", [P, P])
        self.identb = sb("identb", [P, P], BF16)
        self.ones = sb("ones", [P, P])
        self.even_words, self.odd_words = 4096 + 256, 8704 + 256
        self.even = sb("even", [P, self.even_words])
        self.odd = sb("odd", [P, self.odd_words])
        self.ps = [ctx.enter_context(nc.psum_tensor(f"bank{2 * i}_{2 * i + 1}", [P, 2, 512], F32))
                   for i in range(3)]
        self.r6 = ctx.enter_context(nc.psum_tensor("bank6", [P, 512], F32))
        self.r7 = ctx.enter_context(nc.psum_tensor("bank7", [P, 512], F32))
        self.load_even = ctx.enter_context(nc.semaphore("load_even"))
        self.load_odd = ctx.enter_context(nc.semaphore("load_odd"))
        self.loads = {"even": 0, "odd": 0}

    def load(self, eng, side, out, in_):
        sem = self.load_even if side == "even" else self.load_odd
        self.loads[side] += 16
        eng.dma_start(out, in_).then_inc(sem, 16)


def row(ap, n):
    return ap.rearrange("(a n) -> a n", a=1)



class NormSems:
    def __init__(self, nc, ctx, tag):
        self.chain = Signals.new(nc, f"{tag}_stat_step")
        self.root = Signals.new(nc, f"{tag}_root_ready")
        self.ready = Signals.new(nc, f"{tag}_rstd_ready")


def norm_stats_vector(dve, k, n, rms=False):
    me, mo = k.stats[:, :, 1], k.stats[:, :, 4]
    step = 0

    def link(ins):
        nonlocal step
        step += 1
        ins.then_inc(n.chain, 1)
        dve.wait_ge(n.chain, step)

    link(dve.tensor_tensor(k.mean[:, :], me, mo, ALU.add))
    link(dve.tensor_tensor(k.tmp[:, :], me, mo, ALU.subtract))
    link(dve.tensor_scalar(k.mean[:, :], k.mean[:, :], 0.5, None, ALU.mult))
    link(dve.tensor_tensor(k.tmp[:, :], k.tmp[:, :], k.tmp[:, :], ALU.mult))
    link(dve.tensor_tensor(k.var[:, :], k.stats[:, :, 2], k.stats[:, :, 5], ALU.add))
    link(dve.tensor_scalar(k.tmp[:, :], k.tmp[:, :], 0.25, None, ALU.mult))
    if rms:
        link(dve.scalar_tensor_tensor(k.var[:, :], k.var[:, :], 1.0 / D, k.tmp[:, :], ALU.mult, ALU.add))
        link(dve.tensor_tensor(k.tmp[:, :], k.mean[:, :], k.mean[:, :], ALU.mult))
        dve.tensor_tensor(k.var[:, :], k.var[:, :], k.tmp[:, :], ALU.add).then_inc(n.chain, 1)
        dve.wait_ge(n.root, 1)
        link_at = step + 1
        dve.tensor_scalar(k.tmp[:, :], k.tmp2[:, :], LN_EPS, None, ALU.add).then_inc(n.chain, 1)
        dve.wait_ge(n.chain, link_at + 1)
        dve.reciprocal(k.rstd[:, :], k.tmp[:, :]).then_inc(n.ready, 1)
    else:
        dve.scalar_tensor_tensor(k.var[:, :], k.var[:, :], 1.0 / D, k.tmp[:, :], ALU.mult,
                                 ALU.add).then_inc(n.chain, 1)
        dve.wait_ge(n.root, 1)
        dve.reciprocal(k.rstd[:, :], k.tmp2[:, :]).then_inc(n.ready, 1)
    dve.wait_ge(n.ready, 1)


NORM_STEPS, RMS_STEPS = 7, 9


def norm_root_scalar(act, k, n, rms=False):
    act.wait_ge(n.chain, RMS_STEPS if rms else NORM_STEPS)
    act.activation(k.tmp2[:, :], k.var[:, :], ACT.Sqrt,
                   bias=0.0 if rms else k.eps[:, 0:1]).then_inc(n.root, 1)


def normalise(dve, k, out, t):
    return dve.tensor_scalar(out, k.x[:, bass.ds(t, 1), :], k.mean[:, bass.ds(t, 1)],
                             k.rstd[:, bass.ds(t, 1)], ALU.subtract, ALU.mult)



class Attention:

    def __init__(self, k, ctx, tag, kc, vc, scale, narrow=False):
        nc = k.nc
        self.k, self.kc, self.vc, self.scale, self.narrow = k, kc, vc, scale, narrow

        def sb(name, shape, dt=F32):
            return ctx.enter_context(nc.sbuf_tensor(f"{tag}_{name}", shape, dt))

        def sem(name):
            return Signals.new(nc, f"{tag}_{name}")

        self.qh = [sb(f"qh{i}", [kc, H, P if narrow else GT]) for i in range(2)]
        self.keys = [sb(f"keys{i}", [kc, P]) for i in range(2)]
        self.values = [sb(f"values{i}", [P, 2, vc]) for i in range(2)]
        if not narrow:
            self.xn = [sb(f"xn{i}", [P, 2, D]) for i in range(2)]
            self.xnT = [sb(f"xnT{i}", [D, GT]) for i in range(2)]
        self.prob = [sb(f"prob{i}", [P, H, SEQ]) for i in range(2)]
        self.probT = sb("probT", [P, H // 2, P])
        self.oT = sb("oT", [vc, H, P])
        self.top = [sb(f"top{i}", [P, H]) for i in range(2)]
        self.total = [sb(f"total{i}", [P, H]) for i in range(2)]
        self.share = [sb(f"share{i}", [P, H]) for i in range(2)]
        self.wo = sb("wo", [vc, H, D])
        self.S, self.T, self.O = k.ps
        self.norm = NormSems(nc, ctx, tag)
        self.xn_ready = sem("xn_ready")
        self.xnT_done = sem("xnT_done")
        self.xnT_ready = sem("xnT_ready")
        self.keys_ready = sem("keys_ready")
        self.values_ready = sem("values_ready")
        self.scores_done = sem("scores_done")
        self.top_ready = sem("top_ready")
        self.shifted = sem("shifted")
        self.exp_ready = sem("exp_ready")
        self.total_ready = sem("total_ready")
        self.share_ready = sem("share_ready")
        self.prob_ready = sem("prob_ready")
        self.turned = sem("turned")
        self.probT_ready = sem("probT_ready")
        self.weighed = sem("weighed")
        self.o0_ready = sem("o0_ready")
        self.o1_ready = sem("o1_ready")
        self.projected = sem("projected")
        self.updated = sem("updated")
        self.stats_done = sem("stats_done")
        self.q6_done, self.q7_done = sem("q6_done"), sem("q7_done")
        self.q6_ready, self.q7_ready = sem("q6_ready"), sem("q7_ready")


def half(u):
    return (u // 2) % 2, u % 2


def scores_tensor(pe, a, u, s, mask=None):
    g, tt = half(s)
    if a.narrow:
        g, tt = s % 2, 0
    pe.wait_ge(a.keys_ready, u + 1)
    after(pe, a.shifted, u)
    first = mask is None
    if mask is not None:
        for j in range(2):
            pe.matmul(a.S[:, j, :], a.k.identb[:, :], mask, start=True, stop=True)
    for h in range(H):
        for b in range(2):
            last = pe.matmul(a.S[b * SEQ:(b + 1) * SEQ, h // 8, (h % 8) * SEQ:(h % 8 + 1) * SEQ],
                             a.qh[g][:, h, tt * P + b * SEQ:tt * P + (b + 1) * SEQ],
                             a.keys[s % 2][:, b * SEQ:(b + 1) * SEQ], start=first, stop=True,
                             skip_group_check=not first)
    last.then_inc(a.scores_done, 1)


def turn_tensor(pe, a, t, s):
    pe.wait_ge(a.prob_ready, t + 1)
    after(pe, a.o1_ready, t)
    for p in range(H // 2):
        last = pe.transpose(a.T[:, p // 4, (p % 4) * P:(p % 4 + 1) * P],
                            a.prob[s % 2][:, 2 * p:2 * p + 2, :].rearrange("p h k -> p (h k)"),
                            a.k.ident[:, :])
    last.then_inc(a.turned, 1)


def weigh_tensor(pe, a, t, s):
    pe.wait_ge(a.probT_ready, t + 1)
    if a.narrow:
        pe.wait_ge(a.values_in[s % 2], 64 * ((t - s % 2) // 2 + 1))
    else:
        pe.wait_ge(a.values_ready, t + 1)
    after(pe, a.o0_ready, t)
    for b in range(2):
        bank = a.O if b == 0 else a.T
        for par in range(2):
            rows = slice(par * SEQ, (par + 1) * SEQ)
            last = pe.matmul(bank[0:a.vc, par, :], a.values[s % 2][rows, b, :],
                             a.probT[rows, :, b * SEQ:(b + 1) * SEQ], start=True, stop=True)
        last.then_inc(a.weighed, 1)


def project_tensor(pe, a, t, bias):
    pe.wait_ge(a.o0_ready, t + 1)
    pe.wait_ge(a.o1_ready, t + 1)
    for h in range(H):
        last = pe.matmul(a.k.r6[:, 0:D], a.oT[:, h, :], a.wo[:, h, :], start=h == 0,
                         stop=h == H - 1 and bias is None)
    if bias is not None:
        last = pe.matmul(a.k.r6[:, 0:D], a.k.ones[0:1, :], bias, start=False, stop=True)
    last.then_inc(a.projected, 1)


def turn_xn_tensor(pe, a, m, par):
    pe.wait_ge(a.xn_ready, m + 1)
    for j in range(2):
        last = pe.transpose(a.k.r7[:, j * P:(j + 1) * P], a.xn[par][:, j, :], a.k.ident[:, :])
    last.then_inc(a.xnT_done, 1)


def softmax_top_vector(dve, a, u, s):
    dve.wait_ge(a.scores_done, u + 1)
    scores = a.S[:, :, :].rearrange("p a (h k) -> p (a h) k", k=SEQ)
    dve.tensor_reduce(a.top[s % 2][:, :], scores, AX.X, ALU.max).then_inc(a.top_ready, 1)
    dve.wait_ge(a.top_ready, u + 1)
    after(dve, a.turned, u - 1)
    dve.tensor_tensor(a.prob[s % 2][:, :, :], scores,
                      a.top[s % 2][:, :].rearrange("p (h a) -> p h a", a=1).to_broadcast([P, H, SEQ]),
                      ALU.subtract).then_inc(a.shifted, 1)


def softmax_exp_scalar(act, a, u, s):
    act.wait_ge(a.shifted, u + 1)
    act.activation(a.prob[s % 2][:, :, :], a.prob[s % 2][:, :, :], ACT.Exp,
                   scale=a.scale).then_inc(a.exp_ready, 1)


def softmax_total_vector(dve, a, u, s):
    dve.wait_ge(a.exp_ready, u + 1)
    dve.tensor_reduce(a.total[s % 2][:, :], a.prob[s % 2][:, :, :], AX.X,
                      ALU.add).then_inc(a.total_ready, 1)
    dve.wait_ge(a.total_ready, u + 1)
    after(dve, a.prob_ready, u - 1)
    dve.reciprocal(a.share[s % 2][:, :], a.total[s % 2][:, :]).then_inc(a.share_ready, 1)


def softmax_divide_gpsimd(pool, a, u, s):
    pool.wait_ge(a.share_ready, u + 1)
    pool.tensor_tensor(a.prob[s % 2][:, :, :], a.prob[s % 2][:, :, :],
                       a.share[s % 2][:, :].rearrange("p (h a) -> p h a", a=1).to_broadcast([P, H, SEQ]),
                       ALU.mult).then_inc(a.prob_ready, 1)


def copy_probT_scalar(act, a, t):
    act.wait_ge(a.turned, t + 1)
    after(act, a.weighed, 2 * t)
    act.copy(a.probT[:, :, :], a.T[:, :, :].rearrange("p a (c q) -> p (a c) q", q=P)).then_inc(
        a.probT_ready, 1)


def output_views(a, bank, b):
    out = a.oT[:, :, b * SEQ:(b + 1) * SEQ].rearrange("c (p a) q -> c a p q", a=2)
    return out, bank[0:a.vc, :, :].rearrange("c a (p q) -> c a p q", q=SEQ)


def copy_o0_scalar(act, a, t):
    act.wait_ge(a.weighed, 2 * t + 1)
    after(act, a.projected, t)
    out, src = output_views(a, a.O, 0)
    act.copy(out, src).then_inc(a.o0_ready, 1)


def copy_o1_vector(dve, a, t):
    dve.wait_ge(a.weighed, 2 * t + 2)
    after(dve, a.projected, t)
    out, src = output_views(a, a.T, 1)
    dve.tensor_copy(out, src).then_inc(a.o1_ready, 1)


def update_vector(dve, a, t):
    k = a.k
    dve.wait_ge(a.projected, t + 1)
    xt = k.x[:, bass.ds(t, 1), :].rearrange("p a d -> p (a d)")
    dve.tensor_tensor(xt, xt, k.r6[:, 0:D], ALU.add).then_inc(a.updated, 1)
    dve.wait_ge(a.updated, t + 1)
    dve.bn_stats(k.stats[:, bass.ds(t, 1), :].rearrange("p a d -> p (a d)"), xt).then_inc(a.stats_done, 1)


def normalise_group_vector(dve, a, m, par):
    after(dve, a.xnT_done, m - 1)
    for j in range(2):
        last = normalise(dve, a.k, a.xn[par][:, j:j + 1, :], m * 2 + j)
    last.then_inc(a.xn_ready, 1)


def copy_xnT_scalar(act, a, m, par, before=None):
    act.wait_ge(a.xnT_done, m + 1)
    if before is not None:
        after(act, *before)
    act.copy(a.xnT[par][:, :], a.k.r7[:, 0:GT]).then_inc(a.xnT_ready, 1)



DH = 64


def fold_tensors(k, ctx, tag):
    def sb(name, shape):
        return ctx.enter_context(k.nc.sbuf_tensor(f"{tag}_{name}", shape, F32))

    class Fold:
        m = sb("m", [D, H, C])
        turned = [sb(f"turned{i}", [P, D + 2 * C]) for i in range(2)]
        turn_done = Signals.new(k.nc, f"{tag}_fold_turned")
        turn_ready = Signals.new(k.nc, f"{tag}_fold_copied")
        fold_done = Signals.new(k.nc, f"{tag}_folded")
        m_ready = Signals.new(k.nc, f"{tag}_m_ready")
        w_ready = Signals.new(k.nc, f"{tag}_w_ready")
    return Fold


def wide_weights(k):
    w = k.even
    return (w[:, 0:1024], w[0:C, 1024:2048], w[0:C, 2048:3072],
            w[:, 3072:4096].rearrange("p (c n) -> p c n", n=D), w[0:1, 4096:4096 + D])


def load_wide(sp, k, pre):
    wq, wk, wv, wo, bo = wide_weights(k)
    d = k.dram
    k.load(sp, "even", wq, d[f"{pre}Wq"])
    k.load(sp, "even", wk, d[f"{pre}Wk"])
    k.load(sp, "even", wv, d[f"{pre}Wv"])
    k.load(sp, "even", wo, d[f"{pre}Wo"].rearrange("(c p) n -> p c n", p=P))
    k.load(sp, "even", bo, row(d[f"{pre}bo"], D))


def fold_tensor(pe, k, a, f):
    wq, wk, wv, wo, _ = wide_weights(k)
    T = k.ps[0]

    def turn(p):
        after(pe, f.turn_ready, p - 1)
        cols = slice(p * P, (p + 1) * P)
        pe.transpose(T[:, p % 2, 0:D], wq[:, cols], k.ident[:, :])
        pe.transpose(T[:, p % 2, D:D + C], wk[:, cols], k.ident[0:C, 0:C])
        pe.transpose(T[:, p % 2, D + C:D + 2 * C], wv[:, cols], k.ident[0:C, 0:C]).then_inc(
            f.turn_done, 1)

    turn(0)
    for p in range(H // 2):
        if p + 1 < H // 2:
            turn(p + 1)
        pe.wait_ge(f.turn_ready, p + 1)
        after(pe, f.m_ready, p)
        after(pe, f.w_ready, p)
        t, M, W = f.turned[p % 2], k.ps[1], k.ps[2]
        for par in range(2):
            rows = slice(par * DH, (par + 1) * DH)
            pe.matmul(M[:, par, 0:C], t[rows, 0:D], t[rows, D:D + C],
                      start=True, stop=True)
            last = pe.matmul(W[0:C, par, 0:D],
                             t[rows, D + C:D + 2 * C], wo[rows, p, :], start=True, stop=True)
        last.then_inc(f.fold_done, 1)


def fold_scalar(act, k, a, f):
    T = k.ps[0]
    for p in range(H // 2):
        act.wait_ge(f.turn_done, p + 1)
        after(act, f.fold_done, p - 1)
        act.copy(f.turned[p % 2][:, :], T[:, p % 2, 0:D + 2 * C]).then_inc(f.turn_ready, 1)
        act.wait_ge(f.fold_done, p + 1)
        act.copy(f.m[:, 2 * p:2 * p + 2, :],
                 k.ps[1][:, :, 0:C]).then_inc(f.m_ready, 1)


def fold_vector(dve, k, a, f):
    for p in range(H // 2):
        dve.wait_ge(f.fold_done, p + 1)
        dve.tensor_copy(a.wo[:, 2 * p:2 * p + 2, :],
                        k.ps[2][0:C, :, 0:D]).then_inc(
                            f.w_ready, 1)


def wide_queries_tensor(pe, a, f, n, s, freed6, freed7):
    g, hh = half(s)
    pe.wait_ge(a.xnT_ready, (n + 2 - hh) // 2 if isinstance(n, int) else (n - hh) // 2 + 1)
    for j in range(4):
        bank = (a.k.r6, a.k.r7)[j % 2]
        if j == 0:
            after(pe, *freed6)
        elif j == 1:
            after(pe, *freed7)
        elif j == 2:
            pe.wait_ge(a.q6_ready, n * 2 + 1)
        else:
            pe.wait_ge(a.q7_ready, n * 2 + 1)
        for e in range(2):
            last = pe.matmul(bank[0:C, e * GT:(e + 1) * GT], f.m[:, 8 * hh + 2 * j + e, :],
                             a.xnT[g][:, :], start=True, stop=True)
        last.then_inc((a.q6_done, a.q7_done)[j % 2], 1)


def copy_queries(copy, eng, a, n, s, j, done, ready, used):
    g, hh = half(s)
    eng.wait_ge(done, n * 2 + 1 + j // 2)
    after(eng, *used)
    h = 8 * hh + 2 * j
    copy(a.qh[g][:, h:h + 2, :],
         (a.k.r6, a.k.r7)[j % 2][0:C, :].rearrange("c (e q) -> c e q", e=2)).then_inc(ready, 1)


LEAD = 3


def wide_attention(k, tag, pre, load_next, first=None):
    nc = k.nc
    with ExitStack() as ctx:
        a = Attention(k, ctx, tag, C, C, float(DH) ** -0.5)
        f = fold_tensors(k, ctx, tag)
        loaded = k.loads["even"]
        bias = wide_weights(k)[4]
        block = ctx.enter_context(nc.Block())

        @block.sync
        def _(sp):
            load_next(sp)

        @block.tensor
        def _(pe):
            pe.wait_ge(k.load_even, loaded)
            fold_tensor(pe, k, a, f)
            for m in range(2):
                after(pe, a.xnT_ready, m)
                turn_xn_tensor(pe, a, m, m)
            pe.wait_ge(f.m_ready, H // 2)
            pe.wait_ge(f.w_ready, H // 2)
            for n in range(LEAD):
                wide_queries_tensor(pe, a, f, n, n, (a.q6_ready, 2 * n),
                                    (a.q7_ready, 2 * n) if n else (a.xnT_ready, 2))

            def queries_ready(u):
                if isinstance(u, int):
                    u -= u % 2
                    pe.wait_ge(a.q6_ready, u * 2 + 4)
                    pe.wait_ge(a.q7_ready, u * 2 + 4)

            queries_ready(0)
            scores_tensor(pe, a, 0, 0)

            def slot(t, s):
                turn_tensor(pe, a, t, s)
                if not is_last(t):
                    if s % 2:
                        pe.wait_ge(a.q6_ready, t * 2 + 6)
                        pe.wait_ge(a.q7_ready, t * 2 + 6)
                    scores_tensor(pe, a, t + 1, (s + 1) % 4)
                weigh_tensor(pe, a, t, s)
                if not is_last(t, LEAD):
                    wide_queries_tensor(pe, a, f, t + LEAD, (s + LEAD) % 4, (a.updated, t),
                                        (a.xnT_ready, (t + 5) // 2 if isinstance(t, int)
                                         else (t - 1) // 2 + 3) if s % 2 else (a.q7_ready, t * 2 + 6))
                    pe.wait_ge(a.q6_ready, t * 2 + 8)
                    project_tensor(pe, a, t, bias)
                    if s % 2 == 0 and not is_last(t, 4):
                        pe.wait_ge(a.q7_ready, t * 2 + 8)
                        turn_xn_tensor(pe, a, t // 2 + 2, (s // 2) % 2)
                else:
                    after(pe, a.updated, t)
                    project_tensor(pe, a, t, bias)

            over_tiles(pe, slot)

        @block.scalar
        def _(act):
            norm_root_scalar(act, k, a.norm)
            fold_scalar(act, k, a, f)
            for m in range(2):
                copy_xnT_scalar(act, a, m, m)
            for n in range(LEAD):
                for j in (0, 2):
                    copy_queries(act.copy, act, a, n, n, j, a.q6_done, a.q6_ready, (a.scores_done, 0))
            softmax_exp_scalar(act, a, 0, 0)

            def slot(t, s):
                copy_probT_scalar(act, a, t)
                copy_o0_scalar(act, a, t)
                if not is_last(t):
                    softmax_exp_scalar(act, a, t + 1, (s + 1) % 4)
                if not is_last(t, LEAD):
                    for j in (0, 2):
                        copy_queries(act.copy, act, a, t + LEAD, (s + LEAD) % 4, j, a.q6_done, a.q6_ready,
                                     (a.scores_done, t))
                    if s % 2 == 0 and not is_last(t, 4):
                        copy_xnT_scalar(act, a, t // 2 + 2, (s // 2) % 2)

            over_tiles(act, slot)

        @block.vector
        def _(dve):
            if first is not None:
                first(dve)
            norm_stats_vector(dve, k, a.norm)
            fold_vector(dve, k, a, f)
            for m in range(2):
                normalise_group_vector(dve, a, m, m)
            for n in range(LEAD):
                for j in (1, 3):
                    copy_queries(dve.tensor_copy, dve, a, n, n, j, a.q7_done, a.q7_ready, (a.scores_done, 0))
            softmax_top_vector(dve, a, 0, 0)
            softmax_total_vector(dve, a, 0, 0)

            def slot(t, s):
                if s % 2 == 0 and not is_last(t, 4):
                    normalise_group_vector(dve, a, t // 2 + 2, (s // 2) % 2)
                if not is_last(t):
                    softmax_top_vector(dve, a, t + 1, (s + 1) % 4)
                copy_o1_vector(dve, a, t)
                more = not is_last(t, LEAD)
                if more:
                    copy_queries(dve.tensor_copy, dve, a, t + LEAD, (s + LEAD) % 4, 1, a.q7_done,
                                 a.q7_ready, (a.scores_done, t))
                if not is_last(t):
                    softmax_total_vector(dve, a, t + 1, (s + 1) % 4)
                if more:
                    copy_queries(dve.tensor_copy, dve, a, t + LEAD, (s + LEAD) % 4, 3, a.q7_done,
                                 a.q7_ready, (a.scores_done, t))
                update_vector(dve, a, t)

            over_tiles(dve, slot)

        @block.gpsimd
        def _(pool):
            def keys(u, s):
                after(pool, a.scores_done, u - 1)
                pool.tensor_copy(a.keys[s % 2][:, :], k.ctxT[:, bass.ds(u * P, P)]).then_inc(
                    a.keys_ready, 1)

            def values(u, s):
                after(pool, a.weighed, 2 * u - 2)
                pool.tensor_copy(a.values[s % 2][:, :, :],
                                 k.ctx2[:, bass.ds(u * 2, 2), :]).then_inc(a.values_ready, 1)

            for u in range(2):
                keys(u, u)
                values(u, u)
            softmax_divide_gpsimd(pool, a, 0, 0)

            def slot(t, s):
                if not is_last(t):
                    softmax_divide_gpsimd(pool, a, t + 1, (s + 1) % 4)
                if not is_last(t, 2):
                    keys(t + 2, (s + 2) % 4)
                    values(t + 2, (s + 2) % 4)

            over_tiles(pool, slot)



QUAD = 4 * P
QUADS = TOK // QUAD


def linked(eng, sem):
    count = [0]

    def link(ins):
        count[0] += 1
        ins.then_inc(sem, 1)
        eng.wait_ge(sem, count[0])
    return link


def spread(ap, n):
    return ap.rearrange("p (a o) -> p a o", o=1).to_broadcast([ap.shape[0], ap.shape[1], n])


class Turned:

    def __init__(self, k, ctx, tag, rms=False, weight=None, xnT=None):
        def sb(name, shape):
            return ctx.enter_context(k.nc.sbuf_tensor(f"{tag}_{name}", shape, F32))

        def sem(name):
            return Signals.new(k.nc, f"{tag}_{name}")

        self.k, self.rms, self.weight = k, rms, weight
        self.xnT = sb("xnT", [D, TOK]) if xnT is None else xnT
        self.xn = [sb(f"xn{i}", [P, 4, D]) for i in range(2)]
        self.norm = NormSems(k.nc, ctx, tag)
        self.xn_ready = sem("xn_ready")
        self.turned = sem("turned")
        self.ready = sem("xnT_ready")

    def vector(self, dve):
        k = self.k
        norm_stats_vector(dve, k, self.norm, self.rms)
        for n in range(QUADS):
            after(dve, self.turned, n - 1)
            for j in range(4):
                if self.rms:
                    last = dve.tensor_scalar(self.xn[n % 2][:, j, :], k.x[:, 4 * n + j, :],
                                             k.rstd[:, 4 * n + j:4 * n + j + 1], None, ALU.mult)
                else:
                    last = normalise(dve, k, self.xn[n % 2][:, j:j + 1, :], 4 * n + j)
            last.then_inc(self.xn_ready, 1)

    def tensor(self, pe, n):
        pe.wait_ge(self.xn_ready, n + 1)
        after(pe, self.ready, n - 1)
        bank = (self.k.r6, self.k.r7)[n % 2]
        for j in range(4):
            last = pe.transpose(bank[:, j * P:(j + 1) * P], self.xn[n % 2][:, j, :], self.k.ident[:, :])
        last.then_inc(self.turned, 1)

    def scalar(self, act, n):
        act.wait_ge(self.turned, n + 1)
        out, bank = self.xnT[:, n * QUAD:(n + 1) * QUAD], (self.k.r6, self.k.r7)[n % 2]
        if self.weight is None:
            ins = act.copy(out, bank[:, :])
        else:
            ins = act.activation(out, bank[:, :], ACT.Copy, scale=self.weight)
        ins.then_inc(self.ready, 1)



F0, E0 = 352, 8
CHUNKS0 = [(0, 128), (128, 128), (256, 96)]


def ffn0_weights(k):
    w = k.odd
    n = E0 * F0
    return (w[:, 0:n].rearrange("p (e f) -> p e f", e=E0),
            w[:, n:2 * n].rearrange("p (e f) -> p e f", e=E0),
            w[:, 2 * n:2 * n + E0 * 3 * D].rearrange("p (e c n) -> p e c n", e=E0, c=3))


def load_ffn0(sp, k):
    w1, w3, w2 = ffn0_weights(k)
    d = k.dram
    k.load(sp, "odd", w1, d["L0_ffn_w1"].rearrange("e d f -> d e f"))
    k.load(sp, "odd", w3, d["L0_ffn_w3"].rearrange("e d f -> d e f"))
    for c, (at, n) in enumerate(CHUNKS0):
        k.load(sp, "odd", w2[0:n, :, c, :], d["L0_ffn_w2"][:, at:at + n, :].rearrange("e f d -> f e d"))


def ffn0(k, load_next):
    nc = k.nc
    with ExitStack() as ctx:
        def sb(name, shape):
            return ctx.enter_context(nc.sbuf_tensor(f"l0f_{name}", shape, F32))

        def sem(name):
            return Signals.new(nc, f"l0f_{name}")

        tr = Turned(k, ctx, "l0f")
        w1, w3, w2 = ffn0_weights(k)
        gated = [sb(f"gated{i}", [P, QUAD]) for i in range(2)]
        hidden = [sb(f"hidden{i}", [P, QUAD]) for i in range(2)]
        gate_done, up_done = sem("gate_done"), sem("up_done")
        gated_ready, hidden_ready = sem("gated_ready"), sem("hidden_ready")
        down_done, down_ready = sem("down_done"), sem("down_ready")
        back_done, updated, stats_done = sem("back_done"), sem("updated"), sem("stats_done")
        gate_banks, up_banks, down_banks = k.ps
        units = [(e, c) for e in range(E0) for c in range(3)]
        loaded = k.loads["odd"]

        def tokens(e):
            return tr.xnT[:, :].rearrange("p (b e c) -> p b e c", e=E0, c=SEQ // E0)[:, :, e, :]

        block = ctx.enter_context(nc.Block())

        @block.sync
        def _(sp):
            load_next(sp)

        @block.tensor
        def _(pe):
            for n in range(QUADS):
                tr.tensor(pe, n)
            pe.wait_ge(k.load_odd, loaded)
            pe.wait_ge(tr.ready, QUADS)

            def up(v):
                e, c = units[v]
                at, n = CHUNKS0[c]
                after(pe, gated_ready, v - 1)
                after(pe, hidden_ready, v - 1)
                pe.matmul(gate_banks[0:n, v % 2, :], w1[:, e, at:at + n], tokens(e), start=True,
                          stop=True).then_inc(gate_done, 1)
                pe.matmul(up_banks[0:n, v % 2, :], w3[:, e, at:at + n], tokens(e), start=True,
                          stop=True).then_inc(up_done, 1)

            up(0)
            for v, (e, c) in enumerate(units):
                if v + 1 < len(units):
                    up(v + 1)
                n = CHUNKS0[c][1]
                pe.wait_ge(hidden_ready, v + 1)
                if c == 0:
                    after(pe, down_ready, e - 1)
                last = pe.matmul(down_banks[:, e % 2, :], w2[0:n, e, c, :], hidden[v % 2][0:n, :],
                                 start=c == 0, stop=c == 2)
                if c == 2:
                    last.then_inc(down_done, 1)
            pe.wait_ge(down_ready, E0)
            for n in range(QUADS):
                after(pe, updated, n - 1)
                for j in range(4):
                    at = n * QUAD + j * P
                    last = pe.transpose((k.r6, k.r7)[n % 2][:, j * P:(j + 1) * P],
                                        tr.xnT[:, at:at + P], k.ident[:, :])
                last.then_inc(back_done, 1)

        @block.scalar
        def _(act):
            norm_root_scalar(act, k, tr.norm)
            for n in range(QUADS):
                tr.scalar(act, n)
            for v, (e, c) in enumerate(units):
                n = CHUNKS0[c][1]
                act.wait_ge(gate_done, v + 1)
                after(act, hidden_ready, v - 1)
                act.activation(gated[v % 2][0:n, :], gate_banks[0:n, v % 2, :], ACT.Silu).then_inc(
                    gated_ready, 1)
                if c == 2:
                    act.wait_ge(down_done, e + 1)
                    act.copy(tokens(e), down_banks[:, e % 2, :].rearrange("p (b c) -> p b c", c=SEQ // E0)
                             ).then_inc(down_ready, 1)

        @block.vector
        def _(dve):
            tr.vector(dve)
            for v, (e, c) in enumerate(units):
                n = CHUNKS0[c][1]
                dve.wait_ge(gated_ready, v + 1)
                dve.wait_ge(up_done, v + 1)
                dve.tensor_tensor(hidden[v % 2][0:n, :], gated[v % 2][0:n, :], up_banks[0:n, v % 2, :],
                                  ALU.mult).then_inc(hidden_ready, 1)
            for n in range(QUADS):
                dve.wait_ge(back_done, n + 1)
                xq = k.x[:, 4 * n:4 * n + 4, :].rearrange("p a d -> p (a d)")
                dve.tensor_tensor(xq, xq, (k.r6, k.r7)[n % 2][:, :], ALU.add).then_inc(updated, 1)
                dve.wait_ge(updated, n + 1)
                for j in range(4):
                    last = dve.bn_stats(k.stats[:, 4 * n + j, :], k.x[:, 4 * n + j, :])
                last.then_inc(stats_done, 1)



class Experts:

    def __init__(self, k, ctx, tag, xnT, experts, up, down, gated, bias1=None, bias2=None, weight=None):
        def sb(name, shape):
            return ctx.enter_context(k.nc.sbuf_tensor(f"{tag}_{name}", shape, F32))

        def sem(name):
            return Signals.new(k.nc, f"{tag}_{name}")

        self.k, self.xnT, self.experts, self.up, self.down = k, xnT, experts, up, down
        self.gated, self.bias1, self.bias2, self.weight = gated, bias1, bias2, weight
        self.chunks = 1 if gated else 4
        self.hidden = [sb(f"hidden{i}", [P, self.chunks, GT]) for i in range(2)]
        if gated:
            self.silu = [sb(f"silu{i}", [P, GT]) for i in range(2)]
            self.silu_ready = sem("silu_ready")
        self.up_done = sem("up_done")
        self.hidden_ready = sem("hidden_ready")
        self.down_done = sem("down_done")
        self.added = sem("added")
        self.stats_done = sem("stats_done")

    def loop(self, eng, unit):
        E = self.experts

        def pair(g0, static):
            for j in range(2):
                for e in range(E):
                    g = g0 + j
                    unit(g * E + e, g, e, (j * E + e) % 2)

        pair(0, True)
        with eng.Fori(1, GROUPS // 2 - 1) as i:
            pair(i * 2, False)
        pair(GROUPS - 2, True)

    def up_tensor(self, pe, v, g, e, par):
        after(pe, self.hidden_ready, v - 1)
        banks = self.k.ps[par]
        moving = self.xnT[:, bass.ds(g * GT, GT)]
        for c in range(2 if self.gated else 4):
            out = banks[:, c, 0:GT] if self.gated else banks[:, c // 2, (c % 2) * GT:(c % 2 + 1) * GT]
            last = pe.matmul(out, self.up[:, e, c * P:(c + 1) * P], moving, start=True, stop=True)
        last.then_inc(self.up_done, 1)

    def tensor(self, pe):
        E = self.experts
        self.up_tensor(pe, 0, 0, 0, 0)

        def unit(v, g, e, par):
            if not (isinstance(v, int) and v == GROUPS * E - 1):
                self.up_tensor(pe, v + 1, g if e + 1 < E else g + 1, (e + 1) % E, 1 - par)
            pe.wait_ge(self.hidden_ready, v + 1)
            after(pe, self.added, v - 1)
            for j in range(2):
                out = self.k.ps[2][:, par, j * D:(j + 1) * D]
                for c in range(self.chunks):
                    last = pe.matmul(out, self.hidden[par][:, c, j * P:(j + 1) * P], self.down[:, e, c, :],
                                     start=c == 0, stop=c == self.chunks - 1 and self.bias2 is None)
                if self.bias2 is not None:
                    last = pe.matmul(out, self.k.ones[0:1, :], self.bias2[:, e, :], start=False, stop=True)
            last.then_inc(self.down_done, 1)

        self.loop(pe, unit)

    def scalar(self, act):
        def unit(v, g, e, par):
            act.wait_ge(self.up_done, v + 1)
            banks = self.k.ps[par]
            if self.gated:
                after(act, self.hidden_ready, v - 1)
                act.activation(self.silu[par][:, :], banks[:, 0, 0:GT], ACT.Silu).then_inc(
                    self.silu_ready, 1)
                return
            after(act, self.down_done, v - 1)
            for c in range(4):
                last = act.activation(self.hidden[par][:, c, :],
                                      banks[:, c // 2, (c % 2) * GT:(c % 2 + 1) * GT], ACT.Gelu,
                                      bias=self.bias1[:, 4 * e + c:4 * e + c + 1])
            last.then_inc(self.hidden_ready, 1)

        self.loop(act, unit)

    def vector(self, dve):
        k, E = self.k, self.experts

        def multiply(v, par):
            dve.wait_ge(self.silu_ready, v + 1)
            dve.wait_ge(self.up_done, v + 1)
            after(dve, self.down_done, v - 1)
            dve.tensor_tensor(self.hidden[par][:, 0, :], self.silu[par][:, :], k.ps[par][:, 1, 0:GT],
                              ALU.mult).then_inc(self.hidden_ready, 1)

        if self.gated:
            multiply(0, 0)

        def unit(v, g, e, par):
            if self.gated and not (isinstance(v, int) and v == GROUPS * E - 1):
                multiply(v + 1, 1 - par)
            dve.wait_ge(self.down_done, v + 1)
            after(dve, self.added, v)
            xg = k.x[:, bass.ds(g * 2, 2), :]
            if self.weight is None:
                dve.tensor_tensor(xg.rearrange("p a d -> p (a d)"), xg.rearrange("p a d -> p (a d)"),
                                  k.ps[2][:, par, 0:2 * D], ALU.add).then_inc(self.added, 1)
            else:
                for j in range(2):
                    xt = k.x[:, bass.ds(g * 2 + j, 1), :].rearrange("p a d -> p (a d)")
                    w = self.weight[:, bass.ds((g * 2 + j) * 8 + e, 1)]
                    last = dve.scalar_tensor_tensor(xt, k.ps[2][:, par, j * D:(j + 1) * D], w, xt,
                                                    ALU.mult, ALU.add)
                last.then_inc(self.added, 1)
            if e == E - 1:
                dve.wait_ge(self.added, v + 1)
                for j in range(2):
                    last = dve.bn_stats(
                        k.stats[:, bass.ds(g * 2 + j, 1), :].rearrange("p a d -> p (a d)"),
                        k.x[:, bass.ds(g * 2 + j, 1), :].rearrange("p a d -> p (a d)"))
                last.then_inc(self.stats_done, 1)

        self.loop(dve, unit)



class Ternary:

    def __init__(self, k, ctx, tag, floor, width):
        def sb(name, shape):
            return ctx.enter_context(k.nc.sbuf_tensor(f"{tag}_{name}", shape, F32))

        self.k, self.floor = k, floor
        self.sums = sb("tern_sums", [P, 1])
        self.scale = sb("tern_scale", [P, 1])
        self.cut = sb("tern_cut", [P, 2])
        self.low = sb("tern_low", [P, width])
        self.sums_ready = Signals.new(k.nc, f"{tag}_tern_sums")
        self.total_done = Signals.new(k.nc, f"{tag}_tern_total")
        self.step = Signals.new(k.nc, f"{tag}_tern_step")
        self.count = 0

    def tensor(self, pe, rows):
        self.count += 1
        pe.wait_ge(self.sums_ready, self.count)
        pe.matmul(self.k.ps[2][:, 1, 0:1], self.k.ones[0:rows, :], self.sums[0:rows, :], start=True,
                  stop=True).then_inc(self.total_done, 1)


def ternary_vector(dve, tn, nth, link, w, out, size, scale_out):
    rows, n = w.shape
    dve.tensor_reduce(tn.sums[0:rows, :], w, AX.X, ALU.add, apply_absolute_value=True).then_inc(
        tn.sums_ready, 1)
    dve.wait_ge(tn.total_done, nth + 1)
    link(dve.tensor_scalar(scale_out, tn.k.ps[2][:, 1, 0:1], 1.0 / size, tn.floor, ALU.mult, ALU.max))
    link(dve.tensor_scalar(tn.cut[:, 0:1], scale_out, 0.5, None, ALU.mult))
    link(dve.tensor_scalar(tn.cut[:, 1:2], scale_out, -0.5, None, ALU.mult))
    link(dve.tensor_scalar(tn.low[0:rows, 0:n], w, tn.cut[0:rows, 1:2], None, ALU.is_lt))
    link(dve.scalar_tensor_tensor(out, w, tn.cut[0:rows, 0:1], tn.low[0:rows, 0:n], ALU.is_gt,
                                  ALU.subtract))



F1 = 512


def ffn1_weights(k):
    w = k.odd
    return (w[:, 0:512].rearrange("p (c n) -> p c n", n=D), w[:, 512:1024],
            w[:, 1024:1028], w[0:1, 1028:1028 + D])


def load_ffn1(sp, k):
    w1, w2, b1, b2 = ffn1_weights(k)
    d = k.dram
    k.load(sp, "odd", w1, d["L1_ffn_W1"].rearrange("(c p) n -> p c n", p=P))
    k.load(sp, "odd", w2, d["L1_ffn_W2"])
    with k.nc.allow_non_contiguous_dma(reason="a short bias, feature-major"):
        k.load(sp, "odd", b1, d["L1_ffn_b1"].rearrange("(c p) -> p c", p=P))
    k.load(sp, "odd", b2, row(d["L1_ffn_b2"], D))


def ffn1(k, load_next):
    nc = k.nc
    with ExitStack() as ctx:
        def sb(name, shape):
            return ctx.enter_context(nc.sbuf_tensor(f"l1f_{name}", shape, F32))

        def sem(name):
            return Signals.new(nc, f"l1f_{name}")

        tr = Turned(k, ctx, "l1f")
        w1, w2, b1, b2 = ffn1_weights(k)
        up = sb("up", [D, 1, F1])
        down = sb("down", [P, 1, 4, D])
        scales = sb("scales", [P, 2])
        tn = Ternary(k, ctx, "l1f", 1e-8, F1)
        turned, copied, made = sem("weights_turned"), sem("weights_ready"), sem("ternary_made")
        ex = Experts(k, ctx, "l1f", tr.xnT, 1, up, down, False, bias1=b1,
                     bias2=b2.rearrange("p (e n) -> p e n", e=1))
        loaded = k.loads["odd"]
        block = ctx.enter_context(nc.Block())

        @block.sync
        def _(sp):
            load_next(sp)

        @block.tensor
        def _(pe):
            tn.tensor(pe, P)
            tn.tensor(pe, P)
            for i, w in enumerate((w1.rearrange("p c n -> p (c n)"), w2)):
                pe.wait_ge(made, i + 1)
                for c in range(4):
                    last = pe.transpose(k.ps[0][:, i, c * P:(c + 1) * P], w[:, c * P:(c + 1) * P],
                                        k.ident[:, :])
                last.then_inc(turned, 1)
            for n in range(QUADS):
                tr.tensor(pe, n)
            pe.wait_ge(tr.ready, QUADS)
            pe.wait_ge(copied, 2)
            ex.tensor(pe)

        @block.scalar
        def _(act):
            norm_root_scalar(act, k, tr.norm)
            act.wait_ge(turned, 2)
            act.copy(up[:, 0, :], k.ps[0][:, 0, :]).then_inc(copied, 1)
            act.copy(down[:, 0, :, :].rearrange("p c n -> p (c n)"), k.ps[0][:, 1, :]).then_inc(copied, 1)
            for n in range(QUADS):
                tr.scalar(act, n)
            ex.scalar(act)

        @block.vector
        def _(dve):
            link = linked(dve, tn.step)
            dve.wait_ge(k.load_odd, loaded)
            for i, w in enumerate((w1.rearrange("p c n -> p (c n)"), w2)):
                ternary_vector(dve, tn, i, link, w, w, F1 * D, scales[:, i:i + 1])
                dve.sem_inc(made, 1)
            tr.vector(dve)
            ex.vector(dve)



class Router:

    def __init__(self, k, ctx, tag, experts):
        def sb(name, shape):
            return ctx.enter_context(k.nc.sbuf_tensor(f"{tag}_{name}", shape, F32))

        def sem(name):
            return Signals.new(k.nc, f"{tag}_{name}")

        self.k, self.E = k, experts
        self.index = sb("index", [P, TILES, experts])
        self.score = sb("score", [P, TILES, experts])
        self.soft = sb("soft", [P, TILES, experts])
        self.cand = sb("cand", [P, TILES, experts])
        self.hot = [sb(f"hot{i}", [P, TILES, experts]) for i in range(2)]
        self.top = [sb(f"top{i}", [P, TILES]) for i in range(2)]
        self.first = sb("first", [P, TILES])
        self.weight = sb("weight", [P, TILES * 8])
        self.index_ready = sem("index_ready")
        self.scored = sem("scored")
        self.ready = sem("score_ready")
        self.soft_ready = sem("soft_ready")
        self.step = sem("route_step")
        self.done = sem("routed")

    def tensor(self, pe, xnT, w, bias):
        for t in range(TILES):
            out = self.k.ps[2][:, 0, t * self.E:(t + 1) * self.E]
            pe.matmul(out, xnT[:, t * P:(t + 1) * P], w, start=True, stop=False)
            last = pe.matmul(out, self.k.ones[0:1, :], bias, start=False, stop=True)
        last.then_inc(self.scored, 1)

    def gpsimd(self, pool):
        pool.iota(self.index[:, :, :], pattern=[[0, TILES], [1, self.E]], base=0, channel_multiplier=0,
                  allow_small_or_imprecise_dtypes=True).then_inc(self.index_ready, 1)

    def bank(self):
        return self.k.ps[2][:, 0, 0:TILES * self.E].rearrange("p (t e) -> p t e", e=self.E)

    def first_top(self, dve, link, score, n):
        E = self.E
        index = self.index[:, :, :]
        link(dve.tensor_reduce(self.top[n][:, :], score, AX.X, ALU.max))
        link(dve.tensor_tensor(self.cand[:, :, :], score, spread(self.top[n][:, :], E), ALU.is_equal))
        link(dve.scalar_tensor_tensor(self.cand[:, :, :], self.cand[:, :, :], -float(E), index, ALU.mult,
                                      ALU.add))
        link(dve.tensor_reduce(self.first[:, :], self.cand[:, :, :], AX.X, ALU.min))
        link(dve.tensor_scalar(self.first[:, :], self.first[:, :], float(E), None, ALU.add))
        link(dve.tensor_tensor(self.hot[n][:, :, :], index, spread(self.first[:, :], E), ALU.is_equal))



E3, F3 = 8, 512


def ffn3_weights(k):
    w = k.odd
    return (w[:, 0:4096].rearrange("p (e f) -> p e f", e=E3),
            w[:, 4096:8192].rearrange("p (e c n) -> p e c n", e=E3, c=4),
            w[:, 8192:8192 + 32], w[:, 8224:8232], w[0:1, 8232:8240],
            w[0:1, 8256:8256 + 0])


def load_ffn3(sp, k):
    w1, w2, b1, wr, br, _ = ffn3_weights(k)
    d = k.dram
    k.load(sp, "odd", w1, d["L3_ffn_W1"].rearrange("e d f -> d e f"))
    for e in range(E3):
        k.load(sp, "odd", w2[:, e, :, :], d["L3_ffn_W2"][e].rearrange("(c p) n -> p c n", p=P))
    with k.nc.allow_non_contiguous_dma(reason="a short bias, feature-major"):
        k.load(sp, "odd", b1, d["L3_ffn_b1"].rearrange("e (c p) -> p (e c)", p=P))
    k.load(sp, "odd", wr, d["L3_ffn_Wr"])
    k.load(sp, "odd", br, row(d["L3_ffn_br"], E3))


def ffn3(k):
    nc = k.nc
    with ExitStack() as ctx:
        w1, w2, b1, wr, br, _ = ffn3_weights(k)
        b2 = ctx.enter_context(nc.sbuf_tensor("l3f_b2", [1, E3, D], F32))
        b2_in = Signals.new(nc, "l3f_b2_in")
        tr = Turned(k, ctx, "l3f")
        ro = Router(k, ctx, "l3f", E3)
        ex = Experts(k, ctx, "l3f", tr.xnT, E3, w1, w2, False, bias1=b1, bias2=b2, weight=ro.weight)
        loaded = k.loads["odd"]
        block = ctx.enter_context(nc.Block())

        @block.sync
        def _(sp):
            sp.dma_start(b2[:, :, :], k.dram["L3_ffn_b2"].rearrange("(a e) n -> a e n", a=1)).then_inc(b2_in, 16)

        @block.tensor
        def _(pe):
            for n in range(QUADS):
                tr.tensor(pe, n)
            pe.wait_ge(k.load_odd, loaded)
            pe.wait_ge(b2_in, 16)
            pe.wait_ge(tr.ready, QUADS)
            ro.tensor(pe, tr.xnT, wr, br)
            pe.wait_ge(ro.ready, 1)
            ex.tensor(pe)

        @block.scalar
        def _(act):
            norm_root_scalar(act, k, tr.norm)
            for n in range(QUADS):
                tr.scalar(act, n)
            act.wait_ge(ro.ready, 1)
            act.activation(ro.soft[:, :, :], ro.soft[:, :, :], ACT.Exp).then_inc(ro.soft_ready, 1)
            ex.scalar(act)

        @block.vector
        def _(dve):
            tr.vector(dve)
            link = linked(dve, ro.step)
            dve.wait_ge(ro.scored, 1)
            dve.wait_ge(ro.index_ready, 1)
            link(dve.tensor_copy(ro.score[:, :, :], ro.bank()))
            ro.first_top(dve, link, ro.score[:, :, :], 0)
            dve.tensor_tensor(ro.soft[:, :, :], ro.score[:, :, :], spread(ro.top[0][:, :], E3),
                              ALU.subtract).then_inc(ro.ready, 1)
            dve.wait_ge(ro.soft_ready, 1)
            link(dve.tensor_reduce(ro.first[:, :], ro.soft[:, :, :], AX.X, ALU.add))
            link(dve.reciprocal(ro.top[1][:, :], ro.first[:, :]))
            link(dve.tensor_tensor(ro.weight[:, :].rearrange("p (t e) -> p t e", e=E3), ro.hot[0][:, :, :],
                                   spread(ro.top[1][:, :], E3), ALU.mult))
            ex.vector(dve)

        @block.gpsimd
        def _(pool):
            ro.gpsimd(pool)



ROUND = 1.5 * 2.0 ** 23
F1X = 512
LINEARS = ("d2v", "img", "txt", "att0", "att1", "f1", "f2")


def attention1_weights(k):
    w = k.even
    out, at = {}, 0
    for name, rows, n in (("d2v", D, C), ("img", D, D), ("txt", D, D), ("att0", 64, D), ("att1", 64, D),
                          ("f1", D, 4 * 2 * D), ("f2", D, F1X), ("b_d2v", D, 1), ("b_img", D, 1),
                          ("b_txt", D, 1), ("b_att0", D, 1), ("b_att1", D, 1), ("b_f1", D, 4),
                          ("b_f2", 1, D)):
        out[name] = w[0:rows, at:at + n]
        at += n
    return out


def load_attention1(sp, k):
    w = attention1_weights(k)
    d = {n[9:]: v for n, v in k.dram.items() if n.startswith("L1_xattn_")}
    for name in ("d2v", "img", "txt", "att0", "att1", "f2"):
        k.load(sp, "even", w[name], d[f"W_{name}"])
    k.load(sp, "even", w["f1"].rearrange("p (c n) -> p c n", c=4), d["W_f1"].rearrange("(c p) n -> p c n", p=P))
    with k.nc.allow_non_contiguous_dma(reason="short biases, feature-major"):
        for name in ("d2v", "img", "txt"):
            k.load(sp, "even", w[f"b_{name}"], d[f"b_{name}"].rearrange("(p a) -> p a", a=1))
        for name in ("att0", "att1"):
            for part in range(2):
                k.load(sp, "even", w[f"b_{name}"][part * 64:part * 64 + 64],
                       d[f"b_{name}"].rearrange("(p a) -> p a", a=1))
        k.load(sp, "even", w["b_f1"], d["b_f1"].rearrange("(c p) -> p c", p=P))
    k.load(sp, "even", w["b_f2"], row(d["b_f2"], D))


class Rounding:

    INPUTS = ("ctx", "vis", "img", "x", "cat", "h")

    def __init__(self, k, tag, sb):
        self.k = k
        n = len(self.INPUTS)
        self.parts = sb("parts", [P, n, 32])
        self.peak = sb("peak", [P, n])
        self.top = sb("top", [P, n])
        self.scale = sb("scale", [P, n])
        self.inverse = sb("inverse", [P, n])
        self.out_scale = sb("out_scale", [P, 8])
        self.peaks_ready = Signals.new(k.nc, f"{tag}_round_peaks")
        self.top_ready = Signals.new(k.nc, f"{tag}_round_top")
        self.step = Signals.new(k.nc, f"{tag}_scale_step")
        self.done = 0

    def peak_vector(self, dve, name, n, value):
        i = self.INPUTS.index(name)
        return dve.tensor_reduce(self.parts[0:value.shape[0], i, n:n + 1], value, AX.X, ALU.max,
                                 apply_absolute_value=True)

    def scale_vector(self, dve, link, name, count, linears, w_scale):
        i = self.INPUTS.index(name)
        dve.tensor_reduce(self.peak[:, i:i + 1], self.parts[:, i, 0:count], AX.X, ALU.max).then_inc(
            self.peaks_ready, 1)
        self.done += 1
        dve.wait_ge(self.top_ready, self.done)
        link(dve.tensor_scalar(self.scale[:, i:i + 1], self.top[:, i:i + 1], 1e-8, 1.0 / 127.0, ALU.max,
                               ALU.mult))
        link(dve.reciprocal(self.inverse[:, i:i + 1], self.scale[:, i:i + 1]))
        for name in linears:
            j = LINEARS.index(name)
            link(dve.tensor_tensor(self.out_scale[:, j:j + 1], self.scale[:, i:i + 1],
                                   w_scale[:, j:j + 1], ALU.mult))

    def gpsimd(self, pool, names):
        for n, name in enumerate(names):
            i = self.INPUTS.index(name)
            pool.wait_ge(self.peaks_ready, n + 1)
            pool.partition_all_reduce(self.top[:, i:i + 1], self.peak[:, i:i + 1], P, RMAX).then_inc(
                self.top_ready, 1)

    def round_vector(self, dve, link, name, out, value, tmp):
        i, rows = self.INPUTS.index(name), value.shape[0]
        link(dve.tensor_scalar(tmp, value, self.inverse[0:rows, i:i + 1], ROUND, ALU.mult, ALU.add))
        return dve.tensor_scalar(out, tmp, -ROUND, 127.0, ALU.add, ALU.min)


def attention1(k, load_next):
    nc = k.nc
    w = attention1_weights(k)
    loaded = k.loads["even"]
    with ExitStack() as outer:
        def keep(name, shape, dt=F32):
            return outer.enter_context(nc.sbuf_tensor(f"l1x_{name}", shape, dt))

        w_scale = keep("w_scale", [P, 8])
        f1T = keep("f1T", [P, 2, F1X], BF16)
        f2T = keep("f2T", [P, 4, D], BF16)
        rounded = keep("rounded", [P, TOK], BF16)
        average = keep("average", [P, BATCH])
        rounded_average = keep("rounded_average", [P, BATCH], BF16)
        tmp = keep("tmp", [P, QUAD])
        rn = Rounding(k, "l1x", keep)
        fused = keep("fused", [D, TOK])
        with ExitStack() as ctx:
            def sb(name, shape, dt=F32):
                return ctx.enter_context(nc.sbuf_tensor(f"l1x_{name}", shape, dt))

            def sem(name):
                return Signals.new(nc, f"l1x_{name}_")

            tr = Turned(k, ctx, "l1x", xnT=fused)
            tn = Ternary(k, ctx, "l1x", 1e-5, 4 * 2 * D)
            keys = [sb(f"keysT{j}", [D, TOK]) for j in range(2)]
            vis, img = keys
            wT = {name: sb(f"{name}T", [C if name == "d2v" else D, D], BF16)
                  for name in ("d2v", "img", "txt", "att0", "att1")}
            cross = sb("cross", [P, QUAD], BF16)
            cross32 = sb("cross32", [P, P])
            prob = [sb(f"prob{i}", [P, 4, P]) for i in range(2)]
            probT = sb("probT", [P, 4, P])
            tokens = sb("tokens", [P, 4, P])
            top, total, share = ([sb(f"{n}{i}", [P, 4]) for i in range(2)] for n in ("top", "total", "share"))
            cross_in, cross_ready, zeroed = sem("cross_in"), sem("cross_ready"), sem("zeroed")
            made, w_turned, w_ready = sem("made"), sem("w_turned"), sem("w_ready")
            step = sem("step")
            names = ("vis", "img", "key", "txt")
            done = {n: sem(f"{n}_done") for n in names}
            ready = {n: sem(f"{n}_ready") for n in names}
            round_ready = {n: sem(f"{n}_rounded") for n in ("ctx", "vis", "img", "x")}
            scored, top_ready, shifted = sem("scored"), sem("top_ready"), sem("shifted")
            exp_ready, total_ready, share_ready = sem("exp_ready"), sem("total_ready"), sem("share_ready")
            prob_ready, turned, probT_ready = sem("prob_ready"), sem("turned"), sem("probT_ready")
            keys_turned, tokens_ready = sem("keys_turned"), sem("tokens_ready")
            weighed, fused_ready = sem("weighed"), sem("fused_ready")
            units = [(j, n) for j in range(2) for n in range(QUADS)]
            block = ctx.enter_context(nc.Block())

            def quad(n):
                return slice(n * QUAD, (n + 1) * QUAD)

            @block.sync
            def _(sp):
                sp.dma_start(cross32[:, :], k.dram["const_cross"]).then_inc(cross_in, 16)
                sp.wait_ge(cross_in, 16)
                load_next(sp)

            @block.tensor
            def _(pe):
                for _ in LINEARS:
                    tn.tensor(pe, P)
                pe.wait_ge(made, len(LINEARS))
                for i, name in enumerate(("d2v", "img", "txt")):
                    n = C if name == "d2v" else D
                    pe.transpose(k.ps[0][0:n, 0, i * D:(i + 1) * D], w[name], k.ident[:, :])
                for i, name in enumerate(("att0", "att1")):
                    for part in range(2):
                        at = i * D + part * 64
                        pe.transpose(k.ps[0][:, 1, at:at + 64], w[name], k.ident[0:64, 0:64])
                for c in range(4):
                    for half_in in range(2):
                        pe.transpose(k.ps[1][:, half_in, c * P:(c + 1) * P],
                                     w["f1"][:, c * 2 * D + half_in * D:c * 2 * D + (half_in + 1) * D],
                                     k.ident[:, :])
                for c in range(4):
                    last = pe.transpose(k.ps[2][:, 0, c * D:(c + 1) * D], w["f2"][:, c * P:(c + 1) * P],
                                        k.ident[:, :])
                last.then_inc(w_turned, 1)
                for n in range(QUADS):
                    tr.tensor(pe, n)
                pe.wait_ge(w_ready, 7)
                for name, src, banks in (("vis", "ctx", k.ps[0]), ("img", "vis", k.ps[1])):
                    rows, weight = (C, wT["d2v"]) if name == "vis" else (D, wT["img"])
                    for n in range(QUADS):
                        pe.wait_ge(round_ready[src], n + 1)
                        after(pe, ready[name], n - 1)
                        pe.matmul(banks[:, n % 2, :], weight[:, :], rounded[0:rows, quad(n)], start=True,
                                  stop=True).then_inc(done[name], 1)
                for n in range(QUADS):
                    pe.wait_ge(round_ready["img"], n + 1)
                    after(pe, ready["key"], 2 * n - 2)
                    for j in range(2):
                        pe.matmul(k.ps[j][:, n % 2, :], wT[f"att{j}"][:, :], rounded[:, quad(n)],
                                  start=True, stop=True).then_inc(done["key"], 1)
                for n in range(QUADS):
                    pe.wait_ge(round_ready["x"], n + 1)
                    after(pe, ready["txt"], n - 1)
                    pe.matmul(k.ps[2][:, n % 2, :], wT["txt"][:, :], rounded[:, quad(n)], start=True,
                              stop=True).then_inc(done["txt"], 1)
                pe.wait_ge(ready["txt"], QUADS)
                pe.wait_ge(ready["key"], 2 * QUADS)
                pe.wait_ge(cross_ready, 1)

                def score(v):
                    j, n = units[v]
                    after(pe, shifted, v - 1)
                    if j == 1:
                        pe.wait_ge(fused_ready, n + 1)
                    pe.matmul(k.ps[0][:, v % 2, :], k.identb[:, :], cross[:, :], start=True, stop=True)
                    for i in range(4):
                        at = n * QUAD + i * P
                        last = pe.matmul(k.ps[0][:, v % 2, i * P:(i + 1) * P], fused[:, at:at + P],
                                         keys[j][:, at:at + P], start=False, stop=True,
                                         skip_group_check=True)
                    last.then_inc(scored, 1)

                score(0)
                for v, (j, n) in enumerate(units):
                    if v + 1 < len(units):
                        score(v + 1)
                    after(pe, tokens_ready, v)
                    for i in range(4):
                        at = n * QUAD + i * P
                        last = pe.transpose(k.ps[2][:, 0, i * P:(i + 1) * P], keys[j][:, at:at + P],
                                            k.ident[:, :])
                    last.then_inc(keys_turned, 1)
                    pe.wait_ge(prob_ready, v + 1)
                    after(pe, probT_ready, v - 1)
                    for i in range(4):
                        last = pe.transpose(k.ps[1][:, v % 2, i * P:(i + 1) * P], prob[v % 2][:, i, :],
                                            k.ident[:, :])
                    last.then_inc(turned, 1)
                    pe.wait_ge(probT_ready, v + 1)
                    pe.wait_ge(tokens_ready, v + 1)
                    after(pe, fused_ready, v)
                    for i in range(4):
                        last = pe.matmul(k.ps[2][:, 1, i * P:(i + 1) * P], tokens[:, i, :], probT[:, i, :],
                                         start=True, stop=True)
                    last.then_inc(weighed, 1)

            @block.scalar
            def _(act):
                norm_root_scalar(act, k, tr.norm)
                act.wait_ge(w_turned, 1)
                act.copy(wT["d2v"][:, :], k.ps[0][0:C, 0, 0:D]).then_inc(w_ready, 1)
                act.copy(wT["img"][:, :], k.ps[0][:, 0, D:2 * D]).then_inc(w_ready, 1)
                act.copy(wT["txt"][:, :], k.ps[0][:, 0, 2 * D:3 * D]).then_inc(w_ready, 1)
                for j in range(2):
                    act.copy(wT[f"att{j}"][:, :], k.ps[0][:, 1, j * D:(j + 1) * D]).then_inc(w_ready, 1)
                act.copy(f1T[:, :, :], k.ps[1][:, :, :]).then_inc(w_ready, 1)
                act.copy(f2T[:, :, :].rearrange("p c n -> p (c n)"), k.ps[2][:, 0, :]).then_inc(w_ready, 1)
                for n in range(QUADS):
                    tr.scalar(act, n)
                for name, out, linear, banks in (("vis", vis, "d2v", k.ps[0]), ("img", img, "img", k.ps[1])):
                    i = LINEARS.index(linear)
                    for n in range(QUADS):
                        act.wait_ge(done[name], n + 1)
                        act.activation(out[:, quad(n)], banks[:, n % 2, :], ACT.Identity,
                                       bias=w[f"b_{linear}"], scale=rn.out_scale[:, i:i + 1]).then_inc(
                                           ready[name], 1)
                for n in range(QUADS):
                    for j in range(2):
                        i = LINEARS.index(f"att{j}")
                        act.wait_ge(done["key"], 2 * n + j + 1)
                        act.activation(keys[j][:, quad(n)], k.ps[j][:, n % 2, :], ACT.Identity,
                                       bias=w[f"b_att{j}"], scale=rn.out_scale[:, i:i + 1]).then_inc(
                                           ready["key"], 1)
                i = LINEARS.index("txt")
                for n in range(QUADS):
                    act.wait_ge(done["txt"], n + 1)
                    act.activation(fused[:, quad(n)], k.ps[2][:, n % 2, :], ACT.Identity, bias=w["b_txt"],
                                   scale=rn.out_scale[:, i:i + 1]).then_inc(ready["txt"], 1)
                for v in range(len(units)):
                    act.wait_ge(keys_turned, v + 1)
                    after(act, weighed, v)
                    act.copy(tokens[:, :, :].rearrange("p a n -> p (a n)"), k.ps[2][:, 0, :]).then_inc(
                        tokens_ready, 1)
                    act.wait_ge(shifted, v + 1)
                    act.activation(prob[v % 2][:, :, :], prob[v % 2][:, :, :], ACT.Exp,
                                   scale=float(D) ** -0.5).then_inc(exp_ready, 1)
                    act.wait_ge(turned, v + 1)
                    act.copy(probT[:, :, :].rearrange("p a n -> p (a n)"), k.ps[1][:, v % 2, :]).then_inc(
                        probT_ready, 1)

            @block.vector
            def _(dve):
                link = linked(dve, step)
                dve.wait_ge(k.load_even, loaded)
                sizes = {"d2v": D * C, "img": D * D, "txt": D * D, "att0": 64 * D, "att1": 64 * D,
                         "f1": F1X * 2 * D, "f2": F1X * D}
                for i, name in enumerate(LINEARS):
                    ternary_vector(dve, tn, i, link, w[name], w[name], sizes[name], w_scale[:, i:i + 1])
                    dve.sem_inc(made, 1)
                    if name == "txt":
                        link(dve.memset(tn.sums[:, :], 0.0))
                link(dve.memset(rn.parts[:, :, :], 0.0))
                link(rn.peak_vector(dve, "ctx", 0, k.ctxT[:, :]))
                rn.scale_vector(dve, link, "ctx", 1, ("d2v",), w_scale)
                for n in range(QUADS):
                    rn.round_vector(dve, link, "ctx", rounded[0:C, quad(n)], k.ctxT[:, quad(n)],
                                    tmp[0:C, :]).then_inc(round_ready["ctx"], 1)
                    dve.wait_ge(round_ready["ctx"], n + 1)
                tr.vector(dve)
                for n in range(QUADS):
                    dve.wait_ge(ready["vis"], n + 1)
                    link(rn.peak_vector(dve, "vis", n, vis[:, quad(n)]))
                rn.scale_vector(dve, link, "vis", QUADS, ("img",), w_scale)
                for n in range(QUADS):
                    rn.round_vector(dve, link, "vis", rounded[:, quad(n)], vis[:, quad(n)],
                                    tmp[:, :]).then_inc(round_ready["vis"], 1)
                    dve.wait_ge(round_ready["vis"], n + 1)
                for n in range(QUADS):
                    dve.wait_ge(ready["img"], n + 1)
                    link(rn.peak_vector(dve, "img", n, img[:, quad(n)]))
                    link(dve.tensor_reduce(average[:, 8 * n:8 * n + 8],
                                           img[:, quad(n)].rearrange("p (b s) -> p b s", s=SEQ), AX.X,
                                           ALU.add))
                link(dve.tensor_scalar(average[:, :], average[:, :], 1.0 / SEQ, None, ALU.mult))
                rn.scale_vector(dve, link, "img", QUADS, ("att0", "att1"), w_scale)
                for n in range(QUADS):
                    rn.round_vector(dve, link, "img", rounded[:, quad(n)], img[:, quad(n)],
                                    tmp[:, :]).then_inc(round_ready["img"], 1)
                    dve.wait_ge(round_ready["img"], n + 1)
                dve.wait_ge(tr.ready, QUADS)
                link(rn.peak_vector(dve, "x", 0, fused[:, :]))
                rn.scale_vector(dve, link, "x", 1, ("txt",), w_scale)
                for n in range(QUADS):
                    dve.wait_ge(done["key"], 2 * n + 2)
                    rn.round_vector(dve, link, "x", rounded[:, quad(n)], fused[:, quad(n)],
                                    tmp[:, :]).then_inc(round_ready["x"], 1)
                    dve.wait_ge(round_ready["x"], n + 1)

                def softmax(v):
                    i = v % 2
                    dve.wait_ge(scored, v + 1)
                    scores = k.ps[0][:, i, :].rearrange("p (a n) -> p a n", n=P)
                    dve.tensor_reduce(top[i][:, :], scores, AX.X, ALU.max).then_inc(top_ready, 1)
                    dve.wait_ge(top_ready, v + 1)
                    after(dve, turned, v - 1)
                    dve.tensor_tensor(prob[i][:, :, :], scores, spread(top[i][:, :], P),
                                      ALU.subtract).then_inc(shifted, 1)

                def divide(v):
                    i = v % 2
                    dve.wait_ge(exp_ready, v + 1)
                    dve.tensor_reduce(total[i][:, :], prob[i][:, :, :], AX.X, ALU.add).then_inc(total_ready, 1)
                    dve.wait_ge(total_ready, v + 1)
                    dve.reciprocal(share[i][:, :], total[i][:, :]).then_inc(share_ready, 1)
                    dve.wait_ge(share_ready, v + 1)
                    dve.tensor_tensor(prob[i][:, :, :], prob[i][:, :, :], spread(share[i][:, :], P),
                                      ALU.mult).then_inc(prob_ready, 1)

                softmax(0)
                for v, (j, n) in enumerate(units):
                    divide(v)
                    if v + 1 < len(units):
                        softmax(v + 1)
                    dve.wait_ge(weighed, v + 1)
                    dve.scalar_tensor_tensor(fused[:, quad(n)], k.ps[2][:, 1, :], 0.1, fused[:, quad(n)],
                                             ALU.mult, ALU.add).then_inc(fused_ready, 1)

            @block.gpsimd
            def _(pool):
                pool.wait_ge(cross_in, 16)
                pool.tensor_copy(cross[:, :].rearrange("p (a n) -> p a n", n=P),
                                 cross32[:, :].rearrange("p (a n) -> p a n", a=1).to_broadcast([P, 4, P])
                                 ).then_inc(cross_ready, 1)
                rn.gpsimd(pool, ("ctx", "vis", "img", "x"))

        with ExitStack() as ctx:
            def sb(name, shape, dt=F32):
                return ctx.enter_context(nc.sbuf_tensor(f"l1y_{name}", shape, dt))

            def sem(name):
                return Signals.new(nc, f"l1y_{name}")

            hidden = sb("hidden", [P, 4, TOK])
            bias = sb("bias", [P, 4, D])
            step, cat_rounded, average_rounded = sem("step"), sem("cat_rounded"), sem("average_rounded")
            up_done, hidden_ready, h_rounded = sem("up_done"), sem("hidden_ready"), sem("h_rounded")
            down_done, scaled, updated, stats_done = sem("down_done"), sem("scaled"), sem("updated"), sem("stats_done")
            bias_done, bias_ready = sem("bias_done"), sem("bias_ready")
            rn.peaks_ready, rn.top_ready, rn.done = sem("peaks_ready"), sem("top_ready"), 0
            rounded_h = [rounded[:, i * 4 * QUAD:(i + 1) * 4 * QUAD].rearrange("p (c n) -> p c n", c=4)
                         for i in range(2)]
            block = ctx.enter_context(nc.Block())

            def quad(n):
                return slice(n * QUAD, (n + 1) * QUAD)

            @block.tensor
            def _(pe):
                for j in range(4):
                    last = pe.matmul(k.r6[:, j * D:(j + 1) * D], k.ones[0:1, :], w["b_f2"], start=True, stop=True)
                last.then_inc(bias_done, 1)
                pe.wait_ge(average_rounded, 1)
                for n in range(QUADS):
                    pe.wait_ge(cat_rounded, n + 1)
                    avg = rounded_average[:, 8 * n:8 * n + 8].rearrange("p (b a) -> p b a", a=1).to_broadcast(
                        [P, 8, SEQ])
                    for pair in range(2):
                        after(pe, hidden_ready, 2 * n - 1 + pair)
                        for i in range(2):
                            cols = slice((2 * pair + i) * P, (2 * pair + i + 1) * P)
                            out = k.ps[pair][:, i, :]
                            pe.matmul(out, f1T[:, 0, cols], rounded[:, quad(n)], start=True, stop=False)
                            last = pe.matmul(out, f1T[:, 1, cols], avg, start=False, stop=True)
                        last.then_inc(up_done, 1)
                for n in range(QUADS):
                    pe.wait_ge(h_rounded, n + 1)
                    after(pe, scaled, n - 1)
                    for j in range(4):
                        for c in range(4):
                            last = pe.matmul(k.ps[2][:, n % 2, j * D:(j + 1) * D],
                                             rounded_h[n % 2][:, c, j * P:(j + 1) * P], f2T[:, c, :],
                                             start=c == 0, stop=c == 3)
                    last.then_inc(down_done, 1)

            @block.scalar
            def _(act):
                act.wait_ge(bias_done, 1)
                act.copy(bias[:, :, :].rearrange("p a n -> p (a n)"), k.r6[:, :]).then_inc(bias_ready, 1)
                s = LINEARS.index("f1")
                for n in range(QUADS):
                    for pair in range(2):
                        act.wait_ge(up_done, 2 * n + pair + 1)
                        for i in range(2):
                            c = 2 * pair + i
                            last = act.activation(hidden[:, c, quad(n)], k.ps[pair][:, i, :], ACT.Relu,
                                                  bias=w["b_f1"][:, c:c + 1], scale=rn.out_scale[:, s:s + 1])
                        last.then_inc(hidden_ready, 1)

            @block.vector
            def _(dve):
                link = linked(dve, step)
                link(rn.peak_vector(dve, "cat", 0, fused[:, :]))
                link(rn.peak_vector(dve, "cat", 1, average[:, :]))
                rn.scale_vector(dve, link, "cat", 2, ("f1",), w_scale)
                rn.round_vector(dve, link, "cat", rounded_average[:, :], average[:, :],
                                tmp[:, 0:BATCH]).then_inc(average_rounded, 1)
                dve.wait_ge(average_rounded, 1)
                for n in range(QUADS):
                    rn.round_vector(dve, link, "cat", rounded[:, quad(n)], fused[:, quad(n)],
                                    tmp[:, :]).then_inc(cat_rounded, 1)
                    dve.wait_ge(cat_rounded, n + 1)
                for n in range(QUADS):
                    for pair in range(2):
                        dve.wait_ge(hidden_ready, 2 * n + pair + 1)
                        for i in range(2):
                            link(rn.peak_vector(dve, "h", 4 * n + 2 * pair + i,
                                                hidden[:, 2 * pair + i, quad(n)]))
                rn.scale_vector(dve, link, "h", 32, ("f2",), w_scale)
                dve.wait_ge(bias_ready, 1)
                s = LINEARS.index("f2")
                for n in range(QUADS + 1):
                    if n < QUADS:
                        after(dve, down_done, n - 1)
                        last = rn.round_vector(dve, link, "h", rounded_h[n % 2], hidden[:, :, quad(n)],
                                               hidden[:, :, quad(n)])
                        last.then_inc(h_rounded, 1)
                    if n >= 1:
                        m = n - 1
                        dve.wait_ge(down_done, m + 1)
                        dve.scalar_tensor_tensor(tmp[:, :], k.ps[2][:, m % 2, :], rn.out_scale[:, s:s + 1],
                                                 bias[:, :, :].rearrange("p a n -> p (a n)"), ALU.mult,
                                                 ALU.add).then_inc(scaled, 1)
                        dve.wait_ge(scaled, m + 1)
                        xq = k.x[:, 4 * m:4 * m + 4, :].rearrange("p a d -> p (a d)")
                        dve.tensor_tensor(xq, xq, tmp[:, :], ALU.add).then_inc(updated, 1)
                        dve.wait_ge(updated, m + 1)
                        for j in range(4):
                            last = dve.bn_stats(k.stats[:, 4 * m + j, :], k.x[:, 4 * m + j, :])
                        last.then_inc(stats_done, 1)

            @block.gpsimd
            def _(pool):
                rn.gpsimd(pool, ("cat", "h"))



class Narrow:

    def __init__(self, k, ctx, tag):
        def sb(name, shape):
            return ctx.enter_context(k.nc.sbuf_tensor(f"{tag}_{name}", shape, F32))

        self.q = k.odd[:, 4352:4352 + TOK]
        self.k = sb("k_all", [D, TOK])
        self.v = sb("v_all", [P, TILES, D])
        self.own_q = sb("own_q", [P, H])
        self.own_v = sb("own_v", [P, H])
        self.masks_in = Signals.new(k.nc, f"{tag}_masks_in")


def narrow_attention(k, tag, nw, wo, bias, mask, load_next):
    nc = k.nc
    with ExitStack() as ctx:
        a = Attention(k, ctx, tag, D, D, 8.0 ** -0.5, narrow=True)

        def sem(name):
            return Signals.new(nc, f"{tag}_{name}")

        a.values_in = [sem(f"values_in{i}") for i in range(2)]
        own0_ready, own1_ready = sem("own0_ready"), sem("own1_ready")
        wo_ready = sem("wo_ready")
        block = ctx.enter_context(nc.Block())

        def own(eng, u, s, part, ready):
            after(eng, a.scores_done, u - 1)
            heads = slice(8 * part, 8 * part + 8)
            q = nw.q[:, bass.ds(u * P, P)].rearrange("p (a n) -> p a n", a=1).to_broadcast([P, 8, P])
            eng.tensor_tensor(a.qh[s % 2][:, heads, :], q, spread(nw.own_q[:, heads], P),
                              ALU.mult).then_inc(ready, 1)

        @block.sync
        def _(sp):
            load_next(sp)

            def values(u, s):
                after(sp, a.weighed, 2 * u - 2)
                for par in range(2):
                    for b in range(2):
                        sp.dma_start(a.values[s % 2][par * SEQ:(par + 1) * SEQ, b, :],
                                     nw.v[b * SEQ:(b + 1) * SEQ, bass.ds(u, 1), :].rearrange(
                                         "p a n -> p (a n)")).then_inc(a.values_in[s % 2], 16)

            over_tiles(sp, values)

        @block.tensor
        def _(pe):
            def scores(u, s):
                pe.wait_ge(own0_ready, u + 1)
                pe.wait_ge(own1_ready, u + 1)
                scores_tensor(pe, a, u, s, mask)

            scores(0, 0)
            pe.wait_ge(wo_ready, 1)

            def slot(t, s):
                turn_tensor(pe, a, t, s)
                if not is_last(t):
                    scores(t + 1, (s + 1) % 4)
                weigh_tensor(pe, a, t, s)
                after(pe, a.updated, t)
                project_tensor(pe, a, t, bias)

            over_tiles(pe, slot)

        @block.scalar
        def _(act):
            softmax_exp_scalar(act, a, 0, 0)

            def slot(t, s):
                copy_probT_scalar(act, a, t)
                copy_o0_scalar(act, a, t)
                if not is_last(t):
                    softmax_exp_scalar(act, a, t + 1, (s + 1) % 4)

            over_tiles(act, slot)

        @block.vector
        def _(dve):
            own(dve, 0, 0, 0, own0_ready)
            dve.tensor_tensor(a.wo[:, :, :],
                              wo.rearrange("p (a n) -> p a n", a=1).to_broadcast([P, H, D]),
                              spread(nw.own_v[:, :], D), ALU.mult).then_inc(wo_ready, 1)
            own(dve, 1, 1, 0, own0_ready)
            softmax_top_vector(dve, a, 0, 0)
            softmax_total_vector(dve, a, 0, 0)

            def slot(t, s):
                if not is_last(t):
                    softmax_top_vector(dve, a, t + 1, (s + 1) % 4)
                copy_o1_vector(dve, a, t)
                if not is_last(t):
                    softmax_total_vector(dve, a, t + 1, (s + 1) % 4)
                if not is_last(t, 2):
                    own(dve, t + 2, (s + 2) % 4, 0, own0_ready)
                update_vector(dve, a, t)

            over_tiles(dve, slot)

        @block.gpsimd
        def _(pool):
            def keys(u, s):
                own(pool, u, s, 1, own1_ready)
                pool.tensor_copy(a.keys[s % 2][:, :], nw.k[:, bass.ds(u * P, P)]).then_inc(a.keys_ready, 1)

            for u in range(2):
                keys(u, u)
            softmax_divide_gpsimd(pool, a, 0, 0)

            def slot(t, s):
                if not is_last(t):
                    softmax_divide_gpsimd(pool, a, t + 1, (s + 1) % 4)
                if not is_last(t, 2):
                    keys(t + 2, (s + 2) % 4)

            over_tiles(pool, slot)


def attention2_weights(k):
    w = k.even
    return ([w[:, i * D:(i + 1) * D] for i in range(4)], w[:, 512:514], w[0:1, 640:640 + D],
            w[0:1, 768:768 + D])


def load_attention2(sp, k):
    (wq, wk, wv, wo), bqk, bv, bo = attention2_weights(k)
    d = k.dram
    k.load(sp, "even", wq, d["L2_xattn_wq"])
    k.load(sp, "even", wk[0:C], d["L2_xattn_wk"])
    k.load(sp, "even", wv[0:C], d["L2_xattn_wv"])
    k.load(sp, "even", wo, d["L2_xattn_wo"])
    with k.nc.allow_non_contiguous_dma(reason="two short biases, feature-major"):
        k.load(sp, "even", bqk[:, 0:1], d["L2_xattn_bq"].rearrange("(p a) -> p a", a=1))
        k.load(sp, "even", bqk[:, 1:2], d["L2_xattn_bk"].rearrange("(p a) -> p a", a=1))
    k.load(sp, "even", bv, row(d["L2_xattn_bv"], D))
    k.load(sp, "even", bo, row(d["L2_xattn_bo"], D))


def attention2(k, load_next):
    nc = k.nc
    (wq, wk, wv, wo), bqk, bv, bo = attention2_weights(k)
    with ExitStack() as outer:
        nw = Narrow(k, outer, "l2x")
        loaded = k.loads["even"]
        with ExitStack() as ctx:
            def sem(name):
                return Signals.new(nc, f"l2x_{name}")

            tr = Turned(k, ctx, "l2x")
            q_done, k_done, v_done = sem("q_done"), sem("k_done"), sem("v_done")
            q_ready, k_ready, v_ready = sem("q_ready"), sem("k_ready"), sem("v_ready")
            block = ctx.enter_context(nc.Block())

            @block.sync
            def _(sp):
                sp.dma_start(nw.own_q[:, :], k.dram["const_own8"]).then_inc(nw.masks_in, 16)
                sp.dma_start(nw.own_v[:, :], k.dram["const_own8"]).then_inc(nw.masks_in, 16)
                sp.wait_ge(nw.masks_in, 32)

            @block.tensor
            def _(pe):
                pe.wait_ge(k.load_even, loaded)
                for n in range(QUADS):
                    tr.tensor(pe, n)
                for n in range(QUADS):
                    cols = slice(n * QUAD, (n + 1) * QUAD)
                    after(pe, k_ready, n - 1)
                    pe.matmul(k.ps[1][:, n % 2, :], wk[0:C, :], k.ctxT[:, cols], start=True,
                              stop=True).then_inc(k_done, 1)
                    after(pe, v_ready, n - 1)
                    for j in range(4):
                        at = n * QUAD + j * P
                        out = k.ps[2][:, n % 2, j * D:(j + 1) * D]
                        pe.matmul(out, k.ctxT[:, at:at + P], wv[0:C, :], start=True, stop=False)
                        last = pe.matmul(out, k.ones[0:1, :], bv, start=False, stop=True)
                    last.then_inc(v_done, 1)
                    after(pe, q_ready, n - 1)
                    pe.wait_ge(tr.ready, n + 1)
                    pe.matmul(k.ps[0][:, n % 2, :], wq, tr.xnT[:, cols], start=True,
                              stop=True).then_inc(q_done, 1)

            @block.scalar
            def _(act):
                norm_root_scalar(act, k, tr.norm)
                act.wait_ge(k.load_even, loaded)
                for n in range(QUADS):
                    tr.scalar(act, n)
                for n in range(QUADS):
                    act.wait_ge(q_done, n + 1)
                    act.activation(nw.q[:, n * QUAD:(n + 1) * QUAD], k.ps[0][:, n % 2, :], ACT.Identity,
                                   bias=bqk[:, 0:1]).then_inc(q_ready, 1)

            @block.vector
            def _(dve):
                tr.vector(dve)
                dve.wait_ge(k.load_even, loaded)
                for n in range(QUADS):
                    dve.wait_ge(k_done, n + 1)
                    dve.tensor_scalar(nw.k[:, n * QUAD:(n + 1) * QUAD], k.ps[1][:, n % 2, :],
                                      bqk[:, 1:2], None, ALU.add).then_inc(k_ready, 1)
                    dve.wait_ge(v_done, n + 1)
                    dve.tensor_copy(nw.v[:, 4 * n:4 * n + 4, :].rearrange("p t n -> p (t n)"),
                                    k.ps[2][:, n % 2, :]).then_inc(v_ready, 1)

        narrow_attention(k, "l2xa", nw, wo, bo, None, load_next)



L2, E2 = 32, 7
HH = 4


def ffn2_weights(k):
    w = k.odd
    at = 3072
    small = {}
    for name, rows, n in (("kvd", D, L2), ("qd", D, L2), ("ku", L2, 64), ("qu", L2, 64), ("vu", L2, D),
                          ("ropeq", L2, 64), ("ropek", D, 64), ("o", D, D), ("router", D, 8),
                          ("ln1", D, 1), ("ln2", D, 1), ("bias", 1, 8)):
        small[name] = w[0:rows, at:at + n]
        at += n
    assert at <= 4352
    return (w[:, 0:2048].rearrange("p (e f) -> p e f", e=8),
            w[:, 2048:3072].rearrange("p (e c n) -> p e c n", e=8, c=1), small)


def load_ffn2(sp, k):
    up, down, w = ffn2_weights(k)
    d = {n[7:]: v for n, v in k.dram.items() if n.startswith("L2_ffn_")}
    for name, key in (("qd", "W_qd"), ("kvd", "W_kvd"), ("ku", "W_ku"), ("qu", "W_qu"), ("vu", "W_vu"),
                      ("ropeq", "W_ropeq"), ("ropek", "W_ropek"), ("o", "W_o")):
        k.load(sp, "odd", w[name], d[key])
    with k.nc.allow_non_contiguous_dma(reason="short weights, feature-major"):
        k.load(sp, "odd", w["router"][:, 0:E2], d["W_router"])
        k.load(sp, "odd", w["ln1"], d["w_ln1"].rearrange("(p a) -> p a", a=1))
        k.load(sp, "odd", w["ln2"], d["w_ln2"].rearrange("(p a) -> p a", a=1))
    k.load(sp, "odd", w["bias"][:, 0:E2], row(d["routing_bias"], E2))
    k.load(sp, "odd", up[:, 0:E2, 0:D], d["Wg_r"].rearrange("e d f -> d e f"))
    k.load(sp, "odd", up[:, 0:E2, D:2 * D], d["Wu_r"].rearrange("e d f -> d e f"))
    k.load(sp, "odd", down[:, 0:E2, 0, :], d["Wd_r"].rearrange("e d f -> d e f"))
    k.load(sp, "odd", up[:, E2, 0:D], d["Wg_s"])
    k.load(sp, "odd", up[:, E2, D:2 * D], d["Wu_s"])
    k.load(sp, "odd", down[:, E2, 0, :], d["Wd_s"])


def latent_attention(k, load_next):
    nc = k.nc
    _, _, w = ffn2_weights(k)
    with ExitStack() as outer:
        nw = Narrow(k, outer, "mla")
        causal = outer.enter_context(nc.sbuf_tensor("mla_causal", [P, 512], BF16))
        loaded = k.loads["odd"]
        with ExitStack() as ctx:
            def sb(name, shape):
                return ctx.enter_context(nc.sbuf_tensor(f"mla_{name}", shape, F32))

            def sem(name):
                return Signals.new(nc, f"mla_{name}")

            tr = Turned(k, ctx, "mla", rms=True, weight=w["ln1"])
            lat = [sb(f"lat{i}", [L2, 2, QUAD]) for i in range(2)]
            q_w, q_rot = sb("q_w", [L2, D]), sb("q_rot", [L2, D])
            k_w, kx_w, kx_rot = sb("k_w", [L2, D]), sb("kx_w", [D, D]), sb("kx_rot", [D, D])
            cos, sin = sb("cos", [P, SEQ]), sb("sin", [P, SEQ])
            mask32 = sb("mask32", [P, SEQ])
            turned_q, turned_k = sb("turned_q", [P, QUAD]), sb("turned_k", [P, QUAD])
            const_in, zeroed, w_ready = sem("const_in"), sem("zeroed"), sem("w_ready")
            mask_ready = sem("mask_ready")
            lat_done, lat_ready = sem("lat_done"), sem("lat_ready")
            q_done, k_done, v_done = sem("q_done"), sem("k_done"), sem("v_done")
            q_cos, q_sin, k_cos, k_sin = sem("q_cos"), sem("q_sin"), sem("k_cos"), sem("k_sin")
            q_ready, k_ready, v_ready = sem("q_ready"), sem("k_ready"), sem("v_ready")
            block = ctx.enter_context(nc.Block())

            @block.sync
            def _(sp):
                for out, name in ((nw.own_q, "const_own4"), (nw.own_v, "const_own8"), (cos, "const_cos"),
                                  (sin, "const_sin"), (mask32, "const_causal")):
                    sp.dma_start(out[:, :], k.dram[name]).then_inc(const_in, 16)
                sp.wait_ge(const_in, 80)

            @block.gpsimd
            def _(pool):
                for t in (q_rot, k_w, kx_w, kx_rot):
                    pool.memset(t[:, :], 0.0).then_inc(zeroed, 1)
                pool.wait_ge(const_in, 80)
                pool.tensor_copy(causal[:, :].rearrange("p (h k) -> p h k", k=SEQ),
                                 mask32[:, :].rearrange("p (a k) -> p a k", a=1).to_broadcast([P, 8, SEQ])
                                 ).then_inc(mask_ready, 1)
                for n in range(QUADS):
                    cols = slice(n * QUAD, (n + 1) * QUAD)
                    pool.wait_ge(q_sin, n + 1)
                    pool.tensor_tensor(nw.q[:, cols], nw.q[:, cols], turned_q[:, :], ALU.add).then_inc(
                        q_ready, 1)
                    pool.wait_ge(k_sin, n + 1)
                    pool.tensor_tensor(nw.k[:, cols], nw.k[:, cols], turned_k[:, :], ALU.add).then_inc(
                        k_ready, 1)

            @block.tensor
            def _(pe):
                for n in range(QUADS):
                    tr.tensor(pe, n)
                pe.wait_ge(w_ready, 9)
                pe.wait_ge(tr.ready, QUADS)

                def latents(n):
                    cols = slice(n * QUAD, (n + 1) * QUAD)
                    after(pe, lat_ready, n)
                    pe.matmul(k.ps[0][0:L2, 0, :], w["qd"], tr.xnT[:, cols], start=True, stop=True)
                    pe.matmul(k.ps[0][0:L2, 1, :], w["kvd"], tr.xnT[:, cols], start=True,
                              stop=True).then_inc(lat_done, 1)

                latents(0)
                for n in range(QUADS):
                    cols = slice(n * QUAD, (n + 1) * QUAD)
                    if n + 1 < QUADS:
                        latents(n + 1)
                    pe.wait_ge(lat_ready, n + 1)
                    ql, kvl = lat[n % 2][:, 0, :], lat[n % 2][:, 1, :]
                    after(pe, q_sin, n)
                    pe.matmul(k.ps[1][:, 0, :], q_w[:, :], ql, start=True, stop=True)
                    pe.matmul(k.ps[1][:, 1, :], q_rot[:, :], ql, start=True, stop=True).then_inc(q_done, 1)
                    after(pe, k_sin, n)
                    pe.matmul(k.ps[2][:, 0, :], k_w[:, :], kvl, start=True, stop=False)
                    pe.matmul(k.ps[2][:, 0, :], kx_w[:, :], tr.xnT[:, cols], start=False, stop=True)
                    pe.matmul(k.ps[2][:, 1, :], kx_rot[:, :], tr.xnT[:, cols], start=True,
                              stop=True).then_inc(k_done, 1)
                    after(pe, v_ready, n - 1)
                    for j in range(4):
                        last = pe.matmul((k.r6, k.r7)[n % 2][:, j * D:(j + 1) * D],
                                         lat[n % 2][:, 1, j * P:(j + 1) * P], w["vu"], start=True, stop=True)
                    last.then_inc(v_done, 1)

            @block.scalar
            def _(act):
                norm_root_scalar(act, k, tr.norm, rms=True)
                act.wait_ge(k.load_odd, loaded)
                for n in range(QUADS):
                    tr.scalar(act, n)
                for n in range(QUADS):
                    act.wait_ge(lat_done, n + 1)
                    after(act, v_done, n - 1)
                    act.copy(lat[n % 2][:, :, :], k.ps[0][0:L2, :, :]).then_inc(lat_ready, 1)
                    act.wait_ge(v_done, n + 1)
                    act.copy(nw.v[:, 4 * n:4 * n + 4, :].rearrange("p t n -> p (t n)"),
                             (k.r6, k.r7)[n % 2][:, :]).then_inc(v_ready, 1)

            @block.vector
            def _(dve):
                dve.wait_ge(k.load_odd, loaded)
                dve.wait_ge(zeroed, 4)
                dve.tensor_copy(q_w[:, 0:64], w["qu"]).then_inc(w_ready, 1)
                dve.tensor_copy(q_w[:, 64:D], w["ropeq"]).then_inc(w_ready, 1)
                dve.tensor_copy(k_w[:, 0:64], w["ku"]).then_inc(w_ready, 1)
                dve.tensor_copy(kx_w[:, 64:D], w["ropek"]).then_inc(w_ready, 1)
                for src, out in ((w["ropeq"], q_rot), (w["ropek"], kx_rot)):
                    sv = src.rearrange("p (h j) -> p h j", j=HH)
                    ov = out[:, 64:D].rearrange("p (h j) -> p h j", j=HH)
                    dve.tensor_scalar(ov[:, :, 0:2], sv[:, :, 2:4], -1.0, None, ALU.mult).then_inc(w_ready, 1)
                    dve.tensor_copy(ov[:, :, 2:4], sv[:, :, 0:2]).then_inc(w_ready, 1)
                dve.sem_inc(w_ready, 1)
                tr.vector(dve)
                dve.wait_ge(const_in, 80)

                def table(t):
                    return t[:, :].rearrange("p (a n) -> p a n", a=1).to_broadcast([P, QUAD // SEQ, SEQ])

                def items(ap):
                    return ap.rearrange("p (b n) -> p b n", n=SEQ)

                for n in range(QUADS):
                    cols = slice(n * QUAD, (n + 1) * QUAD)
                    for bank, out, tmp, done, c_sem, s_sem, ready in (
                            (k.ps[1], nw.q, turned_q, q_done, q_cos, q_sin, q_ready),
                            (k.ps[2], nw.k, turned_k, k_done, k_cos, k_sin, k_ready)):
                        dve.wait_ge(done, n + 1)
                        dve.tensor_tensor(items(out[:, cols]), items(bank[:, 0, :]), table(cos),
                                          ALU.mult).then_inc(c_sem, 1)
                        after(dve, ready, n)
                        dve.tensor_tensor(items(tmp[:, :]), items(bank[:, 1, :]), table(sin),
                                          ALU.mult).then_inc(s_sem, 1)

        narrow_attention(k, "mlaa", nw, w["o"], None, causal[:, :], load_next)


def experts2(k, load_next):
    nc = k.nc
    up, down, w = ffn2_weights(k)
    with ExitStack() as ctx:
        tr = Turned(k, ctx, "l2f", rms=True, weight=w["ln2"])
        ro = Router(k, ctx, "l2f", E2)
        ex = Experts(k, ctx, "l2f", tr.xnT, 8, up, down, True, weight=ro.weight)
        block = ctx.enter_context(nc.Block())

        @block.sync
        def _(sp):
            load_next(sp)

        @block.tensor
        def _(pe):
            for n in range(QUADS):
                tr.tensor(pe, n)
            pe.wait_ge(tr.ready, QUADS)
            ro.tensor(pe, tr.xnT, w["router"][:, 0:E2], w["bias"][:, 0:E2])
            pe.wait_ge(ro.ready, 1)
            ex.tensor(pe)

        @block.scalar
        def _(act):
            norm_root_scalar(act, k, tr.norm, rms=True)
            for n in range(QUADS):
                tr.scalar(act, n)
            act.wait_ge(ro.ready, 1)
            act.activation(ro.soft[:, :, :], ro.score[:, :, :], ACT.Sigmoid).then_inc(ro.soft_ready, 1)
            ex.scalar(act)

        @block.vector
        def _(dve):
            tr.vector(dve)
            link = linked(dve, ro.step)
            dve.wait_ge(ro.scored, 1)
            dve.wait_ge(ro.index_ready, 1)
            dve.tensor_copy(ro.score[:, :, :], ro.bank()).then_inc(ro.ready, 1)
            dve.wait_ge(ro.soft_ready, 1)
            ro.first_top(dve, link, ro.soft[:, :, :], 0)
            link(dve.scalar_tensor_tensor(ro.score[:, :, :], ro.hot[0][:, :, :], -2.0, ro.soft[:, :, :],
                                          ALU.mult, ALU.add))
            ro.first_top(dve, link, ro.score[:, :, :], 1)
            link(dve.tensor_tensor(ro.first[:, :], ro.top[0][:, :], ro.top[1][:, :], ALU.add))
            link(dve.reciprocal(ro.first[:, :], ro.first[:, :]))
            for n in range(2):
                link(dve.tensor_tensor(ro.hot[n][:, :, :], ro.hot[n][:, :, :],
                                       spread(ro.top[n][:, :], E2), ALU.mult))
            link(dve.tensor_tensor(ro.hot[0][:, :, :], ro.hot[0][:, :, :], ro.hot[1][:, :, :], ALU.add))
            weight = ro.weight[:, :].rearrange("p (t e) -> p t e", e=8)
            link(dve.tensor_tensor(weight[:, :, 0:E2], ro.hot[0][:, :, :], spread(ro.first[:, :], E2),
                                   ALU.mult))
            link(dve.memset(weight[:, :, E2:8], 1.0))
            ex.vector(dve)

        @block.gpsimd
        def _(pool):
            ro.gpsimd(pool)


def ffn2(k, load_next):
    nc, x = k.nc, k.x
    y = k.ctx2[:, :, :].rearrange("p b c -> p (b c)")[:, 0:TILES * D].rearrange("p (t d) -> p t d", d=D)
    with ExitStack() as ctx:
        norm = NormSems(nc, ctx, "l2n")
        y_ready = Signals.new(nc, "l2n_y_ready")
        stats_done = Signals.new(nc, "l2n_stats_done")
        block = ctx.enter_context(nc.Block())

        @block.scalar
        def _(act):
            norm_root_scalar(act, k, norm)

        @block.vector
        def _(dve):
            norm_stats_vector(dve, k, norm)
            for t in range(TILES):
                normalise(dve, k, y[:, t:t + 1, :], t).then_inc(y_ready, 1)
            for t in range(TILES):
                dve.wait_ge(y_ready, t + 1)
                dve.bn_stats(k.stats[:, t, :], y[:, t, :]).then_inc(stats_done, 1)

    k.x = y
    latent_attention(k, load_next)
    experts2(k, lambda sp: None)
    k.x = x
    with ExitStack() as ctx:
        updated = Signals.new(nc, "l2e_updated")
        stats_done = Signals.new(nc, "l2e_stats_done")
        ctx2_in = Signals.new(nc, "l2e_ctx2_in")
        block = ctx.enter_context(nc.Block())

        @block.vector
        def _(dve):
            for n in range(QUADS):
                tiles = slice(4 * n, 4 * n + 4)
                dve.tensor_tensor(x[:, tiles, :], x[:, tiles, :], y[:, tiles, :], ALU.add).then_inc(updated, 1)
            for n in range(QUADS):
                dve.wait_ge(updated, n + 1)
                for j in range(4):
                    last = dve.bn_stats(k.stats[:, 4 * n + j, :], x[:, 4 * n + j, :])
                last.then_inc(stats_done, 1)

        @block.sync
        def _(sp):
            sp.wait_ge(updated, QUADS)
            load_ctx2(sp, k, ctx2_in)
            sp.wait_ge(ctx2_in, 32)


def shape_constants():
    import numpy as np

    feature = np.arange(P)
    head = np.arange(H)
    own8 = (feature[:, None] // (D // H) == head).astype(np.float32)
    own4 = ((feature[:, None] % 64) // HH == head).astype(np.float32)
    position = np.arange(SEQ, dtype=np.float32)
    freq = (np.float32(1.0) / np.float32(10000.0) ** (np.arange(0, HH, 2, dtype=np.float32) / np.float32(HH)))
    angle = np.einsum("i,j->ji", position, np.concatenate([freq, freq]).astype(np.float32))
    cos, sin = np.ones((P, SEQ), np.float32), np.zeros((P, SEQ), np.float32)
    cos[64:], sin[64:] = np.tile(np.cos(angle), (H, 1)), np.tile(np.sin(angle), (H, 1))
    query = feature[:, None] % SEQ
    causal = np.where(np.arange(SEQ)[None, :] <= query, 0.0, -1e30).astype(np.float32)
    cross = np.where(feature[:, None] // SEQ == feature[None, :] // SEQ, 0.0, -1e30).astype(np.float32)
    return {"const_cross": cross, "const_own8": own8, "const_own4": own4, "const_cos": cos, "const_sin": sin,
            "const_causal": causal}



def load_ctx2(sp, k, sem):
    for par in range(2):
        sp.dma_start(k.ctx2[par * SEQ:(par + 1) * SEQ, :, :],
                     k.dram["ctx_768"].rearrange("b s c -> s b c")).then_inc(sem, 16)


def start(k, load_next):
    nc = k.nc
    d = k.dram
    with ExitStack() as ctx:
        def sem(name):
            return Signals.new(nc, name)

        consts, ones_at, zeros_at = sem("consts_ready"), sem("ones_ready"), sem("zeros_ready")
        x_in, ctx_in, ctxT_done, ctxT_ready = sem("x_in"), sem("ctx_in"), sem("ctxT_done"), sem("ctxT_ready")
        stats0 = sem("stats0")
        k.start_stats = stats0
        block = ctx.enter_context(nc.Block())
        HALF = TILES // 2

        @block.sync
        def _(sp):
            load_ctx2(sp, k, ctx_in)
            xv = d["x"].rearrange("b s d -> (b s) d").rearrange("(t p) d -> p t d", p=P)
            for j in range(2):
                sp.dma_start(k.x[:, j * HALF:(j + 1) * HALF, :],
                             xv[:, j * HALF:(j + 1) * HALF, :]).then_inc(x_in, 16)
            load_next(sp)
            sp.wait_ge(ctx_in, 32)

        @block.gpsimd
        def _(pool):
            pool.memset(k.ident[:, :], 0.0).then_inc(zeros_at, 1)
            pool.memset(k.ones[:, :], 1.0).then_inc(ones_at, 1)
            pool.memset(k.eps[:, :], LN_EPS).then_inc(ones_at, 1)
            pool.wait_ge(zeros_at, 1)
            pool.affine_select(out=k.ident[:, :], in_=k.ident[:, :], compare_op=ALU.not_equal, fill=1.0,
                               base=0, pattern=[[-1, P]], channel_multiplier=1).then_inc(consts, 1)
            pool.wait_ge(consts, 1)
            pool.tensor_copy(k.identb[:, :], k.ident[:, :]).then_inc(consts, 1)

        @block.tensor
        def _(pe):
            pe.wait_ge(consts, 1)
            pe.wait_ge(ctx_in, 32)
            for n in range(BATCH // 8):
                after(pe, ctxT_ready, n - 1)
                for j in range(8):
                    last = pe.transpose(k.ps[0][0:C, n % 2, j * SEQ:(j + 1) * SEQ],
                                        k.ctx2[0:SEQ, 8 * n + j, :], k.ident[0:SEQ, 0:SEQ])
                last.then_inc(ctxT_done, 1)

        @block.scalar
        def _(act):
            for n in range(BATCH // 8):
                act.wait_ge(ctxT_done, n + 1)
                act.copy(k.ctxT[:, n * 512:(n + 1) * 512], k.ps[0][0:C, n % 2, :]).then_inc(ctxT_ready, 1)

        @block.vector
        def _(dve):
            dve.wait_ge(x_in, 32)
            with dve.Fori(0, TRIPS) as i:
                for s in range(UNROLL):
                    t = i * UNROLL + s
                    dve.bn_stats(k.stats[:, bass.ds(t, 1), :].rearrange("p a d -> p (a d)"),
                                 k.x[:, bass.ds(t, 1), :].rearrange("p a d -> p (a d)")).then_inc(stats0, 1)


def finish(k, out):
    with ExitStack() as ctx:
        out_done = Signals.new(k.nc, "out_done")
        block = ctx.enter_context(k.nc.Block())

        @block.sync
        def _(sp):
            ov = out.rearrange("b s d -> (b s) d").rearrange("(t p) d -> p t d", p=P)
            sp.wait_ge(k.load_even, k.loads["even"]) if k.loads["even"] else None
            sp.wait_ge(k.load_odd, k.loads["odd"]) if k.loads["odd"] else None
            sp.dma_start(ov, k.x[:, :, :]).then_inc(out_done, 16)
            sp.wait_ge(out_done, 16)


def four_layers(nc, dram, out, upto=8, only=0):
    with ExitStack() as ctx:
        Signals.live = []
        k = Core(nc, ctx, dram)
        nothing = lambda sp: None
        layers = [
            (lambda n: wide_attention(k, "l0x", "L0_xattn_", n), lambda sp: load_wide(sp, k, "L0_xattn_")),
            (lambda n: ffn0(k, n), lambda sp: load_ffn0(sp, k)),
            (lambda n: attention1(k, n), lambda sp: load_attention1(sp, k)),
            (lambda n: ffn1(k, n), lambda sp: load_ffn1(sp, k)),
            (lambda n: attention2(k, n), lambda sp: load_attention2(sp, k)),
            (lambda n: ffn2(k, n), lambda sp: load_ffn2(sp, k)),
            (lambda n: wide_attention(k, "l3x", "L3_xattn_", n), lambda sp: load_wide(sp, k, "L3_xattn_")),
            (lambda n: ffn3(k), lambda sp: load_ffn3(sp, k)),
        ]
        start(k, layers[only][1] if upto else nothing)
        for i in range(only, upto):
            Signals.retire(nc)
            layers[i][0](layers[i + 1][1] if i + 1 < upto else nothing)
        finish(k, out)



def kernel(**inputs):
    import numpy as np
    import concourse.bacc as bacc
    from concourse.bass_utils import run_bass_kernel_spmd

    nc = bacc.Bacc("TRN2", target_bir_lowering=False, num_devices=1)
    arrays, dram = {}, {}
    for name, value in {**inputs, **shape_constants()}.items():
        a = np.ascontiguousarray(value)
        arrays[f"in_{name}"] = a
        dram[name] = nc.dram_tensor(f"in_{name}", a.shape, mybir.dt.from_np(a.dtype),
                                    kind="ExternalInput").ap()
    out = nc.dram_tensor("out_x", inputs["x"].shape, F32, kind="ExternalOutput").ap()
    four_layers(nc, dram, out)
    r = run_bass_kernel_spmd(nc, [arrays], core_ids=[0])
    return r.results[0]["out_x"]
```

```python
from contextlib import ExitStack

import concourse.bass as bass
from concourse import mybir

F32 = mybir.dt.float32
BF16 = mybir.dt.bfloat16
ALU = mybir.AluOpType
ACT = mybir.ActivationFunctionType
AX = mybir.AxisListType
RMAX = bass.bass_isa.ReduceOp.max
RADD = bass.bass_isa.ReduceOp.add

P = 128
D = 128
C = 96
BATCH, SEQ = 64, 64
TOK = BATCH * SEQ
TILES = TOK // P
H = 16
GT = 2 * P
GROUPS = TOK // GT
UNROLL = 4
TRIPS = TILES // UNROLL
LN_EPS = 1e-5


class Signals:

    live = []

    @classmethod
    def new(cls, nc, name):
        sem = nc.alloc_semaphore(name)
        cls.live.append(sem)
        return sem

    @classmethod
    def retire(cls, nc):
        nc.all_engine_barrier()
        nc.clear_and_free_semaphores(cls.live)
        nc.all_engine_barrier()
        cls.live = []


def after(eng, sem, count):
    if not isinstance(count, int) or count > 0:
        eng.wait_ge(sem, count)


def over_tiles(eng, slot):
    for s in range(UNROLL):
        slot(s, s)
    with eng.Fori(1, TRIPS - 1) as i:
        for s in range(UNROLL):
            slot(i * UNROLL + s, s)
    for s in range(UNROLL):
        slot(TILES - UNROLL + s, s)


def is_last(t, n=1):
    return isinstance(t, int) and t >= TILES - n


class Core:

    def __init__(self, nc, ctx, dram):
        self.nc, self.dram = nc, dram

        def sb(name, shape, dt=F32):
            return ctx.enter_context(nc.sbuf_tensor(name, shape, dt))

        self.x = sb("x", [P, TILES, D])
        self.ctxT = sb("ctxT", [C + 1, TOK])
        self.ctx2 = sb("ctx2", [P, BATCH, C])
        self.stats = sb("stats", [P, TILES, 6])
        self.mean = sb("mean", [P, TILES])
        self.var = sb("var", [P, TILES])
        self.rstd = sb("rstd", [P, TILES])
        self.tmp = sb("tmp", [P, TILES])
        self.tmp2 = sb("tmp2", [P, TILES])
        self.eps = sb("eps", [P, 1])
        self.ident = sb("ident", [P, P])
        self.identb = sb("identb", [P, P], BF16)
        self.ones = sb("ones", [P, P])
        self.even_words, self.odd_words = 4096 + 256, 8704 + 256
        self.even = sb("even", [P, self.even_words])
        self.odd = sb("odd", [P, self.odd_words])
        self.ps = [ctx.enter_context(nc.psum_tensor(f"bank{2 * i}_{2 * i + 1}", [P, 2, 512], F32))
                   for i in range(3)]
        self.r6 = ctx.enter_context(nc.psum_tensor("bank6", [P, 512], F32))
        self.r7 = ctx.enter_context(nc.psum_tensor("bank7", [P, 512], F32))
        self.load_even = ctx.enter_context(nc.semaphore("load_even"))
        self.load_odd = ctx.enter_context(nc.semaphore("load_odd"))
        self.loads = {"even": 0, "odd": 0}

    def load(self, eng, side, out, in_):
        sem = self.load_even if side == "even" else self.load_odd
        self.loads[side] += 16
        eng.dma_start(out, in_).then_inc(sem, 16)


def row(ap, n):
    return ap.rearrange("(a n) -> a n", a=1)



class NormSems:
    def __init__(self, nc, ctx, tag):
        self.chain = Signals.new(nc, f"{tag}_stat_step")
        self.root = Signals.new(nc, f"{tag}_root_ready")
        self.ready = Signals.new(nc, f"{tag}_rstd_ready")


def norm_stats_vector(dve, k, n, rms=False):
    me, mo = k.stats[:, :, 1], k.stats[:, :, 4]
    step = 0

    def link(ins):
        nonlocal step
        step += 1
        ins.then_inc(n.chain, 1)
        dve.wait_ge(n.chain, step)

    link(dve.tensor_tensor(k.mean[:, :], me, mo, ALU.add))
    link(dve.tensor_tensor(k.tmp[:, :], me, mo, ALU.subtract))
    link(dve.tensor_scalar(k.mean[:, :], k.mean[:, :], 0.5, None, ALU.mult))
    link(dve.tensor_tensor(k.tmp[:, :], k.tmp[:, :], k.tmp[:, :], ALU.mult))
    link(dve.tensor_tensor(k.var[:, :], k.stats[:, :, 2], k.stats[:, :, 5], ALU.add))
    link(dve.tensor_scalar(k.tmp[:, :], k.tmp[:, :], 0.25, None, ALU.mult))
    if rms:
        link(dve.scalar_tensor_tensor(k.var[:, :], k.var[:, :], 1.0 / D, k.tmp[:, :], ALU.mult, ALU.add))
        link(dve.tensor_tensor(k.tmp[:, :], k.mean[:, :], k.mean[:, :], ALU.mult))
        dve.tensor_tensor(k.var[:, :], k.var[:, :], k.tmp[:, :], ALU.add).then_inc(n.chain, 1)
        dve.wait_ge(n.root, 1)
        link_at = step + 1
        dve.tensor_scalar(k.tmp[:, :], k.tmp2[:, :], LN_EPS, None, ALU.add).then_inc(n.chain, 1)
        dve.wait_ge(n.chain, link_at + 1)
        dve.reciprocal(k.rstd[:, :], k.tmp[:, :]).then_inc(n.ready, 1)
    else:
        dve.scalar_tensor_tensor(k.var[:, :], k.var[:, :], 1.0 / D, k.tmp[:, :], ALU.mult,
                                 ALU.add).then_inc(n.chain, 1)
        dve.wait_ge(n.root, 1)
        dve.reciprocal(k.rstd[:, :], k.tmp2[:, :]).then_inc(n.ready, 1)
    dve.wait_ge(n.ready, 1)


NORM_STEPS, RMS_STEPS = 7, 9


def norm_root_scalar(act, k, n, rms=False):
    act.wait_ge(n.chain, RMS_STEPS if rms else NORM_STEPS)
    act.activation(k.tmp2[:, :], k.var[:, :], ACT.Sqrt,
                   bias=0.0 if rms else k.eps[:, 0:1]).then_inc(n.root, 1)


def normalise(dve, k, out, t):
    return dve.tensor_scalar(out, k.x[:, bass.ds(t, 1), :], k.mean[:, bass.ds(t, 1)],
                             k.rstd[:, bass.ds(t, 1)], ALU.subtract, ALU.mult)



class Attention:

    def __init__(self, k, ctx, tag, kc, vc, scale):
        nc = k.nc
        self.k, self.kc, self.vc, self.scale = k, kc, vc, scale

        def sb(name, shape, dt=F32):
            return ctx.enter_context(nc.sbuf_tensor(f"{tag}_{name}", shape, dt))

        def sem(name):
            return Signals.new(nc, f"{tag}_{name}")

        self.qh = [sb(f"qh{i}", [kc, H, GT]) for i in range(2)]
        self.keys = [sb(f"keys{i}", [kc, P]) for i in range(2)]
        self.values = [sb(f"values{i}", [P, 2, vc]) for i in range(2)]
        self.xn = [sb(f"xn{i}", [P, 2, D]) for i in range(2)]
        self.xnT = [sb(f"xnT{i}", [D, GT]) for i in range(2)]
        self.prob = [sb(f"prob{i}", [P, H, SEQ]) for i in range(2)]
        self.probT = sb("probT", [P, H // 2, P])
        self.oT = sb("oT", [vc, H, P])
        self.top = [sb(f"top{i}", [P, H]) for i in range(2)]
        self.total = [sb(f"total{i}", [P, H]) for i in range(2)]
        self.share = [sb(f"share{i}", [P, H]) for i in range(2)]
        self.wo = sb("wo", [vc, H, D])
        self.S, self.T, self.O = k.ps
        self.norm = NormSems(nc, ctx, tag)
        self.xn_ready = sem("xn_ready")
        self.xnT_done = sem("xnT_done")
        self.xnT_ready = sem("xnT_ready")
        self.keys_ready = sem("keys_ready")
        self.values_ready = sem("values_ready")
        self.scores_done = sem("scores_done")
        self.top_ready = sem("top_ready")
        self.shifted = sem("shifted")
        self.exp_ready = sem("exp_ready")
        self.total_ready = sem("total_ready")
        self.share_ready = sem("share_ready")
        self.prob_ready = sem("prob_ready")
        self.turned = sem("turned")
        self.probT_ready = sem("probT_ready")
        self.weighed = sem("weighed")
        self.o0_ready = sem("o0_ready")
        self.o1_ready = sem("o1_ready")
        self.projected = sem("projected")
        self.updated = sem("updated")
        self.stats_done = sem("stats_done")
        self.q6_done, self.q7_done = sem("q6_done"), sem("q7_done")
        self.q6_ready, self.q7_ready = sem("q6_ready"), sem("q7_ready")


def half(u):
    return (u // 2) % 2, u % 2


def scores_tensor(pe, a, u, s):
    g, tt = half(s)
    pe.wait_ge(a.keys_ready, u + 1)
    after(pe, a.shifted, u)
    for h in range(H):
        for b in range(2):
            last = pe.matmul(a.S[b * SEQ:(b + 1) * SEQ, h // 8, (h % 8) * SEQ:(h % 8 + 1) * SEQ],
                             a.qh[g][:, h, tt * P + b * SEQ:tt * P + (b + 1) * SEQ],
                             a.keys[s % 2][:, b * SEQ:(b + 1) * SEQ], start=True, stop=True)
    last.then_inc(a.scores_done, 1)


def turn_tensor(pe, a, t, s):
    pe.wait_ge(a.prob_ready, t + 1)
    after(pe, a.o1_ready, t)
    for p in range(H // 2):
        last = pe.transpose(a.T[:, p // 4, (p % 4) * P:(p % 4 + 1) * P],
                            a.prob[s % 2][:, 2 * p:2 * p + 2, :].rearrange("p h k -> p (h k)"),
                            a.k.ident[:, :])
    last.then_inc(a.turned, 1)


def weigh_tensor(pe, a, t, s):
    pe.wait_ge(a.probT_ready, t + 1)
    pe.wait_ge(a.values_ready, t + 1)
    after(pe, a.o0_ready, t)
    for b in range(2):
        bank = a.O if b == 0 else a.T
        for par in range(2):
            rows = slice(par * SEQ, (par + 1) * SEQ)
            last = pe.matmul(bank[0:a.vc, par, :], a.values[s % 2][rows, b, :],
                             a.probT[rows, :, b * SEQ:(b + 1) * SEQ], start=True, stop=True)
        last.then_inc(a.weighed, 1)


def project_tensor(pe, a, t, bias):
    pe.wait_ge(a.o0_ready, t + 1)
    pe.wait_ge(a.o1_ready, t + 1)
    for h in range(H):
        last = pe.matmul(a.k.r6[:, 0:D], a.oT[:, h, :], a.wo[:, h, :], start=h == 0,
                         stop=h == H - 1 and bias is None)
    if bias is not None:
        last = pe.matmul(a.k.r6[:, 0:D], a.k.ones[0:1, :], bias, start=False, stop=True)
    last.then_inc(a.projected, 1)


def turn_xn_tensor(pe, a, m, par):
    pe.wait_ge(a.xn_ready, m + 1)
    for j in range(2):
        last = pe.transpose(a.k.r7[:, j * P:(j + 1) * P], a.xn[par][:, j, :], a.k.ident[:, :])
    last.then_inc(a.xnT_done, 1)


def softmax_top_vector(dve, a, u, s):
    dve.wait_ge(a.scores_done, u + 1)
    scores = a.S[:, :, :].rearrange("p a (h k) -> p (a h) k", k=SEQ)
    dve.tensor_reduce(a.top[s % 2][:, :], scores, AX.X, ALU.max).then_inc(a.top_ready, 1)
    dve.wait_ge(a.top_ready, u + 1)
    after(dve, a.turned, u - 1)
    dve.tensor_tensor(a.prob[s % 2][:, :, :], scores,
                      a.top[s % 2][:, :].rearrange("p (h a) -> p h a", a=1).to_broadcast([P, H, SEQ]),
                      ALU.subtract).then_inc(a.shifted, 1)


def softmax_exp_scalar(act, a, u, s):
    act.wait_ge(a.shifted, u + 1)
    act.activation(a.prob[s % 2][:, :, :], a.prob[s % 2][:, :, :], ACT.Exp,
                   scale=a.scale).then_inc(a.exp_ready, 1)


def softmax_total_vector(dve, a, u, s):
    dve.wait_ge(a.exp_ready, u + 1)
    dve.tensor_reduce(a.total[s % 2][:, :], a.prob[s % 2][:, :, :], AX.X,
                      ALU.add).then_inc(a.total_ready, 1)
    dve.wait_ge(a.total_ready, u + 1)
    after(dve, a.prob_ready, u - 1)
    dve.reciprocal(a.share[s % 2][:, :], a.total[s % 2][:, :]).then_inc(a.share_ready, 1)


def softmax_divide_gpsimd(pool, a, u, s):
    pool.wait_ge(a.share_ready, u + 1)
    pool.tensor_tensor(a.prob[s % 2][:, :, :], a.prob[s % 2][:, :, :],
                       a.share[s % 2][:, :].rearrange("p (h a) -> p h a", a=1).to_broadcast([P, H, SEQ]),
                       ALU.mult).then_inc(a.prob_ready, 1)


def copy_probT_scalar(act, a, t):
    act.wait_ge(a.turned, t + 1)
    after(act, a.weighed, 2 * t)
    act.copy(a.probT[:, :, :], a.T[:, :, :].rearrange("p a (c q) -> p (a c) q", q=P)).then_inc(
        a.probT_ready, 1)


def output_views(a, bank, b):
    out = a.oT[:, :, b * SEQ:(b + 1) * SEQ].rearrange("c (p a) q -> c a p q", a=2)
    return out, bank[0:a.vc, :, :].rearrange("c a (p q) -> c a p q", q=SEQ)


def copy_o0_scalar(act, a, t):
    act.wait_ge(a.weighed, 2 * t + 1)
    after(act, a.projected, t)
    out, src = output_views(a, a.O, 0)
    act.copy(out, src).then_inc(a.o0_ready, 1)


def copy_o1_vector(dve, a, t):
    dve.wait_ge(a.weighed, 2 * t + 2)
    after(dve, a.projected, t)
    out, src = output_views(a, a.T, 1)
    dve.tensor_copy(out, src).then_inc(a.o1_ready, 1)


def update_vector(dve, a, t):
    k = a.k
    dve.wait_ge(a.projected, t + 1)
    xt = k.x[:, bass.ds(t, 1), :].rearrange("p a d -> p (a d)")
    dve.tensor_tensor(xt, xt, k.r6[:, 0:D], ALU.add).then_inc(a.updated, 1)
    dve.wait_ge(a.updated, t + 1)
    dve.bn_stats(k.stats[:, bass.ds(t, 1), :].rearrange("p a d -> p (a d)"), xt).then_inc(a.stats_done, 1)


def normalise_group_vector(dve, a, m, par):
    after(dve, a.xnT_done, m - 1)
    for j in range(2):
        last = normalise(dve, a.k, a.xn[par][:, j:j + 1, :], m * 2 + j)
    last.then_inc(a.xn_ready, 1)


def copy_xnT_scalar(act, a, m, par, before=None):
    act.wait_ge(a.xnT_done, m + 1)
    if before is not None:
        after(act, *before)
    act.copy(a.xnT[par][:, :], a.k.r7[:, 0:GT]).then_inc(a.xnT_ready, 1)



DH = 64


def fold_tensors(k, ctx, tag):
    def sb(name, shape):
        return ctx.enter_context(k.nc.sbuf_tensor(f"{tag}_{name}", shape, F32))

    class Fold:
        m = sb("m", [D, H, C])
        turned = [sb(f"turned{i}", [P, D + 2 * C]) for i in range(2)]
        turn_done = Signals.new(k.nc, f"{tag}_fold_turned")
        turn_ready = Signals.new(k.nc, f"{tag}_fold_copied")
        fold_done = Signals.new(k.nc, f"{tag}_folded")
        m_ready = Signals.new(k.nc, f"{tag}_m_ready")
        w_ready = Signals.new(k.nc, f"{tag}_w_ready")
    return Fold


def wide_weights(k):
    w = k.even
    return (w[:, 0:1024], w[0:C, 1024:2048], w[0:C, 2048:3072],
            w[:, 3072:4096].rearrange("p (c n) -> p c n", n=D), w[0:1, 4096:4096 + D])


def load_wide(sp, k, pre):
    wq, wk, wv, wo, bo = wide_weights(k)
    d = k.dram
    k.load(sp, "even", wq, d[f"{pre}Wq"])
    k.load(sp, "even", wk, d[f"{pre}Wk"])
    k.load(sp, "even", wv, d[f"{pre}Wv"])
    k.load(sp, "even", wo, d[f"{pre}Wo"].rearrange("(c p) n -> p c n", p=P))
    k.load(sp, "even", bo, row(d[f"{pre}bo"], D))


def fold_tensor(pe, k, a, f):
    wq, wk, wv, wo, _ = wide_weights(k)
    T = k.ps[0]

    def turn(p):
        after(pe, f.turn_ready, p - 1)
        cols = slice(p * P, (p + 1) * P)
        pe.transpose(T[:, p % 2, 0:D], wq[:, cols], k.ident[:, :])
        pe.transpose(T[:, p % 2, D:D + C], wk[:, cols], k.ident[0:C, 0:C])
        pe.transpose(T[:, p % 2, D + C:D + 2 * C], wv[:, cols], k.ident[0:C, 0:C]).then_inc(
            f.turn_done, 1)

    turn(0)
    for p in range(H // 2):
        if p + 1 < H // 2:
            turn(p + 1)
        pe.wait_ge(f.turn_ready, p + 1)
        after(pe, f.m_ready, p)
        after(pe, f.w_ready, p)
        t, M, W = f.turned[p % 2], k.ps[1], k.ps[2]
        for par in range(2):
            rows = slice(par * DH, (par + 1) * DH)
            pe.matmul(M[:, par, 0:C], t[rows, 0:D], t[rows, D:D + C],
                      start=True, stop=True)
            last = pe.matmul(W[0:C, par, 0:D],
                             t[rows, D + C:D + 2 * C], wo[rows, p, :], start=True, stop=True)
        last.then_inc(f.fold_done, 1)


def fold_scalar(act, k, a, f):
    T = k.ps[0]
    for p in range(H // 2):
        act.wait_ge(f.turn_done, p + 1)
        after(act, f.fold_done, p - 1)
        act.copy(f.turned[p % 2][:, :], T[:, p % 2, 0:D + 2 * C]).then_inc(f.turn_ready, 1)
        act.wait_ge(f.fold_done, p + 1)
        act.copy(f.m[:, 2 * p:2 * p + 2, :],
                 k.ps[1][:, :, 0:C]).then_inc(f.m_ready, 1)


def fold_vector(dve, k, a, f):
    for p in range(H // 2):
        dve.wait_ge(f.fold_done, p + 1)
        dve.tensor_copy(a.wo[:, 2 * p:2 * p + 2, :],
                        k.ps[2][0:C, :, 0:D]).then_inc(
                            f.w_ready, 1)


def wide_queries_tensor(pe, a, f, n, s, freed6, freed7):
    g, hh = half(s)
    pe.wait_ge(a.xnT_ready, (n + 2 - hh) // 2 if isinstance(n, int) else (n - hh) // 2 + 1)
    for j in range(4):
        bank = (a.k.r6, a.k.r7)[j % 2]
        if j == 0:
            after(pe, *freed6)
        elif j == 1:
            after(pe, *freed7)
        elif j == 2:
            pe.wait_ge(a.q6_ready, n * 2 + 1)
        else:
            pe.wait_ge(a.q7_ready, n * 2 + 1)
        for e in range(2):
            last = pe.matmul(bank[0:C, e * GT:(e + 1) * GT], f.m[:, 8 * hh + 2 * j + e, :],
                             a.xnT[g][:, :], start=True, stop=True)
        last.then_inc((a.q6_done, a.q7_done)[j % 2], 1)


def copy_queries(copy, eng, a, n, s, j, done, ready, used):
    g, hh = half(s)
    eng.wait_ge(done, n * 2 + 1 + j // 2)
    after(eng, *used)
    h = 8 * hh + 2 * j
    copy(a.qh[g][:, h:h + 2, :],
         (a.k.r6, a.k.r7)[j % 2][0:C, :].rearrange("c (e q) -> c e q", e=2)).then_inc(ready, 1)


LEAD = 3


def wide_attention(k, tag, pre, load_next, first=None):
    nc = k.nc
    with ExitStack() as ctx:
        a = Attention(k, ctx, tag, C, C, float(DH) ** -0.5)
        f = fold_tensors(k, ctx, tag)
        loaded = k.loads["even"]
        bias = wide_weights(k)[4]
        block = ctx.enter_context(nc.Block())

        @block.sync
        def _(sp):
            load_next(sp)

        @block.tensor
        def _(pe):
            pe.wait_ge(k.load_even, loaded)
            fold_tensor(pe, k, a, f)
            for m in range(2):
                after(pe, a.xnT_ready, m)
                turn_xn_tensor(pe, a, m, m)
            pe.wait_ge(f.m_ready, H // 2)
            pe.wait_ge(f.w_ready, H // 2)
            for n in range(LEAD):
                wide_queries_tensor(pe, a, f, n, n, (a.q6_ready, 2 * n),
                                    (a.q7_ready, 2 * n) if n else (a.xnT_ready, 2))

            def queries_ready(u):
                if isinstance(u, int):
                    u -= u % 2
                    pe.wait_ge(a.q6_ready, u * 2 + 4)
                    pe.wait_ge(a.q7_ready, u * 2 + 4)

            queries_ready(0)
            scores_tensor(pe, a, 0, 0)

            def slot(t, s):
                turn_tensor(pe, a, t, s)
                if not is_last(t):
                    if s % 2:
                        pe.wait_ge(a.q6_ready, t * 2 + 6)
                        pe.wait_ge(a.q7_ready, t * 2 + 6)
                    scores_tensor(pe, a, t + 1, (s + 1) % 4)
                weigh_tensor(pe, a, t, s)
                if not is_last(t, LEAD):
                    wide_queries_tensor(pe, a, f, t + LEAD, (s + LEAD) % 4, (a.updated, t),
                                        (a.xnT_ready, (t + 5) // 2 if isinstance(t, int)
                                         else (t - 1) // 2 + 3) if s % 2 else (a.q7_ready, t * 2 + 6))
                    pe.wait_ge(a.q6_ready, t * 2 + 8)
                    project_tensor(pe, a, t, bias)
                    if s % 2 == 0 and not is_last(t, 4):
                        pe.wait_ge(a.q7_ready, t * 2 + 8)
                        turn_xn_tensor(pe, a, t // 2 + 2, (s // 2) % 2)
                else:
                    after(pe, a.updated, t)
                    project_tensor(pe, a, t, bias)

            over_tiles(pe, slot)

        @block.scalar
        def _(act):
            norm_root_scalar(act, k, a.norm)
            fold_scalar(act, k, a, f)
            for m in range(2):
                copy_xnT_scalar(act, a, m, m)
            for n in range(LEAD):
                for j in (0, 2):
                    copy_queries(act.copy, act, a, n, n, j, a.q6_done, a.q6_ready, (a.scores_done, 0))
            softmax_exp_scalar(act, a, 0, 0)

            def slot(t, s):
                copy_probT_scalar(act, a, t)
                copy_o0_scalar(act, a, t)
                if not is_last(t):
                    softmax_exp_scalar(act, a, t + 1, (s + 1) % 4)
                if not is_last(t, LEAD):
                    for j in (0, 2):
                        copy_queries(act.copy, act, a, t + LEAD, (s + LEAD) % 4, j, a.q6_done, a.q6_ready,
                                     (a.scores_done, t))
                    if s % 2 == 0 and not is_last(t, 4):
                        copy_xnT_scalar(act, a, t // 2 + 2, (s // 2) % 2)

            over_tiles(act, slot)

        @block.vector
        def _(dve):
            if first is not None:
                first(dve)
            norm_stats_vector(dve, k, a.norm)
            fold_vector(dve, k, a, f)
            for m in range(2):
                normalise_group_vector(dve, a, m, m)
            for n in range(LEAD):
                for j in (1, 3):
                    copy_queries(dve.tensor_copy, dve, a, n, n, j, a.q7_done, a.q7_ready, (a.scores_done, 0))
            softmax_top_vector(dve, a, 0, 0)
            softmax_total_vector(dve, a, 0, 0)

            def slot(t, s):
                if s % 2 == 0 and not is_last(t, 4):
                    normalise_group_vector(dve, a, t // 2 + 2, (s // 2) % 2)
                if not is_last(t):
                    softmax_top_vector(dve, a, t + 1, (s + 1) % 4)
                copy_o1_vector(dve, a, t)
                more = not is_last(t, LEAD)
                if more:
                    copy_queries(dve.tensor_copy, dve, a, t + LEAD, (s + LEAD) % 4, 1, a.q7_done,
                                 a.q7_ready, (a.scores_done, t))
                if not is_last(t):
                    softmax_total_vector(dve, a, t + 1, (s + 1) % 4)
                if more:
                    copy_queries(dve.tensor_copy, dve, a, t + LEAD, (s + LEAD) % 4, 3, a.q7_done,
                                 a.q7_ready, (a.scores_done, t))
                update_vector(dve, a, t)

            over_tiles(dve, slot)

        @block.gpsimd
        def _(pool):
            def keys(u, s):
                after(pool, a.scores_done, u - 1)
                pool.tensor_copy(a.keys[s % 2][:, :], k.ctxT[0:C, bass.ds(u * P, P)]).then_inc(
                    a.keys_ready, 1)

            def values(u, s):
                after(pool, a.weighed, 2 * u - 2)
                pool.tensor_copy(a.values[s % 2][:, :, :],
                                 k.ctx2[:, bass.ds(u * 2, 2), :]).then_inc(a.values_ready, 1)

            for u in range(2):
                keys(u, u)
                values(u, u)
            softmax_divide_gpsimd(pool, a, 0, 0)

            def slot(t, s):
                if not is_last(t):
                    softmax_divide_gpsimd(pool, a, t + 1, (s + 1) % 4)
                if not is_last(t, 2):
                    keys(t + 2, (s + 2) % 4)
                    values(t + 2, (s + 2) % 4)

            over_tiles(pool, slot)



QUAD = 4 * P
QUADS = TOK // QUAD


def linked(eng, sem):
    count = [0]

    def link(ins):
        count[0] += 1
        ins.then_inc(sem, 1)
        eng.wait_ge(sem, count[0])
    return link


def spread(ap, n):
    return ap.rearrange("p (a o) -> p a o", o=1).to_broadcast([ap.shape[0], ap.shape[1], n])


class Turned:

    def __init__(self, k, ctx, tag, rms=False, weight=None, xnT=None, xn_all=None):
        def sb(name, shape):
            return ctx.enter_context(k.nc.sbuf_tensor(f"{tag}_{name}", shape, F32))

        def sem(name):
            return Signals.new(k.nc, f"{tag}_{name}")

        self.k, self.rms, self.weight = k, rms, weight
        self.xnT = sb("xnT", [D, TOK]) if xnT is None else xnT
        self.groups = 2 if xn_all is None else QUADS
        self.xn = [sb(f"xn{i}", [P, 4, D]) for i in range(2)] if xn_all is None else [
            xn_all[:, 4 * n:4 * n + 4, :] for n in range(QUADS)]
        self.norm = NormSems(k.nc, ctx, tag)
        self.xn_ready = sem("xn_ready")
        self.turned = sem("turned")
        self.ready = sem("xnT_ready")

    def vector(self, dve):
        k = self.k
        norm_stats_vector(dve, k, self.norm, self.rms)
        for n in range(QUADS):
            if self.groups == 2:
                after(dve, self.turned, n - 1)
            for j in range(4):
                if self.rms:
                    last = dve.tensor_scalar(self.xn[n % self.groups][:, j, :], k.x[:, 4 * n + j, :],
                                             k.rstd[:, 4 * n + j:4 * n + j + 1], None, ALU.mult)
                else:
                    last = normalise(dve, k, self.xn[n % self.groups][:, j:j + 1, :], 4 * n + j)
            last.then_inc(self.xn_ready, 1)

    def tensor(self, pe, n):
        pe.wait_ge(self.xn_ready, n + 1)
        after(pe, self.ready, n - 1)
        bank = (self.k.r6, self.k.r7)[n % 2]
        for j in range(4):
            last = pe.transpose(bank[:, j * P:(j + 1) * P], self.xn[n % self.groups][:, j, :],
                                self.k.ident[:, :])
        last.then_inc(self.turned, 1)

    def scalar(self, act, n):
        act.wait_ge(self.turned, n + 1)
        out, bank = self.xnT[:, n * QUAD:(n + 1) * QUAD], (self.k.r6, self.k.r7)[n % 2]
        if self.weight is None:
            ins = act.copy(out, bank[:, :])
        else:
            ins = act.activation(out, bank[:, :], ACT.Copy, scale=self.weight)
        ins.then_inc(self.ready, 1)



F0, E0 = 352, 8
CHUNKS0 = [(0, 128), (128, 128), (256, 96)]


def ffn0_weights(k):
    w = k.odd
    n = E0 * F0
    return (w[:, 0:n].rearrange("p (e f) -> p e f", e=E0),
            w[:, n:2 * n].rearrange("p (e f) -> p e f", e=E0),
            w[:, 2 * n:2 * n + E0 * 3 * D].rearrange("p (e c n) -> p e c n", e=E0, c=3))


def load_ffn0(sp, k):
    w1, w3, w2 = ffn0_weights(k)
    d = k.dram
    k.load(sp, "odd", w1, d["L0_ffn_w1"].rearrange("e d f -> d e f"))
    k.load(sp, "odd", w3, d["L0_ffn_w3"].rearrange("e d f -> d e f"))
    for c, (at, n) in enumerate(CHUNKS0):
        k.load(sp, "odd", w2[0:n, :, c, :], d["L0_ffn_w2"][:, at:at + n, :].rearrange("e f d -> f e d"))


def ffn0(k, load_next):
    nc = k.nc
    with ExitStack() as ctx:
        def sb(name, shape):
            return ctx.enter_context(nc.sbuf_tensor(f"l0f_{name}", shape, F32))

        def sem(name):
            return Signals.new(nc, f"l0f_{name}")

        tr = Turned(k, ctx, "l0f")
        w1, w3, w2 = ffn0_weights(k)
        gated = [sb(f"gated{i}", [P, QUAD]) for i in range(2)]
        hidden = [sb(f"hidden{i}", [P, QUAD]) for i in range(2)]
        gate_done, up_done = sem("gate_done"), sem("up_done")
        gated_ready, hidden_ready = sem("gated_ready"), sem("hidden_ready")
        down_done, down_ready = sem("down_done"), sem("down_ready")
        back_done, updated, stats_done = sem("back_done"), sem("updated"), sem("stats_done")
        gate_banks, up_banks, down_banks = k.ps
        units = [(e, c) for e in range(E0) for c in range(3)]
        loaded = k.loads["odd"]

        def tokens(e):
            return tr.xnT[:, :].rearrange("p (b e c) -> p b e c", e=E0, c=SEQ // E0)[:, :, e, :]

        block = ctx.enter_context(nc.Block())

        @block.sync
        def _(sp):
            load_next(sp)

        @block.tensor
        def _(pe):
            for n in range(QUADS):
                tr.tensor(pe, n)
            pe.wait_ge(k.load_odd, loaded)
            pe.wait_ge(tr.ready, QUADS)

            def up(v):
                e, c = units[v]
                at, n = CHUNKS0[c]
                after(pe, gated_ready, v - 1)
                after(pe, hidden_ready, v - 1)
                pe.matmul(gate_banks[0:n, v % 2, :], w1[:, e, at:at + n], tokens(e), start=True,
                          stop=True).then_inc(gate_done, 1)
                pe.matmul(up_banks[0:n, v % 2, :], w3[:, e, at:at + n], tokens(e), start=True,
                          stop=True).then_inc(up_done, 1)

            up(0)
            for v, (e, c) in enumerate(units):
                if v + 1 < len(units):
                    up(v + 1)
                n = CHUNKS0[c][1]
                pe.wait_ge(hidden_ready, v + 1)
                if c == 0:
                    after(pe, down_ready, e - 1)
                last = pe.matmul(down_banks[:, e % 2, :], w2[0:n, e, c, :], hidden[v % 2][0:n, :],
                                 start=c == 0, stop=c == 2)
                if c == 2:
                    last.then_inc(down_done, 1)
            pe.wait_ge(down_ready, E0)
            for n in range(QUADS):
                after(pe, updated, n - 1)
                for j in range(4):
                    at = n * QUAD + j * P
                    last = pe.transpose((k.r6, k.r7)[n % 2][:, j * P:(j + 1) * P],
                                        tr.xnT[:, at:at + P], k.ident[:, :])
                last.then_inc(back_done, 1)

        @block.scalar
        def _(act):
            norm_root_scalar(act, k, tr.norm)
            for n in range(QUADS):
                tr.scalar(act, n)
            for v, (e, c) in enumerate(units):
                n = CHUNKS0[c][1]
                act.wait_ge(gate_done, v + 1)
                after(act, hidden_ready, v - 1)
                act.activation(gated[v % 2][0:n, :], gate_banks[0:n, v % 2, :], ACT.Silu).then_inc(
                    gated_ready, 1)
                if c == 2:
                    act.wait_ge(down_done, e + 1)
                    act.copy(tokens(e), down_banks[:, e % 2, :].rearrange("p (b c) -> p b c", c=SEQ // E0)
                             ).then_inc(down_ready, 1)

        @block.vector
        def _(dve):
            tr.vector(dve)
            for v, (e, c) in enumerate(units):
                n = CHUNKS0[c][1]
                dve.wait_ge(gated_ready, v + 1)
                dve.wait_ge(up_done, v + 1)
                dve.tensor_tensor(hidden[v % 2][0:n, :], gated[v % 2][0:n, :], up_banks[0:n, v % 2, :],
                                  ALU.mult).then_inc(hidden_ready, 1)
            for n in range(QUADS):
                dve.wait_ge(back_done, n + 1)
                xq = k.x[:, 4 * n:4 * n + 4, :].rearrange("p a d -> p (a d)")
                dve.tensor_tensor(xq, xq, (k.r6, k.r7)[n % 2][:, :], ALU.add).then_inc(updated, 1)
                dve.wait_ge(updated, n + 1)
                for j in range(4):
                    last = dve.bn_stats(k.stats[:, 4 * n + j, :], k.x[:, 4 * n + j, :])
                last.then_inc(stats_done, 1)



class Experts:

    def __init__(self, k, ctx, tag, xnT, experts, up, down, gated, bias1=None, bias2=None, weight=None):
        def sb(name, shape):
            return ctx.enter_context(k.nc.sbuf_tensor(f"{tag}_{name}", shape, F32))

        def sem(name):
            return Signals.new(k.nc, f"{tag}_{name}")

        self.k, self.xnT, self.experts, self.up, self.down = k, xnT, experts, up, down
        self.gated, self.bias1, self.bias2, self.weight = gated, bias1, bias2, weight
        self.chunks = 1 if gated else 4
        self.hidden = [sb(f"hidden{i}", [P, self.chunks, GT]) for i in range(2)]
        if gated:
            self.silu = [sb(f"silu{i}", [P, GT]) for i in range(2)]
            self.silu_ready = sem("silu_ready")
        self.up_done = sem("up_done")
        self.hidden_ready = sem("hidden_ready")
        self.down_done = sem("down_done")
        self.added = sem("added")
        self.stats_done = sem("stats_done")

    def loop(self, eng, unit):
        E = self.experts

        def pair(g0, static):
            for j in range(2):
                for e in range(E):
                    g = g0 + j
                    unit(g * E + e, g, e, (j * E + e) % 2)

        pair(0, True)
        with eng.Fori(1, GROUPS // 2 - 1) as i:
            pair(i * 2, False)
        pair(GROUPS - 2, True)

    def up_tensor(self, pe, v, g, e, par):
        after(pe, self.hidden_ready, v - 1)
        banks = self.k.ps[par]
        moving = self.xnT[:, bass.ds(g * GT, GT)]
        for c in range(2 if self.gated else 4):
            out = banks[:, c, 0:GT] if self.gated else banks[:, c // 2, (c % 2) * GT:(c % 2 + 1) * GT]
            last = pe.matmul(out, self.up[:, e, c * P:(c + 1) * P], moving, start=True, stop=True)
        last.then_inc(self.up_done, 1)

    def tensor(self, pe):
        E = self.experts
        self.up_tensor(pe, 0, 0, 0, 0)

        def unit(v, g, e, par):
            if not (isinstance(v, int) and v == GROUPS * E - 1):
                self.up_tensor(pe, v + 1, g if e + 1 < E else g + 1, (e + 1) % E, 1 - par)
            pe.wait_ge(self.hidden_ready, v + 1)
            after(pe, self.added, v - 1)
            for j in range(2):
                out = self.k.ps[2][:, par, j * D:(j + 1) * D]
                for c in range(self.chunks):
                    last = pe.matmul(out, self.hidden[par][:, c, j * P:(j + 1) * P], self.down[:, e, c, :],
                                     start=c == 0, stop=c == self.chunks - 1 and self.bias2 is None)
                if self.bias2 is not None:
                    last = pe.matmul(out, self.k.ones[0:1, :], self.bias2[:, e, :], start=False, stop=True)
            last.then_inc(self.down_done, 1)

        self.loop(pe, unit)

    def scalar(self, act):
        def unit(v, g, e, par):
            act.wait_ge(self.up_done, v + 1)
            banks = self.k.ps[par]
            if self.gated:
                after(act, self.hidden_ready, v - 1)
                act.activation(self.silu[par][:, :], banks[:, 0, 0:GT], ACT.Silu).then_inc(
                    self.silu_ready, 1)
                return
            after(act, self.down_done, v - 1)
            for c in range(4):
                last = act.activation(self.hidden[par][:, c, :],
                                      banks[:, c // 2, (c % 2) * GT:(c % 2 + 1) * GT], ACT.Gelu,
                                      bias=self.bias1[:, 4 * e + c:4 * e + c + 1])
            last.then_inc(self.hidden_ready, 1)

        self.loop(act, unit)

    def vector(self, dve):
        k, E = self.k, self.experts

        def multiply(v, par):
            dve.wait_ge(self.silu_ready, v + 1)
            dve.wait_ge(self.up_done, v + 1)
            after(dve, self.down_done, v - 1)
            dve.tensor_tensor(self.hidden[par][:, 0, :], self.silu[par][:, :], k.ps[par][:, 1, 0:GT],
                              ALU.mult).then_inc(self.hidden_ready, 1)

        if self.gated:
            multiply(0, 0)

        def unit(v, g, e, par):
            if self.gated and not (isinstance(v, int) and v == GROUPS * E - 1):
                multiply(v + 1, 1 - par)
            dve.wait_ge(self.down_done, v + 1)
            after(dve, self.added, v)
            xg = k.x[:, bass.ds(g * 2, 2), :]
            if self.weight is None:
                dve.tensor_tensor(xg.rearrange("p a d -> p (a d)"), xg.rearrange("p a d -> p (a d)"),
                                  k.ps[2][:, par, 0:2 * D], ALU.add).then_inc(self.added, 1)
            else:
                for j in range(2):
                    xt = k.x[:, bass.ds(g * 2 + j, 1), :].rearrange("p a d -> p (a d)")
                    w = self.weight[:, bass.ds((g * 2 + j) * 8 + e, 1)]
                    last = dve.scalar_tensor_tensor(xt, k.ps[2][:, par, j * D:(j + 1) * D], w, xt,
                                                    ALU.mult, ALU.add)
                last.then_inc(self.added, 1)
            if e == E - 1:
                dve.wait_ge(self.added, v + 1)
                for j in range(2):
                    last = dve.bn_stats(
                        k.stats[:, bass.ds(g * 2 + j, 1), :].rearrange("p a d -> p (a d)"),
                        k.x[:, bass.ds(g * 2 + j, 1), :].rearrange("p a d -> p (a d)"))
                last.then_inc(self.stats_done, 1)

        self.loop(dve, unit)



class Ternary:

    def __init__(self, k, ctx, tag, floor, width):
        def sb(name, shape):
            return ctx.enter_context(k.nc.sbuf_tensor(f"{tag}_{name}", shape, F32))

        self.k, self.floor = k, floor
        self.sums = sb("tern_sums", [P, 1])
        self.scale = sb("tern_scale", [P, 1])
        self.cut = sb("tern_cut", [P, 2])
        self.low = sb("tern_low", [P, width])
        self.sums_ready = Signals.new(k.nc, f"{tag}_tern_sums")
        self.total_done = Signals.new(k.nc, f"{tag}_tern_total")
        self.step = Signals.new(k.nc, f"{tag}_tern_step")
        self.count = 0

    def tensor(self, pe, rows):
        self.count += 1
        pe.wait_ge(self.sums_ready, self.count)
        pe.matmul(self.k.ps[2][:, 1, 0:1], self.k.ones[0:rows, :], self.sums[0:rows, :], start=True,
                  stop=True).then_inc(self.total_done, 1)


def ternary_vector(dve, tn, nth, link, w, out, size, scale_out):
    rows, n = w.shape
    dve.tensor_reduce(tn.sums[0:rows, :], w, AX.X, ALU.add, apply_absolute_value=True).then_inc(
        tn.sums_ready, 1)
    dve.wait_ge(tn.total_done, nth + 1)
    link(dve.tensor_scalar(scale_out, tn.k.ps[2][:, 1, 0:1], 1.0 / size, tn.floor, ALU.mult, ALU.max))
    link(dve.tensor_scalar(tn.cut[:, 0:1], scale_out, 0.5, None, ALU.mult))
    link(dve.tensor_scalar(tn.cut[:, 1:2], scale_out, -0.5, None, ALU.mult))
    link(dve.tensor_scalar(tn.low[0:rows, 0:n], w, tn.cut[0:rows, 1:2], None, ALU.is_lt))
    link(dve.scalar_tensor_tensor(out, w, tn.cut[0:rows, 0:1], tn.low[0:rows, 0:n], ALU.is_gt,
                                  ALU.subtract))



F1 = 512


def ffn1_weights(k):
    w = k.odd
    return (w[:, 0:512].rearrange("p (c n) -> p c n", n=D), w[:, 512:1024],
            w[:, 1024:1028], w[0:1, 1028:1028 + D])


def load_ffn1(sp, k):
    w1, w2, b1, b2 = ffn1_weights(k)
    d = k.dram
    k.load(sp, "odd", w1, d["L1_ffn_W1"].rearrange("(c p) n -> p c n", p=P))
    k.load(sp, "odd", w2, d["L1_ffn_W2"])
    with k.nc.allow_non_contiguous_dma(reason="a short bias, feature-major"):
        k.load(sp, "odd", b1, d["L1_ffn_b1"].rearrange("(c p) -> p c", p=P))
    k.load(sp, "odd", b2, row(d["L1_ffn_b2"], D))


def ffn1(k, load_next):
    nc = k.nc
    with ExitStack() as ctx:
        def sb(name, shape):
            return ctx.enter_context(nc.sbuf_tensor(f"l1f_{name}", shape, F32))

        def sem(name):
            return Signals.new(nc, f"l1f_{name}")

        tr = Turned(k, ctx, "l1f")
        w1, w2, b1, b2 = ffn1_weights(k)
        up = sb("up", [D, 1, F1])
        down = sb("down", [P, 1, 4, D])
        scales = sb("scales", [P, 2])
        tn = Ternary(k, ctx, "l1f", 1e-8, F1)
        turned, copied, made = sem("weights_turned"), sem("weights_ready"), sem("ternary_made")
        ex = Experts(k, ctx, "l1f", tr.xnT, 1, up, down, False, bias1=b1,
                     bias2=b2.rearrange("p (e n) -> p e n", e=1))
        loaded = k.loads["odd"]
        block = ctx.enter_context(nc.Block())

        @block.sync
        def _(sp):
            load_next(sp)

        @block.tensor
        def _(pe):
            tn.tensor(pe, P)
            tn.tensor(pe, P)
            for i, w in enumerate((w1.rearrange("p c n -> p (c n)"), w2)):
                pe.wait_ge(made, i + 1)
                for c in range(4):
                    last = pe.transpose(k.ps[0][:, i, c * P:(c + 1) * P], w[:, c * P:(c + 1) * P],
                                        k.ident[:, :])
                last.then_inc(turned, 1)
            for n in range(QUADS):
                tr.tensor(pe, n)
            pe.wait_ge(tr.ready, QUADS)
            pe.wait_ge(copied, 2)
            ex.tensor(pe)

        @block.scalar
        def _(act):
            norm_root_scalar(act, k, tr.norm)
            act.wait_ge(turned, 2)
            act.copy(up[:, 0, :], k.ps[0][:, 0, :]).then_inc(copied, 1)
            act.copy(down[:, 0, :, :].rearrange("p c n -> p (c n)"), k.ps[0][:, 1, :]).then_inc(copied, 1)
            for n in range(QUADS):
                tr.scalar(act, n)
            ex.scalar(act)

        @block.vector
        def _(dve):
            link = linked(dve, tn.step)
            dve.wait_ge(k.load_odd, loaded)
            for i, w in enumerate((w1.rearrange("p c n -> p (c n)"), w2)):
                ternary_vector(dve, tn, i, link, w, w, F1 * D, scales[:, i:i + 1])
                dve.sem_inc(made, 1)
            tr.vector(dve)
            ex.vector(dve)



class Router:

    def __init__(self, k, ctx, tag, experts):
        def sb(name, shape):
            return ctx.enter_context(k.nc.sbuf_tensor(f"{tag}_{name}", shape, F32))

        def sem(name):
            return Signals.new(k.nc, f"{tag}_{name}")

        self.k, self.E = k, experts
        self.index = sb("index", [P, TILES, experts])
        self.score = sb("score", [P, TILES, experts])
        self.soft = sb("soft", [P, TILES, experts])
        self.cand = sb("cand", [P, TILES, experts])
        self.hot = [sb(f"hot{i}", [P, TILES, experts]) for i in range(2)]
        self.top = [sb(f"top{i}", [P, TILES]) for i in range(2)]
        self.first = sb("first", [P, TILES])
        self.weight = sb("weight", [P, TILES * 8])
        self.index_ready = sem("index_ready")
        self.scored = sem("scored")
        self.ready = sem("score_ready")
        self.soft_ready = sem("soft_ready")
        self.step = sem("route_step")
        self.done = sem("routed")

    def tensor(self, pe, xnT, w, bias):
        for t in range(TILES):
            out = self.k.ps[2][:, 0, t * self.E:(t + 1) * self.E]
            pe.matmul(out, xnT[:, t * P:(t + 1) * P], w, start=True, stop=False)
            last = pe.matmul(out, self.k.ones[0:1, :], bias, start=False, stop=True)
        last.then_inc(self.scored, 1)

    def gpsimd(self, pool):
        pool.iota(self.index[:, :, :], pattern=[[0, TILES], [1, self.E]], base=0, channel_multiplier=0,
                  allow_small_or_imprecise_dtypes=True).then_inc(self.index_ready, 1)

    def bank(self):
        return self.k.ps[2][:, 0, 0:TILES * self.E].rearrange("p (t e) -> p t e", e=self.E)

    def first_top(self, dve, link, score, n):
        E = self.E
        index = self.index[:, :, :]
        link(dve.tensor_reduce(self.top[n][:, :], score, AX.X, ALU.max))
        link(dve.tensor_tensor(self.cand[:, :, :], score, spread(self.top[n][:, :], E), ALU.is_equal))
        link(dve.scalar_tensor_tensor(self.cand[:, :, :], self.cand[:, :, :], -float(E), index, ALU.mult,
                                      ALU.add))
        link(dve.tensor_reduce(self.first[:, :], self.cand[:, :, :], AX.X, ALU.min))
        link(dve.tensor_scalar(self.first[:, :], self.first[:, :], float(E), None, ALU.add))
        link(dve.tensor_tensor(self.hot[n][:, :, :], index, spread(self.first[:, :], E), ALU.is_equal))



E3, F3 = 8, 512
SLOTS = 40


def ffn3_weights(k):
    w = k.odd
    return (w[:, 0:4096].rearrange("p (e f) -> p e f", e=E3),
            w[:, 4096:8192].rearrange("p (e c n) -> p e c n", e=E3, c=4),
            w[:, 8192:8200], w[0:1, 8200:8208])


def load_ffn3(sp, k):
    w1, w2, wr, br = ffn3_weights(k)
    d = k.dram
    k.load(sp, "odd", wr, d["L3_ffn_Wr"])
    k.load(sp, "odd", br, row(d["L3_ffn_br"], E3))
    k.load(sp, "odd", w1, d["L3_ffn_W1"].rearrange("e d f -> d e f"))
    for e in range(E3):
        k.load(sp, "odd", w2[:, e, :, :], d["L3_ffn_W2"][e].rearrange("(c p) n -> p c n", p=P))


def over_slots(eng, slot):
    for s in range(UNROLL):
        slot(s, s)
    with eng.Fori(1, SLOTS // UNROLL - 1) as i:
        for s in range(UNROLL):
            slot(i * UNROLL + s, s)
    for s in range(UNROLL):
        slot(SLOTS - UNROLL + s, s)


class Places:

    def __init__(self, k, ctx, ro):
        def sb(name, shape, dt=F32):
            return ctx.enter_context(k.nc.sbuf_tensor(f"place_{name}", shape, dt))

        def sem(name):
            return Signals.new(k.nc, f"place_{name}")

        self.k, self.ro = k, ro
        self.before = sb("before", [P, P])
        self.not_first = sb("not_first", [P, E3, TILES])
        self.slot_index = sb("slot_index", [1, SLOTS, E3 - 1])
        self.count = sb("count", [P, E3, TILES])
        self.upto = sb("upto", [P, E3, TILES])
        self.tiles = sb("tiles", [P, E3])
        self.end = sb("end", [P, E3])
        self.base = sb("base", [P, E3])
        self.at = sb("at", [P, TILES, E3])
        self.place = sb("place", [P, TILES])
        self.index = sb("index", [P, TILES], mybir.dt.int32)
        self.past = sb("past", [1, SLOTS, E3 - 1])
        self.expert = sb("expert", [1, SLOTS])
        self.expert_index = sb("expert_index", [1, SLOTS], mybir.dt.int32)
        self.consts = sem("consts")
        self.chosen = sem("chosen")
        self.counted = sem("counted")
        self.ready = sem("ready")
        self.expert_ready = sem("expert_ready")

    def gpsimd(self, pool):
        pool.memset(self.not_first[:, :, :], 1.0).then_inc(self.consts, 1)
        pool.wait_ge(self.consts, 1)
        pool.memset(self.not_first[:, :, 0:1], 0.0).then_inc(self.consts, 1)
        pool.wait_ge(self.consts, 2)
        pool.affine_select(out=self.before[:, :], in_=self.k.ones[:, :], compare_op=ALU.is_gt, fill=0.0,
                           base=0, pattern=[[1, P]], channel_multiplier=-1).then_inc(self.consts, 1)
        pool.wait_ge(self.consts, 3)
        pool.iota(self.slot_index[:, :, :], pattern=[[1, SLOTS], [0, E3 - 1]], base=0,
                  channel_multiplier=0, allow_small_or_imprecise_dtypes=True).then_inc(self.consts, 1)

    def tensor(self, pe):
        pe.wait_ge(self.consts, 3)
        pe.wait_ge(self.chosen, 1)
        hot = self.ro.hot[0][:, :, :].rearrange("p t e -> p (t e)")
        n = TILES * E3
        pe.matmul(self.k.ps[2][:, 0, 0:n], self.before[:, :], hot, start=True, stop=True)
        pe.matmul(self.k.ps[2][:, 1, 0:n], self.k.ones[:, :], hot, start=True, stop=True).then_inc(
            self.counted, 1)

    def vector(self, dve, link):
        k, n = self.k, TILES * E3
        earlier = k.ps[2][:, 0, 0:n].rearrange("p (t e) -> p t e", e=E3)
        totals = k.ps[2][:, 1, 0:n].rearrange("p (t e) -> p e t", e=E3)
        flat = "p e t -> p (e t)"
        dve.wait_ge(self.consts, 4)
        dve.wait_ge(self.counted, 1)
        link(dve.tensor_copy(self.count[:, :, :], totals))
        link(dve.tensor_tensor_scan(self.upto[:, :, :].rearrange(flat), self.not_first[:, :, :].rearrange(flat),
                                    self.count[:, :, :].rearrange(flat), 0.0, ALU.mult, ALU.add))
        link(dve.tensor_scalar(self.tiles[:, :], self.upto[:, :, TILES - 1], 1.0 / P, (P - 1) / (2.0 * P),
                               ALU.mult, ALU.add))
        link(dve.tensor_scalar(self.tiles[:, :], self.tiles[:, :], ROUND, None, ALU.add))
        link(dve.tensor_scalar(self.tiles[:, :], self.tiles[:, :], -ROUND, None, ALU.add))
        link(dve.tensor_tensor_scan(self.end[:, :], k.ones[:, 0:E3], self.tiles[:, :], 0.0, ALU.mult, ALU.add))
        link(dve.tensor_tensor(self.base[:, :], self.end[:, :], self.tiles[:, :], ALU.subtract))
        link(dve.tensor_scalar(self.base[:, :], self.base[:, :], float(P), None, ALU.mult))
        link(dve.tensor_tensor(self.upto[:, :, :], self.upto[:, :, :], self.count[:, :, :], ALU.subtract))
        link(dve.tensor_tensor(self.upto[:, :, :], self.upto[:, :, :], spread(self.base[:, :], TILES), ALU.add))
        link(dve.tensor_tensor(self.at[:, :, :], self.upto[:, :, :].rearrange("p e t -> p t e"), earlier,
                               ALU.add))
        link(dve.tensor_tensor(self.at[:, :, :], self.at[:, :, :], self.ro.hot[0][:, :, :], ALU.mult))
        link(dve.tensor_reduce(self.place[:, :], self.at[:, :, :], AX.X, ALU.add))
        dve.tensor_copy(self.index[:, :], self.place[:, :]).then_inc(self.ready, 1)
        end = self.end[0:1, 0:E3 - 1].rearrange("p (a e) -> p a e", a=1).to_broadcast([1, SLOTS, E3 - 1])
        link(dve.tensor_tensor(self.past[:, :, :], self.slot_index[:, :, :], end, ALU.is_ge))
        link(dve.tensor_reduce(self.expert[:, :], self.past[:, :, :], AX.X, ALU.add))
        dve.tensor_copy(self.expert_index[:, :], self.expert[:, :]).then_inc(self.expert_ready, 1)

    def of_slot(self, eng, j):
        return eng.value_load(self.expert_index[0:1, bass.ds(j, 1)], min_val=0, max_val=E3 - 1)


def ffn3(k, out):
    nc = k.nc
    with ExitStack() as ctx:
        def sb(name, shape):
            return ctx.enter_context(nc.sbuf_tensor(f"l3f_{name}", shape, F32))

        def sem(name):
            return Signals.new(nc, f"l3f_{name}")

        w1, w2, wr, br = ffn3_weights(k)
        loaded = k.loads["odd"]
        xn = k.even[:, 0:TOK].rearrange("p (t d) -> p t d", d=D)
        b1 = k.ctx2[:, :, :].rearrange("p b c -> p (b c)")[:, 0:E3 * F3].rearrange("p (e f) -> p e f", e=E3)
        b2 = sb("b2", [P, E3, D])
        rows = [sb(f"rows{i}", [P, D]) for i in range(4)]
        results = sb("results", [P, SLOTS, D])
        xsT = [sb(f"xsT{i}", [D, P]) for i in range(2)]
        hidden = [sb(f"hidden{i}", [P, F3]) for i in range(4)]
        hiddenT = [sb(f"hiddenT{i}", [P, F3]) for i in range(2)]
        table = nc.dram_tensor("expert_rows", [SLOTS * P, D], F32, kind="Internal").ap()
        result_table = nc.dram_tensor("expert_results", [SLOTS * P, D], F32, kind="Internal").ap()
        tr = Turned(k, ctx, "l3f", xn_all=xn)
        ro = Router(k, ctx, "l3f", E3)
        pl = Places(k, ctx, ro)
        biases_in, zeroed, table_zeroed = sem("biases_in"), sem("rows_zeroed"), sem("table_zeroed")
        scattered = sem("scattered")
        rows_in = [sem(f"rows_in{i}") for i in range(4)]
        row_turned, xsT_ready = sem("row_turned"), sem("xsT_ready")
        up_done, biased, hidden_ready = sem("up_done"), sem("biased"), sem("hidden_ready")
        hidden_turned, hiddenT_ready = sem("hidden_turned"), sem("hiddenT_ready")
        down_done, result_ready, results_out = sem("down_done"), sem("result_ready"), sem("results_out")
        gathered = [sem(f"gathered{i}") for i in range(4)]
        updated, x_out = sem("updated"), sem("x_out")
        QUARTER = TILES // 4
        block = ctx.enter_context(nc.Block())

        def by_slot(ap):
            return ap.rearrange("(j p) d -> p j d", p=P)

        @block.sync
        def _(sp):
            with nc.allow_non_contiguous_dma(reason="biases, the same on every partition"):
                sp.dma_start(b1, k.dram["L3_ffn_b1"].partition_broadcast(P)).then_inc(biases_in, 16)
                sp.dma_start(b2[:, :, :], k.dram["L3_ffn_b2"].partition_broadcast(P)).then_inc(biases_in, 16)
            sp.wait_ge(zeroed, 1)
            sp.dma_start(by_slot(table), results[:, :, :]).then_inc(table_zeroed, 16)
            sp.wait_ge(table_zeroed, 16)
            sp.wait_ge(scattered, 16 * TILES)

            def load_rows(j, s):
                after(sp, row_turned, j - 3)
                sp.dma_start(rows[s][:, :], by_slot(table)[:, bass.ds(j, 1), :].rearrange(
                    "p a d -> p (a d)")).then_inc(rows_in[s], 16)

            for j in range(UNROLL):
                load_rows(j, j)

            def slot(j, s):
                if not (isinstance(j, int) and j >= SLOTS - UNROLL):
                    load_rows(j + UNROLL, s)

            over_slots(sp, slot)
            ov = out.rearrange("b s d -> (b s) d").rearrange("(t p) d -> p t d", p=P)
            for n in range(4):
                sp.wait_ge(updated, n + 1)
                tiles = slice(n * QUARTER, (n + 1) * QUARTER)
                sp.dma_start(ov[:, tiles, :], k.x[:, tiles, :]).then_inc(x_out, 16)
            sp.wait_ge(x_out, 64)

        @block.gpsimd
        def _(pool):
            pool.memset(results[:, :, :], 0.0).then_inc(zeroed, 1)
            pool.wait_ge(zeroed, 1)
            ro.gpsimd(pool)
            pool.wait_ge(ro.index_ready, 1)
            pl.gpsimd(pool)
            pool.wait_ge(table_zeroed, 16)
            pool.wait_ge(pl.ready, 1)
            for t in range(TILES):
                at = bass.IndirectOffsetOnAxis(ap=pl.index[:, t:t + 1], axis=0)
                pool.indirect_dma_start(table, at, xn[:, t, :], None).then_inc(scattered, 16)
            with pool.Fori(0, SLOTS // UNROLL) as i:
                pool.wait_ge(result_ready, i * UNROLL + UNROLL)
                pool.dma_start(by_slot(result_table)[:, bass.ds(i * UNROLL, UNROLL), :],
                               results[:, bass.ds(i * UNROLL, UNROLL), :]).then_inc(results_out, 16)
            pool.wait_ge(results_out, 16 * (SLOTS // UNROLL))
            for t in range(TILES):
                at = bass.IndirectOffsetOnAxis(ap=pl.index[:, t:t + 1], axis=0)
                pool.indirect_dma_start(results[:, t, :], None, result_table, at).then_inc(
                    gathered[t // QUARTER], 16)

        @block.tensor
        def _(pe):
            for n in range(QUADS):
                tr.tensor(pe, n)
            pe.wait_ge(k.load_odd, loaded)
            pe.wait_ge(tr.ready, QUADS)
            ro.tensor(pe, tr.xnT, wr, br)
            pe.wait_ge(ro.ready, 1)
            pl.tensor(pe)

            def turn_row(j, s):
                pe.wait_ge(rows_in[s], (j - s) * (16 // UNROLL) + 16)
                after(pe, xsT_ready, j)
                pe.transpose(k.r6[:, 0:P], rows[s][:, :], k.ident[:, :]).then_inc(row_turned, 1)

            def up(j, s):
                e = pl.of_slot(pe, j)
                pe.wait_ge(xsT_ready, j + 1)
                after(pe, biased, j - 1)
                pe.matmul(k.ps[0][:, s % 2, :], xsT[s % 2][:, :], w1[:, bass.ds(e, 1), :].rearrange("p a f -> p (a f)"), start=True,
                          stop=True).then_inc(up_done, 1)

            def turn_hidden(j, s):
                pe.wait_ge(hidden_ready, j + 1)
                after(pe, hiddenT_ready, j - 1)
                for c in range(4):
                    last = pe.transpose(k.ps[1][:, s % 2, c * P:(c + 1) * P],
                                        hidden[s][:, c * P:(c + 1) * P], k.ident[:, :])
                last.then_inc(hidden_turned, 1)

            def down(j, s):
                e = pl.of_slot(pe, j)
                pe.wait_ge(hiddenT_ready, j + 1)
                after(pe, result_ready, j - 1)
                for c in range(4):
                    last = pe.matmul(k.ps[2][:, s % 2, 0:D], hiddenT[s % 2][:, c * P:(c + 1) * P],
                                     w2[:, bass.ds(e, 1), c, :].rearrange("p a f -> p (a f)"), start=c == 0, stop=c == 3)
                last.then_inc(down_done, 1)

            pe.wait_ge(pl.expert_ready, 1)
            for j in range(2):
                turn_row(j, j)
                up(j, j)
            turn_row(2, 2)

            def slot(j, s):
                if not (isinstance(j, int) and j >= SLOTS - 3):
                    turn_row(j + 3, (s + 3) % 4)
                if not (isinstance(j, int) and j >= SLOTS - 2):
                    up(j + 2, (s + 2) % 4)
                turn_hidden(j, s)
                if not (isinstance(j, int) and j == 0):
                    down(j - 1, (s + 3) % 4)

            over_slots(pe, slot)
            down(SLOTS - 1, 3)

        @block.scalar
        def _(act):
            norm_root_scalar(act, k, tr.norm)
            for n in range(QUADS):
                tr.scalar(act, n)
            act.wait_ge(ro.ready, 1)
            act.activation(ro.soft[:, :, :], ro.soft[:, :, :], ACT.Exp).then_inc(ro.soft_ready, 1)

            def copy_xsT(j, s):
                act.wait_ge(row_turned, j + 1)
                after(act, up_done, j - 1)
                act.copy(xsT[s % 2][:, :], k.r6[:, 0:P]).then_inc(xsT_ready, 1)

            for j in range(3):
                copy_xsT(j, j)

            def slot(j, s):
                act.wait_ge(biased, j + 1)
                act.activation(hidden[s][:, :], hidden[s][:, :], ACT.Gelu).then_inc(hidden_ready, 1)
                if not (isinstance(j, int) and j >= SLOTS - 3):
                    copy_xsT(j + 3, (s + 3) % 4)

            over_slots(act, slot)

        @block.vector
        def _(dve):
            tr.vector(dve)
            link = linked(dve, ro.step)
            dve.wait_ge(ro.scored, 1)
            dve.wait_ge(ro.index_ready, 1)
            link(dve.tensor_copy(ro.score[:, :, :], ro.bank()))
            ro.first_top(dve, link, ro.score[:, :, :], 0)
            dve.sem_inc(pl.chosen, 1)
            dve.tensor_tensor(ro.soft[:, :, :], ro.score[:, :, :], spread(ro.top[0][:, :], E3),
                              ALU.subtract).then_inc(ro.ready, 1)
            pl.vector(dve, link)
            dve.wait_ge(ro.soft_ready, 1)
            link(dve.tensor_reduce(ro.first[:, :], ro.soft[:, :, :], AX.X, ALU.add))
            link(dve.reciprocal(ro.top[1][:, :], ro.first[:, :]))
            dve.wait_ge(biases_in, 32)
            dve.wait_ge(pl.expert_ready, 1)

            def bias(j, s):
                e = pl.of_slot(dve, j)
                dve.wait_ge(up_done, j + 1)
                after(dve, hidden_turned, j - 3)
                dve.tensor_tensor(hidden[s][:, :], k.ps[0][:, s % 2, :],
                                  b1[:, bass.ds(e, 1), :].rearrange("p a f -> p (a f)"),
                                  ALU.add).then_inc(biased, 1)

            def copy_hiddenT(j, s):
                dve.wait_ge(hidden_turned, j + 1)
                after(dve, down_done, j - 1)
                dve.tensor_copy(hiddenT[s % 2][:, :], k.ps[1][:, s % 2, :]).then_inc(hiddenT_ready, 1)

            def result(j, s):
                e = pl.of_slot(dve, j)
                dve.wait_ge(down_done, j + 1)
                dve.tensor_tensor(results[:, bass.ds(j, 1), :].rearrange("p a d -> p (a d)"),
                                  k.ps[2][:, s % 2, 0:D],
                                  b2[:, bass.ds(e, 1), :].rearrange("p a d -> p (a d)"),
                                  ALU.add).then_inc(result_ready, 1)

            for j in range(2):
                bias(j, j)

            def slot(j, s):
                if not (isinstance(j, int) and j >= SLOTS - 2):
                    bias(j + 2, (s + 2) % 4)
                copy_hiddenT(j, s)
                if not (isinstance(j, int) and j == 0):
                    result(j - 1, (s + 3) % 4)

            over_slots(dve, slot)
            result(SLOTS - 1, 3)
            for n in range(4):
                dve.wait_ge(gathered[n], 16 * QUARTER)
                for t in range(n * QUARTER, (n + 1) * QUARTER):
                    last = dve.scalar_tensor_tensor(k.x[:, t, :], results[:, t, :], ro.top[1][:, t:t + 1],
                                                    k.x[:, t, :], ALU.mult, ALU.add)
                last.then_inc(updated, 1)



ROUND = 1.5 * 2.0 ** 23
F1X = 512
LINEARS = ("d2v", "img", "txt", "att0", "att1", "f1", "f2")


def attention1_weights(k):
    w = k.even
    out, at = {}, 0
    for name, rows, n in (("d2v", D, C), ("img", D, D), ("txt", D, D), ("att0", 64, D), ("att1", 64, D),
                          ("f1", D, 4 * 2 * D), ("f2", D, F1X), ("b_d2v", D, 1), ("b_img", D, 1),
                          ("b_txt", D, 1), ("b_att0", D, 1), ("b_att1", D, 1), ("b_f1", D, 4),
                          ("b_f2", 1, D)):
        out[name] = w[0:rows, at:at + n]
        at += n
    return out


def load_attention1(sp, k):
    w = attention1_weights(k)
    d = {n[9:]: v for n, v in k.dram.items() if n.startswith("L1_xattn_")}
    for name in ("d2v", "img", "txt", "att0", "att1", "f2"):
        k.load(sp, "even", w[name], d[f"W_{name}"])
    k.load(sp, "even", w["f1"].rearrange("p (c n) -> p c n", c=4), d["W_f1"].rearrange("(c p) n -> p c n", p=P))
    with k.nc.allow_non_contiguous_dma(reason="short biases, feature-major"):
        for name in ("d2v", "img", "txt"):
            k.load(sp, "even", w[f"b_{name}"], d[f"b_{name}"].rearrange("(p a) -> p a", a=1))
        for name in ("att0", "att1"):
            for part in range(2):
                k.load(sp, "even", w[f"b_{name}"][part * 64:part * 64 + 64],
                       d[f"b_{name}"].rearrange("(p a) -> p a", a=1))
        k.load(sp, "even", w["b_f1"], d["b_f1"].rearrange("(c p) -> p c", p=P))
    k.load(sp, "even", w["b_f2"], row(d["b_f2"], D))


class Rounding:

    INPUTS = ("ctx", "vis", "img", "x", "cat", "h")

    def __init__(self, k, tag, sb):
        self.k = k
        n = len(self.INPUTS)
        self.parts = sb("parts", [P, n, 32])
        self.peak = sb("peak", [P, n])
        self.top = sb("top", [P, n])
        self.scale = sb("scale", [P, n])
        self.inverse = sb("inverse", [P, n])
        self.out_scale = sb("out_scale", [P, 8])
        self.peaks_ready = Signals.new(k.nc, f"{tag}_round_peaks")
        self.top_ready = Signals.new(k.nc, f"{tag}_round_top")
        self.step = Signals.new(k.nc, f"{tag}_scale_step")
        self.done = 0

    def peak_vector(self, dve, name, n, value):
        i = self.INPUTS.index(name)
        return dve.tensor_reduce(self.parts[0:value.shape[0], i, n:n + 1], value, AX.X, ALU.max,
                                 apply_absolute_value=True)

    def scale_vector(self, dve, link, name, count, linears, w_scale):
        i = self.INPUTS.index(name)
        dve.tensor_reduce(self.peak[:, i:i + 1], self.parts[:, i, 0:count], AX.X, ALU.max).then_inc(
            self.peaks_ready, 1)
        self.done += 1
        dve.wait_ge(self.top_ready, self.done)
        link(dve.tensor_scalar(self.scale[:, i:i + 1], self.top[:, i:i + 1], 1e-8, 1.0 / 127.0, ALU.max,
                               ALU.mult))
        link(dve.reciprocal(self.inverse[:, i:i + 1], self.scale[:, i:i + 1]))
        for name in linears:
            j = LINEARS.index(name)
            link(dve.tensor_tensor(self.out_scale[:, j:j + 1], self.scale[:, i:i + 1],
                                   w_scale[:, j:j + 1], ALU.mult))

    def gpsimd(self, pool, names):
        for n, name in enumerate(names):
            i = self.INPUTS.index(name)
            pool.wait_ge(self.peaks_ready, n + 1)
            pool.partition_all_reduce(self.top[:, i:i + 1], self.peak[:, i:i + 1], P, RMAX).then_inc(
                self.top_ready, 1)

    def round_vector(self, dve, link, name, out, value, tmp):
        i, rows = self.INPUTS.index(name), value.shape[0]
        link(dve.tensor_scalar(tmp, value, self.inverse[0:rows, i:i + 1], ROUND, ALU.mult, ALU.add))
        return dve.tensor_scalar(out, tmp, -ROUND, 127.0, ALU.add, ALU.min)


def attention1(k, load_next):
    nc = k.nc
    w = attention1_weights(k)
    loaded = k.loads["even"]
    with ExitStack() as outer:
        def keep(name, shape, dt=F32):
            return outer.enter_context(nc.sbuf_tensor(f"l1x_{name}", shape, dt))

        w_scale = keep("w_scale", [P, 8])
        f1T = keep("f1T", [P, 2, F1X], BF16)
        f2T = keep("f2T", [P, 4, D], BF16)
        rounded = keep("rounded", [P, TOK], BF16)
        average = keep("average", [P, BATCH])
        rounded_average = keep("rounded_average", [P, BATCH], BF16)
        tmp = keep("tmp", [P, QUAD])
        rn = Rounding(k, "l1x", keep)
        fused = keep("fused", [D, TOK])
        with ExitStack() as ctx:
            def sb(name, shape, dt=F32):
                return ctx.enter_context(nc.sbuf_tensor(f"l1x_{name}", shape, dt))

            def sem(name):
                return Signals.new(nc, f"l1x_{name}_")

            tr = Turned(k, ctx, "l1x", xnT=fused)
            tn = Ternary(k, ctx, "l1x", 1e-5, 4 * 2 * D)
            keys = [sb(f"keysT{j}", [D, TOK]) for j in range(2)]
            vis, img = keys
            wT = {name: sb(f"{name}T", [C if name == "d2v" else D, D], BF16)
                  for name in ("d2v", "img", "txt", "att0", "att1")}
            cross = sb("cross", [P, QUAD], BF16)
            cross32 = sb("cross32", [P, P])
            prob = [sb(f"prob{i}", [P, 4, P]) for i in range(2)]
            probT = sb("probT", [P, 4, P])
            tokens = sb("tokens", [P, 4, P])
            top, total, share = ([sb(f"{n}{i}", [P, 4]) for i in range(2)] for n in ("top", "total", "share"))
            cross_in, cross_ready, zeroed = sem("cross_in"), sem("cross_ready"), sem("zeroed")
            made, w_turned, w_ready = sem("made"), sem("w_turned"), sem("w_ready")
            step = sem("step")
            names = ("vis", "img", "key", "txt")
            done = {n: sem(f"{n}_done") for n in names}
            ready = {n: sem(f"{n}_ready") for n in names}
            round_ready = {n: sem(f"{n}_rounded") for n in ("ctx", "vis", "img", "x")}
            scored, top_ready, shifted = sem("scored"), sem("top_ready"), sem("shifted")
            exp_ready, total_ready, share_ready = sem("exp_ready"), sem("total_ready"), sem("share_ready")
            prob_ready, turned, probT_ready = sem("prob_ready"), sem("turned"), sem("probT_ready")
            keys_turned, tokens_ready = sem("keys_turned"), sem("tokens_ready")
            weighed, fused_ready = sem("weighed"), sem("fused_ready")
            units = [(j, n) for j in range(2) for n in range(QUADS)]
            block = ctx.enter_context(nc.Block())

            def quad(n):
                return slice(n * QUAD, (n + 1) * QUAD)

            @block.sync
            def _(sp):
                sp.dma_start(cross32[:, :], k.dram["const_cross"]).then_inc(cross_in, 16)
                sp.wait_ge(cross_in, 16)
                load_next(sp)

            @block.tensor
            def _(pe):
                for _ in LINEARS:
                    tn.tensor(pe, P)
                pe.wait_ge(made, len(LINEARS))
                for i, name in enumerate(("d2v", "img", "txt")):
                    n = C if name == "d2v" else D
                    pe.transpose(k.ps[0][0:n, 0, i * D:(i + 1) * D], w[name], k.ident[:, :])
                for i, name in enumerate(("att0", "att1")):
                    for part in range(2):
                        at = i * D + part * 64
                        pe.transpose(k.ps[0][:, 1, at:at + 64], w[name], k.ident[0:64, 0:64])
                for c in range(4):
                    for half_in in range(2):
                        pe.transpose(k.ps[1][:, half_in, c * P:(c + 1) * P],
                                     w["f1"][:, c * 2 * D + half_in * D:c * 2 * D + (half_in + 1) * D],
                                     k.ident[:, :])
                for c in range(4):
                    last = pe.transpose(k.ps[2][:, 0, c * D:(c + 1) * D], w["f2"][:, c * P:(c + 1) * P],
                                        k.ident[:, :])
                last.then_inc(w_turned, 1)
                for n in range(QUADS):
                    tr.tensor(pe, n)
                pe.wait_ge(w_ready, 7)
                for name, src, banks in (("vis", "ctx", k.ps[0]), ("img", "vis", k.ps[1])):
                    rows, weight = (C, wT["d2v"]) if name == "vis" else (D, wT["img"])
                    for n in range(QUADS):
                        pe.wait_ge(round_ready[src], n + 1)
                        after(pe, ready[name], n - 1)
                        pe.matmul(banks[:, n % 2, :], weight[:, :], rounded[0:rows, quad(n)], start=True,
                                  stop=True).then_inc(done[name], 1)
                for n in range(QUADS):
                    pe.wait_ge(round_ready["img"], n + 1)
                    after(pe, ready["key"], 2 * n - 2)
                    for j in range(2):
                        pe.matmul(k.ps[j][:, n % 2, :], wT[f"att{j}"][:, :], rounded[:, quad(n)],
                                  start=True, stop=True).then_inc(done["key"], 1)
                for n in range(QUADS):
                    pe.wait_ge(round_ready["x"], n + 1)
                    after(pe, ready["txt"], n - 1)
                    pe.matmul(k.ps[2][:, n % 2, :], wT["txt"][:, :], rounded[:, quad(n)], start=True,
                              stop=True).then_inc(done["txt"], 1)
                pe.wait_ge(ready["txt"], QUADS)
                pe.wait_ge(ready["key"], 2 * QUADS)
                pe.wait_ge(cross_ready, 1)

                def score(v):
                    j, n = units[v]
                    after(pe, shifted, v - 1)
                    if j == 1:
                        pe.wait_ge(fused_ready, n + 1)
                    pe.matmul(k.ps[0][:, v % 2, :], k.identb[:, :], cross[:, :], start=True, stop=True)
                    for i in range(4):
                        at = n * QUAD + i * P
                        last = pe.matmul(k.ps[0][:, v % 2, i * P:(i + 1) * P], fused[:, at:at + P],
                                         keys[j][:, at:at + P], start=False, stop=True,
                                         skip_group_check=True)
                    last.then_inc(scored, 1)

                score(0)
                for v, (j, n) in enumerate(units):
                    if v + 1 < len(units):
                        score(v + 1)
                    after(pe, tokens_ready, v)
                    for i in range(4):
                        at = n * QUAD + i * P
                        last = pe.transpose(k.ps[2][:, 0, i * P:(i + 1) * P], keys[j][:, at:at + P],
                                            k.ident[:, :])
                    last.then_inc(keys_turned, 1)
                    pe.wait_ge(prob_ready, v + 1)
                    after(pe, probT_ready, v - 1)
                    for i in range(4):
                        last = pe.transpose(k.ps[1][:, v % 2, i * P:(i + 1) * P], prob[v % 2][:, i, :],
                                            k.ident[:, :])
                    last.then_inc(turned, 1)
                    pe.wait_ge(probT_ready, v + 1)
                    pe.wait_ge(tokens_ready, v + 1)
                    after(pe, fused_ready, v)
                    for i in range(4):
                        last = pe.matmul(k.ps[2][:, 1, i * P:(i + 1) * P], tokens[:, i, :], probT[:, i, :],
                                         start=True, stop=True)
                    last.then_inc(weighed, 1)

            @block.scalar
            def _(act):
                norm_root_scalar(act, k, tr.norm)
                act.wait_ge(w_turned, 1)
                act.copy(wT["d2v"][:, :], k.ps[0][0:C, 0, 0:D]).then_inc(w_ready, 1)
                act.copy(wT["img"][:, :], k.ps[0][:, 0, D:2 * D]).then_inc(w_ready, 1)
                act.copy(wT["txt"][:, :], k.ps[0][:, 0, 2 * D:3 * D]).then_inc(w_ready, 1)
                for j in range(2):
                    act.copy(wT[f"att{j}"][:, :], k.ps[0][:, 1, j * D:(j + 1) * D]).then_inc(w_ready, 1)
                act.copy(f1T[:, :, :], k.ps[1][:, :, :]).then_inc(w_ready, 1)
                act.copy(f2T[:, :, :].rearrange("p c n -> p (c n)"), k.ps[2][:, 0, :]).then_inc(w_ready, 1)
                for n in range(QUADS):
                    tr.scalar(act, n)
                for name, out, linear, banks in (("vis", vis, "d2v", k.ps[0]), ("img", img, "img", k.ps[1])):
                    i = LINEARS.index(linear)
                    for n in range(QUADS):
                        act.wait_ge(done[name], n + 1)
                        act.activation(out[:, quad(n)], banks[:, n % 2, :], ACT.Identity,
                                       bias=w[f"b_{linear}"], scale=rn.out_scale[:, i:i + 1]).then_inc(
                                           ready[name], 1)
                for n in range(QUADS):
                    for j in range(2):
                        i = LINEARS.index(f"att{j}")
                        act.wait_ge(done["key"], 2 * n + j + 1)
                        act.activation(keys[j][:, quad(n)], k.ps[j][:, n % 2, :], ACT.Identity,
                                       bias=w[f"b_att{j}"], scale=rn.out_scale[:, i:i + 1]).then_inc(
                                           ready["key"], 1)
                i = LINEARS.index("txt")
                for n in range(QUADS):
                    act.wait_ge(done["txt"], n + 1)
                    act.activation(fused[:, quad(n)], k.ps[2][:, n % 2, :], ACT.Identity, bias=w["b_txt"],
                                   scale=rn.out_scale[:, i:i + 1]).then_inc(ready["txt"], 1)
                for v in range(len(units)):
                    act.wait_ge(keys_turned, v + 1)
                    after(act, weighed, v)
                    act.copy(tokens[:, :, :].rearrange("p a n -> p (a n)"), k.ps[2][:, 0, :]).then_inc(
                        tokens_ready, 1)
                    act.wait_ge(shifted, v + 1)
                    act.activation(prob[v % 2][:, :, :], prob[v % 2][:, :, :], ACT.Exp,
                                   scale=float(D) ** -0.5).then_inc(exp_ready, 1)
                    act.wait_ge(turned, v + 1)
                    act.copy(probT[:, :, :].rearrange("p a n -> p (a n)"), k.ps[1][:, v % 2, :]).then_inc(
                        probT_ready, 1)

            @block.vector
            def _(dve):
                link = linked(dve, step)
                dve.wait_ge(k.load_even, loaded)
                sizes = {"d2v": D * C, "img": D * D, "txt": D * D, "att0": 64 * D, "att1": 64 * D,
                         "f1": F1X * 2 * D, "f2": F1X * D}
                for i, name in enumerate(LINEARS):
                    ternary_vector(dve, tn, i, link, w[name], w[name], sizes[name], w_scale[:, i:i + 1])
                    dve.sem_inc(made, 1)
                    if name == "txt":
                        link(dve.memset(tn.sums[:, :], 0.0))
                link(dve.memset(rn.parts[:, :, :], 0.0))
                link(rn.peak_vector(dve, "ctx", 0, k.ctxT[0:C, :]))
                rn.scale_vector(dve, link, "ctx", 1, ("d2v",), w_scale)
                for n in range(QUADS):
                    rn.round_vector(dve, link, "ctx", rounded[0:C, quad(n)], k.ctxT[0:C, quad(n)],
                                    tmp[0:C, :]).then_inc(round_ready["ctx"], 1)
                    dve.wait_ge(round_ready["ctx"], n + 1)
                tr.vector(dve)
                for n in range(QUADS):
                    dve.wait_ge(ready["vis"], n + 1)
                    link(rn.peak_vector(dve, "vis", n, vis[:, quad(n)]))
                rn.scale_vector(dve, link, "vis", QUADS, ("img",), w_scale)
                for n in range(QUADS):
                    rn.round_vector(dve, link, "vis", rounded[:, quad(n)], vis[:, quad(n)],
                                    tmp[:, :]).then_inc(round_ready["vis"], 1)
                    dve.wait_ge(round_ready["vis"], n + 1)
                for n in range(QUADS):
                    dve.wait_ge(ready["img"], n + 1)
                    link(rn.peak_vector(dve, "img", n, img[:, quad(n)]))
                    link(dve.tensor_reduce(average[:, 8 * n:8 * n + 8],
                                           img[:, quad(n)].rearrange("p (b s) -> p b s", s=SEQ), AX.X,
                                           ALU.add))
                link(dve.tensor_scalar(average[:, :], average[:, :], 1.0 / SEQ, None, ALU.mult))
                rn.scale_vector(dve, link, "img", QUADS, ("att0", "att1"), w_scale)
                for n in range(QUADS):
                    rn.round_vector(dve, link, "img", rounded[:, quad(n)], img[:, quad(n)],
                                    tmp[:, :]).then_inc(round_ready["img"], 1)
                    dve.wait_ge(round_ready["img"], n + 1)
                dve.wait_ge(tr.ready, QUADS)
                link(rn.peak_vector(dve, "x", 0, fused[:, :]))
                rn.scale_vector(dve, link, "x", 1, ("txt",), w_scale)
                for n in range(QUADS):
                    dve.wait_ge(done["key"], 2 * n + 2)
                    rn.round_vector(dve, link, "x", rounded[:, quad(n)], fused[:, quad(n)],
                                    tmp[:, :]).then_inc(round_ready["x"], 1)
                    dve.wait_ge(round_ready["x"], n + 1)

                def softmax(v):
                    i = v % 2
                    dve.wait_ge(scored, v + 1)
                    scores = k.ps[0][:, i, :].rearrange("p (a n) -> p a n", n=P)
                    dve.tensor_reduce(top[i][:, :], scores, AX.X, ALU.max).then_inc(top_ready, 1)
                    dve.wait_ge(top_ready, v + 1)
                    after(dve, turned, v - 1)
                    dve.tensor_tensor(prob[i][:, :, :], scores, spread(top[i][:, :], P),
                                      ALU.subtract).then_inc(shifted, 1)

                def divide(v):
                    i = v % 2
                    dve.wait_ge(exp_ready, v + 1)
                    dve.tensor_reduce(total[i][:, :], prob[i][:, :, :], AX.X, ALU.add).then_inc(total_ready, 1)
                    dve.wait_ge(total_ready, v + 1)
                    dve.reciprocal(share[i][:, :], total[i][:, :]).then_inc(share_ready, 1)
                    dve.wait_ge(share_ready, v + 1)
                    dve.tensor_tensor(prob[i][:, :, :], prob[i][:, :, :], spread(share[i][:, :], P),
                                      ALU.mult).then_inc(prob_ready, 1)

                softmax(0)
                for v, (j, n) in enumerate(units):
                    divide(v)
                    if v + 1 < len(units):
                        softmax(v + 1)
                    dve.wait_ge(weighed, v + 1)
                    dve.scalar_tensor_tensor(fused[:, quad(n)], k.ps[2][:, 1, :], 0.1, fused[:, quad(n)],
                                             ALU.mult, ALU.add).then_inc(fused_ready, 1)

            @block.gpsimd
            def _(pool):
                pool.wait_ge(cross_in, 16)
                pool.tensor_copy(cross[:, :].rearrange("p (a n) -> p a n", n=P),
                                 cross32[:, :].rearrange("p (a n) -> p a n", a=1).to_broadcast([P, 4, P])
                                 ).then_inc(cross_ready, 1)
                rn.gpsimd(pool, ("ctx", "vis", "img", "x"))

        with ExitStack() as ctx:
            def sb(name, shape, dt=F32):
                return ctx.enter_context(nc.sbuf_tensor(f"l1y_{name}", shape, dt))

            def sem(name):
                return Signals.new(nc, f"l1y_{name}")

            hidden = sb("hidden", [P, 4, TOK])
            bias = sb("bias", [P, 4, D])
            step, cat_rounded, average_rounded = sem("step"), sem("cat_rounded"), sem("average_rounded")
            up_done, hidden_ready, h_rounded = sem("up_done"), sem("hidden_ready"), sem("h_rounded")
            down_done, scaled, updated, stats_done = sem("down_done"), sem("scaled"), sem("updated"), sem("stats_done")
            bias_done, bias_ready = sem("bias_done"), sem("bias_ready")
            rn.peaks_ready, rn.top_ready, rn.done = sem("peaks_ready"), sem("top_ready"), 0
            rounded_h = [rounded[:, i * 4 * QUAD:(i + 1) * 4 * QUAD].rearrange("p (c n) -> p c n", c=4)
                         for i in range(2)]
            block = ctx.enter_context(nc.Block())

            def quad(n):
                return slice(n * QUAD, (n + 1) * QUAD)

            @block.tensor
            def _(pe):
                for j in range(4):
                    last = pe.matmul(k.r6[:, j * D:(j + 1) * D], k.ones[0:1, :], w["b_f2"], start=True, stop=True)
                last.then_inc(bias_done, 1)
                pe.wait_ge(average_rounded, 1)
                for n in range(QUADS):
                    pe.wait_ge(cat_rounded, n + 1)
                    avg = rounded_average[:, 8 * n:8 * n + 8].rearrange("p (b a) -> p b a", a=1).to_broadcast(
                        [P, 8, SEQ])
                    for pair in range(2):
                        after(pe, hidden_ready, 2 * n - 1 + pair)
                        for i in range(2):
                            cols = slice((2 * pair + i) * P, (2 * pair + i + 1) * P)
                            out = k.ps[pair][:, i, :]
                            pe.matmul(out, f1T[:, 0, cols], rounded[:, quad(n)], start=True, stop=False)
                            last = pe.matmul(out, f1T[:, 1, cols], avg, start=False, stop=True)
                        last.then_inc(up_done, 1)
                for n in range(QUADS):
                    pe.wait_ge(h_rounded, n + 1)
                    after(pe, scaled, n - 1)
                    for j in range(4):
                        for c in range(4):
                            last = pe.matmul(k.ps[2][:, n % 2, j * D:(j + 1) * D],
                                             rounded_h[n % 2][:, c, j * P:(j + 1) * P], f2T[:, c, :],
                                             start=c == 0, stop=c == 3)
                    last.then_inc(down_done, 1)

            @block.scalar
            def _(act):
                act.wait_ge(bias_done, 1)
                act.copy(bias[:, :, :].rearrange("p a n -> p (a n)"), k.r6[:, :]).then_inc(bias_ready, 1)
                s = LINEARS.index("f1")
                for n in range(QUADS):
                    for pair in range(2):
                        act.wait_ge(up_done, 2 * n + pair + 1)
                        for i in range(2):
                            c = 2 * pair + i
                            last = act.activation(hidden[:, c, quad(n)], k.ps[pair][:, i, :], ACT.Relu,
                                                  bias=w["b_f1"][:, c:c + 1], scale=rn.out_scale[:, s:s + 1])
                        last.then_inc(hidden_ready, 1)

            @block.vector
            def _(dve):
                link = linked(dve, step)
                link(rn.peak_vector(dve, "cat", 0, fused[:, :]))
                link(rn.peak_vector(dve, "cat", 1, average[:, :]))
                rn.scale_vector(dve, link, "cat", 2, ("f1",), w_scale)
                rn.round_vector(dve, link, "cat", rounded_average[:, :], average[:, :],
                                tmp[:, 0:BATCH]).then_inc(average_rounded, 1)
                dve.wait_ge(average_rounded, 1)
                for n in range(QUADS):
                    rn.round_vector(dve, link, "cat", rounded[:, quad(n)], fused[:, quad(n)],
                                    tmp[:, :]).then_inc(cat_rounded, 1)
                    dve.wait_ge(cat_rounded, n + 1)
                for n in range(QUADS):
                    for pair in range(2):
                        dve.wait_ge(hidden_ready, 2 * n + pair + 1)
                        for i in range(2):
                            link(rn.peak_vector(dve, "h", 4 * n + 2 * pair + i,
                                                hidden[:, 2 * pair + i, quad(n)]))
                rn.scale_vector(dve, link, "h", 32, ("f2",), w_scale)
                dve.wait_ge(bias_ready, 1)
                s = LINEARS.index("f2")
                for n in range(QUADS + 1):
                    if n < QUADS:
                        after(dve, down_done, n - 1)
                        last = rn.round_vector(dve, link, "h", rounded_h[n % 2], hidden[:, :, quad(n)],
                                               hidden[:, :, quad(n)])
                        last.then_inc(h_rounded, 1)
                    if n >= 1:
                        m = n - 1
                        dve.wait_ge(down_done, m + 1)
                        dve.scalar_tensor_tensor(tmp[:, :], k.ps[2][:, m % 2, :], rn.out_scale[:, s:s + 1],
                                                 bias[:, :, :].rearrange("p a n -> p (a n)"), ALU.mult,
                                                 ALU.add).then_inc(scaled, 1)
                        dve.wait_ge(scaled, m + 1)
                        xq = k.x[:, 4 * m:4 * m + 4, :].rearrange("p a d -> p (a d)")
                        dve.tensor_tensor(xq, xq, tmp[:, :], ALU.add).then_inc(updated, 1)
                        dve.wait_ge(updated, m + 1)
                        for j in range(4):
                            last = dve.bn_stats(k.stats[:, 4 * m + j, :], k.x[:, 4 * m + j, :])
                        last.then_inc(stats_done, 1)

            @block.gpsimd
            def _(pool):
                rn.gpsimd(pool, ("cat", "h"))



PAIR = 18
VCOLS = H // 2 * PAIR


class Narrow:

    def __init__(self, k, ctx, tag):
        def sb(name, shape):
            return ctx.enter_context(k.nc.sbuf_tensor(f"{tag}_{name}", shape, F32))

        self.q = k.odd[:, 4352:4352 + TOK]
        self.k = sb("k_all", [D, TOK])
        self.v = sb("v_all", [P, BATCH, VCOLS])
        self.own = sb("own", [P, H])
        self.parity = sb("parity", [P, 16])
        self.masks_in = Signals.new(k.nc, f"{tag}_masks_in")
        self.ones_ready = Signals.new(k.nc, f"{tag}_ones_ready")

    def load(self, sp, k, own):
        sp.dma_start(self.own[:, :], k.dram[own]).then_inc(self.masks_in, 16)
        sp.dma_start(self.parity[:, :], k.dram["const_parity"]).then_inc(self.masks_in, 16)

    def ones_gpsimd(self, pool):
        v = self.v[:, :, :].rearrange("p b (c n) -> p (b c) n", n=PAIR)
        for half_at in range(2):
            rows = slice(half_at * SEQ, (half_at + 1) * SEQ)
            for par in range(2):
                pool.memset(v[rows, :, 16 + par:17 + par], 1.0 if par == half_at else 0.0).then_inc(
                    self.ones_ready, 1)

    def values_vector(self, dve, n, bank):
        v = self.v[:, 4 * n:4 * n + 4, :].rearrange("p b (c n) -> p (b c) n", n=PAIR)[:, :, 0:16]
        mask = self.parity[:, :].rearrange("p (a n) -> p a n", a=1).to_broadcast([P, 32, 16])
        return dve.tensor_tensor(v, bank.rearrange("p (c n) -> p c n", n=16), mask, ALU.mult)


def narrow_attention(k, tag, nw, wo, bias, mask, load_next):
    nc = k.nc
    scale = 8.0 ** -0.5
    own_dve = 4
    with ExitStack() as ctx:
        def sb(name, shape):
            return ctx.enter_context(nc.sbuf_tensor(f"{tag}_{name}", shape, F32))

        def sem(name):
            return Signals.new(nc, f"{tag}_{name}")

        queries = [sb(f"queries{i}", [D, P]) for i in range(2)]
        keys = [sb(f"keys{i}", [D, H, P]) for i in range(2)]
        values = [sb(f"values{i}", [P, 2, VCOLS]) for i in range(2)]
        prob = [sb(f"prob{i}", [P, H, SEQ]) for i in range(2)]
        probT = sb("probT", [P, H // 2, P])
        top = [sb(f"top{i}", [P, H]) for i in range(2)]
        share = [sb(f"share{i}", [P, H]) for i in range(2)]
        heads = [sb(f"heads{i}", [P, D]) for i in range(2)]
        headsT = sb("headsT", [D, P])
        S, T, O = k.ps
        queries_ready, values_ready = sem("queries_ready"), sem("values_ready")
        own0_ready, own1_ready = sem("own0_ready"), sem("own1_ready")
        scored, top_ready, shifted = sem("scored"), sem("top_ready"), sem("shifted")
        exp_ready, turned, probT_ready = sem("exp_ready"), sem("turned"), sem("probT_ready")
        weighed, share_ready, heads_ready = sem("weighed"), sem("share_ready"), sem("heads_ready")
        heads_turned, headsT_ready = sem("heads_turned"), sem("headsT_ready")
        projected, updated, stats_done = sem("projected"), sem("updated"), sem("stats_done")
        block = ctx.enter_context(nc.Block())
        AHEAD = 2

        def own(eng, u, s, hs, ready):
            after(eng, scored, u - 1)
            kt = nw.k[:, bass.ds(u * P, P)].rearrange("p (a n) -> p a n", a=1).to_broadcast(
                [P, hs.stop - hs.start, P])
            eng.tensor_tensor(keys[s % 2][:, hs, :], kt, spread(nw.own[:, hs], P), ALU.mult).then_inc(ready, 1)

        @block.sync
        def _(sp):
            load_next(sp)

        @block.tensor
        def _(pe):
            def scores(u, s):
                pe.wait_ge(queries_ready, u + 1)
                pe.wait_ge(own0_ready, u + 1)
                pe.wait_ge(own1_ready, u + 1)
                after(pe, shifted, u)
                if mask is not None:
                    for j in range(2):
                        pe.matmul(S[:, j, :], k.identb[:, :], mask, start=True, stop=True)
                for j in range(2):
                    for b in range(2):
                        rows = slice(b * SEQ, (b + 1) * SEQ)
                        last = pe.matmul(S[rows, j, :], queries[s % 2][:, rows],
                                         keys[s % 2][:, 8 * j:8 * j + 8, rows], start=mask is None,
                                         stop=True, skip_group_check=mask is not None)
                last.then_inc(scored, 1)

            def turn(t, s):
                pe.wait_ge(exp_ready, t + 1)
                after(pe, probT_ready, t)
                for p in range(H // 2):
                    last = pe.transpose(T[:, p // 4, (p % 4) * P:(p % 4 + 1) * P],
                                        prob[s % 2][:, 2 * p:2 * p + 2, :].rearrange("p h k -> p (h k)"),
                                        k.ident[:, :])
                last.then_inc(turned, 1)

            def weigh(t, s):
                pe.wait_ge(probT_ready, t + 1)
                pe.wait_ge(values_ready, t + 1)
                after(pe, heads_ready, t - 1)
                for p in range(H // 2):
                    for b in range(2):
                        rows = slice(b * SEQ, (b + 1) * SEQ)
                        last = pe.matmul(O[rows, s % 2, p * PAIR:(p + 1) * PAIR], probT[:, p, rows],
                                         values[s % 2][:, b, p * PAIR:(p + 1) * PAIR], start=True, stop=True)
                last.then_inc(weighed, 1)

            def turn_heads(t, s):
                pe.wait_ge(heads_ready, t + 1)
                after(pe, headsT_ready, t)
                pe.transpose(k.r7[:, 0:P], heads[s % 2][:, :], k.ident[:, :]).then_inc(heads_turned, 1)

            def project(t):
                pe.wait_ge(headsT_ready, t + 1)
                after(pe, updated, t)
                last = pe.matmul(k.r6[:, 0:D], headsT[:, :], wo, start=True, stop=bias is None)
                if bias is not None:
                    last = pe.matmul(k.r6[:, 0:D], k.ones[0:1, :], bias, start=False, stop=True)
                last.then_inc(projected, 1)

            for u in range(AHEAD):
                scores(u, u)

            def slot(t, s):
                turn(t, s)
                if not is_last(t, AHEAD):
                    scores(t + AHEAD, (s + AHEAD) % 4)
                before = not (isinstance(t, int) and t == 0)
                if before:
                    turn_heads(t - 1, (s + 3) % 4)
                weigh(t, s)
                if before:
                    project(t - 1)

            over_tiles(pe, slot)
            turn_heads(TILES - 1, 3)
            project(TILES - 1)

        @block.scalar
        def _(act):
            def exp(u, s):
                act.wait_ge(shifted, u + 1)
                act.activation(prob[s % 2][:, :, :], prob[s % 2][:, :, :], ACT.Exp, scale=scale).then_inc(
                    exp_ready, 1)

            def copy_values(u, s):
                after(act, weighed, u - 1)
                act.copy(values[s % 2][:, :, :], nw.v[:, bass.ds(u * 2, 2), :]).then_inc(values_ready, 1)

            for u in range(AHEAD):
                copy_values(u, u)
            exp(0, 0)

            def copy_headsT(t):
                act.wait_ge(heads_turned, t + 1)
                after(act, projected, t)
                act.copy(headsT[:, :], k.r7[:, 0:P]).then_inc(headsT_ready, 1)

            def slot(t, s):
                act.wait_ge(turned, t + 1)
                after(act, weighed, t)
                act.copy(probT[:, :, :], T[:, :, :].rearrange("p a (c q) -> p (a c) q", q=P)).then_inc(
                    probT_ready, 1)
                if not is_last(t):
                    exp(t + 1, (s + 1) % 4)
                if not (isinstance(t, int) and t == 0):
                    copy_headsT(t - 1)
                if not is_last(t, AHEAD):
                    copy_values(t + AHEAD, (s + AHEAD) % 4)

            over_tiles(act, slot)
            copy_headsT(TILES - 1)

        @block.vector
        def _(dve):
            def softmax(u, s):
                dve.wait_ge(scored, u + 1)
                scores = S[:, :, :].rearrange("p a (h k) -> p (a h) k", k=SEQ)
                dve.tensor_reduce(top[s % 2][:, :], scores, AX.X, ALU.max).then_inc(top_ready, 1)
                dve.wait_ge(top_ready, u + 1)
                after(dve, turned, u - 1)
                dve.tensor_tensor(prob[s % 2][:, :, :], scores, spread(top[s % 2][:, :], SEQ),
                                  ALU.subtract).then_inc(shifted, 1)

            def divide(t, s):
                dve.wait_ge(weighed, t + 1)
                o = O[:, s % 2, 0:VCOLS].rearrange("p (c n) -> p c n", n=PAIR)
                r = share[s % 2][:, :].rearrange("p (c a) -> p c a", a=2)
                dve.reciprocal(r, o[:, :, 16:18]).then_inc(share_ready, 1)
                dve.wait_ge(share_ready, t + 1)
                after(dve, heads_turned, t - 1)
                dve.tensor_tensor(heads[s % 2][:, :].rearrange("p (c a n) -> p c a n", a=2, n=8),
                                  o[:, :, 0:16].rearrange("p c (a n) -> p c a n", n=8),
                                  share[s % 2][:, :].rearrange("p (c a o) -> p c a o", a=2, o=1).to_broadcast(
                                      [P, H // 2, 2, 8]), ALU.mult).then_inc(heads_ready, 1)

            def update(t):
                dve.wait_ge(projected, t + 1)
                xt = k.x[:, bass.ds(t, 1), :].rearrange("p a d -> p (a d)")
                dve.tensor_tensor(xt, xt, k.r6[:, 0:D], ALU.add).then_inc(updated, 1)
                dve.wait_ge(updated, t + 1)
                dve.bn_stats(k.stats[:, bass.ds(t, 1), :].rearrange("p a d -> p (a d)"), xt).then_inc(
                    stats_done, 1)

            for u in range(AHEAD):
                own(dve, u, u, slice(0, own_dve), own0_ready)
            for u in range(AHEAD):
                softmax(u, u)
            own(dve, AHEAD, AHEAD, slice(0, own_dve), own0_ready)

            def slot(t, s):
                if not is_last(t, AHEAD + 1):
                    own(dve, t + AHEAD + 1, (s + AHEAD + 1) % 4, slice(0, own_dve), own0_ready)
                if not is_last(t, AHEAD):
                    softmax(t + AHEAD, (s + AHEAD) % 4)
                divide(t, s)
                if not (isinstance(t, int) and t == 0):
                    update(t - 1)

            over_tiles(dve, slot)
            update(TILES - 1)

        @block.gpsimd
        def _(pool):
            def stage(u, s):
                own(pool, u, s, slice(own_dve, H), own1_ready)
                pool.tensor_copy(queries[s % 2][:, :], nw.q[:, bass.ds(u * P, P)]).then_inc(queries_ready, 1)

            for u in range(AHEAD):
                stage(u, u)

            def slot(t, s):
                if not is_last(t, AHEAD):
                    stage(t + AHEAD, (s + AHEAD) % 4)

            over_tiles(pool, slot)


def attention2_weights(k):
    w = k.even
    return [w[:, i * D:(i + 1) * D] for i in range(4)], w[:, 512:514], w[0:1, 768:768 + D]


def load_attention2(sp, k):
    (wq, wk, wv, wo), bqk, bo = attention2_weights(k)
    d = k.dram
    k.load(sp, "even", wq, d["L2_xattn_wq"])
    k.load(sp, "even", wk[0:C], d["L2_xattn_wk"])
    k.load(sp, "even", wv[0:C], d["L2_xattn_wv"])
    k.load(sp, "even", wo, d["L2_xattn_wo"])
    with k.nc.allow_non_contiguous_dma(reason="two short biases, feature-major"):
        k.load(sp, "even", bqk[:, 0:1], d["L2_xattn_bq"].rearrange("(p a) -> p a", a=1))
        k.load(sp, "even", bqk[:, 1:2], d["L2_xattn_bk"].rearrange("(p a) -> p a", a=1))
    k.load(sp, "even", wv[C:C + 1], row(d["L2_xattn_bv"], D))
    k.load(sp, "even", bo, row(d["L2_xattn_bo"], D))


def attention2(k, load_next):
    nc = k.nc
    (wq, wk, wv, wo), bqk, bo = attention2_weights(k)
    with ExitStack() as outer:
        nw = Narrow(k, outer, "l2x")
        loaded = k.loads["even"]
        with ExitStack() as ctx:
            def sem(name):
                return Signals.new(nc, f"l2x_{name}")

            tr = Turned(k, ctx, "l2x")
            q_done, k_done, v_done = sem("q_done"), sem("k_done"), sem("v_done")
            q_ready, k_ready, v_ready = sem("q_ready"), sem("k_ready"), sem("v_ready")
            block = ctx.enter_context(nc.Block())

            @block.sync
            def _(sp):
                nw.load(sp, k, "const_own8")
                sp.wait_ge(nw.masks_in, 32)

            @block.gpsimd
            def _(pool):
                nw.ones_gpsimd(pool)

            @block.tensor
            def _(pe):
                pe.wait_ge(k.load_even, loaded)
                for n in range(QUADS):
                    tr.tensor(pe, n)
                for n in range(QUADS):
                    cols = slice(n * QUAD, (n + 1) * QUAD)
                    after(pe, k_ready, n - 1)
                    pe.matmul(k.ps[1][:, n % 2, :], wk[0:C, :], k.ctxT[0:C, cols], start=True,
                              stop=True).then_inc(k_done, 1)
                    for j in range(2):
                        after(pe, v_ready, 2 * n + j - 1)
                        for i in range(4):
                            at = n * QUAD + (4 * j + i) * SEQ
                            for half_at in range(2):
                                last = pe.matmul(k.ps[2][half_at * SEQ:(half_at + 1) * SEQ, j,
                                                         i * D:(i + 1) * D],
                                                 k.ctxT[0:C + 1, at:at + SEQ], wv[0:C + 1, :],
                                                 start=True, stop=True)
                        last.then_inc(v_done, 1)
                    after(pe, q_ready, n - 1)
                    pe.wait_ge(tr.ready, n + 1)
                    pe.matmul(k.ps[0][:, n % 2, :], wq, tr.xnT[:, cols], start=True,
                              stop=True).then_inc(q_done, 1)

            @block.scalar
            def _(act):
                norm_root_scalar(act, k, tr.norm)
                act.wait_ge(k.load_even, loaded)
                for n in range(QUADS):
                    tr.scalar(act, n)
                for n in range(QUADS):
                    act.wait_ge(q_done, n + 1)
                    act.activation(nw.q[:, n * QUAD:(n + 1) * QUAD], k.ps[0][:, n % 2, :], ACT.Identity,
                                   bias=bqk[:, 0:1]).then_inc(q_ready, 1)

            @block.vector
            def _(dve):
                tr.vector(dve)
                dve.wait_ge(k.load_even, loaded)
                dve.wait_ge(nw.masks_in, 32)
                for n in range(QUADS):
                    dve.wait_ge(k_done, n + 1)
                    dve.tensor_scalar(nw.k[:, n * QUAD:(n + 1) * QUAD], k.ps[1][:, n % 2, :],
                                      bqk[:, 1:2], None, ALU.add).then_inc(k_ready, 1)
                    for j in range(2):
                        dve.wait_ge(v_done, 2 * n + j + 1)
                        nw.values_vector(dve, 2 * n + j, k.ps[2][:, j, :]).then_inc(v_ready, 1)

        narrow_attention(k, "l2xa", nw, wo, bo, None, load_next)



L2, E2 = 32, 7
HH = 4


def ffn2_weights(k):
    w = k.odd
    at = 3072
    small = {}
    for name, rows, n in (("kvd", D, L2), ("qd", D, L2), ("ku", L2, 64), ("qu", L2, 64), ("vu", L2, D),
                          ("ropeq", L2, 64), ("ropek", D, 64), ("o", D, D), ("router", D, 8),
                          ("ln1", D, 1), ("ln2", D, 1), ("bias", 1, 8)):
        small[name] = w[0:rows, at:at + n]
        at += n
    assert at <= 4352
    return (w[:, 0:2048].rearrange("p (e f) -> p e f", e=8),
            w[:, 2048:3072].rearrange("p (e c n) -> p e c n", e=8, c=1), small)


def load_ffn2(sp, k):
    up, down, w = ffn2_weights(k)
    d = {n[7:]: v for n, v in k.dram.items() if n.startswith("L2_ffn_")}
    for name, key in (("qd", "W_qd"), ("kvd", "W_kvd"), ("ku", "W_ku"), ("qu", "W_qu"), ("vu", "W_vu"),
                      ("ropeq", "W_ropeq"), ("ropek", "W_ropek"), ("o", "W_o")):
        k.load(sp, "odd", w[name], d[key])
    with k.nc.allow_non_contiguous_dma(reason="short weights, feature-major"):
        k.load(sp, "odd", w["router"][:, 0:E2], d["W_router"])
        k.load(sp, "odd", w["ln1"], d["w_ln1"].rearrange("(p a) -> p a", a=1))
        k.load(sp, "odd", w["ln2"], d["w_ln2"].rearrange("(p a) -> p a", a=1))
    k.load(sp, "odd", w["bias"][:, 0:E2], row(d["routing_bias"], E2))
    k.load(sp, "odd", up[:, 0:E2, 0:D], d["Wg_r"].rearrange("e d f -> d e f"))
    k.load(sp, "odd", up[:, 0:E2, D:2 * D], d["Wu_r"].rearrange("e d f -> d e f"))
    k.load(sp, "odd", down[:, 0:E2, 0, :], d["Wd_r"].rearrange("e d f -> d e f"))
    k.load(sp, "odd", up[:, E2, 0:D], d["Wg_s"])
    k.load(sp, "odd", up[:, E2, D:2 * D], d["Wu_s"])
    k.load(sp, "odd", down[:, E2, 0, :], d["Wd_s"])


def latent_attention(k, load_next):
    nc = k.nc
    _, _, w = ffn2_weights(k)
    with ExitStack() as outer:
        nw = Narrow(k, outer, "mla")
        causal = outer.enter_context(nc.sbuf_tensor("mla_causal", [P, 512], BF16))
        loaded = k.loads["odd"]
        with ExitStack() as ctx:
            def sb(name, shape):
                return ctx.enter_context(nc.sbuf_tensor(f"mla_{name}", shape, F32))

            def sem(name):
                return Signals.new(nc, f"mla_{name}")

            tr = Turned(k, ctx, "mla", rms=True, weight=w["ln1"])
            lat = [sb(f"lat{i}", [L2, 2, QUAD]) for i in range(2)]
            q_w, q_rot = sb("q_w", [L2, D]), sb("q_rot", [L2, D])
            k_w, kx_w, kx_rot = sb("k_w", [L2, D]), sb("kx_w", [D, D]), sb("kx_rot", [D, D])
            cos, sin = sb("cos", [P, SEQ]), sb("sin", [P, SEQ])
            mask32 = sb("mask32", [P, SEQ])
            turned_q, turned_k = sb("turned_q", [P, QUAD]), sb("turned_k", [P, QUAD])
            const_in, zeroed, w_ready = sem("const_in"), sem("zeroed"), sem("w_ready")
            mask_ready = sem("mask_ready")
            lat_done, lat_ready = sem("lat_done"), sem("lat_ready")
            q_done, k_done, v_done = sem("q_done"), sem("k_done"), sem("v_done")
            q_cos, q_sin, k_cos, k_sin = sem("q_cos"), sem("q_sin"), sem("k_cos"), sem("k_sin")
            q_ready, k_ready, v_ready = sem("q_ready"), sem("k_ready"), sem("v_ready")
            block = ctx.enter_context(nc.Block())

            @block.sync
            def _(sp):
                for out, name in ((cos, "const_cos"), (sin, "const_sin"), (mask32, "const_causal")):
                    sp.dma_start(out[:, :], k.dram[name]).then_inc(const_in, 16)
                nw.load(sp, k, "const_own4")
                sp.wait_ge(const_in, 48)
                sp.wait_ge(nw.masks_in, 32)

            @block.gpsimd
            def _(pool):
                for t in (q_rot, k_w, kx_w, kx_rot):
                    pool.memset(t[:, :], 0.0).then_inc(zeroed, 1)
                pool.wait_ge(zeroed, 4)
                nw.ones_gpsimd(pool)
                pool.wait_ge(nw.ones_ready, 4)
                pool.wait_ge(const_in, 48)
                pool.tensor_copy(causal[:, :].rearrange("p (h k) -> p h k", k=SEQ),
                                 mask32[:, :].rearrange("p (a k) -> p a k", a=1).to_broadcast([P, 8, SEQ])
                                 ).then_inc(mask_ready, 1)
                for n in range(QUADS):
                    cols = slice(n * QUAD, (n + 1) * QUAD)
                    pool.wait_ge(q_sin, n + 1)
                    pool.tensor_tensor(nw.q[:, cols], nw.q[:, cols], turned_q[:, :], ALU.add).then_inc(
                        q_ready, 1)
                    pool.wait_ge(k_sin, n + 1)
                    pool.tensor_tensor(nw.k[:, cols], nw.k[:, cols], turned_k[:, :], ALU.add).then_inc(
                        k_ready, 1)

            @block.tensor
            def _(pe):
                for n in range(QUADS):
                    tr.tensor(pe, n)
                pe.wait_ge(w_ready, 9)
                pe.wait_ge(tr.ready, QUADS)

                def latents(n):
                    cols = slice(n * QUAD, (n + 1) * QUAD)
                    after(pe, lat_ready, n)
                    pe.matmul(k.ps[0][0:L2, 0, :], w["qd"], tr.xnT[:, cols], start=True, stop=True)
                    pe.matmul(k.ps[0][0:L2, 1, :], w["kvd"], tr.xnT[:, cols], start=True,
                              stop=True).then_inc(lat_done, 1)

                latents(0)
                for n in range(QUADS):
                    cols = slice(n * QUAD, (n + 1) * QUAD)
                    if n + 1 < QUADS:
                        latents(n + 1)
                    pe.wait_ge(lat_ready, n + 1)
                    ql, kvl = lat[n % 2][:, 0, :], lat[n % 2][:, 1, :]
                    after(pe, q_sin, n)
                    pe.matmul(k.ps[1][:, 0, :], q_w[:, :], ql, start=True, stop=True)
                    pe.matmul(k.ps[1][:, 1, :], q_rot[:, :], ql, start=True, stop=True).then_inc(q_done, 1)
                    after(pe, k_sin, n)
                    pe.matmul(k.ps[2][:, 0, :], k_w[:, :], kvl, start=True, stop=False)
                    pe.matmul(k.ps[2][:, 0, :], kx_w[:, :], tr.xnT[:, cols], start=False, stop=True)
                    pe.matmul(k.ps[2][:, 1, :], kx_rot[:, :], tr.xnT[:, cols], start=True,
                              stop=True).then_inc(k_done, 1)
                    for j in range(2):
                        after(pe, v_ready, 2 * n + j - 1)
                        for i in range(4):
                            at = (4 * j + i) * SEQ
                            for half_at in range(2):
                                last = pe.matmul((k.r6, k.r7)[j][half_at * SEQ:(half_at + 1) * SEQ,
                                                                 i * D:(i + 1) * D],
                                                 lat[n % 2][:, 1, at:at + SEQ], w["vu"], start=True,
                                                 stop=True)
                        last.then_inc(v_done, 1)

            @block.scalar
            def _(act):
                norm_root_scalar(act, k, tr.norm, rms=True)
                act.wait_ge(k.load_odd, loaded)
                for n in range(QUADS):
                    tr.scalar(act, n)
                for n in range(QUADS):
                    act.wait_ge(lat_done, n + 1)
                    after(act, v_done, 2 * n - 2)
                    act.copy(lat[n % 2][:, :, :], k.ps[0][0:L2, :, :]).then_inc(lat_ready, 1)

            @block.vector
            def _(dve):
                dve.wait_ge(k.load_odd, loaded)
                dve.wait_ge(zeroed, 4)
                dve.tensor_copy(q_w[:, 0:64], w["qu"]).then_inc(w_ready, 1)
                dve.tensor_copy(q_w[:, 64:D], w["ropeq"]).then_inc(w_ready, 1)
                dve.tensor_copy(k_w[:, 0:64], w["ku"]).then_inc(w_ready, 1)
                dve.tensor_copy(kx_w[:, 64:D], w["ropek"]).then_inc(w_ready, 1)
                for src, out in ((w["ropeq"], q_rot), (w["ropek"], kx_rot)):
                    sv = src.rearrange("p (h j) -> p h j", j=HH)
                    ov = out[:, 64:D].rearrange("p (h j) -> p h j", j=HH)
                    dve.tensor_scalar(ov[:, :, 0:2], sv[:, :, 2:4], -1.0, None, ALU.mult).then_inc(w_ready, 1)
                    dve.tensor_copy(ov[:, :, 2:4], sv[:, :, 0:2]).then_inc(w_ready, 1)
                dve.sem_inc(w_ready, 1)
                tr.vector(dve)
                dve.wait_ge(const_in, 48)
                dve.wait_ge(nw.masks_in, 32)

                def table(t):
                    return t[:, :].rearrange("p (a n) -> p a n", a=1).to_broadcast([P, QUAD // SEQ, SEQ])

                def items(ap):
                    return ap.rearrange("p (b n) -> p b n", n=SEQ)

                for n in range(QUADS):
                    cols = slice(n * QUAD, (n + 1) * QUAD)
                    for bank, out, tmp, done, c_sem, s_sem, ready in (
                            (k.ps[1], nw.q, turned_q, q_done, q_cos, q_sin, q_ready),
                            (k.ps[2], nw.k, turned_k, k_done, k_cos, k_sin, k_ready)):
                        dve.wait_ge(done, n + 1)
                        dve.tensor_tensor(items(out[:, cols]), items(bank[:, 0, :]), table(cos),
                                          ALU.mult).then_inc(c_sem, 1)
                        after(dve, ready, n)
                        dve.tensor_tensor(items(tmp[:, :]), items(bank[:, 1, :]), table(sin),
                                          ALU.mult).then_inc(s_sem, 1)
                    for j in range(2):
                        dve.wait_ge(v_done, 2 * n + j + 1)
                        nw.values_vector(dve, 2 * n + j, (k.r6, k.r7)[j][:, :]).then_inc(v_ready, 1)

        narrow_attention(k, "mlaa", nw, w["o"], None, causal[:, :], load_next)


def experts2(k, load_next):
    nc = k.nc
    up, down, w = ffn2_weights(k)
    with ExitStack() as ctx:
        tr = Turned(k, ctx, "l2f", rms=True, weight=w["ln2"])
        ro = Router(k, ctx, "l2f", E2)
        ex = Experts(k, ctx, "l2f", tr.xnT, 8, up, down, True, weight=ro.weight)
        block = ctx.enter_context(nc.Block())

        @block.sync
        def _(sp):
            load_next(sp)

        @block.tensor
        def _(pe):
            for n in range(QUADS):
                tr.tensor(pe, n)
            pe.wait_ge(tr.ready, QUADS)
            ro.tensor(pe, tr.xnT, w["router"][:, 0:E2], w["bias"][:, 0:E2])
            pe.wait_ge(ro.ready, 1)
            ex.tensor(pe)

        @block.scalar
        def _(act):
            norm_root_scalar(act, k, tr.norm, rms=True)
            for n in range(QUADS):
                tr.scalar(act, n)
            act.wait_ge(ro.ready, 1)
            act.activation(ro.soft[:, :, :], ro.score[:, :, :], ACT.Sigmoid).then_inc(ro.soft_ready, 1)
            ex.scalar(act)

        @block.vector
        def _(dve):
            tr.vector(dve)
            link = linked(dve, ro.step)
            dve.wait_ge(ro.scored, 1)
            dve.wait_ge(ro.index_ready, 1)
            dve.tensor_copy(ro.score[:, :, :], ro.bank()).then_inc(ro.ready, 1)
            dve.wait_ge(ro.soft_ready, 1)
            ro.first_top(dve, link, ro.soft[:, :, :], 0)
            link(dve.scalar_tensor_tensor(ro.score[:, :, :], ro.hot[0][:, :, :], -2.0, ro.soft[:, :, :],
                                          ALU.mult, ALU.add))
            ro.first_top(dve, link, ro.score[:, :, :], 1)
            link(dve.tensor_tensor(ro.first[:, :], ro.top[0][:, :], ro.top[1][:, :], ALU.add))
            link(dve.reciprocal(ro.first[:, :], ro.first[:, :]))
            for n in range(2):
                link(dve.tensor_tensor(ro.hot[n][:, :, :], ro.hot[n][:, :, :],
                                       spread(ro.top[n][:, :], E2), ALU.mult))
            link(dve.tensor_tensor(ro.hot[0][:, :, :], ro.hot[0][:, :, :], ro.hot[1][:, :, :], ALU.add))
            weight = ro.weight[:, :].rearrange("p (t e) -> p t e", e=8)
            link(dve.tensor_tensor(weight[:, :, 0:E2], ro.hot[0][:, :, :], spread(ro.first[:, :], E2),
                                   ALU.mult))
            link(dve.memset(weight[:, :, E2:8], 1.0))
            ex.vector(dve)

        @block.gpsimd
        def _(pool):
            ro.gpsimd(pool)


def ffn2(k, load_next):
    nc, x = k.nc, k.x
    y = k.ctx2[:, :, :].rearrange("p b c -> p (b c)")[:, 0:TILES * D].rearrange("p (t d) -> p t d", d=D)
    with ExitStack() as ctx:
        norm = NormSems(nc, ctx, "l2n")
        y_ready = Signals.new(nc, "l2n_y_ready")
        stats_done = Signals.new(nc, "l2n_stats_done")
        block = ctx.enter_context(nc.Block())

        @block.scalar
        def _(act):
            norm_root_scalar(act, k, norm)

        @block.vector
        def _(dve):
            norm_stats_vector(dve, k, norm)
            for t in range(TILES):
                normalise(dve, k, y[:, t:t + 1, :], t).then_inc(y_ready, 1)
            for t in range(TILES):
                dve.wait_ge(y_ready, t + 1)
                dve.bn_stats(k.stats[:, t, :], y[:, t, :]).then_inc(stats_done, 1)

    k.x = y
    latent_attention(k, load_next)
    experts2(k, lambda sp: None)
    k.x = x
    with ExitStack() as ctx:
        updated = Signals.new(nc, "l2e_updated")
        stats_done = Signals.new(nc, "l2e_stats_done")
        ctx2_in = Signals.new(nc, "l2e_ctx2_in")
        block = ctx.enter_context(nc.Block())

        @block.vector
        def _(dve):
            for n in range(QUADS):
                tiles = slice(4 * n, 4 * n + 4)
                dve.tensor_tensor(x[:, tiles, :], x[:, tiles, :], y[:, tiles, :], ALU.add).then_inc(updated, 1)
            for n in range(QUADS):
                dve.wait_ge(updated, n + 1)
                for j in range(4):
                    last = dve.bn_stats(k.stats[:, 4 * n + j, :], x[:, 4 * n + j, :])
                last.then_inc(stats_done, 1)

        @block.sync
        def _(sp):
            sp.wait_ge(updated, QUADS)
            load_ctx2(sp, k, ctx2_in)
            sp.wait_ge(ctx2_in, 32)


def shape_constants():
    import numpy as np

    feature = np.arange(P)
    head = np.arange(H)
    own8 = (feature[:, None] // (D // H) == head).astype(np.float32)
    own4 = ((feature[:, None] % 64) // HH == head).astype(np.float32)
    position = np.arange(SEQ, dtype=np.float32)
    freq = (np.float32(1.0) / np.float32(10000.0) ** (np.arange(0, HH, 2, dtype=np.float32) / np.float32(HH)))
    angle = np.einsum("i,j->ji", position, np.concatenate([freq, freq]).astype(np.float32))
    cos, sin = np.ones((P, SEQ), np.float32), np.zeros((P, SEQ), np.float32)
    cos[64:], sin[64:] = np.tile(np.cos(angle), (H, 1)), np.tile(np.sin(angle), (H, 1))
    query = feature[:, None] % SEQ
    causal = np.where(np.arange(SEQ)[None, :] <= query, 0.0, -1e30).astype(np.float32)
    cross = np.where(feature[:, None] // SEQ == feature[None, :] // SEQ, 0.0, -1e30).astype(np.float32)
    parity = (np.arange(16)[None, :] // 8 == feature[:, None] // SEQ).astype(np.float32)
    return {"const_cross": cross, "const_parity": parity, "const_own8": own8, "const_own4": own4, "const_cos": cos, "const_sin": sin,
            "const_causal": causal}



def load_ctx2(sp, k, sem):
    for par in range(2):
        sp.dma_start(k.ctx2[par * SEQ:(par + 1) * SEQ, :, :],
                     k.dram["ctx_768"].rearrange("b s c -> s b c")).then_inc(sem, 16)


def start(k, load_next):
    nc = k.nc
    d = k.dram
    with ExitStack() as ctx:
        def sem(name):
            return Signals.new(nc, name)

        consts, ones_at, zeros_at = sem("consts_ready"), sem("ones_ready"), sem("zeros_ready")
        x_in, ctx_in, ctxT_done, ctxT_ready = sem("x_in"), sem("ctx_in"), sem("ctxT_done"), sem("ctxT_ready")
        stats0 = sem("stats0")
        k.start_stats = stats0
        block = ctx.enter_context(nc.Block())
        HALF = TILES // 2

        @block.sync
        def _(sp):
            load_ctx2(sp, k, ctx_in)
            xv = d["x"].rearrange("b s d -> (b s) d").rearrange("(t p) d -> p t d", p=P)
            for j in range(2):
                sp.dma_start(k.x[:, j * HALF:(j + 1) * HALF, :],
                             xv[:, j * HALF:(j + 1) * HALF, :]).then_inc(x_in, 16)
            load_next(sp)
            sp.wait_ge(ctx_in, 32)

        @block.gpsimd
        def _(pool):
            pool.memset(k.ident[:, :], 0.0).then_inc(zeros_at, 1)
            pool.memset(k.ones[:, :], 1.0).then_inc(ones_at, 1)
            pool.memset(k.eps[:, :], LN_EPS).then_inc(ones_at, 1)
            pool.wait_ge(ones_at, 2)
            pool.wait_ge(zeros_at, 1)
            pool.memset(k.ctxT[C:C + 1, :], 1.0).then_inc(ones_at, 1)
            pool.wait_ge(ones_at, 3)
            pool.affine_select(out=k.ident[:, :], in_=k.ident[:, :], compare_op=ALU.not_equal, fill=1.0,
                               base=0, pattern=[[-1, P]], channel_multiplier=1).then_inc(consts, 1)
            pool.wait_ge(consts, 1)
            pool.tensor_copy(k.identb[:, :], k.ident[:, :]).then_inc(consts, 1)

        @block.tensor
        def _(pe):
            pe.wait_ge(consts, 1)
            pe.wait_ge(ctx_in, 32)
            for n in range(BATCH // 8):
                after(pe, ctxT_ready, n - 1)
                for j in range(8):
                    last = pe.transpose(k.ps[0][0:C, n % 2, j * SEQ:(j + 1) * SEQ],
                                        k.ctx2[0:SEQ, 8 * n + j, :], k.ident[0:SEQ, 0:SEQ])
                last.then_inc(ctxT_done, 1)

        @block.scalar
        def _(act):
            for n in range(BATCH // 8):
                act.wait_ge(ctxT_done, n + 1)
                act.copy(k.ctxT[0:C, n * 512:(n + 1) * 512], k.ps[0][0:C, n % 2, :]).then_inc(ctxT_ready, 1)

        @block.vector
        def _(dve):
            dve.wait_ge(x_in, 32)
            with dve.Fori(0, TRIPS) as i:
                for s in range(UNROLL):
                    t = i * UNROLL + s
                    dve.bn_stats(k.stats[:, bass.ds(t, 1), :].rearrange("p a d -> p (a d)"),
                                 k.x[:, bass.ds(t, 1), :].rearrange("p a d -> p (a d)")).then_inc(stats0, 1)


def finish(k, out):
    with ExitStack() as ctx:
        out_done = Signals.new(k.nc, "out_done")
        block = ctx.enter_context(k.nc.Block())

        @block.sync
        def _(sp):
            ov = out.rearrange("b s d -> (b s) d").rearrange("(t p) d -> p t d", p=P)
            sp.wait_ge(k.load_even, k.loads["even"]) if k.loads["even"] else None
            sp.wait_ge(k.load_odd, k.loads["odd"]) if k.loads["odd"] else None
            sp.dma_start(ov, k.x[:, :, :]).then_inc(out_done, 16)
            sp.wait_ge(out_done, 16)


def four_layers(nc, dram, out, upto=8, only=0):
    with ExitStack() as ctx:
        Signals.live = []
        k = Core(nc, ctx, dram)
        nothing = lambda sp: None
        layers = [
            (lambda n: wide_attention(k, "l0x", "L0_xattn_", n), lambda sp: load_wide(sp, k, "L0_xattn_")),
            (lambda n: ffn0(k, n), lambda sp: load_ffn0(sp, k)),
            (lambda n: attention1(k, n), lambda sp: load_attention1(sp, k)),
            (lambda n: ffn1(k, n), lambda sp: load_ffn1(sp, k)),
            (lambda n: attention2(k, n), lambda sp: load_attention2(sp, k)),
            (lambda n: ffn2(k, n), lambda sp: load_ffn2(sp, k)),
            (lambda n: wide_attention(k, "l3x", "L3_xattn_", n), lambda sp: load_wide(sp, k, "L3_xattn_")),
            (lambda n: ffn3(k, out), lambda sp: load_ffn3(sp, k)),
        ]
        start(k, layers[only][1] if upto else nothing)
        for i in range(only, upto):
            Signals.retire(nc)
            layers[i][0](layers[i + 1][1] if i + 1 < upto else nothing)
        if upto < 8:
            finish(k, out)



def kernel(**inputs):
    import numpy as np
    import concourse.bacc as bacc
    from concourse.bass_utils import run_bass_kernel_spmd

    nc = bacc.Bacc("TRN2", target_bir_lowering=False, num_devices=1)
    arrays, dram = {}, {}
    for name, value in {**inputs, **shape_constants()}.items():
        a = np.ascontiguousarray(value)
        arrays[f"in_{name}"] = a
        dram[name] = nc.dram_tensor(f"in_{name}", a.shape, mybir.dt.from_np(a.dtype),
                                    kind="ExternalInput").ap()
    out = nc.dram_tensor("out_x", inputs["x"].shape, F32, kind="ExternalOutput").ap()
    four_layers(nc, dram, out)
    r = run_bass_kernel_spmd(nc, [arrays], core_ids=[0])
    return r.results[0]["out_x"]
```

```python
from contextlib import ExitStack

import concourse.bass as bass
from concourse import mybir

F32 = mybir.dt.float32
BF16 = mybir.dt.bfloat16
ALU = mybir.AluOpType
ACT = mybir.ActivationFunctionType
AX = mybir.AxisListType
RMAX = bass.bass_isa.ReduceOp.max

P = 128
D = 128
C = 96
BATCH, SEQ = 64, 64
TOK = BATCH * SEQ
TILES = TOK // P
H = 16
GT = 2 * P
GROUPS = TOK // GT
UNROLL = 4
TRIPS = TILES // UNROLL
LN_EPS = 1e-5


class Signals:

    live = []

    @classmethod
    def new(cls, nc, name):
        sem = nc.alloc_semaphore(name)
        cls.live.append(sem)
        return sem

    @classmethod
    def retire(cls, nc):
        nc.all_engine_barrier()
        nc.clear_and_free_semaphores(cls.live)
        nc.all_engine_barrier()
        cls.live = []


def after(eng, sem, count):
    if not isinstance(count, int) or count > 0:
        eng.wait_ge(sem, count)


def over_tiles(eng, slot):
    for s in range(UNROLL):
        slot(s, s)
    with eng.Fori(1, TRIPS - 1) as i:
        for s in range(UNROLL):
            slot(i * UNROLL + s, s)
    for s in range(UNROLL):
        slot(TILES - UNROLL + s, s)


def is_last(t, n=1):
    return isinstance(t, int) and t >= TILES - n


class Core:

    def __init__(self, nc, ctx, dram):
        self.nc, self.dram = nc, dram

        def sb(name, shape, dt=F32):
            return ctx.enter_context(nc.sbuf_tensor(name, shape, dt))

        self.x = sb("x", [P, TILES, D])
        self.ctxT = sb("ctxT", [C + 1, TOK])
        self.ctx_peaks = sb("ctx_peaks", [P, BATCH // 8])
        self.spare = sb("spare", [P, BATCH * C])
        self.stats = sb("stats", [P, TILES, 6])
        self.mean = sb("mean", [P, TILES])
        self.var = sb("var", [P, TILES])
        self.rstd = sb("rstd", [P, TILES])
        self.tmp = sb("tmp", [P, TILES])
        self.tmp2 = sb("tmp2", [P, TILES])
        self.eps = sb("eps", [P, 1])
        self.ident = sb("ident", [P, P])
        self.identb = sb("identb", [P, P], BF16)
        self.ones = sb("ones", [P, P])
        self.even_words, self.odd_words = 4096 + 256, 8704 + 256
        self.even = sb("even", [P, self.even_words])
        self.odd = sb("odd", [P, self.odd_words])
        self.ps = [ctx.enter_context(nc.psum_tensor(f"bank{2 * i}_{2 * i + 1}", [P, 2, 512], F32))
                   for i in range(3)]
        self.r6 = ctx.enter_context(nc.psum_tensor("bank6", [P, 512], F32))
        self.r7 = ctx.enter_context(nc.psum_tensor("bank7", [P, 512], F32))
        self.load_even = ctx.enter_context(nc.semaphore("load_even"))
        self.load_odd = ctx.enter_context(nc.semaphore("load_odd"))
        self.loads = {"even": 0, "odd": 0}

    def load(self, eng, side, out, in_):
        sem = self.load_even if side == "even" else self.load_odd
        self.loads[side] += 16
        eng.dma_start(out, in_).then_inc(sem, 16)


def add_bias(pool, k, bias, t, n):
    xt = k.x[:, bass.ds(t, n), :]
    return pool.tensor_tensor(xt, xt, bias.rearrange("p (a d) -> p a d", a=1).to_broadcast([P, n, D]), ALU.add)


def row(ap, n):
    return ap.rearrange("(a n) -> a n", a=1)



class NormSems:
    def __init__(self, nc, ctx, tag):
        self.chain = Signals.new(nc, f"{tag}_stat_step")
        self.root = Signals.new(nc, f"{tag}_root_ready")
        self.ready = Signals.new(nc, f"{tag}_rstd_ready")


def norm_stats_vector(dve, k, n, rms=False):
    me, mo = k.stats[:, :, 1], k.stats[:, :, 4]
    step = 0

    def link(ins):
        nonlocal step
        step += 1
        ins.then_inc(n.chain, 1)
        dve.wait_ge(n.chain, step)

    link(dve.tensor_tensor(k.mean[:, :], me, mo, ALU.add))
    link(dve.tensor_tensor(k.tmp[:, :], me, mo, ALU.subtract))
    link(dve.tensor_scalar(k.mean[:, :], k.mean[:, :], 0.5, None, ALU.mult))
    link(dve.tensor_tensor(k.tmp[:, :], k.tmp[:, :], k.tmp[:, :], ALU.mult))
    link(dve.tensor_tensor(k.var[:, :], k.stats[:, :, 2], k.stats[:, :, 5], ALU.add))
    link(dve.tensor_scalar(k.tmp[:, :], k.tmp[:, :], 0.25, None, ALU.mult))
    if rms:
        link(dve.scalar_tensor_tensor(k.var[:, :], k.var[:, :], 1.0 / D, k.tmp[:, :], ALU.mult, ALU.add))
        link(dve.tensor_tensor(k.tmp[:, :], k.mean[:, :], k.mean[:, :], ALU.mult))
        dve.tensor_tensor(k.var[:, :], k.var[:, :], k.tmp[:, :], ALU.add).then_inc(n.chain, 1)
        dve.wait_ge(n.root, 1)
        link_at = step + 1
        dve.tensor_scalar(k.tmp[:, :], k.tmp2[:, :], LN_EPS, None, ALU.add).then_inc(n.chain, 1)
        dve.wait_ge(n.chain, link_at + 1)
        dve.reciprocal(k.rstd[:, :], k.tmp[:, :]).then_inc(n.ready, 1)
    else:
        dve.scalar_tensor_tensor(k.var[:, :], k.var[:, :], 1.0 / D, k.tmp[:, :], ALU.mult,
                                 ALU.add).then_inc(n.chain, 1)
        dve.wait_ge(n.root, 1)
        dve.reciprocal(k.rstd[:, :], k.tmp2[:, :]).then_inc(n.ready, 1)
    dve.wait_ge(n.ready, 1)


NORM_STEPS, RMS_STEPS = 7, 9


def norm_root_scalar(act, k, n, rms=False):
    act.wait_ge(n.chain, RMS_STEPS if rms else NORM_STEPS)
    act.activation(k.tmp2[:, :], k.var[:, :], ACT.Sqrt,
                   bias=0.0 if rms else k.eps[:, 0:1]).then_inc(n.root, 1)


def normalise(dve, k, out, t):
    return dve.tensor_scalar(out, k.x[:, bass.ds(t, 1), :], k.mean[:, bass.ds(t, 1)],
                             k.rstd[:, bass.ds(t, 1)], ALU.subtract, ALU.mult)



class Attention:

    def __init__(self, k, ctx, tag, scale):
        nc = k.nc
        self.k, self.scale = k, scale

        def sb(name, shape, dt=F32):
            return ctx.enter_context(nc.sbuf_tensor(f"{tag}_{name}", shape, dt))

        def sem(name):
            return Signals.new(nc, f"{tag}_{name}")

        self.qh = [sb(f"qh{i}", [C, H, GT]) for i in range(2)]
        self.keys = [sb(f"keys{i}", [P, P]) for i in range(2)]
        self.values = [sb(f"values{i}", [P, 2, H // 2, D]) for i in range(2)]
        self.xn = [sb(f"xn{i}", [P, 2, D]) for i in range(2)]
        self.xnT = [sb(f"xnT{i}", [D, GT]) for i in range(2)]
        self.prob = [sb(f"prob{i}", [P, H, SEQ]) for i in range(2)]
        self.probT = sb("probT", [P, H // 2, P])
        self.top = [sb(f"top{i}", [P, H]) for i in range(2)]
        self.total = [sb(f"total{i}", [P, H]) for i in range(2)]
        self.share = [sb(f"share{i}", [P, H]) for i in range(2)]
        self.S, self.T, self.V = k.ps
        self.norm = NormSems(nc, ctx, tag)
        self.xn_ready = sem("xn_ready")
        self.xnT_done = sem("xnT_done")
        self.xnT_ready = sem("xnT_ready")
        self.keys_ready = sem("keys_ready")
        self.zeroed = sem("zeroed")
        self.values_done = sem("values_done")
        self.v0_ready = sem("v0_ready")
        self.v1_ready = sem("v1_ready")
        self.scores_done = sem("scores_done")
        self.top_ready = sem("top_ready")
        self.shifted = sem("shifted")
        self.exp_ready = sem("exp_ready")
        self.total_ready = sem("total_ready")
        self.share_ready = sem("share_ready")
        self.prob_ready = sem("prob_ready")
        self.turned = sem("turned")
        self.probT_ready = sem("probT_ready")
        self.weighed = sem("weighed")
        self.biased = sem("biased")
        self.updated = sem("updated")
        self.stats_done = sem("stats_done")
        self.q6_done, self.q7_done = sem("q6_done"), sem("q7_done")
        self.q6_ready, self.q7_ready = sem("q6_ready"), sem("q7_ready")


def half(u):
    return (u // 2) % 2, u % 2


def scores_tensor(pe, a, u, s):
    g, tt = half(s)
    pe.wait_ge(a.keys_ready, u + 1)
    after(pe, a.shifted, u)
    for h in range(H):
        for b in range(2):
            last = pe.matmul(a.S[b * SEQ:(b + 1) * SEQ, h // 8, (h % 8) * SEQ:(h % 8 + 1) * SEQ],
                             a.qh[g][:, h, tt * P + b * SEQ:tt * P + (b + 1) * SEQ],
                             a.keys[s % 2][0:C, b * SEQ:(b + 1) * SEQ], start=True, stop=True)
    last.then_inc(a.scores_done, 1)


def turn_tensor(pe, a, t, s):
    pe.wait_ge(a.prob_ready, t + 1)
    after(pe, a.probT_ready, t)
    for p in range(H // 2):
        last = pe.transpose(a.T[:, p // 4, (p % 4) * P:(p % 4 + 1) * P],
                            a.prob[s % 2][:, 2 * p:2 * p + 2, :].rearrange("p h k -> p (h k)"),
                            a.k.ident[:, :])
    last.then_inc(a.turned, 1)


def values_tensor(pe, a, f, u, s, b):
    pe.wait_ge(a.keys_ready, u + 1)
    if b == 0:
        after(pe, a.v1_ready, u)
    else:
        pe.wait_ge(a.v0_ready, u + 1)
    w = f.w[:, :, :].rearrange("c (j p a) n -> c j p a n", j=2, a=2)
    for j in range(2):
        for par in range(2):
            last = pe.matmul(a.V[par * SEQ:(par + 1) * SEQ, j, :], a.keys[s % 2][:, b * SEQ:(b + 1) * SEQ],
                             w[:, j, :, par, :], start=True, stop=True)
    last.then_inc(a.values_done, 1)


def copy_values(copy, eng, a, u, s, b):
    eng.wait_ge(a.values_done, 2 * u + 1 + b)
    after(eng, a.weighed, u - 1)
    copy(a.values[s % 2][:, b, :, :], a.V[:, :, :].rearrange("p j (c n) -> p (j c) n", n=D)).then_inc(
        (a.v0_ready, a.v1_ready)[b], 1)


def weigh_tensor(pe, a, t, s):
    pe.wait_ge(a.probT_ready, t + 1)
    pe.wait_ge(a.v0_ready, t + 1)
    pe.wait_ge(a.v1_ready, t + 1)
    for p in range(H // 2):
        for b in range(2):
            rows = slice(b * SEQ, (b + 1) * SEQ)
            last = pe.matmul(a.k.r6[rows, 0:D], a.probT[:, p, rows], a.values[s % 2][:, b, p, :],
                             start=p == 0, stop=p == H // 2 - 1)
    last.then_inc(a.weighed, 1)


def turn_xn_tensor(pe, a, m, par):
    pe.wait_ge(a.xn_ready, m + 1)
    for j in range(2):
        last = pe.transpose(a.k.r7[:, j * P:(j + 1) * P], a.xn[par][:, j, :], a.k.ident[:, :])
    last.then_inc(a.xnT_done, 1)


def softmax_top_vector(dve, a, u, s):
    dve.wait_ge(a.scores_done, u + 1)
    scores = a.S[:, :, :].rearrange("p a (h k) -> p (a h) k", k=SEQ)
    dve.tensor_reduce(a.top[s % 2][:, :], scores, AX.X, ALU.max).then_inc(a.top_ready, 1)
    dve.wait_ge(a.top_ready, u + 1)
    after(dve, a.turned, u - 1)
    dve.tensor_tensor(a.prob[s % 2][:, :, :], scores,
                      a.top[s % 2][:, :].rearrange("p (h a) -> p h a", a=1).to_broadcast([P, H, SEQ]),
                      ALU.subtract).then_inc(a.shifted, 1)


def softmax_exp_scalar(act, a, u, s):
    act.wait_ge(a.shifted, u + 1)
    act.activation(a.prob[s % 2][:, :, :], a.prob[s % 2][:, :, :], ACT.Exp,
                   scale=a.scale).then_inc(a.exp_ready, 1)


def softmax_total_vector(dve, a, u, s):
    dve.wait_ge(a.exp_ready, u + 1)
    dve.tensor_reduce(a.total[s % 2][:, :], a.prob[s % 2][:, :, :], AX.X,
                      ALU.add).then_inc(a.total_ready, 1)
    dve.wait_ge(a.total_ready, u + 1)
    after(dve, a.prob_ready, u - 1)
    dve.reciprocal(a.share[s % 2][:, :], a.total[s % 2][:, :]).then_inc(a.share_ready, 1)


def softmax_divide_gpsimd(pool, a, u, s):
    pool.wait_ge(a.share_ready, u + 1)
    pool.tensor_tensor(a.prob[s % 2][:, :, :], a.prob[s % 2][:, :, :],
                       a.share[s % 2][:, :].rearrange("p (h a) -> p h a", a=1).to_broadcast([P, H, SEQ]),
                       ALU.mult).then_inc(a.prob_ready, 1)


def copy_probT_scalar(act, a, t):
    act.wait_ge(a.turned, t + 1)
    after(act, a.weighed, t)
    act.copy(a.probT[:, :, :], a.T[:, :, :].rearrange("p a (c q) -> p (a c) q", q=P)).then_inc(
        a.probT_ready, 1)


def update_vector(dve, a, t):
    k = a.k
    dve.wait_ge(a.weighed, t + 1)
    dve.wait_ge(a.biased, t + 1)
    xt = k.x[:, bass.ds(t, 1), :].rearrange("p a d -> p (a d)")
    dve.tensor_tensor(xt, xt, k.r6[:, 0:D], ALU.add).then_inc(a.updated, 1)
    dve.wait_ge(a.updated, t + 1)
    dve.bn_stats(k.stats[:, bass.ds(t, 1), :].rearrange("p a d -> p (a d)"), xt).then_inc(a.stats_done, 1)


def normalise_group_vector(dve, a, m, par):
    after(dve, a.xnT_done, m - 1)
    for j in range(2):
        last = normalise(dve, a.k, a.xn[par][:, j:j + 1, :], m * 2 + j)
    last.then_inc(a.xn_ready, 1)


def copy_xnT_scalar(act, a, m, par, before=None):
    act.wait_ge(a.xnT_done, m + 1)
    if before is not None:
        after(act, *before)
    act.copy(a.xnT[par][:, :], a.k.r7[:, 0:GT]).then_inc(a.xnT_ready, 1)



DH = 64


class Folded:

    def __init__(self, k, ctx, tag):
        self.m = ctx.enter_context(k.nc.sbuf_tensor(f"{tag}_m", [D, H, C], F32))
        self.w = ctx.enter_context(k.nc.sbuf_tensor(f"{tag}_w", [P, H, D], F32))


class Fold:

    def __init__(self, k, ctx, tag, folded):
        self.k, self.folded = k, folded
        self.turned = [ctx.enter_context(k.nc.sbuf_tensor(f"{tag}_fold{i}", [P, D + 2 * C], F32))
                       for i in range(2)]
        self.turn_done = Signals.new(k.nc, f"{tag}_fold_turned")
        self.turn_ready = Signals.new(k.nc, f"{tag}_fold_copied")
        self.done = Signals.new(k.nc, f"{tag}_folded")
        self.ready = Signals.new(k.nc, f"{tag}_fold_ready")

    def tensor(self, pe):
        k = self.k
        wq, wk, wv, wo, _ = wide_weights(k)
        T = k.ps[0]

        def turn(p):
            after(pe, self.turn_ready, p - 1)
            cols = slice(p * P, (p + 1) * P)
            pe.transpose(T[:, p % 2, 0:D], wq[:, cols], k.ident[:, :])
            pe.transpose(T[:, p % 2, D:D + C], wk[:, cols], k.ident[0:C, 0:C])
            pe.transpose(T[:, p % 2, D + C:D + 2 * C], wv[:, cols], k.ident[0:C, 0:C]).then_inc(
                self.turn_done, 1)

        turn(0)
        for p in range(H // 2):
            if p + 1 < H // 2:
                turn(p + 1)
            pe.wait_ge(self.turn_ready, p + 1)
            after(pe, self.ready, p - 1)
            t, banks = self.turned[p % 2], k.ps[1 + p % 2]
            for par in range(2):
                rows = slice(par * DH, (par + 1) * DH)
                pe.matmul(banks[:, par, 0:C], t[rows, 0:D], t[rows, D:D + C], start=True, stop=True)
                last = pe.matmul(banks[0:C, par, P:P + D], t[rows, D + C:D + 2 * C], wo[rows, p, :],
                                 start=True, stop=True)
            last.then_inc(self.done, 1)

    def scalar(self, act):
        for p in range(H // 2):
            act.wait_ge(self.turn_done, p + 1)
            after(act, self.done, p - 1)
            act.copy(self.turned[p % 2][:, :], self.k.ps[0][:, p % 2, 0:D + 2 * C]).then_inc(
                self.turn_ready, 1)

    def vector(self, dve, p):
        dve.wait_ge(self.done, p + 1)
        banks, heads = self.k.ps[1 + p % 2], slice(2 * p, 2 * p + 2)
        dve.tensor_copy(self.folded.m[:, heads, :], banks[:, :, 0:C])
        dve.tensor_copy(self.folded.w[0:C, heads, :], banks[0:C, :, P:P + D]).then_inc(self.ready, 1)


def wide_weights(k):
    w = k.even
    return (w[:, 0:1024], w[0:C, 1024:2048], w[0:C, 2048:3072],
            w[:, 3072:4096].rearrange("p (c n) -> p c n", n=D), w[:, 4096:4096 + D])


def load_wide(sp, k, pre):
    wq, wk, wv, wo, bo = wide_weights(k)
    d = k.dram
    k.load(sp, "even", wq, d[f"{pre}Wq"])
    k.load(sp, "even", wk, d[f"{pre}Wk"])
    k.load(sp, "even", wv, d[f"{pre}Wv"])
    k.load(sp, "even", wo, d[f"{pre}Wo"].rearrange("(c p) n -> p c n", p=P))
    with k.nc.allow_non_contiguous_dma(reason="a bias, the same on every partition"):
        k.load(sp, "even", bo, d[f"{pre}bo"].partition_broadcast(P))


def wide_queries_tensor(pe, a, f, n, s, freed6, freed7):
    g, hh = half(s)
    pe.wait_ge(a.xnT_ready, (n + 2 - hh) // 2 if isinstance(n, int) else (n - hh) // 2 + 1)
    for j in range(4):
        bank = (a.k.r6, a.k.r7)[j % 2]
        if j == 0:
            after(pe, *freed6)
        elif j == 1:
            after(pe, *freed7)
        elif j == 2:
            pe.wait_ge(a.q6_ready, n * 2 + 1)
        else:
            pe.wait_ge(a.q7_ready, n * 2 + 1)
        for e in range(2):
            last = pe.matmul(bank[0:C, e * GT:(e + 1) * GT], f.m[:, 8 * hh + 2 * j + e, :],
                             a.xnT[g][:, :], start=True, stop=True)
        last.then_inc((a.q6_done, a.q7_done)[j % 2], 1)


def copy_queries(copy, eng, a, n, s, j, done, ready, used):
    g, hh = half(s)
    eng.wait_ge(done, n * 2 + 1 + j // 2)
    after(eng, *used)
    h = 8 * hh + 2 * j
    copy(a.qh[g][:, h:h + 2, :],
         (a.k.r6, a.k.r7)[j % 2][0:C, :].rearrange("c (e q) -> c e q", e=2)).then_inc(ready, 1)


LEAD = 3


def wide_attention(k, f, tag, load_next):
    nc = k.nc
    with ExitStack() as ctx:
        a = Attention(k, ctx, tag, float(DH) ** -0.5)
        bias = wide_weights(k)[4]
        block = ctx.enter_context(nc.Block())

        @block.sync
        def _(sp):
            load_next(sp)

        @block.tensor
        def _(pe):
            def first_steps():
                for m in range(2):
                    after(pe, a.xnT_ready, m)
                    turn_xn_tensor(pe, a, m, m)
                for n in range(LEAD):
                    if n == 2:
                        queries_ready(0)
                        scores_tensor(pe, a, 0, 0)
                    wide_queries_tensor(pe, a, f, n, n, (a.q6_ready, 2 * n),
                                        (a.q7_ready, 2 * n) if n else (a.xnT_ready, 2))

            def queries_ready(u):
                if isinstance(u, int):
                    u -= u % 2
                    pe.wait_ge(a.q6_ready, u * 2 + 4)
                    pe.wait_ge(a.q7_ready, u * 2 + 4)

            first_steps()
            pe.wait_ge(a.zeroed, 3)
            for b in range(2):
                values_tensor(pe, a, f, 0, 0, b)

            def slot(t, s):
                turn_tensor(pe, a, t, s)
                if not is_last(t):
                    if s % 2:
                        pe.wait_ge(a.q6_ready, t * 2 + 6)
                        pe.wait_ge(a.q7_ready, t * 2 + 6)
                    scores_tensor(pe, a, t + 1, (s + 1) % 4)
                    values_tensor(pe, a, f, t + 1, (s + 1) % 4, 0)
                if not is_last(t, LEAD):
                    wide_queries_tensor(pe, a, f, t + LEAD, (s + LEAD) % 4, (a.updated, t),
                                        (a.xnT_ready, (t + 5) // 2 if isinstance(t, int)
                                         else (t - 1) // 2 + 3) if s % 2 else (a.q7_ready, t * 2 + 6))
                if not is_last(t):
                    values_tensor(pe, a, f, t + 1, (s + 1) % 4, 1)
                if not is_last(t, LEAD):
                    pe.wait_ge(a.q6_ready, t * 2 + 8)
                else:
                    after(pe, a.updated, t)
                weigh_tensor(pe, a, t, s)
                if s % 2 == 0 and not is_last(t, 4):
                    pe.wait_ge(a.q7_ready, t * 2 + 8)
                    turn_xn_tensor(pe, a, t // 2 + 2, (s // 2) % 2)

            over_tiles(pe, slot)

        @block.scalar
        def _(act):
            norm_root_scalar(act, k, a.norm)
            for m in range(2):
                copy_xnT_scalar(act, a, m, m)
            for n in range(LEAD):
                for j in (0, 2):
                    copy_queries(act.copy, act, a, n, n, j, a.q6_done, a.q6_ready, (a.scores_done, 0))
                if n == 1:
                    softmax_exp_scalar(act, a, 0, 0)
            copy_values(act.copy, act, a, 0, 0, 0)

            def slot(t, s):
                copy_probT_scalar(act, a, t)
                if not is_last(t):
                    copy_values(act.copy, act, a, t + 1, (s + 1) % 4, 0)
                if not is_last(t, LEAD):
                    copy_queries(act.copy, act, a, t + LEAD, (s + LEAD) % 4, 0, a.q6_done, a.q6_ready,
                                 (a.scores_done, t))
                if not is_last(t):
                    softmax_exp_scalar(act, a, t + 1, (s + 1) % 4)
                if not is_last(t, LEAD):
                    copy_queries(act.copy, act, a, t + LEAD, (s + LEAD) % 4, 2, a.q6_done, a.q6_ready,
                                 (a.scores_done, t))
                    if s % 2 == 0 and not is_last(t, 4):
                        copy_xnT_scalar(act, a, t // 2 + 2, (s // 2) % 2)

            over_tiles(act, slot)

        @block.vector
        def _(dve):
            norm_stats_vector(dve, k, a.norm)
            for m in range(2):
                normalise_group_vector(dve, a, m, m)
            for n in range(LEAD):
                for j in (1, 3):
                    copy_queries(dve.tensor_copy, dve, a, n, n, j, a.q7_done, a.q7_ready, (a.scores_done, 0))
                if n == 1:
                    softmax_top_vector(dve, a, 0, 0)
            softmax_total_vector(dve, a, 0, 0)
            copy_values(dve.tensor_copy, dve, a, 0, 0, 1)

            def slot(t, s):
                if s % 2 == 0 and not is_last(t, 4):
                    normalise_group_vector(dve, a, t // 2 + 2, (s // 2) % 2)
                if not is_last(t):
                    softmax_top_vector(dve, a, t + 1, (s + 1) % 4)
                more = not is_last(t, LEAD)
                if more:
                    copy_queries(dve.tensor_copy, dve, a, t + LEAD, (s + LEAD) % 4, 1, a.q7_done,
                                 a.q7_ready, (a.scores_done, t))
                if not is_last(t):
                    softmax_total_vector(dve, a, t + 1, (s + 1) % 4)
                if more:
                    copy_queries(dve.tensor_copy, dve, a, t + LEAD, (s + LEAD) % 4, 3, a.q7_done,
                                 a.q7_ready, (a.scores_done, t))
                if not is_last(t):
                    copy_values(dve.tensor_copy, dve, a, t + 1, (s + 1) % 4, 1)
                update_vector(dve, a, t)

            over_tiles(dve, slot)

        @block.gpsimd
        def _(pool):
            for i, rows in enumerate((a.keys[0][:, :], a.keys[1][:, :], f.w[C:P, :, :])):
                pool.memset(rows, 0.0).then_inc(a.zeroed, 1)
                pool.wait_ge(a.zeroed, i + 1)

            def keys(u, s):
                after(pool, a.scores_done, u - 1)
                after(pool, a.values_done, 2 * u - 2)
                pool.tensor_copy(a.keys[s % 2][0:C, :], k.ctxT[0:C, bass.ds(u * P, P)]).then_inc(
                    a.keys_ready, 1)

            for u in range(2):
                keys(u, u)
            softmax_divide_gpsimd(pool, a, 0, 0)

            def slot(t, s):
                if not is_last(t):
                    softmax_divide_gpsimd(pool, a, t + 1, (s + 1) % 4)
                pool.wait_ge(a.xn_ready, (t - s % 2) // 2 + 1)
                add_bias(pool, k, bias, t, 1).then_inc(a.biased, 1)
                if not is_last(t, 2):
                    keys(t + 2, (s + 2) % 4)

            over_tiles(pool, slot)



QUAD = 4 * P
QUADS = TOK // QUAD


def linked(eng, sem):
    count = [0]

    def link(ins):
        count[0] += 1
        ins.then_inc(sem, 1)
        eng.wait_ge(sem, count[0])
    return link


def spread(ap, n):
    return ap.rearrange("p (a o) -> p a o", o=1).to_broadcast([ap.shape[0], ap.shape[1], n])


class Turned:

    def __init__(self, k, ctx, tag, rms=False, weight=None, xnT=None, xn_all=None):
        def sb(name, shape):
            return ctx.enter_context(k.nc.sbuf_tensor(f"{tag}_{name}", shape, F32))

        def sem(name):
            return Signals.new(k.nc, f"{tag}_{name}")

        self.k, self.rms, self.weight = k, rms, weight
        self.xnT = sb("xnT", [D, TOK]) if xnT is None else xnT
        self.groups = 2 if xn_all is None else QUADS
        self.xn = [sb(f"xn{i}", [P, 4, D]) for i in range(2)] if xn_all is None else [
            xn_all[:, 4 * n:4 * n + 4, :] for n in range(QUADS)]
        self.norm = NormSems(k.nc, ctx, tag)
        self.xn_ready = sem("xn_ready")
        self.turned = sem("turned")
        self.ready = sem("xnT_ready")

    def vector(self, dve):
        k = self.k
        norm_stats_vector(dve, k, self.norm, self.rms)
        for n in range(QUADS):
            if self.groups == 2:
                after(dve, self.turned, n - 1)
            for j in range(4):
                if self.rms:
                    last = dve.tensor_scalar(self.xn[n % self.groups][:, j, :], k.x[:, 4 * n + j, :],
                                             k.rstd[:, 4 * n + j:4 * n + j + 1], None, ALU.mult)
                else:
                    last = normalise(dve, k, self.xn[n % self.groups][:, j:j + 1, :], 4 * n + j)
            last.then_inc(self.xn_ready, 1)

    def tensor(self, pe, n):
        pe.wait_ge(self.xn_ready, n + 1)
        after(pe, self.ready, n - 1)
        bank = (self.k.r6, self.k.r7)[n % 2]
        for j in range(4):
            last = pe.transpose(bank[:, j * P:(j + 1) * P], self.xn[n % self.groups][:, j, :],
                                self.k.ident[:, :])
        last.then_inc(self.turned, 1)

    def scalar(self, act, n):
        act.wait_ge(self.turned, n + 1)
        out, bank = self.xnT[:, n * QUAD:(n + 1) * QUAD], (self.k.r6, self.k.r7)[n % 2]
        if self.weight is None:
            ins = act.copy(out, bank[:, :])
        else:
            ins = act.activation(out, bank[:, :], ACT.Copy, scale=self.weight)
        ins.then_inc(self.ready, 1)



F0, E0 = 352, 8
CHUNKS0 = [(0, 128), (128, 128), (256, 96)]


def ffn0_weights(k):
    w = k.odd
    n = E0 * F0
    return (w[:, 0:n].rearrange("p (e f) -> p e f", e=E0),
            w[:, n:2 * n].rearrange("p (e f) -> p e f", e=E0),
            w[:, 2 * n:2 * n + E0 * 3 * D].rearrange("p (e c n) -> p e c n", e=E0, c=3))


def load_ffn0(sp, k):
    w1, w3, w2 = ffn0_weights(k)
    d = k.dram
    k.load(sp, "odd", w1, d["L0_ffn_w1"].rearrange("e d f -> d e f"))
    k.load(sp, "odd", w3, d["L0_ffn_w3"].rearrange("e d f -> d e f"))
    for c, (at, n) in enumerate(CHUNKS0):
        k.load(sp, "odd", w2[0:n, :, c, :], d["L0_ffn_w2"][:, at:at + n, :].rearrange("e f d -> f e d"))


def ffn0(k, load_next):
    nc = k.nc
    with ExitStack() as ctx:
        def sb(name, shape):
            return ctx.enter_context(nc.sbuf_tensor(f"l0f_{name}", shape, F32))

        def sem(name):
            return Signals.new(nc, f"l0f_{name}")

        tr = Turned(k, ctx, "l0f")
        w1, w3, w2 = ffn0_weights(k)
        gated = [sb(f"gated{i}", [P, QUAD]) for i in range(2)]
        hidden = [sb(f"hidden{i}", [P, QUAD]) for i in range(2)]
        gate_done, up_done = sem("gate_done"), sem("up_done")
        gated_ready, hidden_ready = sem("gated_ready"), sem("hidden_ready")
        down_done, down_ready = sem("down_done"), sem("down_ready")
        back_done, updated, stats_done = sem("back_done"), sem("updated"), sem("stats_done")
        gate_banks, up_banks, down_banks = k.ps
        units = [(e, c) for e in range(E0) for c in range(3)]
        loaded = k.loads["odd"]

        def tokens(e):
            return tr.xnT[:, :].rearrange("p (b e c) -> p b e c", e=E0, c=SEQ // E0)[:, :, e, :]

        block = ctx.enter_context(nc.Block())

        @block.sync
        def _(sp):
            load_next(sp)

        @block.tensor
        def _(pe):
            for n in range(QUADS):
                tr.tensor(pe, n)
            pe.wait_ge(k.load_odd, loaded)
            pe.wait_ge(tr.ready, QUADS)

            def up(v):
                e, c = units[v]
                at, n = CHUNKS0[c]
                after(pe, gated_ready, v - 1)
                after(pe, hidden_ready, v - 1)
                pe.matmul(gate_banks[0:n, v % 2, :], w1[:, e, at:at + n], tokens(e), start=True,
                          stop=True).then_inc(gate_done, 1)
                pe.matmul(up_banks[0:n, v % 2, :], w3[:, e, at:at + n], tokens(e), start=True,
                          stop=True).then_inc(up_done, 1)

            up(0)
            for v, (e, c) in enumerate(units):
                if v + 1 < len(units):
                    up(v + 1)
                n = CHUNKS0[c][1]
                pe.wait_ge(hidden_ready, v + 1)
                if c == 0:
                    after(pe, down_ready, e - 1)
                last = pe.matmul(down_banks[:, e % 2, :], w2[0:n, e, c, :], hidden[v % 2][0:n, :],
                                 start=c == 0, stop=c == 2)
                if c == 2:
                    last.then_inc(down_done, 1)
            pe.wait_ge(down_ready, E0)
            for n in range(QUADS):
                after(pe, updated, n - 1)
                for j in range(4):
                    at = n * QUAD + j * P
                    last = pe.transpose((k.r6, k.r7)[n % 2][:, j * P:(j + 1) * P],
                                        tr.xnT[:, at:at + P], k.ident[:, :])
                last.then_inc(back_done, 1)

        @block.scalar
        def _(act):
            norm_root_scalar(act, k, tr.norm)
            for n in range(QUADS):
                tr.scalar(act, n)
            for v, (e, c) in enumerate(units):
                n = CHUNKS0[c][1]
                act.wait_ge(gate_done, v + 1)
                after(act, hidden_ready, v - 1)
                act.activation(gated[v % 2][0:n, :], gate_banks[0:n, v % 2, :], ACT.Silu).then_inc(
                    gated_ready, 1)
                if c == 2:
                    act.wait_ge(down_done, e + 1)
                    act.copy(tokens(e), down_banks[:, e % 2, :].rearrange("p (b c) -> p b c", c=SEQ // E0)
                             ).then_inc(down_ready, 1)

        @block.vector
        def _(dve):
            tr.vector(dve)
            for v, (e, c) in enumerate(units):
                n = CHUNKS0[c][1]
                dve.wait_ge(gated_ready, v + 1)
                dve.wait_ge(up_done, v + 1)
                dve.tensor_tensor(hidden[v % 2][0:n, :], gated[v % 2][0:n, :], up_banks[0:n, v % 2, :],
                                  ALU.mult).then_inc(hidden_ready, 1)
            for n in range(QUADS):
                dve.wait_ge(back_done, n + 1)
                xq = k.x[:, 4 * n:4 * n + 4, :].rearrange("p a d -> p (a d)")
                dve.tensor_tensor(xq, xq, (k.r6, k.r7)[n % 2][:, :], ALU.add).then_inc(updated, 1)
                dve.wait_ge(updated, n + 1)
                for j in range(4):
                    last = dve.bn_stats(k.stats[:, 4 * n + j, :], k.x[:, 4 * n + j, :])
                last.then_inc(stats_done, 1)



class Experts:

    def __init__(self, k, ctx, tag, xnT, experts, up, down, gated, bias1=None, biased=None, weight=None):
        def sb(name, shape):
            return ctx.enter_context(k.nc.sbuf_tensor(f"{tag}_{name}", shape, F32))

        def sem(name):
            return Signals.new(k.nc, f"{tag}_{name}")

        self.k, self.xnT, self.experts, self.up, self.down = k, xnT, experts, up, down
        self.gated, self.bias1, self.weight = gated, bias1, weight
        self.biased = biased
        self.chunks = 1 if gated else 4
        self.hidden = [sb(f"hidden{i}", [P, self.chunks, GT]) for i in range(2)]
        if gated:
            self.silu = [sb(f"silu{i}", [P, GT]) for i in range(2)]
            self.silu_ready = sem("silu_ready")
        self.up_done = sem("up_done")
        self.hidden_ready = sem("hidden_ready")
        self.down_done = sem("down_done")
        self.added = sem("added")
        self.stats_done = sem("stats_done")

    def loop(self, eng, unit):
        E = self.experts

        def pair(g0, static):
            for j in range(2):
                for e in range(E):
                    g = g0 + j
                    unit(g * E + e, g, e, (j * E + e) % 2)

        pair(0, True)
        with eng.Fori(1, GROUPS // 2 - 1) as i:
            pair(i * 2, False)
        pair(GROUPS - 2, True)

    def up_tensor(self, pe, v, g, e, par):
        after(pe, self.hidden_ready, v - 1)
        banks = self.k.ps[par]
        moving = self.xnT[:, bass.ds(g * GT, GT)]
        for c in range(2 if self.gated else 4):
            out = banks[:, c, 0:GT] if self.gated else banks[:, c // 2, (c % 2) * GT:(c % 2 + 1) * GT]
            last = pe.matmul(out, self.up[:, e, c * P:(c + 1) * P], moving, start=True, stop=True)
        last.then_inc(self.up_done, 1)

    def tensor(self, pe):
        E = self.experts
        self.up_tensor(pe, 0, 0, 0, 0)

        def unit(v, g, e, par):
            if not (isinstance(v, int) and v == GROUPS * E - 1):
                self.up_tensor(pe, v + 1, g if e + 1 < E else g + 1, (e + 1) % E, 1 - par)
            pe.wait_ge(self.hidden_ready, v + 1)
            after(pe, self.added, v - 1)
            for j in range(2):
                out = self.k.ps[2][:, par, j * D:(j + 1) * D]
                for c in range(self.chunks):
                    last = pe.matmul(out, self.hidden[par][:, c, j * P:(j + 1) * P], self.down[:, e, c, :],
                                     start=c == 0, stop=c == self.chunks - 1)
            last.then_inc(self.down_done, 1)

        self.loop(pe, unit)

    def scalar(self, act):
        def unit(v, g, e, par):
            act.wait_ge(self.up_done, v + 1)
            banks = self.k.ps[par]
            if self.gated:
                after(act, self.hidden_ready, v - 1)
                act.activation(self.silu[par][:, :], banks[:, 0, 0:GT], ACT.Silu).then_inc(
                    self.silu_ready, 1)
                return
            after(act, self.down_done, v - 1)
            for c in range(4):
                last = act.activation(self.hidden[par][:, c, :],
                                      banks[:, c // 2, (c % 2) * GT:(c % 2 + 1) * GT], ACT.Gelu,
                                      bias=self.bias1[:, 4 * e + c:4 * e + c + 1])
            last.then_inc(self.hidden_ready, 1)

        self.loop(act, unit)

    def vector(self, dve):
        k, E = self.k, self.experts

        def multiply(v, par):
            dve.wait_ge(self.silu_ready, v + 1)
            dve.wait_ge(self.up_done, v + 1)
            after(dve, self.down_done, v - 1)
            dve.tensor_tensor(self.hidden[par][:, 0, :], self.silu[par][:, :], k.ps[par][:, 1, 0:GT],
                              ALU.mult).then_inc(self.hidden_ready, 1)

        if self.gated:
            multiply(0, 0)

        def unit(v, g, e, par):
            if self.gated and not (isinstance(v, int) and v == GROUPS * E - 1):
                multiply(v + 1, 1 - par)
            dve.wait_ge(self.down_done, v + 1)
            after(dve, self.added, v)
            if self.biased is not None:
                dve.wait_ge(self.biased, g + 1)
            xg = k.x[:, bass.ds(g * 2, 2), :]
            if self.weight is None:
                dve.tensor_tensor(xg.rearrange("p a d -> p (a d)"), xg.rearrange("p a d -> p (a d)"),
                                  k.ps[2][:, par, 0:2 * D], ALU.add).then_inc(self.added, 1)
            else:
                for j in range(2):
                    xt = k.x[:, bass.ds(g * 2 + j, 1), :].rearrange("p a d -> p (a d)")
                    w = self.weight[:, bass.ds((g * 2 + j) * 8 + e, 1)]
                    last = dve.scalar_tensor_tensor(xt, k.ps[2][:, par, j * D:(j + 1) * D], w, xt,
                                                    ALU.mult, ALU.add)
                last.then_inc(self.added, 1)
            if e == E - 1:
                dve.wait_ge(self.added, v + 1)
                for j in range(2):
                    last = dve.bn_stats(
                        k.stats[:, bass.ds(g * 2 + j, 1), :].rearrange("p a d -> p (a d)"),
                        k.x[:, bass.ds(g * 2 + j, 1), :].rearrange("p a d -> p (a d)"))
                last.then_inc(self.stats_done, 1)

        self.loop(dve, unit)



class Ternary:

    def __init__(self, k, ctx, tag, floor, weights):
        def sb(name, shape):
            return ctx.enter_context(k.nc.sbuf_tensor(f"{tag}_{name}", shape, F32))

        self.k, self.floor, self.weights = k, floor, weights
        self.sums = sb("tern_sums", [P, len(weights)])
        self.cut = sb("tern_cut", [P, 2, len(weights)])
        self.low = [sb(f"tern_low{i}", [P, w.shape[1]]) for i, w in enumerate(weights)]
        self.sums_ready = Signals.new(k.nc, f"{tag}_tern_sums")
        self.total_done = Signals.new(k.nc, f"{tag}_tern_total")
        self.made = Signals.new(k.nc, f"{tag}_tern_made")

    def tensor(self, pe):
        pe.wait_ge(self.sums_ready, 1)
        pe.matmul(self.k.ps[2][:, 1, 0:len(self.weights)], self.k.ones[:, :], self.sums[:, :], start=True,
                  stop=True).then_inc(self.total_done, 1)

    def vector(self, dve, link, scales):
        n = len(self.weights)
        link(dve.memset(self.sums[:, :], 0.0))
        for i, w in enumerate(self.weights):
            last = dve.tensor_reduce(self.sums[0:w.shape[0], i:i + 1], w, AX.X, ALU.add,
                                     apply_absolute_value=True)
        last.then_inc(self.sums_ready, 1)
        dve.wait_ge(self.total_done, 1)
        for i, w in enumerate(self.weights):
            last = dve.tensor_scalar(scales[:, i:i + 1], self.k.ps[2][:, 1, i:i + 1],
                                     1.0 / (w.shape[0] * w.shape[1]),
                                     self.floor, ALU.mult, ALU.max)
        link(last)
        for i, factor in enumerate((0.5, -0.5)):
            last = dve.tensor_scalar(self.cut[:, i, :], scales[:, 0:n], factor, None, ALU.mult)
        link(last)
        for i, w in enumerate(self.weights):
            rows = w.shape[0]
            last = dve.tensor_scalar(self.low[i][0:rows, :], w, self.cut[0:rows, 1, i:i + 1], None, ALU.is_lt)
        link(last)
        for i, w in enumerate(self.weights):
            rows = w.shape[0]
            last = dve.scalar_tensor_tensor(w, w, self.cut[0:rows, 0, i:i + 1], self.low[i][0:rows, :],
                                            ALU.is_gt, ALU.subtract)
        last.then_inc(self.made, 1)



F1 = 512


def ffn1_weights(k):
    w = k.odd
    return (w[:, 0:512].rearrange("p (c n) -> p c n", n=D), w[:, 512:1024],
            w[:, 1024:1028], w[:, 1028:1028 + D])


def load_ffn1(sp, k):
    w1, w2, b1, b2 = ffn1_weights(k)
    d = k.dram
    k.load(sp, "odd", w1, d["L1_ffn_W1"].rearrange("(c p) n -> p c n", p=P))
    k.load(sp, "odd", w2, d["L1_ffn_W2"])
    with k.nc.allow_non_contiguous_dma(reason="a short bias, feature-major"):
        k.load(sp, "odd", b1, d["L1_ffn_b1"].rearrange("(c p) -> p c", p=P))
        k.load(sp, "odd", b2, d["L1_ffn_b2"].partition_broadcast(P))


def ffn1(k, load_next):
    nc = k.nc
    with ExitStack() as ctx:
        def sb(name, shape):
            return ctx.enter_context(nc.sbuf_tensor(f"l1f_{name}", shape, F32))

        def sem(name):
            return Signals.new(nc, f"l1f_{name}")

        tr = Turned(k, ctx, "l1f")
        w1, w2, b1, b2 = ffn1_weights(k)
        up = sb("up", [D, 1, F1])
        down = sb("down", [P, 1, 4, D])
        scales = sb("scales", [P, 2])
        weights = (w1.rearrange("p c n -> p (c n)"), w2)
        tn = Ternary(k, ctx, "l1f", 1e-8, weights)
        step, turned, copied = sem("step"), sem("weights_turned"), sem("weights_ready")
        biased = sem("biased")
        ex = Experts(k, ctx, "l1f", tr.xnT, 1, up, down, False, bias1=b1, biased=biased)
        loaded = k.loads["odd"]
        block = ctx.enter_context(nc.Block())

        @block.sync
        def _(sp):
            load_next(sp)

        @block.gpsimd
        def _(pool):
            pool.wait_ge(k.load_odd, loaded)
            for g in range(GROUPS):
                pool.wait_ge(tr.xn_ready, g // 2 + 1)
                add_bias(pool, k, b2, 2 * g, 2).then_inc(biased, 1)

        @block.tensor
        def _(pe):
            tn.tensor(pe)
            pe.wait_ge(tn.made, 1)
            for i, w in enumerate(weights):
                for c in range(4):
                    last = pe.transpose(k.ps[0][:, i, c * P:(c + 1) * P], w[:, c * P:(c + 1) * P],
                                        k.ident[:, :])
                last.then_inc(turned, 1)
            for n in range(QUADS):
                tr.tensor(pe, n)
            pe.wait_ge(tr.ready, QUADS)
            pe.wait_ge(copied, 2)
            ex.tensor(pe)

        @block.scalar
        def _(act):
            norm_root_scalar(act, k, tr.norm)
            act.wait_ge(turned, 2)
            act.copy(up[:, 0, :], k.ps[0][:, 0, :]).then_inc(copied, 1)
            act.copy(down[:, 0, :, :].rearrange("p c n -> p (c n)"), k.ps[0][:, 1, :]).then_inc(copied, 1)
            for n in range(QUADS):
                tr.scalar(act, n)
            ex.scalar(act)

        @block.vector
        def _(dve):
            link = linked(dve, step)
            dve.wait_ge(k.load_odd, loaded)
            tn.vector(dve, link, scales)
            tr.vector(dve)
            ex.vector(dve)



class Router:

    SLOT = 32

    def __init__(self, k, ctx, tag, experts, w, bias):
        def sb(name, shape):
            return ctx.enter_context(k.nc.sbuf_tensor(f"{tag}_{name}", shape, F32))

        def sem(name):
            return Signals.new(k.nc, f"{tag}_{name}")

        self.k, self.E, self.w, self.bias = k, experts, w, bias
        self.padded = sb("router", [P, self.SLOT])
        self.scoreT = sb("scoreT", [P, 2, QUAD])
        self.index = sb("index", [P, TILES, experts])
        self.score = sb("score", [P, TILES, experts])
        self.soft = sb("soft", [P, TILES, experts])
        self.cand = sb("cand", [P, TILES, experts])
        self.hot = [sb(f"hot{i}", [P, TILES, experts]) for i in range(2)]
        self.top = [sb(f"top{i}", [P, TILES]) for i in range(2)]
        self.first = sb("first", [P, TILES])
        self.weight = sb("weight", [P, TILES * 8])
        self.index_ready = sem("index_ready")
        self.padded_ready = sem("router_ready")
        self.scoredT = sem("scoredT")
        self.scoreT_ready = sem("scoreT_ready")
        self.scored = sem("scored")
        self.score_step = sem("score_step")
        self.ready = sem("score_ready")
        self.soft_ready = sem("soft_ready")
        self.step = sem("route_step")

    def tensor(self, pe, xnT):
        k = self.k
        pe.wait_ge(self.padded_ready, 1)
        for n in range(QUADS):
            j = n % 4
            last = pe.matmul(k.ps[0][j * self.SLOT:(j + 1) * self.SLOT, n // 4, :], self.padded[:, :],
                             xnT[:, n * QUAD:(n + 1) * QUAD], start=True, stop=True)
        last.then_inc(self.scoredT, 1)
        pe.wait_ge(self.scoreT_ready, 1)
        for a in range(2):
            for i in range(4):
                last = pe.transpose(k.ps[1][:, a, i * P:(i + 1) * P], self.scoreT[:, a, i * P:(i + 1) * P],
                                    k.ident[:, :])
        last.then_inc(self.scored, 1)

    def scalar(self, act):
        act.wait_ge(self.scoredT, 1)
        act.copy(self.scoreT[:, :, :], self.k.ps[0][:, :, :]).then_inc(self.scoreT_ready, 1)

    def gpsimd(self, pool):
        pool.memset(self.padded[:, :], 0.0).then_inc(self.index_ready, 1)
        pool.wait_ge(self.index_ready, 1)
        pool.iota(self.index[:, :, :], pattern=[[0, TILES], [1, self.E]], base=0, channel_multiplier=0,
                  allow_small_or_imprecise_dtypes=True).then_inc(self.index_ready, 1)

    def pad_vector(self, dve):
        dve.wait_ge(self.index_ready, 1)
        dve.tensor_copy(self.padded[:, 0:self.E], self.w).then_inc(self.padded_ready, 1)

    def score_vector(self, dve):
        dve.wait_ge(self.scored, 1)
        dve.wait_ge(self.index_ready, 2)
        bias = self.bias.rearrange("p (o u e) -> p o u e", o=1, u=1).to_broadcast([P, 4, 4, self.E])
        for a in range(2):
            dve.tensor_tensor(
                self.score[:, 16 * a:16 * a + 16, :].rearrange("p (j i) e -> p j i e", i=4),
                self.k.ps[1][:, a, :].rearrange("p (i j e) -> p j i e", i=4, j=4)[:, :, :, 0:self.E],
                bias, ALU.add).then_inc(self.score_step, 1)
        dve.wait_ge(self.score_step, 2)

    def first_top(self, dve, link, score, n):
        E = self.E
        index = self.index[:, :, :]
        link(dve.tensor_reduce(self.top[n][:, :], score, AX.X, ALU.max))
        link(dve.tensor_tensor(self.cand[:, :, :], score, spread(self.top[n][:, :], E), ALU.is_equal))
        link(dve.scalar_tensor_tensor(self.cand[:, :, :], self.cand[:, :, :], -float(E), index, ALU.mult,
                                      ALU.add))
        link(dve.tensor_reduce(self.first[:, :], self.cand[:, :, :], AX.X, ALU.min))
        link(dve.tensor_scalar(self.first[:, :], self.first[:, :], float(E), None, ALU.add))
        link(dve.tensor_tensor(self.hot[n][:, :, :], index, spread(self.first[:, :], E), ALU.is_equal))



E3, F3 = 8, 512
ROW = D + 1
SLOTS = 40


def ffn3_weights(k):
    w = k.odd
    return (w[:, 0:4096].rearrange("p (e f) -> p e f", e=E3),
            w[:, 4096:8192].rearrange("p (e c n) -> p e c n", e=E3, c=4),
            w[:, 8192:8200], w[:, 8200:8208])


def load_ffn3(sp, k):
    w1, w2, wr, br = ffn3_weights(k)
    d = k.dram
    k.load(sp, "odd", wr, d["L3_ffn_Wr"])
    with k.nc.allow_non_contiguous_dma(reason="a short bias, the same on every partition"):
        k.load(sp, "odd", br, d["L3_ffn_br"].partition_broadcast(P))
    k.load(sp, "odd", w1, d["L3_ffn_W1"].rearrange("e d f -> d e f"))
    for e in range(E3):
        k.load(sp, "odd", w2[:, e, :, :], d["L3_ffn_W2"][e].rearrange("(c p) n -> p c n", p=P))


def over_slots(eng, slot):
    for s in range(UNROLL):
        slot(s, s)
    with eng.Fori(1, SLOTS // UNROLL - 1) as i:
        for s in range(UNROLL):
            slot(i * UNROLL + s, s)
    for s in range(UNROLL):
        slot(SLOTS - UNROLL + s, s)


class Places:

    def __init__(self, k, ctx, ro):
        def sb(name, shape, dt=F32):
            return ctx.enter_context(k.nc.sbuf_tensor(f"place_{name}", shape, dt))

        def sem(name):
            return Signals.new(k.nc, f"place_{name}")

        self.k, self.ro = k, ro
        self.before = sb("before", [P, P])
        self.not_first = sb("not_first", [P, E3, TILES])
        self.slot_index = sb("slot_index", [1, SLOTS, E3 - 1])
        self.count = sb("count", [P, E3, TILES])
        self.upto = sb("upto", [P, E3, TILES])
        self.tiles = sb("tiles", [P, E3])
        self.end = sb("end", [P, E3])
        self.base = sb("base", [P, E3])
        self.at = sb("at", [P, TILES, E3])
        self.place = sb("place", [P, TILES])
        self.index = sb("index", [P, TILES], mybir.dt.int32)
        self.past = sb("past", [1, SLOTS, E3 - 1])
        self.expert = sb("expert", [1, SLOTS])
        self.expert_index = sb("expert_index", [1, SLOTS], mybir.dt.int32)
        self.consts = sem("consts")
        self.chosen = sem("chosen")
        self.counted = sem("counted")
        self.ready = sem("ready")
        self.expert_ready = sem("expert_ready")

    def gpsimd(self, pool):
        pool.memset(self.not_first[:, :, :], 1.0).then_inc(self.consts, 1)
        pool.wait_ge(self.consts, 1)
        pool.memset(self.not_first[:, :, 0:1], 0.0).then_inc(self.consts, 1)
        pool.wait_ge(self.consts, 2)
        pool.affine_select(out=self.before[:, :], in_=self.k.ones[:, :], compare_op=ALU.is_gt, fill=0.0,
                           base=0, pattern=[[1, P]], channel_multiplier=-1).then_inc(self.consts, 1)
        pool.wait_ge(self.consts, 3)
        pool.iota(self.slot_index[:, :, :], pattern=[[1, SLOTS], [0, E3 - 1]], base=0,
                  channel_multiplier=0, allow_small_or_imprecise_dtypes=True).then_inc(self.consts, 1)

    def tensor(self, pe):
        pe.wait_ge(self.consts, 3)
        pe.wait_ge(self.chosen, 1)
        hot = self.ro.hot[0][:, :, :].rearrange("p t e -> p (t e)")
        n = TILES * E3
        pe.matmul(self.k.ps[2][:, 0, 0:n], self.before[:, :], hot, start=True, stop=True)
        pe.matmul(self.k.ps[2][:, 1, 0:n], self.k.ones[:, :], hot, start=True, stop=True).then_inc(
            self.counted, 1)

    def vector(self, dve, link):
        k, n = self.k, TILES * E3
        earlier = k.ps[2][:, 0, 0:n].rearrange("p (t e) -> p t e", e=E3)
        totals = k.ps[2][:, 1, 0:n].rearrange("p (t e) -> p e t", e=E3)
        flat = "p e t -> p (e t)"
        dve.wait_ge(self.consts, 4)
        dve.wait_ge(self.counted, 1)
        link(dve.tensor_copy(self.count[:, :, :], totals))
        link(dve.tensor_tensor_scan(self.upto[:, :, :].rearrange(flat), self.not_first[:, :, :].rearrange(flat),
                                    self.count[:, :, :].rearrange(flat), 0.0, ALU.mult, ALU.add))
        link(dve.tensor_scalar(self.tiles[:, :], self.upto[:, :, TILES - 1], 1.0 / P, (P - 1) / (2.0 * P),
                               ALU.mult, ALU.add))
        link(dve.tensor_scalar(self.tiles[:, :], self.tiles[:, :], ROUND, None, ALU.add))
        link(dve.tensor_scalar(self.tiles[:, :], self.tiles[:, :], -ROUND, None, ALU.add))
        link(dve.tensor_tensor_scan(self.end[:, :], k.ones[:, 0:E3], self.tiles[:, :], 0.0, ALU.mult, ALU.add))
        link(dve.tensor_tensor(self.base[:, :], self.end[:, :], self.tiles[:, :], ALU.subtract))
        link(dve.tensor_scalar(self.base[:, :], self.base[:, :], float(P), None, ALU.mult))
        link(dve.tensor_tensor(self.upto[:, :, :], self.upto[:, :, :], self.count[:, :, :], ALU.subtract))
        link(dve.tensor_tensor(self.upto[:, :, :], self.upto[:, :, :], spread(self.base[:, :], TILES), ALU.add))
        link(dve.tensor_tensor(self.at[:, :, :], self.upto[:, :, :].rearrange("p e t -> p t e"), earlier,
                               ALU.add))
        link(dve.tensor_tensor(self.at[:, :, :], self.at[:, :, :], self.ro.hot[0][:, :, :], ALU.mult))
        link(dve.tensor_reduce(self.place[:, :], self.at[:, :, :], AX.X, ALU.add))
        dve.tensor_copy(self.index[:, :], self.place[:, :]).then_inc(self.ready, 1)
        end = self.end[0:1, 0:E3 - 1].rearrange("p (a e) -> p a e", a=1).to_broadcast([1, SLOTS, E3 - 1])
        link(dve.tensor_tensor(self.past[:, :, :], self.slot_index[:, :, :], end, ALU.is_ge))
        link(dve.tensor_reduce(self.expert[:, :], self.past[:, :, :], AX.X, ALU.add))
        dve.tensor_copy(self.expert_index[:, :], self.expert[:, :]).then_inc(self.expert_ready, 1)

    def of_slot(self, eng, j):
        return eng.value_load(self.expert_index[0:1, bass.ds(j, 1)], min_val=0, max_val=E3 - 1)


def ffn3(k, out):
    nc = k.nc
    with ExitStack() as ctx:
        def sb(name, shape):
            return ctx.enter_context(nc.sbuf_tensor(f"l3f_{name}", shape, F32))

        def sem(name):
            return Signals.new(nc, f"l3f_{name}")

        w1, w2, wr, br = ffn3_weights(k)
        loaded = k.loads["odd"]
        sent = k.even[:, 0:TILES * ROW].rearrange("p (t d) -> p t d", d=ROW)
        xn = sent[:, :, 0:D]
        b1 = k.spare[:, 0:E3 * F3].rearrange("p (e f) -> p e f", e=E3)
        b2 = sb("b2", [P, E3, D])
        blank = sb("blank", [P, SLOTS, ROW])
        results = blank[:, 0:TILES, 0:D]
        rows = [sb(f"rows{i}", [P, ROW]) for i in range(4)]
        owner = [ctx.enter_context(nc.sbuf_tensor(f"l3f_owner{i}", [P, 1], mybir.dt.int32))
                 for i in range(4)]
        result = [sb(f"result{i}", [P, D]) for i in range(4)]
        xsT = [sb(f"xsT{i}", [D, P]) for i in range(2)]
        hidden = [sb(f"hidden{i}", [P, F3]) for i in range(4)]
        hiddenT = [sb(f"hiddenT{i}", [P, F3]) for i in range(2)]
        table = nc.dram_tensor("expert_rows", [SLOTS * P, ROW], F32, kind="Internal").ap()
        result_table = nc.dram_tensor("expert_results", [TOK + SLOTS * P, D], F32, kind="Internal").ap()
        tr = Turned(k, ctx, "l3f", xn_all=xn)
        ro = Router(k, ctx, "l3f", E3, wr, br)
        pl = Places(k, ctx, ro)
        biases_in, zeroed, table_zeroed = sem("biases_in"), sem("rows_zeroed"), sem("table_zeroed")
        scattered = sem("scattered")
        rows_in = [sem(f"rows_in{i}") for i in range(4)]
        row_turned, xsT_ready = sem("row_turned"), sem("xsT_ready")
        up_done, biased, hidden_ready = sem("up_done"), sem("biased"), sem("hidden_ready")
        hidden_turned, hiddenT_ready = sem("hidden_turned"), sem("hiddenT_ready")
        down_done, result_ready, owner_ready = sem("down_done"), sem("result_ready"), sem("owner_ready")
        results_out = [sem(f"results_out{i}") for i in range(4)]
        results_in = [sem(f"results_in{i}") for i in range(4)]
        numbered = sem("numbered")
        updated, x_out = sem("updated"), sem("x_out")
        QUARTER = TILES // 4
        block = ctx.enter_context(nc.Block())

        def by_slot(ap):
            return ap.rearrange("(j p) d -> p j d", p=P)

        @block.sync
        def _(sp):
            with nc.allow_non_contiguous_dma(reason="biases, the same on every partition"):
                sp.dma_start(b1, k.dram["L3_ffn_b1"].partition_broadcast(P)).then_inc(biases_in, 16)
                sp.dma_start(b2[:, :, :], k.dram["L3_ffn_b2"].partition_broadcast(P)).then_inc(biases_in, 16)
            sp.wait_ge(zeroed, 2)
            sp.dma_start(by_slot(table), blank[:, :, :]).then_inc(table_zeroed, 16)
            sp.wait_ge(table_zeroed, 16)
            sp.wait_ge(scattered, 16 * TILES)

            def load_rows(j, s):
                after(sp, row_turned, j - 3)
                after(sp, owner_ready, j - 3)
                sp.dma_start(rows[s][:, :], by_slot(table)[:, bass.ds(j, 1), :].rearrange(
                    "p a d -> p (a d)")).then_inc(rows_in[s], 16)

            for j in range(UNROLL):
                load_rows(j, j)

            def slot(j, s):
                if not (isinstance(j, int) and j >= SLOTS - UNROLL):
                    load_rows(j + UNROLL, s)

            over_slots(sp, slot)
            for s in range(UNROLL):
                sp.wait_ge(results_out[s], 16 * (SLOTS // UNROLL))
            for n in range(4):
                tiles = slice(n * QUARTER, (n + 1) * QUARTER)
                sp.dma_start(results[:, tiles, :], by_slot(result_table[0:TOK, :])[:, tiles, :]).then_inc(
                    results_in[n], 16)
            ov = out.rearrange("b s d -> (b s) d").rearrange("(t p) d -> p t d", p=P)
            for n in range(4):
                sp.wait_ge(updated, n + 1)
                tiles = slice(n * QUARTER, (n + 1) * QUARTER)
                sp.dma_start(ov[:, tiles, :], k.x[:, tiles, :]).then_inc(x_out, 16)
            sp.wait_ge(x_out, 64)

        @block.gpsimd
        def _(pool):
            pool.memset(blank[:, :, 0:D], 0.0).then_inc(zeroed, 1)
            pool.iota(blank[:, :, D:ROW], pattern=[[P, SLOTS], [0, 1]], base=TOK, channel_multiplier=1,
                      allow_small_or_imprecise_dtypes=True).then_inc(zeroed, 1)
            pool.wait_ge(zeroed, 2)
            pool.iota(sent[:, :, D:ROW], pattern=[[P, TILES], [0, 1]], base=0, channel_multiplier=1,
                      allow_small_or_imprecise_dtypes=True).then_inc(numbered, 1)
            ro.gpsimd(pool)
            pool.wait_ge(ro.index_ready, 2)
            pl.gpsimd(pool)
            pool.wait_ge(table_zeroed, 16)
            pool.wait_ge(numbered, 1)
            pool.wait_ge(pl.ready, 1)
            for t in range(TILES):
                at = bass.IndirectOffsetOnAxis(ap=pl.index[:, t:t + 1], axis=0)
                pool.indirect_dma_start(table, at, sent[:, t, :], None).then_inc(scattered, 16)

            def copy_owner(j, s):
                pool.wait_ge(rows_in[s], (j - s) * (16 // UNROLL) + 16)
                after(pool, results_out[s], (j - s) * (16 // UNROLL))
                pool.tensor_copy(owner[s][:, :], rows[s][:, D:ROW]).then_inc(owner_ready, 1)

            def send(j, s):
                pool.wait_ge(owner_ready, j + 1)
                pool.wait_ge(result_ready, j + 1)
                to = bass.IndirectOffsetOnAxis(ap=owner[s][:, :], axis=0)
                pool.indirect_dma_start(result_table, to, result[s][:, :], None).then_inc(results_out[s], 16)

            for j in range(2):
                copy_owner(j, j)

            def slot(j, s):
                if not (isinstance(j, int) and j >= SLOTS - 2):
                    copy_owner(j + 2, (s + 2) % 4)
                send(j, s)

            for j in range(SLOTS):
                slot(j, j % UNROLL)

        @block.tensor
        def _(pe):
            for n in range(QUADS):
                tr.tensor(pe, n)
            pe.wait_ge(k.load_odd, loaded)
            pe.wait_ge(tr.ready, QUADS)
            ro.tensor(pe, tr.xnT)
            pl.tensor(pe)

            def turn_row(j, s):
                pe.wait_ge(rows_in[s], (j - s) * (16 // UNROLL) + 16)
                after(pe, xsT_ready, j)
                pe.transpose(k.r6[:, 0:P], rows[s][:, 0:D], k.ident[:, :]).then_inc(row_turned, 1)

            def up(j, s):
                e = pl.of_slot(pe, j)
                pe.wait_ge(xsT_ready, j + 1)
                after(pe, biased, j - 1)
                pe.matmul(k.ps[0][:, s % 2, :], xsT[s % 2][:, :],
                          w1[:, bass.ds(e, 1), :].rearrange("p a f -> p (a f)"), start=True, stop=True).then_inc(up_done, 1)

            def turn_hidden(j, s):
                pe.wait_ge(hidden_ready, j + 1)
                after(pe, hiddenT_ready, j - 1)
                for c in range(4):
                    last = pe.transpose(k.ps[1][:, s % 2, c * P:(c + 1) * P],
                                        hidden[s][:, c * P:(c + 1) * P], k.ident[:, :])
                last.then_inc(hidden_turned, 1)

            def down(j, s):
                e = pl.of_slot(pe, j)
                pe.wait_ge(hiddenT_ready, j + 1)
                after(pe, result_ready, j - 1)
                for c in range(4):
                    last = pe.matmul(k.ps[2][:, s % 2, 0:D], hiddenT[s % 2][:, c * P:(c + 1) * P],
                                     w2[:, bass.ds(e, 1), c, :].rearrange("p a f -> p (a f)"),
                                     start=c == 0, stop=c == 3)
                last.then_inc(down_done, 1)

            pe.wait_ge(pl.expert_ready, 1)
            for j in range(2):
                turn_row(j, j)
                up(j, j)
            turn_row(2, 2)

            def slot(j, s):
                if not (isinstance(j, int) and j >= SLOTS - 3):
                    turn_row(j + 3, (s + 3) % 4)
                if not (isinstance(j, int) and j >= SLOTS - 2):
                    up(j + 2, (s + 2) % 4)
                turn_hidden(j, s)
                if not (isinstance(j, int) and j == 0):
                    down(j - 1, (s + 3) % 4)

            over_slots(pe, slot)
            down(SLOTS - 1, 3)

        @block.scalar
        def _(act):
            norm_root_scalar(act, k, tr.norm)
            for n in range(QUADS):
                tr.scalar(act, n)
            ro.scalar(act)
            act.wait_ge(ro.ready, 1)
            act.activation(ro.soft[:, :, :], ro.soft[:, :, :], ACT.Exp).then_inc(ro.soft_ready, 1)

            def copy_xsT(j, s):
                act.wait_ge(row_turned, j + 1)
                after(act, up_done, j - 1)
                act.copy(xsT[s % 2][:, :], k.r6[:, 0:P]).then_inc(xsT_ready, 1)

            for j in range(3):
                copy_xsT(j, j)

            def slot(j, s):
                act.wait_ge(biased, j + 1)
                act.activation(hidden[s][:, :], hidden[s][:, :], ACT.Gelu).then_inc(hidden_ready, 1)
                if not (isinstance(j, int) and j >= SLOTS - 3):
                    copy_xsT(j + 3, (s + 3) % 4)

            over_slots(act, slot)

        @block.vector
        def _(dve):
            dve.wait_ge(k.load_odd, loaded)
            ro.pad_vector(dve)
            tr.vector(dve)
            link = linked(dve, ro.step)
            ro.score_vector(dve)
            ro.first_top(dve, link, ro.score[:, :, :], 0)
            dve.sem_inc(pl.chosen, 1)
            dve.tensor_tensor(ro.soft[:, :, :], ro.score[:, :, :], spread(ro.top[0][:, :], E3),
                              ALU.subtract).then_inc(ro.ready, 1)
            pl.vector(dve, link)
            dve.wait_ge(ro.soft_ready, 1)
            link(dve.tensor_reduce(ro.first[:, :], ro.soft[:, :, :], AX.X, ALU.add))
            link(dve.reciprocal(ro.top[1][:, :], ro.first[:, :]))
            dve.wait_ge(biases_in, 32)
            dve.wait_ge(pl.expert_ready, 1)

            def bias(j, s):
                e = pl.of_slot(dve, j)
                dve.wait_ge(up_done, j + 1)
                after(dve, hidden_turned, j - 3)
                dve.tensor_tensor(hidden[s][:, :], k.ps[0][:, s % 2, :],
                                  b1[:, bass.ds(e, 1), :].rearrange("p a f -> p (a f)"),
                                  ALU.add).then_inc(biased, 1)

            def copy_hiddenT(j, s):
                dve.wait_ge(hidden_turned, j + 1)
                after(dve, down_done, j - 1)
                dve.tensor_copy(hiddenT[s % 2][:, :], k.ps[1][:, s % 2, :]).then_inc(hiddenT_ready, 1)

            def add_b2(j, s):
                e = pl.of_slot(dve, j)
                dve.wait_ge(down_done, j + 1)
                after(dve, results_out[s], (j - s) * (16 // UNROLL))
                dve.tensor_tensor(result[s][:, :],
                                  k.ps[2][:, s % 2, 0:D],
                                  b2[:, bass.ds(e, 1), :].rearrange("p a d -> p (a d)"),
                                  ALU.add).then_inc(result_ready, 1)

            for j in range(2):
                bias(j, j)

            def slot(j, s):
                if not (isinstance(j, int) and j >= SLOTS - 2):
                    bias(j + 2, (s + 2) % 4)
                copy_hiddenT(j, s)
                if not (isinstance(j, int) and j == 0):
                    add_b2(j - 1, (s + 3) % 4)

            over_slots(dve, slot)
            add_b2(SLOTS - 1, 3)
            for n in range(4):
                dve.wait_ge(results_in[n], 16)
                for t in range(n * QUARTER, (n + 1) * QUARTER):
                    last = dve.scalar_tensor_tensor(k.x[:, t, :], results[:, t, :], ro.top[1][:, t:t + 1],
                                                    k.x[:, t, :], ALU.mult, ALU.add)
                last.then_inc(updated, 1)



ROUND = 1.5 * 2.0 ** 23
F1X = 512
LINEARS = ("d2v", "img", "txt", "att0", "att1", "f1", "f2")


def attention1_weights(k):
    w = k.even
    out, at = {}, 0
    for name, rows, n in (("d2v", D, C), ("img", D, D), ("txt", D, D), ("att0", 64, D), ("att1", 64, D),
                          ("f1", D, 4 * 2 * D), ("f2", D, F1X), ("b_d2v", D, 1), ("b_img", D, 1),
                          ("b_txt", D, 1), ("b_att0", D, 1), ("b_att1", D, 1), ("b_f1", D, 4),
                          ("b_f2", 1, D)):
        out[name] = w[0:rows, at:at + n]
        at += n
    return out


def load_attention1(sp, k):
    w = attention1_weights(k)
    d = {n[9:]: v for n, v in k.dram.items() if n.startswith("L1_xattn_")}
    for name in ("d2v", "img", "txt", "att0", "att1", "f2"):
        k.load(sp, "even", w[name], d[f"W_{name}"])
    k.load(sp, "even", w["f1"].rearrange("p (c n) -> p c n", c=4), d["W_f1"].rearrange("(c p) n -> p c n", p=P))
    with k.nc.allow_non_contiguous_dma(reason="short biases, feature-major"):
        for name in ("d2v", "img", "txt"):
            k.load(sp, "even", w[f"b_{name}"], d[f"b_{name}"].rearrange("(p a) -> p a", a=1))
        for name in ("att0", "att1"):
            for part in range(2):
                k.load(sp, "even", w[f"b_{name}"][part * 64:part * 64 + 64],
                       d[f"b_{name}"].rearrange("(p a) -> p a", a=1))
        k.load(sp, "even", w["b_f1"], d["b_f1"].rearrange("(c p) -> p c", p=P))
    k.load(sp, "even", w["b_f2"], row(d["b_f2"], D))


class Rounding:

    INPUTS = ("ctx", "vis", "img", "x", "cat", "h")

    def __init__(self, k, tag, sb):
        self.k = k
        n = len(self.INPUTS)
        self.parts = sb("parts", [P, n, 32])
        self.peak = sb("peak", [P, n])
        self.top = sb("top", [P, n])
        self.scale = sb("scale", [P, n])
        self.inverse = sb("inverse", [P, n])
        self.out_scale = sb("out_scale", [P, 8])
        self.peaks_ready = Signals.new(k.nc, f"{tag}_round_peaks")
        self.top_ready = Signals.new(k.nc, f"{tag}_round_top")
        self.step = Signals.new(k.nc, f"{tag}_scale_step")
        self.round = sb("round", [P, 1])
        self.tmp = [sb(f"round_tmp{i}", [P, QUAD]) for i in range(2)]
        self.scaled = Signals.new(k.nc, f"{tag}_scaled")
        self.shifted = {}
        for name in self.INPUTS:
            self.shifted[name] = Signals.new(k.nc, f"{tag}_shifted_{name}")
        self.done = 0

    def peak_vector(self, dve, name, n, value):
        i = self.INPUTS.index(name)
        return dve.tensor_reduce(self.parts[0:value.shape[0], i, n:n + 1], value, AX.X, ALU.max,
                                 apply_absolute_value=True)

    def scale_vector(self, dve, link, name, count, linears, w_scale):
        i = self.INPUTS.index(name)
        dve.tensor_reduce(self.peak[:, i:i + 1], self.parts[:, i, 0:count], AX.X, ALU.max).then_inc(
            self.peaks_ready, 1)
        self.done += 1
        dve.wait_ge(self.top_ready, self.done)
        link(dve.tensor_scalar(self.scale[:, i:i + 1], self.top[:, i:i + 1], 1e-8, 1.0 / 127.0, ALU.max,
                               ALU.mult))
        link(dve.reciprocal(self.inverse[:, i:i + 1], self.scale[:, i:i + 1]))
        self.out_scale_vector(dve, link, i, linears, w_scale)
        dve.sem_inc(self.scaled, 1)

    def out_scale_vector(self, dve, link, i, linears, w_scale):
        for name in linears:
            j = LINEARS.index(name)
            link(dve.tensor_tensor(self.out_scale[:, j:j + 1], self.scale[:, i:i + 1],
                                   w_scale[:, j:j + 1], ALU.mult))

    def gpsimd(self, pool, names, nth=1):
        for n, name in enumerate(names):
            i = self.INPUTS.index(name)
            pool.wait_ge(self.peaks_ready, n + nth)
            pool.partition_all_reduce(self.top[:, i:i + 1], self.peak[:, i:i + 1], P, RMAX).then_inc(
                self.top_ready, 1)

    def shift_scalar(self, act, name, out, value):
        i, rows = self.INPUTS.index(name), value.shape[0]
        act.activation(out, value, ACT.Identity, bias=self.round[0:rows, :],
                       scale=self.inverse[0:rows, i:i + 1]).then_inc(self.shifted[name], 1)

    def shift_vector(self, dve, name, out, value):
        i = self.INPUTS.index(name)
        dve.tensor_scalar(out, value, self.inverse[:, i:i + 1], ROUND, ALU.mult, ALU.add).then_inc(
            self.shifted[name], 1)

    def round_vector(self, dve, name, n, out, shifted):
        dve.wait_ge(self.shifted[name], n + 1)
        return dve.tensor_scalar(out, shifted, -ROUND, 127.0, ALU.add, ALU.min)


def attention1(k, load_next):
    nc = k.nc
    w = attention1_weights(k)
    loaded = k.loads["even"]
    with ExitStack() as outer:
        def keep(name, shape, dt=F32):
            return outer.enter_context(nc.sbuf_tensor(f"l1x_{name}", shape, dt))

        w_scale = keep("w_scale", [P, 8])
        f1T = keep("f1T", [P, 2, F1X], BF16)
        f2T = keep("f2T", [P, 4, D], BF16)
        rounded = keep("rounded", [P, TOK], BF16)
        average = keep("average", [P, BATCH])
        rounded_average = keep("rounded_average", [P, BATCH], BF16)
        rn = Rounding(k, "l1x", keep)
        fused = keep("fused", [D, TOK])
        with ExitStack() as ctx:
            def sb(name, shape, dt=F32):
                return ctx.enter_context(nc.sbuf_tensor(f"l1x_{name}", shape, dt))

            def sem(name):
                return Signals.new(nc, f"l1x_{name}_")

            tr = Turned(k, ctx, "l1x", xnT=fused)
            tn = Ternary(k, ctx, "l1x", 1e-5, [w[name] for name in LINEARS])
            keys = [sb(f"keysT{j}", [D, TOK]) for j in range(2)]
            vis, img = keys
            wT = {name: sb(f"{name}T", [C if name == "d2v" else D, D], BF16)
                  for name in ("d2v", "img", "txt", "att0", "att1")}
            prob = [sb(f"prob{i}", [P, 4, SEQ]) for i in range(2)]
            padded = [sb(f"padded{i}", [P, 4, P]) for i in range(2)]
            probT = [sb(f"probT{i}", [P, 4, P]) for i in range(2)]
            tokens = [sb(f"tokens{i}", [P, 4, P]) for i in range(2)]
            top, total, share = ([sb(f"{n}{i}", [P, 4]) for i in range(2)] for n in ("top", "total", "share"))
            zeroed = sem("zeroed")
            w_turned, w_ready = sem("w_turned"), sem("w_ready")
            step = sem("step")
            names = ("vis", "img", "key", "txt")
            key0_ready, key1_ready = sem("key0_ready"), sem("key1_ready")
            done = {n: sem(f"{n}_done") for n in names}
            ready = {n: sem(f"{n}_ready") for n in names}
            round_ready = {n: sem(f"{n}_rounded") for n in ("ctx", "vis", "img", "x")}
            scored, top_ready, shifted = sem("scored"), sem("top_ready"), sem("shifted")
            exp_ready, total_ready, share_ready = sem("exp_ready"), sem("total_ready"), sem("share_ready")
            prob_ready, turned, probT_ready = sem("prob_ready"), sem("turned"), sem("probT_ready")
            keys_turned, tokens_ready = sem("keys_turned"), sem("tokens_ready")
            weighed, fused_ready = sem("weighed"), sem("fused_ready")
            cat_peaks = sem("cat_peaks")
            units = [(j, n) for j in range(2) for n in range(QUADS)]
            block = ctx.enter_context(nc.Block())

            def quad(n):
                return slice(n * QUAD, (n + 1) * QUAD)

            @block.sync
            def _(sp):
                load_next(sp)

            @block.tensor
            def _(pe):
                for n in range(QUADS):
                    tr.tensor(pe, n)
                tn.tensor(pe)
                pe.wait_ge(tn.made, 1)
                for i, name in enumerate(("d2v", "img", "txt")):
                    n = C if name == "d2v" else D
                    pe.transpose(k.ps[0][0:n, 0, i * D:(i + 1) * D], w[name], k.ident[:, :])
                for i, name in enumerate(("att0", "att1")):
                    for part in range(2):
                        at = i * D + part * 64
                        last = pe.transpose(k.ps[0][:, 1, at:at + 64], w[name], k.ident[0:64, 0:64])
                last.then_inc(w_turned, 1)
                for c in range(4):
                    for half_in in range(2):
                        pe.transpose(k.ps[1][:, half_in, c * P:(c + 1) * P],
                                     w["f1"][:, c * 2 * D + half_in * D:c * 2 * D + (half_in + 1) * D],
                                     k.ident[:, :])
                for c in range(4):
                    last = pe.transpose(k.ps[2][:, 0, c * D:(c + 1) * D], w["f2"][:, c * P:(c + 1) * P],
                                        k.ident[:, :])
                last.then_inc(w_turned, 1)
                pe.wait_ge(w_ready, 5)
                for name, src, banks in (("vis", "ctx", k.ps[0]), ("img", "vis", k.ps[1])):
                    rows, weight = (C, wT["d2v"]) if name == "vis" else (D, wT["img"])
                    if name == "img":
                        pe.wait_ge(w_ready, 7)
                    for n in range(QUADS):
                        pe.wait_ge(round_ready[src], n + 1)
                        after(pe, ready[name], n - 1)
                        pe.matmul(banks[:, n % 2, :], weight[:, :], rounded[0:rows, quad(n)], start=True,
                                  stop=True).then_inc(done[name], 1)
                for n in range(QUADS + 1):
                    if n < QUADS:
                        pe.wait_ge(round_ready["img"], n + 1)
                        after(pe, key0_ready, n - 1)
                        after(pe, key1_ready, n - 1)
                        for j in range(2):
                            pe.matmul(k.ps[j][:, n % 2, :], wT[f"att{j}"][:, :], rounded[:, quad(n)],
                                      start=True, stop=True).then_inc(done["key"], 1)
                    if n >= 1:
                        pe.wait_ge(round_ready["x"], n)
                        after(pe, ready["txt"], n - 2)
                        pe.matmul(k.ps[2][:, (n - 1) % 2, :], wT["txt"][:, :], rounded[:, quad(n - 1)],
                                  start=True, stop=True).then_inc(done["txt"], 1)
                pe.wait_ge(ready["txt"], QUADS)
                pe.wait_ge(key0_ready, QUADS)
                pe.wait_ge(key1_ready, QUADS)

                def score(v):
                    j, n = units[v]
                    after(pe, shifted, v - 1)
                    if j == 1:
                        pe.wait_ge(fused_ready, n + 1)
                    for i in range(4):
                        for b in range(2):
                            at = n * QUAD + i * P + b * SEQ
                            last = pe.matmul(k.ps[0][b * SEQ:(b + 1) * SEQ, v % 2, i * SEQ:(i + 1) * SEQ],
                                             fused[:, at:at + SEQ], keys[j][:, at:at + SEQ],
                                             start=True, stop=True)
                    last.then_inc(scored, 1)

                def turn_keys(v):
                    j, n = units[v]
                    after(pe, tokens_ready, v)
                    for i in range(4):
                        at = n * QUAD + i * P
                        last = pe.transpose(k.ps[2][:, 0, i * P:(i + 1) * P], keys[j][:, at:at + P],
                                            k.ident[:, :])
                    last.then_inc(keys_turned, 1)

                def turn(v):
                    pe.wait_ge(prob_ready, 2 * v + 2)
                    after(pe, probT_ready, v - 1)
                    for i in range(4):
                        last = pe.transpose(k.ps[1][:, v % 2, i * P:(i + 1) * P], padded[v % 2][:, i, :],
                                            k.ident[:, :])
                    last.then_inc(turned, 1)

                def weigh(v):
                    pe.wait_ge(probT_ready, v + 1)
                    pe.wait_ge(tokens_ready, v + 1)
                    after(pe, fused_ready, v - 1)
                    for i in range(4):
                        last = pe.matmul((k.r6, k.r7)[v % 2][:, i * P:(i + 1) * P], tokens[v % 2][:, i, :],
                                         probT[v % 2][:, i, :], start=True, stop=True)
                    last.then_inc(weighed, 1)

                score(0)
                score(1)
                turn_keys(0)
                turn(0)
                for v in range(len(units)):
                    if v + 2 < len(units):
                        score(v + 2)
                    if v + 1 < len(units):
                        turn_keys(v + 1)
                        turn(v + 1)
                    weigh(v)

            @block.scalar
            def _(act):
                norm_root_scalar(act, k, tr.norm)
                act.wait_ge(rn.scaled, 1)
                for n in range(QUADS):
                    rn.shift_scalar(act, "ctx", k.spare[0:C, quad(n)], k.ctxT[0:C, quad(n)])
                    tr.scalar(act, n)
                act.wait_ge(w_turned, 1)
                act.copy(wT["d2v"][:, :], k.ps[0][0:C, 0, 0:D]).then_inc(w_ready, 1)
                act.copy(wT["img"][:, :], k.ps[0][:, 0, D:2 * D]).then_inc(w_ready, 1)
                act.copy(wT["txt"][:, :], k.ps[0][:, 0, 2 * D:3 * D]).then_inc(w_ready, 1)
                for j in range(2):
                    act.copy(wT[f"att{j}"][:, :], k.ps[0][:, 1, j * D:(j + 1) * D]).then_inc(w_ready, 1)

                def shift(nth, name, value, before):
                    act.wait_ge(rn.scaled, nth)
                    rows = value.shape[0]
                    for n in range(QUADS):
                        if n >= 2:
                            act.wait_ge(round_ready[name], n - 1)
                        elif before is not None:
                            act.wait_ge(round_ready[before], QUADS - 1 + n)
                        rn.shift_scalar(act, name, rn.tmp[n % 2][0:rows, :], value[:, quad(n)])

                for name, out, linear, banks in (("vis", vis, "d2v", k.ps[0]), ("img", img, "img", k.ps[1])):
                    i = LINEARS.index(linear)
                    for n in range(QUADS):
                        act.wait_ge(done[name], n + 1)
                        act.activation(out[:, quad(n)], banks[:, n % 2, :], ACT.Identity,
                                       bias=w[f"b_{linear}"], scale=rn.out_scale[:, i:i + 1]).then_inc(
                                           ready[name], 1)
                    if name == "vis":
                        act.wait_ge(w_turned, 2)
                        act.copy(f1T[:, :, :], k.ps[1][:, :, :]).then_inc(w_ready, 1)
                        act.copy(f2T[:, :, :].rearrange("p c n -> p (c n)"), k.ps[2][:, 0, :]).then_inc(
                            w_ready, 1)
                        shift(2, "vis", vis, None)
                shift(4, "img", img, "vis")
                i = LINEARS.index("att0")
                for n in range(QUADS + 1):
                    if n < QUADS:
                        act.wait_ge(done["key"], 2 * n + 1)
                        act.activation(keys[0][:, quad(n)], k.ps[0][:, n % 2, :], ACT.Identity,
                                       bias=w["b_att0"], scale=rn.out_scale[:, i:i + 1]).then_inc(
                                           key0_ready, 1)
                    if n >= 1:
                        t = LINEARS.index("txt")
                        act.wait_ge(done["txt"], n)
                        act.activation(fused[:, quad(n - 1)], k.ps[2][:, (n - 1) % 2, :], ACT.Identity,
                                       bias=w["b_txt"], scale=rn.out_scale[:, t:t + 1]).then_inc(
                                           ready["txt"], 1)

                def copy_tokens(v):
                    act.wait_ge(keys_turned, v + 1)
                    after(act, weighed, v - 1)
                    act.copy(tokens[v % 2][:, :, :].rearrange("p a n -> p (a n)"), k.ps[2][:, 0, :]).then_inc(
                        tokens_ready, 1)

                def exp(v):
                    act.wait_ge(shifted, v + 1)
                    act.activation(prob[v % 2][:, :, :], prob[v % 2][:, :, :], ACT.Exp,
                                   scale=float(D) ** -0.5).then_inc(exp_ready, 1)

                def copy_probT(v):
                    act.wait_ge(turned, v + 1)
                    after(act, weighed, v - 1)
                    act.copy(probT[v % 2][:, :, :].rearrange("p a n -> p (a n)"),
                             k.ps[1][:, v % 2, :]).then_inc(probT_ready, 1)

                exp(0)
                exp(1)
                copy_tokens(0)
                copy_probT(0)
                for v in range(len(units)):
                    if v + 2 < len(units):
                        exp(v + 2)
                    if v + 1 < len(units):
                        copy_tokens(v + 1)
                        copy_probT(v + 1)

            @block.vector
            def _(dve):
                link = linked(dve, step)
                link(dve.memset(rn.round[:, :], ROUND))
                link(dve.memset(rn.parts[:, :, :], 0.0))
                link(rn.peak_vector(dve, "ctx", 0, k.ctx_peaks[:, :]))
                rn.scale_vector(dve, link, "ctx", 1, (), w_scale)
                tr.vector(dve)
                dve.wait_ge(k.load_even, loaded)
                tn.vector(dve, link, w_scale)
                rn.out_scale_vector(dve, link, rn.INPUTS.index("ctx"), ("d2v",), w_scale)
                for n in range(QUADS):
                    rn.round_vector(dve, "ctx", n, rounded[0:C, quad(n)], k.spare[0:C, quad(n)]).then_inc(
                        round_ready["ctx"], 1)
                dve.wait_ge(tr.ready, QUADS)
                link(rn.peak_vector(dve, "x", 0, fused[:, :]))
                for n in range(QUADS):
                    dve.wait_ge(ready["vis"], n + 1)
                    link(rn.peak_vector(dve, "vis", n, vis[:, quad(n)]))
                rn.scale_vector(dve, link, "vis", QUADS, ("img",), w_scale)
                for n in range(QUADS):
                    rn.round_vector(dve, "vis", n, rounded[:, quad(n)], rn.tmp[n % 2][:, :]).then_inc(
                        round_ready["vis"], 1)
                rn.scale_vector(dve, link, "x", 1, ("txt",), w_scale)
                for n in range(QUADS):
                    dve.wait_ge(ready["img"], n + 1)
                    link(rn.peak_vector(dve, "img", n, img[:, quad(n)]))
                rn.scale_vector(dve, link, "img", QUADS, ("att0", "att1"), w_scale)
                for n in range(QUADS):
                    rn.round_vector(dve, "img", n, rounded[:, quad(n)], rn.tmp[n % 2][:, :]).then_inc(
                        round_ready["img"], 1)
                    rn.shift_vector(dve, "x", fused[:, quad(n)], fused[:, quad(n)])
                for n in range(QUADS):
                    link(dve.tensor_reduce(average[:, 8 * n:8 * n + 8],
                                           img[:, quad(n)].rearrange("p (b s) -> p b s", s=SEQ), AX.X,
                                           ALU.add))
                    i = LINEARS.index("att1")
                    dve.wait_ge(done["key"], 2 * n + 2)
                    dve.tensor_scalar(keys[1][:, quad(n)], k.ps[1][:, n % 2, :], rn.out_scale[:, i:i + 1],
                                      w["b_att1"], ALU.mult, ALU.add).then_inc(key1_ready, 1)
                    rn.round_vector(dve, "x", n, rounded[:, quad(n)], fused[:, quad(n)]).then_inc(
                        round_ready["x"], 1)
                link(dve.tensor_scalar(average[:, :], average[:, :], 1.0 / SEQ, None, ALU.mult))

                def softmax(v):
                    i = v % 2
                    dve.wait_ge(scored, v + 1)
                    scores = k.ps[0][:, i, 0:4 * SEQ].rearrange("p (a n) -> p a n", n=SEQ)
                    dve.tensor_reduce(top[i][:, :], scores, AX.X, ALU.max).then_inc(top_ready, 1)
                    dve.wait_ge(top_ready, v + 1)
                    after(dve, prob_ready, 2 * v - 2)
                    dve.tensor_tensor(prob[i][:, :, :], scores, spread(top[i][:, :], SEQ),
                                      ALU.subtract).then_inc(shifted, 1)

                def divide(v):
                    i = v % 2
                    dve.wait_ge(exp_ready, v + 1)
                    dve.tensor_reduce(total[i][:, :], prob[i][:, :, :], AX.X, ALU.add).then_inc(total_ready, 1)
                    dve.wait_ge(total_ready, v + 1)
                    after(dve, prob_ready, 2 * v - 2)
                    dve.reciprocal(share[i][:, :], total[i][:, :]).then_inc(share_ready, 1)

                def fuse(v):
                    dve.wait_ge(weighed, v + 1)
                    out = fused[:, quad(units[v][1])]
                    dve.scalar_tensor_tensor(out, (k.r6, k.r7)[v % 2][:, :], 0.1, out, ALU.mult,
                                             ALU.add).then_inc(fused_ready, 1)
                    if units[v][0] == 1:
                        dve.wait_ge(fused_ready, v + 1)
                        rn.peak_vector(dve, "cat", units[v][1], out).then_inc(cat_peaks, 1)

                softmax(0)
                softmax(1)
                divide(0)
                divide(1)
                for v in range(len(units)):
                    if v + 2 < len(units):
                        softmax(v + 2)
                        divide(v + 2)
                    fuse(v)

            @block.gpsimd
            def _(pool):
                for i in range(2):
                    pool.memset(padded[i][:, :, :], 0.0).then_inc(zeroed, 1)
                pool.wait_ge(zeroed, 2)
                rn.gpsimd(pool, ("ctx", "vis", "x", "img"))
                for v in range(len(units)):
                    pool.wait_ge(share_ready, v + 1)
                    after(pool, turned, v - 1)
                    for b in range(2):
                        rows = slice(b * SEQ, (b + 1) * SEQ)
                        pool.tensor_tensor(padded[v % 2][rows, :, rows], prob[v % 2][rows, :, :],
                                           spread(share[v % 2][rows, :], SEQ), ALU.mult).then_inc(prob_ready, 1)

        with ExitStack() as ctx:
            def sb(name, shape, dt=F32):
                return ctx.enter_context(nc.sbuf_tensor(f"l1y_{name}", shape, dt))

            def sem(name):
                return Signals.new(nc, f"l1y_{name}")

            hidden = sb("hidden", [P, 4, TOK])
            shifted_average = sb("shifted_average", [P, BATCH])
            bias = sb("bias", [P, D])
            step, cat_rounded, average_rounded = sem("step"), sem("cat_rounded"), sem("average_rounded")
            up_done, hidden_ready, h_rounded = sem("up_done"), sem("hidden_ready"), sem("h_rounded")
            down_done, updated, stats_done = sem("down_done"), sem("updated"), sem("stats_done")
            biased = sem("biased")
            bias_done, bias_ready = sem("bias_done"), sem("bias_ready")
            rn.peaks_ready, rn.top_ready, rn.done = sem("peaks_ready"), sem("top_ready"), 0
            rn.scaled = sem("scaled_")
            rounded_h = [rounded[:, i * 4 * QUAD:(i + 1) * 4 * QUAD].rearrange("p (c n) -> p c n", c=4)
                         for i in range(2)]
            block = ctx.enter_context(nc.Block())

            def quad(n):
                return slice(n * QUAD, (n + 1) * QUAD)

            @block.tensor
            def _(pe):
                pe.matmul(k.r6[:, 0:D], k.ones[0:1, :], w["b_f2"], start=True, stop=True).then_inc(bias_done, 1)
                pe.wait_ge(average_rounded, 1)
                for n in range(QUADS):
                    pe.wait_ge(cat_rounded, n + 1)
                    avg = rounded_average[:, 8 * n:8 * n + 8].rearrange("p (b a) -> p b a", a=1).to_broadcast(
                        [P, 8, SEQ])
                    for pair in range(2):
                        after(pe, hidden_ready, 2 * n - 1 + pair)
                        for i in range(2):
                            cols = slice((2 * pair + i) * P, (2 * pair + i + 1) * P)
                            out = k.ps[pair][:, i, :]
                            pe.matmul(out, f1T[:, 0, cols], rounded[:, quad(n)], start=True, stop=False)
                            last = pe.matmul(out, f1T[:, 1, cols], avg, start=False, stop=True)
                        last.then_inc(up_done, 1)
                for n in range(QUADS):
                    pe.wait_ge(h_rounded, n + 1)
                    after(pe, updated, n - 1)
                    for j in range(4):
                        for c in range(4):
                            last = pe.matmul(k.ps[2][:, n % 2, j * D:(j + 1) * D],
                                             rounded_h[n % 2][:, c, j * P:(j + 1) * P], f2T[:, c, :],
                                             start=c == 0, stop=c == 3)
                    last.then_inc(down_done, 1)

            @block.scalar
            def _(act):
                act.wait_ge(bias_done, 1)
                act.copy(bias[:, :], k.r6[:, 0:D]).then_inc(bias_ready, 1)
                s = LINEARS.index("f1")
                for n in range(QUADS):
                    for pair in range(2):
                        act.wait_ge(up_done, 2 * n + pair + 1)
                        for i in range(2):
                            c = 2 * pair + i
                            last = act.activation(hidden[:, c, quad(n)], k.ps[pair][:, i, :], ACT.Relu,
                                                  bias=w["b_f1"][:, c:c + 1], scale=rn.out_scale[:, s:s + 1])
                        last.then_inc(hidden_ready, 1)
                act.wait_ge(rn.scaled, 2)
                for n in range(QUADS):
                    rn.shift_scalar(act, "h", hidden[:, :, quad(n)], hidden[:, :, quad(n)])

            @block.vector
            def _(dve):
                link = linked(dve, step)
                link(rn.peak_vector(dve, "cat", QUADS, average[:, :]))
                rn.scale_vector(dve, link, "cat", QUADS + 1, ("f1",), w_scale)
                rn.shift_vector(dve, "cat", shifted_average[:, :], average[:, :])
                rn.round_vector(dve, "cat", 0, rounded_average[:, :], shifted_average[:, :]).then_inc(
                    average_rounded, 1)
                for n in range(QUADS):
                    rn.shift_vector(dve, "cat", rn.tmp[n % 2][:, :], fused[:, quad(n)])
                    rn.round_vector(dve, "cat", n + 1, rounded[:, quad(n)], rn.tmp[n % 2][:, :]).then_inc(
                        cat_rounded, 1)
                for n in range(QUADS):
                    for pair in range(2):
                        dve.wait_ge(hidden_ready, 2 * n + pair + 1)
                        for i in range(2):
                            last = rn.peak_vector(dve, "h", 4 * n + 2 * pair + i,
                                                  hidden[:, 2 * pair + i, quad(n)])
                link(last)
                rn.scale_vector(dve, link, "h", 32, ("f2",), w_scale)
                dve.wait_ge(biased, QUADS)
                s = LINEARS.index("f2")
                for n in range(QUADS + 1):
                    if n < QUADS:
                        after(dve, down_done, n - 1)
                        rn.round_vector(dve, "h", n, rounded_h[n % 2], hidden[:, :, quad(n)]).then_inc(
                            h_rounded, 1)
                    if n >= 1:
                        m = n - 1
                        dve.wait_ge(down_done, m + 1)
                        xq = k.x[:, 4 * m:4 * m + 4, :].rearrange("p a d -> p (a d)")
                        dve.scalar_tensor_tensor(xq, k.ps[2][:, m % 2, :], rn.out_scale[:, s:s + 1], xq,
                                                 ALU.mult, ALU.add).then_inc(updated, 1)
                        dve.wait_ge(updated, m + 1)
                        for j in range(4):
                            last = dve.bn_stats(k.stats[:, 4 * m + j, :], k.x[:, 4 * m + j, :])
                        last.then_inc(stats_done, 1)

            @block.gpsimd
            def _(pool):
                rn.gpsimd(pool, ("cat",))
                pool.wait_ge(bias_ready, 1)
                bias4 = bias[:, :].rearrange("p (a n) -> p a n", a=1).to_broadcast([P, 4, D])
                for n in range(QUADS):
                    xq = k.x[:, 4 * n:4 * n + 4, :]
                    pool.tensor_tensor(xq, xq, bias4, ALU.add).then_inc(biased, 1)
                rn.gpsimd(pool, ("h",), 2)



PAIR = 18
VCOLS = H // 2 * PAIR


class Narrow:

    def __init__(self, k, ctx, tag):
        def sb(name, shape):
            return ctx.enter_context(k.nc.sbuf_tensor(f"{tag}_{name}", shape, F32))

        self.q = k.odd[:, 4352:4352 + TOK]
        self.k = sb("k_all", [D, TOK])
        self.v = sb("v_all", [P, BATCH, VCOLS])
        self.own = sb("own", [P, H])
        self.parity = sb("parity", [P, 16])
        self.masks_in = Signals.new(k.nc, f"{tag}_masks_in")
        self.ones_ready = Signals.new(k.nc, f"{tag}_ones_ready")

    def load(self, sp, k, own):
        sp.dma_start(self.own[:, :], k.dram[own]).then_inc(self.masks_in, 16)
        sp.dma_start(self.parity[:, :], k.dram["const_parity"]).then_inc(self.masks_in, 16)

    def ones_gpsimd(self, pool):
        v = self.v[:, :, :].rearrange("p b (c n) -> p (b c) n", n=PAIR)
        for half_at in range(2):
            rows = slice(half_at * SEQ, (half_at + 1) * SEQ)
            for par in range(2):
                pool.memset(v[rows, :, 16 + par:17 + par], 1.0 if par == half_at else 0.0).then_inc(
                    self.ones_ready, 1)

    def values_vector(self, dve, n, bank):
        v = self.v[:, 4 * n:4 * n + 4, :].rearrange("p b (c n) -> p (b c) n", n=PAIR)[:, :, 0:16]
        mask = self.parity[:, :].rearrange("p (a n) -> p a n", a=1).to_broadcast([P, 32, 16])
        return dve.tensor_tensor(v, bank.rearrange("p (c n) -> p c n", n=16), mask, ALU.mult)


def narrow_attention(k, tag, nw, wo, mask, load_next):
    nc = k.nc
    scale = 8.0 ** -0.5
    own_dve = 4
    with ExitStack() as ctx:
        def sb(name, shape):
            return ctx.enter_context(nc.sbuf_tensor(f"{tag}_{name}", shape, F32))

        def sem(name):
            return Signals.new(nc, f"{tag}_{name}")

        queries = [sb(f"queries{i}", [D, P]) for i in range(2)]
        keys = [sb(f"keys{i}", [D, H, P]) for i in range(2)]
        values = [sb(f"values{i}", [P, 2, VCOLS]) for i in range(2)]
        prob = [sb(f"prob{i}", [P, H, SEQ]) for i in range(2)]
        probT = sb("probT", [P, H // 2, P])
        top = [sb(f"top{i}", [P, H]) for i in range(2)]
        share = [sb(f"share{i}", [P, H]) for i in range(2)]
        heads = [sb(f"heads{i}", [P, D]) for i in range(2)]
        headsT = sb("headsT", [D, P])
        S, T, O = k.ps
        queries_ready, values_ready = sem("queries_ready"), sem("values_ready")
        own0_ready, own1_ready = sem("own0_ready"), sem("own1_ready")
        scored, top_ready, shifted = sem("scored"), sem("top_ready"), sem("shifted")
        exp_ready, turned, probT_ready = sem("exp_ready"), sem("turned"), sem("probT_ready")
        weighed, share_ready, heads_ready = sem("weighed"), sem("share_ready"), sem("heads_ready")
        heads_turned, headsT_ready = sem("heads_turned"), sem("headsT_ready")
        projected, updated, stats_done = sem("projected"), sem("updated"), sem("stats_done")
        block = ctx.enter_context(nc.Block())
        AHEAD = 2

        def own(eng, u, s, hs, ready):
            after(eng, scored, 2 * u - 2)
            kt = nw.k[:, bass.ds(u * P, P)].rearrange("p (a n) -> p a n", a=1).to_broadcast(
                [P, hs.stop - hs.start, P])
            eng.tensor_tensor(keys[s % 2][:, hs, :], kt, spread(nw.own[:, hs], P), ALU.mult).then_inc(ready, 1)

        @block.sync
        def _(sp):
            load_next(sp)

        @block.tensor
        def _(pe):
            def scores(u, s):
                pe.wait_ge(queries_ready, u + 1)
                pe.wait_ge(own0_ready, u + 1)
                pe.wait_ge(own1_ready, u + 1)
                for j in range(2):
                    after(pe, shifted, 2 * u - 1 + j)
                    if mask is not None:
                        pe.matmul(S[:, j, :], k.identb[:, :], mask, start=True, stop=True)
                    for b in range(2):
                        rows = slice(b * SEQ, (b + 1) * SEQ)
                        last = pe.matmul(S[rows, j, :], queries[s % 2][:, rows],
                                         keys[s % 2][:, 8 * j:8 * j + 8, rows], start=mask is None,
                                         stop=True, skip_group_check=mask is not None)
                    last.then_inc(scored, 1)

            def turn(t, s):
                pe.wait_ge(exp_ready, t + 1)
                after(pe, probT_ready, t)
                for p in range(H // 2):
                    last = pe.transpose(T[:, p // 4, (p % 4) * P:(p % 4 + 1) * P],
                                        prob[s % 2][:, 2 * p:2 * p + 2, :].rearrange("p h k -> p (h k)"),
                                        k.ident[:, :])
                last.then_inc(turned, 1)

            def weigh(t, s):
                pe.wait_ge(probT_ready, t + 1)
                pe.wait_ge(values_ready, t + 1)
                after(pe, heads_ready, t - 1)
                for p in range(H // 2):
                    for b in range(2):
                        rows = slice(b * SEQ, (b + 1) * SEQ)
                        last = pe.matmul(O[rows, s % 2, p * PAIR:(p + 1) * PAIR], probT[:, p, rows],
                                         values[s % 2][:, b, p * PAIR:(p + 1) * PAIR], start=True, stop=True)
                last.then_inc(weighed, 1)

            def turn_heads(t, s):
                pe.wait_ge(heads_ready, t + 1)
                after(pe, headsT_ready, t)
                pe.transpose(k.r7[:, 0:P], heads[s % 2][:, :], k.ident[:, :]).then_inc(heads_turned, 1)

            def project(t):
                pe.wait_ge(headsT_ready, t + 1)
                after(pe, updated, t)
                pe.matmul(k.r6[:, 0:D], headsT[:, :], wo, start=True, stop=True).then_inc(projected, 1)

            for u in range(AHEAD):
                scores(u, u)

            def slot(t, s):
                turn(t, s)
                if not is_last(t, AHEAD):
                    scores(t + AHEAD, (s + AHEAD) % 4)
                before = not (isinstance(t, int) and t == 0)
                if before:
                    turn_heads(t - 1, (s + 3) % 4)
                weigh(t, s)
                if before:
                    project(t - 1)

            over_tiles(pe, slot)
            turn_heads(TILES - 1, 3)
            project(TILES - 1)

        @block.scalar
        def _(act):
            def exp(u, s):
                act.wait_ge(shifted, 2 * u + 2)
                act.activation(prob[s % 2][:, :, :], prob[s % 2][:, :, :], ACT.Exp, scale=scale).then_inc(
                    exp_ready, 1)

            def copy_values(u, s):
                after(act, weighed, u - 1)
                act.copy(values[s % 2][:, :, :], nw.v[:, bass.ds(u * 2, 2), :]).then_inc(values_ready, 1)

            for u in range(AHEAD):
                copy_values(u, u)
            exp(0, 0)

            def copy_headsT(t):
                act.wait_ge(heads_turned, t + 1)
                after(act, projected, t)
                act.copy(headsT[:, :], k.r7[:, 0:P]).then_inc(headsT_ready, 1)

            def slot(t, s):
                act.wait_ge(turned, t + 1)
                after(act, weighed, t)
                act.copy(probT[:, :, :], T[:, :, :].rearrange("p a (c q) -> p (a c) q", q=P)).then_inc(
                    probT_ready, 1)
                if not is_last(t):
                    exp(t + 1, (s + 1) % 4)
                if not (isinstance(t, int) and t == 0):
                    copy_headsT(t - 1)
                if not is_last(t, AHEAD):
                    copy_values(t + AHEAD, (s + AHEAD) % 4)

            over_tiles(act, slot)
            copy_headsT(TILES - 1)

        @block.vector
        def _(dve):
            def softmax(u, s):
                scores = [S[:, j, :].rearrange("p (h k) -> p h k", k=SEQ) for j in range(2)]
                heads_of = [slice(8 * j, 8 * j + 8) for j in range(2)]
                for j in range(2):
                    dve.wait_ge(scored, 2 * u + 1 + j)
                    dve.tensor_reduce(top[s % 2][:, heads_of[j]], scores[j], AX.X, ALU.max).then_inc(top_ready, 1)
                after(dve, turned, u - 1)
                for j in range(2):
                    dve.wait_ge(top_ready, 2 * u + 1 + j)
                    dve.tensor_tensor(prob[s % 2][:, heads_of[j], :], scores[j],
                                      spread(top[s % 2][:, heads_of[j]], SEQ), ALU.subtract).then_inc(shifted, 1)

            def divide(t, s):
                dve.wait_ge(weighed, t + 1)
                o = O[:, s % 2, 0:VCOLS].rearrange("p (c n) -> p c n", n=PAIR)
                r = share[s % 2][:, :].rearrange("p (c a) -> p c a", a=2)
                dve.reciprocal(r, o[:, :, 16:18]).then_inc(share_ready, 1)
                dve.wait_ge(share_ready, t + 1)
                after(dve, heads_turned, t - 1)
                dve.tensor_tensor(heads[s % 2][:, :].rearrange("p (c a n) -> p c a n", a=2, n=8),
                                  o[:, :, 0:16].rearrange("p c (a n) -> p c a n", n=8),
                                  share[s % 2][:, :].rearrange("p (c a o) -> p c a o", a=2, o=1).to_broadcast(
                                      [P, H // 2, 2, 8]), ALU.mult).then_inc(heads_ready, 1)

            def update(t):
                dve.wait_ge(projected, t + 1)
                xt = k.x[:, bass.ds(t, 1), :].rearrange("p a d -> p (a d)")
                dve.tensor_tensor(xt, xt, k.r6[:, 0:D], ALU.add).then_inc(updated, 1)
                dve.wait_ge(updated, t + 1)
                dve.bn_stats(k.stats[:, bass.ds(t, 1), :].rearrange("p a d -> p (a d)"), xt).then_inc(
                    stats_done, 1)

            for u in range(AHEAD):
                own(dve, u, u, slice(0, own_dve), own0_ready)
            for u in range(AHEAD):
                softmax(u, u)
            own(dve, AHEAD, AHEAD, slice(0, own_dve), own0_ready)

            def slot(t, s):
                if not is_last(t, AHEAD + 1):
                    own(dve, t + AHEAD + 1, (s + AHEAD + 1) % 4, slice(0, own_dve), own0_ready)
                if not is_last(t, AHEAD):
                    softmax(t + AHEAD, (s + AHEAD) % 4)
                divide(t, s)
                if not (isinstance(t, int) and t == 0):
                    update(t - 1)

            over_tiles(dve, slot)
            update(TILES - 1)

        @block.gpsimd
        def _(pool):
            def stage(u, s):
                own(pool, u, s, slice(own_dve, H), own1_ready)
                pool.tensor_copy(queries[s % 2][:, :], nw.q[:, bass.ds(u * P, P)]).then_inc(queries_ready, 1)

            for u in range(AHEAD):
                stage(u, u)

            def slot(t, s):
                if not is_last(t, AHEAD):
                    stage(t + AHEAD, (s + AHEAD) % 4)

            over_tiles(pool, slot)


def attention2_weights(k):
    w = k.even
    return [w[:, i * D:(i + 1) * D] for i in range(4)], w[:, 512:514], w[:, 768:768 + D]


def load_attention2(sp, k):
    (wq, wk, wv, wo), bqk, bo = attention2_weights(k)
    d = k.dram
    k.load(sp, "even", wq, d["L2_xattn_wq"])
    k.load(sp, "even", wk[0:C], d["L2_xattn_wk"])
    k.load(sp, "even", wv[0:C], d["L2_xattn_wv"])
    k.load(sp, "even", wo, d["L2_xattn_wo"])
    with k.nc.allow_non_contiguous_dma(reason="two short biases, feature-major"):
        k.load(sp, "even", bqk[:, 0:1], d["L2_xattn_bq"].rearrange("(p a) -> p a", a=1))
        k.load(sp, "even", bqk[:, 1:2], d["L2_xattn_bk"].rearrange("(p a) -> p a", a=1))
        k.load(sp, "even", bo, d["L2_xattn_bo"].partition_broadcast(P))
    k.load(sp, "even", wv[C:C + 1], row(d["L2_xattn_bv"], D))


def attention2(k, load_next):
    nc = k.nc
    (wq, wk, wv, wo), bqk, bo = attention2_weights(k)
    with ExitStack() as outer:
        nw = Narrow(k, outer, "l2x")
        loaded = k.loads["even"]
        with ExitStack() as ctx:
            def sem(name):
                return Signals.new(nc, f"l2x_{name}")

            tr = Turned(k, ctx, "l2x")
            q_done, k_done, v_done = sem("q_done"), sem("k_done"), sem("v_done")
            q_ready, k_ready, v_ready = sem("q_ready"), sem("k_ready"), sem("v_ready")
            biased = sem("biased")
            block = ctx.enter_context(nc.Block())

            @block.sync
            def _(sp):
                nw.load(sp, k, "const_own8")
                sp.wait_ge(nw.masks_in, 32)

            @block.gpsimd
            def _(pool):
                nw.ones_gpsimd(pool)
                pool.wait_ge(nw.ones_ready, 4)
                pool.wait_ge(k.load_even, loaded)
                for n in range(QUADS):
                    pool.wait_ge(tr.xn_ready, n + 1)
                    add_bias(pool, k, bo, 4 * n, 4).then_inc(biased, 1)

            @block.tensor
            def _(pe):
                pe.wait_ge(k.load_even, loaded)
                for n in range(QUADS):
                    tr.tensor(pe, n)
                for n in range(QUADS):
                    cols = slice(n * QUAD, (n + 1) * QUAD)
                    after(pe, k_ready, n - 1)
                    pe.matmul(k.ps[1][:, n % 2, :], wk[0:C, :], k.ctxT[0:C, cols], start=True,
                              stop=True).then_inc(k_done, 1)
                    for j in range(2):
                        after(pe, v_ready, 2 * n + j - 1)
                        for i in range(4):
                            at = n * QUAD + (4 * j + i) * SEQ
                            for half_at in range(2):
                                last = pe.matmul(k.ps[2][half_at * SEQ:(half_at + 1) * SEQ, j,
                                                         i * D:(i + 1) * D],
                                                 k.ctxT[0:C + 1, at:at + SEQ], wv[0:C + 1, :],
                                                 start=True, stop=True)
                        last.then_inc(v_done, 1)
                    after(pe, q_ready, n - 1)
                    pe.wait_ge(tr.ready, n + 1)
                    pe.matmul(k.ps[0][:, n % 2, :], wq, tr.xnT[:, cols], start=True,
                              stop=True).then_inc(q_done, 1)

            @block.scalar
            def _(act):
                norm_root_scalar(act, k, tr.norm)
                act.wait_ge(k.load_even, loaded)
                for n in range(QUADS):
                    tr.scalar(act, n)
                for n in range(QUADS):
                    act.wait_ge(q_done, n + 1)
                    act.activation(nw.q[:, n * QUAD:(n + 1) * QUAD], k.ps[0][:, n % 2, :], ACT.Identity,
                                   bias=bqk[:, 0:1]).then_inc(q_ready, 1)

            @block.vector
            def _(dve):
                tr.vector(dve)
                dve.wait_ge(k.load_even, loaded)
                dve.wait_ge(nw.masks_in, 32)
                for n in range(QUADS):
                    dve.wait_ge(k_done, n + 1)
                    dve.tensor_scalar(nw.k[:, n * QUAD:(n + 1) * QUAD], k.ps[1][:, n % 2, :],
                                      bqk[:, 1:2], None, ALU.add).then_inc(k_ready, 1)
                    for j in range(2):
                        dve.wait_ge(v_done, 2 * n + j + 1)
                        nw.values_vector(dve, 2 * n + j, k.ps[2][:, j, :]).then_inc(v_ready, 1)

        narrow_attention(k, "l2xa", nw, wo, None, load_next)



L2, E2 = 32, 7
HH = 4


def ffn2_weights(k):
    w = k.odd
    at = 3072
    small = {}
    for name, rows, n in (("kvd", D, L2), ("qd", D, L2), ("ku", L2, 64), ("qu", L2, 64), ("vu", L2, D),
                          ("ropeq", L2, 64), ("ropek", D, 64), ("o", D, D), ("router", D, 8),
                          ("ln1", D, 1), ("ln2", D, 1), ("bias", D, 8)):
        small[name] = w[0:rows, at:at + n]
        at += n
    assert at <= 4352
    return (w[:, 0:2048].rearrange("p (e f) -> p e f", e=8),
            w[:, 2048:3072].rearrange("p (e c n) -> p e c n", e=8, c=1), small)


def load_ffn2(sp, k):
    up, down, w = ffn2_weights(k)
    d = {n[7:]: v for n, v in k.dram.items() if n.startswith("L2_ffn_")}
    for name, key in (("qd", "W_qd"), ("kvd", "W_kvd"), ("ku", "W_ku"), ("qu", "W_qu"), ("vu", "W_vu"),
                      ("ropeq", "W_ropeq"), ("ropek", "W_ropek"), ("o", "W_o")):
        k.load(sp, "odd", w[name], d[key])
    with k.nc.allow_non_contiguous_dma(reason="short weights, feature-major"):
        k.load(sp, "odd", w["router"][:, 0:E2], d["W_router"])
        k.load(sp, "odd", w["ln1"], d["w_ln1"].rearrange("(p a) -> p a", a=1))
        k.load(sp, "odd", w["ln2"], d["w_ln2"].rearrange("(p a) -> p a", a=1))
        k.load(sp, "odd", w["bias"][:, 0:E2], d["routing_bias"].partition_broadcast(P))
    k.load(sp, "odd", up[:, 0:E2, 0:D], d["Wg_r"].rearrange("e d f -> d e f"))
    k.load(sp, "odd", up[:, 0:E2, D:2 * D], d["Wu_r"].rearrange("e d f -> d e f"))
    k.load(sp, "odd", down[:, 0:E2, 0, :], d["Wd_r"].rearrange("e d f -> d e f"))
    k.load(sp, "odd", up[:, E2, 0:D], d["Wg_s"])
    k.load(sp, "odd", up[:, E2, D:2 * D], d["Wu_s"])
    k.load(sp, "odd", down[:, E2, 0, :], d["Wd_s"])


def latent_attention(k, load_next):
    nc = k.nc
    _, _, w = ffn2_weights(k)
    with ExitStack() as outer:
        nw = Narrow(k, outer, "mla")
        causal = outer.enter_context(nc.sbuf_tensor("mla_causal", [P, 512], BF16))
        loaded = k.loads["odd"]
        with ExitStack() as ctx:
            def sb(name, shape):
                return ctx.enter_context(nc.sbuf_tensor(f"mla_{name}", shape, F32))

            def sem(name):
                return Signals.new(nc, f"mla_{name}")

            tr = Turned(k, ctx, "mla", rms=True, weight=w["ln1"])
            q_w, q_rot, k_w = sb("q_w", [L2, D]), sb("q_rot", [L2, D]), sb("k_w", [L2, D])
            downT = sb("downT", [L2, 2, D])
            full = sb("full", [D, 4, D])
            kx_rot = sb("kx_rot", [D, D])
            cos, sin = sb("cos", [P, SEQ]), sb("sin", [P, SEQ])
            mask32 = sb("mask32", [P, SEQ])
            turned_q, turned_k = sb("turned_q", [P, QUAD]), sb("turned_k", [P, QUAD])
            const_in, zeroed, w_ready = sem("const_in"), sem("zeroed"), sem("w_ready")
            mask_ready = sem("mask_ready")
            down_turned, downT_ready = sem("down_turned"), sem("downT_ready")
            full_done, full_copied, full_ready = sem("full_done"), sem("full_copied"), sem("full_ready")
            q_done, k_done, v_done = sem("q_done"), sem("k_done"), sem("v_done")
            q_cos, q_sin, k_cos, k_sin = sem("q_cos"), sem("q_sin"), sem("k_cos"), sem("k_sin")
            q_ready, k_ready, v_ready = sem("q_ready"), sem("k_ready"), sem("v_ready")
            block = ctx.enter_context(nc.Block())

            @block.sync
            def _(sp):
                for out, name in ((cos, "const_cos"), (sin, "const_sin"), (mask32, "const_causal")):
                    sp.dma_start(out[:, :], k.dram[name]).then_inc(const_in, 16)
                nw.load(sp, k, "const_own4")
                sp.wait_ge(const_in, 48)
                sp.wait_ge(nw.masks_in, 32)

            @block.gpsimd
            def _(pool):
                for t in (q_rot, k_w, kx_rot):
                    pool.memset(t[:, :], 0.0).then_inc(zeroed, 1)
                pool.wait_ge(zeroed, 3)
                nw.ones_gpsimd(pool)
                pool.wait_ge(nw.ones_ready, 4)
                pool.wait_ge(const_in, 48)
                pool.tensor_copy(causal[:, :].rearrange("p (h k) -> p h k", k=SEQ),
                                 mask32[:, :].rearrange("p (a k) -> p a k", a=1).to_broadcast([P, 8, SEQ])
                                 ).then_inc(mask_ready, 1)
                for n in range(QUADS):
                    cols = slice(n * QUAD, (n + 1) * QUAD)
                    pool.wait_ge(q_sin, n + 1)
                    pool.tensor_tensor(nw.q[:, cols], nw.q[:, cols], turned_q[:, :], ALU.add).then_inc(
                        q_ready, 1)
                    pool.wait_ge(k_sin, n + 1)
                    pool.tensor_tensor(nw.k[:, cols], nw.k[:, cols], turned_k[:, :], ALU.add).then_inc(
                        k_ready, 1)

            @block.tensor
            def _(pe):
                pe.wait_ge(k.load_odd, loaded)
                pe.transpose(k.ps[0][0:L2, 0, 0:D], w["qd"], k.ident[:, :])
                pe.transpose(k.ps[0][0:L2, 0, D:2 * D], w["kvd"], k.ident[:, :]).then_inc(down_turned, 1)
                pe.wait_ge(downT_ready, 1)
                pe.wait_ge(w_ready, 1)
                for i, (side, up) in enumerate(((0, q_w[:, :]), (0, q_rot[:, :]), (1, k_w[:, :]), (1, w["vu"]))):
                    last = pe.matmul(k.ps[0][:, 1, i * D:(i + 1) * D], downT[:, side, :], up, start=True,
                                     stop=True)
                last.then_inc(full_done, 1)
                for n in range(QUADS):
                    tr.tensor(pe, n)
                pe.wait_ge(full_ready, 1)
                pe.wait_ge(tr.ready, QUADS)

                for n in range(QUADS):
                    cols = slice(n * QUAD, (n + 1) * QUAD)
                    xn = tr.xnT[:, cols]
                    after(pe, q_sin, n)
                    pe.matmul(k.ps[1][:, 0, :], full[:, 0, :], xn, start=True, stop=True)
                    pe.matmul(k.ps[1][:, 1, :], full[:, 1, :], xn, start=True, stop=True).then_inc(q_done, 1)
                    after(pe, k_sin, n)
                    pe.matmul(k.ps[2][:, 0, :], full[:, 2, :], xn, start=True, stop=True)
                    pe.matmul(k.ps[2][:, 1, :], kx_rot[:, :], xn, start=True, stop=True).then_inc(k_done, 1)
                    for j in range(2):
                        after(pe, v_ready, 2 * n + j - 1)
                        for i in range(4):
                            at = n * QUAD + (4 * j + i) * SEQ
                            for half_at in range(2):
                                last = pe.matmul((k.r6, k.r7)[j][half_at * SEQ:(half_at + 1) * SEQ,
                                                                 i * D:(i + 1) * D],
                                                 tr.xnT[:, at:at + SEQ], full[:, 3, :], start=True,
                                                 stop=True)
                        last.then_inc(v_done, 1)

            @block.scalar
            def _(act):
                act.wait_ge(down_turned, 1)
                act.copy(downT[:, :, :].rearrange("p a n -> p (a n)"), k.ps[0][0:L2, 0, 0:2 * D]).then_inc(
                    downT_ready, 1)
                norm_root_scalar(act, k, tr.norm, rms=True)
                act.wait_ge(k.load_odd, loaded)
                for n in range(QUADS):
                    tr.scalar(act, n)

            @block.vector
            def _(dve):
                dve.wait_ge(k.load_odd, loaded)
                dve.wait_ge(zeroed, 3)
                dve.tensor_copy(q_w[:, 0:64], w["qu"])
                dve.tensor_copy(q_w[:, 64:D], w["ropeq"])
                dve.tensor_copy(k_w[:, 0:64], w["ku"])
                for src, out in ((w["ropeq"], q_rot), (w["ropek"], kx_rot)):
                    sv = src.rearrange("p (h j) -> p h j", j=HH)
                    ov = out[:, 64:D].rearrange("p (h j) -> p h j", j=HH)
                    dve.tensor_scalar(ov[:, :, 0:2], sv[:, :, 2:4], -1.0, None, ALU.mult)
                    last = dve.tensor_copy(ov[:, :, 2:4], sv[:, :, 0:2])
                last.then_inc(w_ready, 1)
                dve.wait_ge(full_done, 1)
                dve.tensor_copy(full[:, :, :].rearrange("p a n -> p (a n)"), k.ps[0][:, 1, :]).then_inc(
                    full_copied, 1)
                dve.wait_ge(full_copied, 1)
                dve.tensor_copy(full[:, 2, 64:D], w["ropek"]).then_inc(full_ready, 1)
                tr.vector(dve)
                dve.wait_ge(const_in, 48)
                dve.wait_ge(nw.masks_in, 32)

                def table(t):
                    return t[:, :].rearrange("p (a n) -> p a n", a=1).to_broadcast([P, QUAD // SEQ, SEQ])

                def items(ap):
                    return ap.rearrange("p (b n) -> p b n", n=SEQ)

                for n in range(QUADS):
                    cols = slice(n * QUAD, (n + 1) * QUAD)
                    for bank, out, tmp, done, c_sem, s_sem, ready in (
                            (k.ps[1], nw.q, turned_q, q_done, q_cos, q_sin, q_ready),
                            (k.ps[2], nw.k, turned_k, k_done, k_cos, k_sin, k_ready)):
                        dve.wait_ge(done, n + 1)
                        dve.tensor_tensor(items(out[:, cols]), items(bank[:, 0, :]), table(cos),
                                          ALU.mult).then_inc(c_sem, 1)
                        after(dve, ready, n)
                        dve.tensor_tensor(items(tmp[:, :]), items(bank[:, 1, :]), table(sin),
                                          ALU.mult).then_inc(s_sem, 1)
                    for j in range(2):
                        dve.wait_ge(v_done, 2 * n + j + 1)
                        nw.values_vector(dve, 2 * n + j, (k.r6, k.r7)[j][:, :]).then_inc(v_ready, 1)

        narrow_attention(k, "mlaa", nw, w["o"], causal[:, :], load_next)


def experts2(k, load_next):
    nc = k.nc
    up, down, w = ffn2_weights(k)
    with ExitStack() as ctx:
        tr = Turned(k, ctx, "l2f", rms=True, weight=w["ln2"])
        ro = Router(k, ctx, "l2f", E2, w["router"][:, 0:E2], w["bias"][:, 0:E2])
        ex = Experts(k, ctx, "l2f", tr.xnT, 8, up, down, True, weight=ro.weight)
        block = ctx.enter_context(nc.Block())

        @block.sync
        def _(sp):
            load_next(sp)

        @block.tensor
        def _(pe):
            for n in range(QUADS):
                tr.tensor(pe, n)
            pe.wait_ge(tr.ready, QUADS)
            ro.tensor(pe, tr.xnT)
            pe.wait_ge(ro.ready, 1)
            ex.tensor(pe)

        @block.scalar
        def _(act):
            norm_root_scalar(act, k, tr.norm, rms=True)
            for n in range(QUADS):
                tr.scalar(act, n)
            ro.scalar(act)
            act.wait_ge(ro.ready, 1)
            act.activation(ro.soft[:, :, :], ro.score[:, :, :], ACT.Sigmoid).then_inc(ro.soft_ready, 1)
            ex.scalar(act)

        @block.vector
        def _(dve):
            ro.pad_vector(dve)
            tr.vector(dve)
            link = linked(dve, ro.step)
            ro.score_vector(dve)
            dve.sem_inc(ro.ready, 1)
            dve.wait_ge(ro.soft_ready, 1)
            ro.first_top(dve, link, ro.soft[:, :, :], 0)
            link(dve.scalar_tensor_tensor(ro.score[:, :, :], ro.hot[0][:, :, :], -2.0, ro.soft[:, :, :],
                                          ALU.mult, ALU.add))
            ro.first_top(dve, link, ro.score[:, :, :], 1)
            link(dve.tensor_tensor(ro.first[:, :], ro.top[0][:, :], ro.top[1][:, :], ALU.add))
            link(dve.reciprocal(ro.first[:, :], ro.first[:, :]))
            for n in range(2):
                link(dve.tensor_tensor(ro.hot[n][:, :, :], ro.hot[n][:, :, :],
                                       spread(ro.top[n][:, :], E2), ALU.mult))
            link(dve.tensor_tensor(ro.hot[0][:, :, :], ro.hot[0][:, :, :], ro.hot[1][:, :, :], ALU.add))
            weight = ro.weight[:, :].rearrange("p (t e) -> p t e", e=8)
            link(dve.tensor_tensor(weight[:, :, 0:E2], ro.hot[0][:, :, :], spread(ro.first[:, :], E2),
                                   ALU.mult))
            link(dve.memset(weight[:, :, E2:8], 1.0))
            ex.vector(dve)

        @block.gpsimd
        def _(pool):
            ro.gpsimd(pool)


def ffn2(k, load_next):
    nc, x = k.nc, k.x
    y = k.spare[:, 0:TILES * D].rearrange("p (t d) -> p t d", d=D)
    with ExitStack() as ctx:
        norm = NormSems(nc, ctx, "l2n")
        y_ready = Signals.new(nc, "l2n_y_ready")
        stats_done = Signals.new(nc, "l2n_stats_done")
        block = ctx.enter_context(nc.Block())

        @block.scalar
        def _(act):
            norm_root_scalar(act, k, norm)

        @block.vector
        def _(dve):
            norm_stats_vector(dve, k, norm)
            for t in range(TILES):
                normalise(dve, k, y[:, t:t + 1, :], t).then_inc(y_ready, 1)
            for t in range(TILES):
                dve.wait_ge(y_ready, t + 1)
                dve.bn_stats(k.stats[:, t, :], y[:, t, :]).then_inc(stats_done, 1)

    k.x = y
    latent_attention(k, load_next)
    experts2(k, lambda sp: None)
    k.x = x


def leave_ffn2(k, folded):
    nc, x = k.nc, k.x
    y = k.spare[:, 0:TILES * D].rearrange("p (t d) -> p t d", d=D)
    with ExitStack() as ctx:
        updated = Signals.new(nc, "l2e_updated")
        stats_done = Signals.new(nc, "l2e_stats_done")
        f = Fold(k, ctx, "l3x", folded)
        loaded = k.loads["even"]
        block = ctx.enter_context(nc.Block())

        @block.tensor
        def _(pe):
            pe.wait_ge(k.load_even, loaded)
            f.tensor(pe)

        @block.scalar
        def _(act):
            f.scalar(act)

        @block.vector
        def _(dve):
            for n in range(QUADS):
                f.vector(dve, n)
                dve.wait_ge(updated, n + 1)
                for j in range(4):
                    last = dve.bn_stats(k.stats[:, 4 * n + j, :], x[:, 4 * n + j, :])
                last.then_inc(stats_done, 1)

        @block.gpsimd
        def _(pool):
            for n in range(QUADS):
                tiles = slice(4 * n, 4 * n + 4)
                pool.tensor_tensor(x[:, tiles, :], x[:, tiles, :], y[:, tiles, :], ALU.add).then_inc(updated, 1)


def shape_constants():
    import numpy as np

    feature = np.arange(P)
    head = np.arange(H)
    own8 = (feature[:, None] // (D // H) == head).astype(np.float32)
    own4 = ((feature[:, None] % 64) // HH == head).astype(np.float32)
    position = np.arange(SEQ, dtype=np.float32)
    freq = (np.float32(1.0) / np.float32(10000.0) ** (np.arange(0, HH, 2, dtype=np.float32) / np.float32(HH)))
    angle = np.einsum("i,j->ji", position, np.concatenate([freq, freq]).astype(np.float32))
    cos, sin = np.ones((P, SEQ), np.float32), np.zeros((P, SEQ), np.float32)
    cos[64:], sin[64:] = np.tile(np.cos(angle), (H, 1)), np.tile(np.sin(angle), (H, 1))
    query = feature[:, None] % SEQ
    causal = np.where(np.arange(SEQ)[None, :] <= query, 0.0, -1e30).astype(np.float32)
    parity = (np.arange(16)[None, :] // 8 == feature[:, None] // SEQ).astype(np.float32)
    return {"const_parity": parity, "const_own8": own8, "const_own4": own4, "const_cos": cos,
            "const_sin": sin, "const_causal": causal}



def start(k, load_next, folded):
    nc = k.nc
    d = k.dram
    with ExitStack() as ctx:
        def sem(name):
            return Signals.new(nc, name)

        consts, ones_at, zeros_at = sem("consts_ready"), sem("ones_ready"), sem("zeros_ready")
        ctxT_done, ctxT_ready, stats_done = sem("ctxT_done"), sem("ctxT_ready"), sem("stats_done")
        PARTS = 4
        PART = TILES // PARTS
        x_in = [sem(f"x_in{i}") for i in range(PARTS)]
        ctx_in = sem("ctx_in")
        peaks_zeroed, peaks_done = sem("peaks_zeroed"), sem("peaks_done")
        ctx_in_order = k.spare[0:SEQ, :].rearrange("p (b c) -> p b c", c=C)
        f = Fold(k, ctx, "l0x", folded)
        block = ctx.enter_context(nc.Block())

        @block.sync
        def _(sp):
            sp.dma_start(ctx_in_order, d["ctx_768"].rearrange("b s c -> s b c")).then_inc(ctx_in, 16)
            load_next(sp)
            xv = d["x"].rearrange("b s d -> (b s) d").rearrange("(t p) d -> p t d", p=P)
            for i in range(PARTS):
                sp.dma_start(k.x[:, i * PART:(i + 1) * PART, :],
                             xv[:, i * PART:(i + 1) * PART, :]).then_inc(x_in[i], 16)

        @block.gpsimd
        def _(pool):
            pool.memset(k.ident[:, :], 0.0).then_inc(zeros_at, 1)
            pool.memset(k.ones[:, :], 1.0).then_inc(ones_at, 1)
            pool.memset(k.eps[:, :], LN_EPS).then_inc(ones_at, 1)
            pool.wait_ge(ones_at, 2)
            pool.wait_ge(zeros_at, 1)
            pool.memset(k.ctxT[C:C + 1, :], 1.0).then_inc(ones_at, 1)
            pool.wait_ge(ones_at, 3)
            pool.affine_select(out=k.ident[:, :], in_=k.ident[:, :], compare_op=ALU.not_equal, fill=1.0,
                               base=0, pattern=[[-1, P]], channel_multiplier=1).then_inc(consts, 1)
            pool.wait_ge(consts, 1)
            pool.tensor_copy(k.identb[:, :], k.ident[:, :]).then_inc(consts, 1)

        @block.tensor
        def _(pe):
            pe.wait_ge(consts, 1)
            pe.wait_ge(ctx_in, 16)
            for n in range(BATCH // 8):
                after(pe, ctxT_ready, n - 1)
                for j in range(8):
                    last = pe.transpose((k.r6, k.r7)[n % 2][0:C, j * SEQ:(j + 1) * SEQ],
                                        ctx_in_order[:, 8 * n + j, :], k.ident[0:SEQ, 0:SEQ])
                last.then_inc(ctxT_done, 1)
            pe.wait_ge(k.load_even, k.loads["even"])
            f.tensor(pe)

        @block.scalar
        def _(act):
            for n in range(BATCH // 8):
                act.wait_ge(ctxT_done, n + 1)
                act.copy(k.ctxT[0:C, n * 512:(n + 1) * 512], (k.r6, k.r7)[n % 2][0:C, :]).then_inc(
                    ctxT_ready, 1)
            f.scalar(act)

        @block.vector
        def _(dve):
            dve.memset(k.ctx_peaks[:, :], 0.0).then_inc(peaks_zeroed, 1)
            dve.wait_ge(peaks_zeroed, 1)
            for n in range(BATCH // 8):
                dve.wait_ge(ctxT_ready, n + 1)
                last = dve.tensor_reduce(k.ctx_peaks[0:C, n:n + 1], k.ctxT[0:C, n * 512:(n + 1) * 512], AX.X,
                                         ALU.max, apply_absolute_value=True)
            last.then_inc(peaks_done, 1)
            for n in range(QUADS):
                f.vector(dve, n)
                dve.wait_ge(x_in[4 * n // PART], 16)
                for t in range(4 * n, 4 * n + 4):
                    last = dve.bn_stats(k.stats[:, t, :], k.x[:, t, :])
                last.then_inc(stats_done, 1)


def four_layers(nc, dram, out):
    with ExitStack() as ctx:
        Signals.live = []
        k = Core(nc, ctx, dram)
        loads = [lambda sp: load_wide(sp, k, "L0_xattn_"), lambda sp: load_ffn0(sp, k),
                 lambda sp: load_attention1(sp, k), lambda sp: load_ffn1(sp, k),
                 lambda sp: load_attention2(sp, k), lambda sp: load_ffn2(sp, k),
                 lambda sp: load_wide(sp, k, "L3_xattn_"), lambda sp: load_ffn3(sp, k), lambda sp: None]

        def layer0(load_next):
            with ExitStack() as inner:
                folded = Folded(k, inner, "l0x")
                start(k, loads[0], folded)
                Signals.retire(nc)
                wide_attention(k, folded, "l0x", load_next)

        def layer3(load_next):
            with ExitStack() as inner:
                folded = Folded(k, inner, "l3x")
                leave_ffn2(k, folded)
                Signals.retire(nc)
                wide_attention(k, folded, "l3x", load_next)

        sublayers = [layer0, lambda n: ffn0(k, n), lambda n: attention1(k, n), lambda n: ffn1(k, n),
                     lambda n: attention2(k, n), lambda n: ffn2(k, n), layer3, lambda n: ffn3(k, out)]
        for i, sublayer in enumerate(sublayers):
            if i:
                Signals.retire(nc)
            sublayer(loads[i + 1])



def kernel(**inputs):
    import numpy as np
    import concourse.bacc as bacc
    from concourse.bass_utils import run_bass_kernel_spmd

    nc = bacc.Bacc("TRN2", target_bir_lowering=False, num_devices=1)
    arrays, dram = {}, {}
    for name, value in {**inputs, **shape_constants()}.items():
        a = np.ascontiguousarray(value)
        arrays[f"in_{name}"] = a
        dram[name] = nc.dram_tensor(f"in_{name}", a.shape, mybir.dt.from_np(a.dtype),
                                    kind="ExternalInput").ap()
    out = nc.dram_tensor("out_x", inputs["x"].shape, F32, kind="ExternalOutput").ap()
    four_layers(nc, dram, out)
    r = run_bass_kernel_spmd(nc, [arrays], core_ids=[0])
    return r.results[0]["out_x"]
```
